# Optimizing a Trainium2 kernel written in Bass

```python
import numpy as np
import jax
import jax.numpy as jnp

def _softmax(x, axis=-1):
    return jax.nn.softmax(x, axis=axis)

def _gelu(x):
    return jax.nn.gelu(x, approximate=True)

def _silu(x):
    return jax.nn.silu(x)

def _sigmoid(x):
    return jax.nn.sigmoid(x)

def _layernorm(x, axis=-1, eps=1e-05):
    m = jnp.mean(x, axis=axis, keepdims=True)
    v = jnp.var(x, axis=axis, keepdims=True)
    return (x - m) / jnp.sqrt(v + eps)

def _scatter_add(tgt, idx, src, axis=0):
    return tgt.at[idx].add(src)

def _segment_sum(src, seg, n):
    return jax.ops.segment_sum(src, seg, n)
kernel_name = 'mk_decoder_preln_d4_seqx_r8_048017'

def setup_inputs(seed: int=0):
    np.random.seed(seed)
    _w = jnp.asarray

    def _rec_inputs():
        import jax
        import jax.numpy as jnp
        _rk = jax.random.key(seed)
        x = -0.0002928 + 1 * jax.random.normal(jax.random.fold_in(_rk, 1), (32, 128, 128), jnp.float32)
        _lenS = 128 - jax.random.randint(jax.random.fold_in(_rk, 7), (32,), 0, max(1, 128 // 4) + 1, jnp.int32)
        _lenS2 = 128 - jax.random.randint(jax.random.fold_in(_rk, 8), (32,), 0, max(1, 128 // 4) + 1, jnp.int32)
        _ctx_1024P = jax.random.normal(jax.random.fold_in(_rk, 11), (32, 16, 128), jnp.float32)
        _ctx_1024c = jax.random.dirichlet(jax.random.fold_in(_rk, 511), 0.3 * jnp.ones((16,), jnp.float32), (32, 128))
        _ctx_1024t = jnp.einsum('bsk,bkd->bsd', _ctx_1024c, _ctx_1024P)
        _ctx_1024t = _ctx_1024t * jax.lax.rsqrt(jnp.mean(jnp.square(_ctx_1024t)) + 1e-12) * 0.953939
        ctx_1024 = -1.39393e-06 + 0.999914 * (_ctx_1024t + 0.3 * jax.random.normal(jax.random.fold_in(_rk, 611), (32, 128, 128), jnp.float32))
        _validS = jnp.arange(128)[None, :] < _lenS[:, None]
        _validS2 = jnp.arange(128)[None, :] < _lenS2[:, None]
        _causal = jnp.tril(jnp.ones((128, 128), dtype=bool))
        mask_Bx1xSxS2_if1 = jnp.where(jnp.ones((32, 1, 128, 128), dtype=bool), 1, 0).astype(jnp.int32)
        mask_BxS2_ik0 = jnp.where(jnp.broadcast_to(_validS2[:, :], (32, 128)), 0, 1).astype(jnp.int32)
        mask_BxS2xS_ik0 = jnp.where(jnp.broadcast_to(_validS[:, None, :], (32, 128, 128)), 0, 1).astype(jnp.int32)
        return (x, ctx_1024, mask_Bx1xSxS2_if1, mask_BxS2_ik0, mask_BxS2xS_ik0)
    x, ctx_1024, mask_Bx1xSxS2_if1, mask_BxS2_ik0, mask_BxS2xS_ik0 = _rec_inputs()

    def _L0_attn_setup():
        import jax, jax.numpy as jnp
        import numpy as np
        NUM_HEADS = 16
        NEG = -1000000000.0

        def _split_heads(t, h):
            *lead, s, hd = t.shape
            return jnp.swapaxes(t.reshape(*lead, s, h, hd // h), -3, -2)
        key = jax.random.key(seed)
        ks = jax.random.split(key, 5)
        B, S, D = (4, 256, 128)
        scale = 1.0 / np.sqrt(D)
        return {'x': jax.random.normal(ks[0], (B, S, D), dtype=jnp.float32), 'WQ': jax.random.normal(ks[1], (D, D), dtype=jnp.float32) * scale, 'WK': jax.random.normal(ks[2], (D, D), dtype=jnp.float32) * scale, 'WV': jax.random.normal(ks[3], (D, D), dtype=jnp.float32) * scale, 'WO': jax.random.normal(ks[4], (D, D), dtype=jnp.float32) * scale}
    _L0_attn_all = _L0_attn_setup()
    _L0_attn_in = {k: v for k, v in _L0_attn_all.items() if k in ('WQ', 'WK', 'WV', 'WO')}
    del _L0_attn_all

    def _L0_xattn_setup():
        import jax, jax.numpy as jnp
        import numpy as np
        HIDDEN = 128
        N_HEAD = 16
        D_HEAD = HIDDEN // N_HEAD
        key = jax.random.key(seed)
        ks = jax.random.split(key, 12)
        B, S, H = (2, 256, HIDDEN)
        scale = 1.0 / np.sqrt(H)
        inp = {'q': jax.random.normal(ks[0], (B, S, H), jnp.float32), 'k': jax.random.normal(ks[1], (B, S, H), jnp.float32), 'v': jax.random.normal(ks[2], (B, S, H), jnp.float32), 'mask': jnp.ones((B, 1, S, S), jnp.int32), 'w_q': jax.random.normal(ks[3], (H, H), jnp.float32) * scale, 'b_q': jnp.zeros((H,), jnp.float32), 'w_k': jax.random.normal(ks[4], (H, H), jnp.float32) * scale, 'b_k': jnp.zeros((H,), jnp.float32), 'w_v': jax.random.normal(ks[5], (H, H), jnp.float32) * scale, 'b_v': jnp.zeros((H,), jnp.float32), 'w_o': jax.random.normal(ks[6], (H, H), jnp.float32) * scale, 'b_o': jnp.zeros((H,), jnp.float32)}
        return inp
    _L0_xattn_all = _L0_xattn_setup()
    _L0_xattn_in = {k: v for k, v in _L0_xattn_all.items() if k in ('w_q', 'b_q', 'w_k', 'b_k', 'w_v', 'b_v', 'w_o', 'b_o')}
    del _L0_xattn_all

    def _L0_ffn_setup():
        import jax, jax.numpy as jnp
        import numpy as np
        TOP_K = 2
        key = jax.random.key(seed)
        kx, kg, k1, k2 = jax.random.split(key, 4)
        B, T, D, E, H = (4, 128, 128, 8, 256)
        x = jax.random.normal(kx, (B, T, D), dtype=jnp.float32)
        Wg = jax.random.normal(kg, (D, E), dtype=jnp.float32) * 0.02
        W1 = jax.random.normal(k1, (E, D, H), dtype=jnp.float32) * 0.02
        W2 = jax.random.normal(k2, (E, H, D), dtype=jnp.float32) * 0.02
        return {'x': x, 'Wg': Wg, 'W1': W1, 'W2': W2}
    _L0_ffn_all = _L0_ffn_setup()
    _L0_ffn_in = {k: v for k, v in _L0_ffn_all.items() if k in ('Wg', 'W1', 'W2')}
    del _L0_ffn_all

    def _L1_attn_setup():
        import jax, jax.numpy as jnp
        import numpy as np
        N_EMBD = 128
        N_HEAD = 8
        HEAD_DIM = N_EMBD // N_HEAD
        EPS = 1e-06

        def _lrpe(xh, theta, n):
            idx = jnp.arange(n, dtype=xh.dtype).reshape(1, n, 1)
            th = theta * idx
            th = th[None]
            return jnp.concatenate([xh * jnp.cos(th), xh * jnp.sin(th)], axis=-1)

        def _srmsnorm(y):
            ms = jnp.mean(jnp.square(y), axis=-1, keepdims=True)
            return y * jax.lax.rsqrt(ms + EPS)
        key = jax.random.key(seed)
        ks = jax.random.split(key, 8)
        b, n = (2, 256)
        x = jax.random.normal(ks[0], (b, n, N_EMBD), dtype=jnp.float32)
        slope_rate = -jax.random.uniform(ks[1], (N_HEAD, 1, 1), dtype=jnp.float32)
        s = 0.02
        qkvu_w = jax.random.normal(ks[2], (4 * N_EMBD, N_EMBD), dtype=jnp.float32) * s
        qkvu_b = jnp.zeros((4 * N_EMBD,), dtype=jnp.float32)
        out_w = jax.random.normal(ks[3], (N_EMBD, N_EMBD), dtype=jnp.float32) * s
        out_b = jnp.zeros((N_EMBD,), dtype=jnp.float32)
        d = N_EMBD
        theta = (10000.0 ** (-2.0 / d * jnp.arange(d, dtype=jnp.float32))).reshape(N_HEAD, 1, HEAD_DIM)
        return {'x': x, 'slope_rate': slope_rate, 'qkvu_w': qkvu_w, 'qkvu_b': qkvu_b, 'out_w': out_w, 'out_b': out_b, 'theta': theta}
    _L1_attn_all = _L1_attn_setup()
    _L1_attn_in = {k: v for k, v in _L1_attn_all.items() if k in ('slope_rate', 'qkvu_w', 'qkvu_b', 'out_w', 'out_b', 'theta')}
    del _L1_attn_all

    def _L1_xattn_setup():
        import jax, jax.numpy as jnp
        import numpy as np
        HEADS = 16
        LOCAL_ATTN_CTX = 128
        BLOCKSIZE = 32

        def _strided_transpose(x, n_ctx, local_attn_ctx):
            bT_ctx = n_ctx // local_attn_ctx
            n, t, e = x.shape
            x = x.reshape(n, bT_ctx, local_attn_ctx, e)
            x = jnp.transpose(x, (0, 2, 1, 3))
            return x.reshape(n, t, e)
        key = jax.random.key(seed)
        kq, kk, kv = jax.random.split(key, 3)
        shape = (4, 512, 128)
        return {'q': jax.random.normal(kq, shape, dtype=jnp.float32), 'k': jax.random.normal(kk, shape, dtype=jnp.float32), 'v': jax.random.normal(kv, shape, dtype=jnp.float32)}
    _L1_xattn_all = _L1_xattn_setup()
    _L1_xattn_in = {k: v for k, v in _L1_xattn_all.items() if k in ()}
    del _L1_xattn_all

    def _L1_ffn_setup():
        import jax, jax.numpy as jnp
        import numpy as np
        N_HEADS = 4
        key = jax.random.key(seed)
        k1, k2, k3, k4 = jax.random.split(key, 4)
        dmodel, n_experts, expert_size = (128, 64, 128)
        B, S = (4, 256)
        x = jax.random.normal(k1, (B, S, dmodel), dtype=jnp.float32)
        expert_sel = jax.random.normal(k2, (n_experts, dmodel), dtype=jnp.float32) * dmodel ** (-0.5)
        keys = jax.random.normal(k3, (n_experts, dmodel, expert_size), dtype=jnp.float32) * dmodel ** (-0.5)
        values = jax.random.normal(k4, (n_experts, expert_size, dmodel), dtype=jnp.float32) * (n_experts * expert_size) ** (-0.5)
        return {'x': x, 'expert_sel': expert_sel, 'keys': keys, 'values': values}
    _L1_ffn_all = _L1_ffn_setup()
    _L1_ffn_in = {k: v for k, v in _L1_ffn_all.items() if k in ('expert_sel', 'keys', 'values')}
    del _L1_ffn_all

    def _L2_attn_setup():
        import jax, jax.numpy as jnp
        import numpy as np
        B, T, D, H = (4, 128, 128, 16)
        key = jax.random.key(seed)
        ks = jax.random.split(key, 7)
        x = jax.random.normal(ks[0], (B, T, D), dtype=jnp.float32)
        scale = 0.02
        Wq = jax.random.normal(ks[1], (D, D), dtype=jnp.float32) * scale
        Wk = jax.random.normal(ks[2], (D, D), dtype=jnp.float32) * scale
        Wv = jax.random.normal(ks[3], (D, D), dtype=jnp.float32) * scale
        bq = jax.random.normal(ks[4], (D,), dtype=jnp.float32) * scale
        bk = jax.random.normal(ks[5], (D,), dtype=jnp.float32) * scale
        bv = jax.random.normal(ks[6], (D,), dtype=jnp.float32) * scale
        temperature = jnp.ones((H, 1, 1), dtype=jnp.float32)
        return {'x': x, 'Wq': Wq, 'bq': bq, 'Wk': Wk, 'bk': bk, 'Wv': Wv, 'bv': bv, 'temperature': temperature}
    _L2_attn_all = _L2_attn_setup()
    _L2_attn_in = {k: v for k, v in _L2_attn_all.items() if k in ('Wq', 'bq', 'Wk', 'bk', 'Wv', 'bv', 'temperature')}
    del _L2_attn_all

    def _L2_xattn_setup():
        import jax, jax.numpy as jnp
        import numpy as np
        B, S, H = (2, 256, 128)
        NUM_HEAD = 16
        HEAD = H // NUM_HEAD
        NEG = -10000000000.0
        key = jax.random.key(seed)
        ks = jax.random.split(key, 10)
        scale = 1.0 / np.sqrt(H)
        return {'query': jax.random.normal(ks[0], (B, S, H), jnp.float32), 'key': jax.random.normal(ks[1], (B, S, H), jnp.float32), 'value': jax.random.normal(ks[2], (B, S, H), jnp.float32), 'mask': jax.random.randint(ks[3], (B, S), 0, 2, jnp.int32), 'Wq': jax.random.normal(ks[4], (H, H), jnp.float32) * scale, 'bq': jnp.zeros((H,), jnp.float32), 'Wk': jax.random.normal(ks[5], (H, H), jnp.float32) * scale, 'bk': jnp.zeros((H,), jnp.float32), 'Wv': jax.random.normal(ks[6], (H, H), jnp.float32) * scale, 'bv': jnp.zeros((H,), jnp.float32)}
    _L2_xattn_all = _L2_xattn_setup()
    _L2_xattn_in = {k: v for k, v in _L2_xattn_all.items() if k in ('Wq', 'bq', 'Wk', 'bk', 'Wv', 'bv')}
    del _L2_xattn_all

    def _L2_ffn_setup():
        import jax, jax.numpy as jnp
        import numpy as np
        B, S, D, H, DOUT, E, K = (4, 256, 128, 128, 128, 8, 2)
        key = jax.random.key(seed)
        k1, k2, k3, k4 = jax.random.split(key, 4)
        x = jax.random.normal(k1, (B, S, D), dtype=jnp.float32)
        Wr = jax.random.normal(k2, (D, E), dtype=jnp.float32) * 0.02
        Wi = jax.random.normal(k3, (E, D, H), dtype=jnp.float32) * 0.02
        Wo = jax.random.normal(k4, (E, H, DOUT), dtype=jnp.float32) * 0.02
        return {'x': x, 'Wr': Wr, 'Wi': Wi, 'Wo': Wo}
    _L2_ffn_all = _L2_ffn_setup()
    _L2_ffn_in = {k: v for k, v in _L2_ffn_all.items() if k in ('Wr', 'Wi', 'Wo')}
    del _L2_ffn_all

    def _L3_attn_setup():
        import jax, jax.numpy as jnp
        import numpy as np
        import math
        B, S, D = (4, 256, 128)
        H = 16
        HD = D // H
        DL = 32
        LAMBDA_DECAY = 0.01
        key = jax.random.key(seed)
        ks = jax.random.split(key, 8)
        sc = lambda fan_in: 1.0 / math.sqrt(fan_in)
        return {'x': jax.random.normal(ks[0], (B, S, D), dtype=jnp.float32), 'W_q': jax.random.normal(ks[1], (D, D), dtype=jnp.float32) * sc(D), 'W_k': jax.random.normal(ks[2], (D, D), dtype=jnp.float32) * sc(D), 'W_v': jax.random.normal(ks[3], (D, D), dtype=jnp.float32) * sc(D), 'W_o': jax.random.normal(ks[4], (D, D), dtype=jnp.float32) * sc(D), 'W_down_kv': jax.random.normal(ks[5], (D, DL), dtype=jnp.float32) * sc(D), 'W_up_k': jax.random.normal(ks[6], (DL, D), dtype=jnp.float32) * sc(DL), 'W_up_v': jax.random.normal(ks[7], (DL, D), dtype=jnp.float32) * sc(DL)}
    _L3_attn_all = _L3_attn_setup()
    _L3_attn_in = {k: v for k, v in _L3_attn_all.items() if k in ('W_q', 'W_k', 'W_v', 'W_o', 'W_down_kv', 'W_up_k', 'W_up_v')}
    del _L3_attn_all

    def _L3_xattn_setup():
        import jax, jax.numpy as jnp
        import numpy as np
        B, T, V, C = (32, 32, 125, 128)
        H, DH = (8, 64)
        INNER = H * DH
        K = 5
        SCALE = DH ** (-0.5)

        def layer_norm(x, w, b, eps=1e-05):
            mu = jnp.mean(x, axis=-1, keepdims=True)
            var = jnp.mean(jnp.square(x - mu), axis=-1, keepdims=True)
            return (x - mu) * jax.lax.rsqrt(var + eps) * w + b
        key = jax.random.key(seed)
        ks = jax.random.split(key, 8)
        x = jax.random.normal(ks[0], (B, T, C), dtype=jnp.float32)
        vision = jax.random.normal(ks[1], (B, V, C), dtype=jnp.float32)
        idx = jax.random.randint(ks[2], (B, T, K), 0, V)
        mask = jnp.zeros((B, V, T), jnp.int32)
        mask = mask.at[jnp.arange(B)[:, None, None], idx, jnp.arange(T)[None, :, None]].set(1)
        Wq = jax.random.normal(ks[3], (C, INNER), dtype=jnp.float32) * 0.02
        Wkv = jax.random.normal(ks[4], (C, 2 * INNER), dtype=jnp.float32) * 0.02
        Wout = jax.random.normal(ks[5], (INNER, C), dtype=jnp.float32) * 0.02
        return {'x': x, 'vision': vision, 'ln_w': jnp.ones((C,), jnp.float32), 'ln_b': jnp.zeros((C,), jnp.float32), 'Wq': Wq, 'Wkv': Wkv, 'Wout': Wout, 'attention_mask': mask, 'num_support': K}
    _L3_xattn_all = _L3_xattn_setup()
    _L3_xattn_in = {k: v for k, v in _L3_xattn_all.items() if k in ('ln_w', 'ln_b', 'Wq', 'Wkv', 'Wout')}
    del _L3_xattn_all

    def _L3_ffn_setup():
        import jax, jax.numpy as jnp
        import numpy as np
        EPS = 1e-05

        def rmsnorm(x):
            var = jnp.mean(jnp.square(x), axis=-1, keepdims=True)
            return x * jax.lax.rsqrt(var + 1e-06)

        def activation_quant(x):
            scale = 127.0 / jnp.clip(jnp.max(jnp.abs(x), axis=-1, keepdims=True), EPS, None)
            return jnp.clip(jnp.round(x * scale), -128, 127) / scale

        def weight_quant(w):
            scale = 1.0 / jnp.clip(jnp.mean(jnp.abs(w)), EPS, None)
            return jnp.clip(jnp.round(w * scale), -1, 1) / scale

        def bitlinear(x, w, b):
            xn = rmsnorm(x)
            xq = xn + jax.lax.stop_gradient(activation_quant(xn) - xn)
            wq = w + jax.lax.stop_gradient(weight_quant(w) - w)
            return jnp.einsum('bsi,oi->bso', xq, wq) + b
        key = jax.random.key(seed)
        k1, k2, k3 = jax.random.split(key, 3)
        B, S, D, H = (4, 256, 128, 512)
        x = jax.random.normal(k1, (B, S, D), dtype=jnp.float32)
        w1 = jax.random.normal(k2, (H, D), dtype=jnp.float32) * D ** (-0.5)
        b1 = jnp.zeros((H,), dtype=jnp.float32)
        w2 = jax.random.normal(k3, (D, H), dtype=jnp.float32) * H ** (-0.5)
        b2 = jnp.zeros((D,), dtype=jnp.float32)
        return {'x': x, 'w1': w1, 'b1': b1, 'w2': w2, 'b2': b2}
    _L3_ffn_all = _L3_ffn_setup()
    _L3_ffn_in = {k: v for k, v in _L3_ffn_all.items() if k in ('w1', 'b1', 'w2', 'b2')}
    del _L3_ffn_all
    return {'x': x, 'ctx_1024': ctx_1024, 'mask_Bx1xSxS2_if1': mask_Bx1xSxS2_if1, 'mask_BxS2_ik0': mask_BxS2_ik0, 'mask_BxS2xS_ik0': mask_BxS2xS_ik0, 'L0_attn_WQ': _L0_attn_in['WQ'], 'L0_attn_WK': _L0_attn_in['WK'], 'L0_attn_WV': _L0_attn_in['WV'], 'L0_attn_WO': _L0_attn_in['WO'], 'L0_xattn_w_q': _L0_xattn_in['w_q'], 'L0_xattn_b_q': _L0_xattn_in['b_q'], 'L0_xattn_w_k': _L0_xattn_in['w_k'], 'L0_xattn_b_k': _L0_xattn_in['b_k'], 'L0_xattn_w_v': _L0_xattn_in['w_v'], 'L0_xattn_b_v': _L0_xattn_in['b_v'], 'L0_xattn_w_o': _L0_xattn_in['w_o'], 'L0_xattn_b_o': _L0_xattn_in['b_o'], 'L0_ffn_Wg': _L0_ffn_in['Wg'], 'L0_ffn_W1': _L0_ffn_in['W1'], 'L0_ffn_W2': _L0_ffn_in['W2'], 'L1_attn_slope_rate': _L1_attn_in['slope_rate'], 'L1_attn_qkvu_w': _L1_attn_in['qkvu_w'], 'L1_attn_qkvu_b': _L1_attn_in['qkvu_b'], 'L1_attn_out_w': _L1_attn_in['out_w'], 'L1_attn_out_b': _L1_attn_in['out_b'], 'L1_attn_theta': _L1_attn_in['theta'], 'L1_ffn_expert_sel': _L1_ffn_in['expert_sel'], 'L1_ffn_keys': _L1_ffn_in['keys'], 'L1_ffn_values': _L1_ffn_in['values'], 'L2_attn_Wq': _L2_attn_in['Wq'], 'L2_attn_bq': _L2_attn_in['bq'], 'L2_attn_Wk': _L2_attn_in['Wk'], 'L2_attn_bk': _L2_attn_in['bk'], 'L2_attn_Wv': _L2_attn_in['Wv'], 'L2_attn_bv': _L2_attn_in['bv'], 'L2_attn_temperature': _L2_attn_in['temperature'], 'L2_xattn_Wq': _L2_xattn_in['Wq'], 'L2_xattn_bq': _L2_xattn_in['bq'], 'L2_xattn_Wk': _L2_xattn_in['Wk'], 'L2_xattn_bk': _L2_xattn_in['bk'], 'L2_xattn_Wv': _L2_xattn_in['Wv'], 'L2_xattn_bv': _L2_xattn_in['bv'], 'L2_ffn_Wr': _L2_ffn_in['Wr'], 'L2_ffn_Wi': _L2_ffn_in['Wi'], 'L2_ffn_Wo': _L2_ffn_in['Wo'], 'L3_attn_W_q': _L3_attn_in['W_q'], 'L3_attn_W_k': _L3_attn_in['W_k'], 'L3_attn_W_v': _L3_attn_in['W_v'], 'L3_attn_W_o': _L3_attn_in['W_o'], 'L3_attn_W_down_kv': _L3_attn_in['W_down_kv'], 'L3_attn_W_up_k': _L3_attn_in['W_up_k'], 'L3_attn_W_up_v': _L3_attn_in['W_up_v'], 'L3_xattn_ln_w': _L3_xattn_in['ln_w'], 'L3_xattn_ln_b': _L3_xattn_in['ln_b'], 'L3_xattn_Wq': _L3_xattn_in['Wq'], 'L3_xattn_Wkv': _L3_xattn_in['Wkv'], 'L3_xattn_Wout': _L3_xattn_in['Wout'], 'L3_ffn_w1': _L3_ffn_in['w1'], 'L3_ffn_b1': _L3_ffn_in['b1'], 'L3_ffn_w2': _L3_ffn_in['w2'], 'L3_ffn_b2': _L3_ffn_in['b2']}

def reference(x, ctx_1024, mask_Bx1xSxS2_if1, mask_BxS2_ik0, mask_BxS2xS_ik0, L0_attn_WQ, L0_attn_WK, L0_attn_WV, L0_attn_WO, L0_xattn_w_q, L0_xattn_b_q, L0_xattn_w_k, L0_xattn_b_k, L0_xattn_w_v, L0_xattn_b_v, L0_xattn_w_o, L0_xattn_b_o, L0_ffn_Wg, L0_ffn_W1, L0_ffn_W2, L1_attn_slope_rate, L1_attn_qkvu_w, L1_attn_qkvu_b, L1_attn_out_w, L1_attn_out_b, L1_attn_theta, L1_ffn_expert_sel, L1_ffn_keys, L1_ffn_values, L2_attn_Wq, L2_attn_bq, L2_attn_Wk, L2_attn_bk, L2_attn_Wv, L2_attn_bv, L2_attn_temperature, L2_xattn_Wq, L2_xattn_bq, L2_xattn_Wk, L2_xattn_bk, L2_xattn_Wv, L2_xattn_bv, L2_ffn_Wr, L2_ffn_Wi, L2_ffn_Wo, L3_attn_W_q, L3_attn_W_k, L3_attn_W_v, L3_attn_W_o, L3_attn_W_down_kv, L3_attn_W_up_k, L3_attn_W_up_v, L3_xattn_ln_w, L3_xattn_ln_b, L3_xattn_Wq, L3_xattn_Wkv, L3_xattn_Wout, L3_ffn_w1, L3_ffn_b1, L3_ffn_w2, L3_ffn_b2):
    import jax
    import jax.numpy as jnp

    def _L0_attn_ref(x, WQ, WK, WV, WO):
        import jax, jax.numpy as jnp
        import numpy as np
        NUM_HEADS = 16
        NEG = -1000000000.0

        def _split_heads(t, h):
            *lead, s, hd = t.shape
            return jnp.swapaxes(t.reshape(*lead, s, h, hd // h), -3, -2)
        h = NUM_HEADS
        S = x.shape[-2]
        Q = _split_heads(x @ WQ.T, h)
        K = _split_heads(x @ WK.T, h)
        V = _split_heads(x @ WV.T, h)
        dk = Q.shape[-1]
        scores = jnp.einsum('bhqd,bhkd->bhqk', Q, K) / jnp.sqrt(jnp.float32(dk))
        causal = jnp.tril(jnp.ones((S, S), dtype=bool))
        scores = jnp.where(causal, scores, NEG)
        m = jnp.max(scores, axis=-1, keepdims=True)
        e = jnp.exp(scores - m)
        attn = e / jnp.sum(e, axis=-1, keepdims=True)
        out = jnp.einsum('bhqk,bhkd->bhqd', attn, V)
        out = jnp.swapaxes(out, -3, -2).reshape(*x.shape[:-1], -1)
        return out @ WO.T

    def _L0_xattn_ref(q, k, v, mask, w_q, b_q, w_k, b_k, w_v, b_v, w_o, b_o):
        import jax, jax.numpy as jnp
        import numpy as np
        HIDDEN = 128
        N_HEAD = 16
        D_HEAD = HIDDEN // N_HEAD
        B, Sq, H = q.shape
        Sk = k.shape[1]
        qh = (q @ w_q + b_q).reshape(B, Sq, N_HEAD, D_HEAD).transpose(0, 2, 1, 3)
        kh = (k @ w_k + b_k).reshape(B, Sk, N_HEAD, D_HEAD).transpose(0, 2, 1, 3)
        vh = (v @ w_v + b_v).reshape(B, Sk, N_HEAD, D_HEAD).transpose(0, 2, 1, 3)
        scores = jnp.einsum('bhqd,bhkd->bhqk', qh, kh) * D_HEAD ** (-0.5)
        scores = jnp.where(mask == 0, jnp.float32(-10000.0), scores)
        attn = jax.nn.softmax(scores, axis=-1)
        out = jnp.einsum('bhqk,bhkd->bhqd', attn, vh)
        out = out.transpose(0, 2, 1, 3).reshape(B, Sq, H)
        return out @ w_o + b_o

    def _L0_ffn_ref(x, Wg, W1, W2):
        import jax, jax.numpy as jnp
        import numpy as np
        TOP_K = 2
        B, T, D = x.shape
        E = W1.shape[0]
        logits = jnp.einsum('btd,de->bte', x, Wg)
        probs = jax.nn.softmax(logits, axis=-1)
        top_w, top_i = jax.lax.top_k(probs, TOP_K)
        top_w = top_w / (jnp.sum(top_w, axis=-1, keepdims=True) + 1e-08)
        N = B * T
        oh = jax.nn.one_hot(top_i.reshape(N, TOP_K), E, dtype=x.dtype)
        combine = jnp.sum(oh * top_w.reshape(N, TOP_K)[..., None], axis=1)
        xt = x.reshape(N, D)
        h = jnp.einsum('td,edh->teh', xt, W1)
        h = jnp.square(jax.nn.relu(h))
        y = jnp.einsum('teh,ehd->ted', h, W2)
        out = jnp.einsum('te,ted->td', combine, y)
        return out.reshape(B, T, D)

    def _L1_attn_ref(x, slope_rate, qkvu_w, qkvu_b, out_w, out_b, theta):
        import jax, jax.numpy as jnp
        import numpy as np
        N_EMBD = 128
        N_HEAD = 8
        HEAD_DIM = N_EMBD // N_HEAD
        EPS = 1e-06

        def _lrpe(xh, theta, n):
            idx = jnp.arange(n, dtype=xh.dtype).reshape(1, n, 1)
            th = theta * idx
            th = th[None]
            return jnp.concatenate([xh * jnp.cos(th), xh * jnp.sin(th)], axis=-1)

        def _srmsnorm(y):
            ms = jnp.mean(jnp.square(y), axis=-1, keepdims=True)
            return y * jax.lax.rsqrt(ms + EPS)
        b, n, hd = x.shape
        h = N_HEAD
        qkvu = x @ qkvu_w.T + qkvu_b
        q, k, v, u = jnp.split(qkvu, 4, axis=-1)

        def to_heads(t):
            return t.reshape(b, n, h, hd // h).transpose(0, 2, 1, 3)
        q, k, v = (to_heads(q), to_heads(k), to_heads(v))
        q = jax.nn.silu(q)
        k = jax.nn.silu(k)
        q = _lrpe(q, theta, n)
        k = _lrpe(k, theta, n)
        tril = jnp.tril(jnp.ones((n, n), dtype=x.dtype))
        mask = jnp.exp(slope_rate * tril)
        energy = jnp.einsum('bhne,bhme->bhnm', q, k) * mask[None]
        out = jnp.einsum('bhnm,bhmd->bhnd', energy, v)
        out = out.transpose(0, 2, 1, 3).reshape(b, n, hd)
        out = _srmsnorm(out)
        out = u * out
        out = out @ out_w.T + out_b
        return out

    def _L1_xattn_ref(q, k, v):
        import jax, jax.numpy as jnp
        import numpy as np
        HEADS = 16
        LOCAL_ATTN_CTX = 128
        BLOCKSIZE = 32

        def _strided_transpose(x, n_ctx, local_attn_ctx):
            bT_ctx = n_ctx // local_attn_ctx
            n, t, e = x.shape
            x = x.reshape(n, bT_ctx, local_attn_ctx, e)
            x = jnp.transpose(x, (0, 2, 1, 3))
            return x.reshape(n, t, e)
        n_ctx = q.shape[1]
        q = _strided_transpose(q, n_ctx, LOCAL_ATTN_CTX)
        k = _strided_transpose(k, n_ctx, LOCAL_ATTN_CTX)
        v = _strided_transpose(v, n_ctx, LOCAL_ATTN_CTX)
        n_state = q.shape[-1] // HEADS
        scale = 1.0 / np.sqrt(n_state)
        w = jnp.einsum('nte,nse->nts', q, k)
        w = jax.nn.softmax(w * scale, axis=-1)
        a = jnp.einsum('nts,nse->nte', w, v)
        n, t, e = a.shape
        bT_ctx = n_ctx // LOCAL_ATTN_CTX
        a = a.reshape(n, LOCAL_ATTN_CTX, bT_ctx, e)
        a = jnp.transpose(a, (0, 2, 1, 3))
        return a.reshape(n, t, e)

    def _L1_ffn_ref(x, expert_sel, keys, values):
        import jax, jax.numpy as jnp
        import numpy as np
        N_HEADS = 4
        B, S, d = x.shape
        n_experts = keys.shape[0]
        xf = x.reshape(-1, d)
        N = xf.shape[0]
        logits = xf @ expert_sel.T
        sel = jax.nn.sigmoid(logits)
        sel_val, sel_idx = jax.lax.top_k(sel, N_HEADS)
        gates = jnp.zeros((N, n_experts), dtype=x.dtype)
        gates = gates.at[jnp.arange(N)[:, None], sel_idx].set(sel_val)
        h = jnp.einsum('nd,kde->nke', xf, keys)
        scores = jax.nn.relu(h) * gates[:, :, None]
        out = jnp.einsum('nke,kev->nv', scores, values)
        return out.reshape(B, S, -1)

    def _L2_attn_ref(x, Wq, bq, Wk, bk, Wv, bv, temperature):
        import jax, jax.numpy as jnp
        import numpy as np
        B, T, D, H = (4, 128, 128, 16)
        b, t, d = x.shape
        h = temperature.shape[0]
        dh = d // h
        q = (x @ Wq + bq).reshape(b, h, dh, t)
        k = (x @ Wk + bk).reshape(b, h, dh, t)
        v = (x @ Wv + bv).reshape(b, h, dh, t)
        attn = jnp.einsum('bhdt,bhds->bhts', k, v) * temperature
        attn = jax.nn.softmax(attn, axis=-1)
        out = jnp.einsum('bhdt,bhts->bhds', q, attn)
        return out.reshape(b, t, d)

    def _L2_xattn_ref(query, key, value, mask, Wq, bq, Wk, bk, Wv, bv):
        import jax, jax.numpy as jnp
        import numpy as np
        B, S, H = (2, 256, 128)
        NUM_HEAD = 16
        HEAD = H // NUM_HEAD
        NEG = -10000000000.0
        b, s, h = query.shape

        def proj(x, W, bias):
            y = x @ W.T + bias
            return y.reshape(b, s, NUM_HEAD, HEAD).transpose(0, 2, 1, 3)
        q = proj(query, Wq, bq)
        k = proj(key, Wk, bk)
        v = proj(value, Wv, bv)
        attn_score = jnp.einsum('bhqd,bhkd->bhqk', q, k)
        bias_add = jnp.where(mask[:, None, None, :] == 0, NEG, 0.0).astype(attn_score.dtype)
        attn_score = attn_score + bias_add
        attn_ratio = jax.nn.softmax(attn_score, axis=-1)
        out = jnp.einsum('bhqk,bhkd->bhqd', attn_ratio, v)
        out = out.transpose(0, 2, 1, 3).reshape(b, s, h)
        return out

    def _L2_ffn_ref(x, Wr, Wi, Wo):
        import jax, jax.numpy as jnp
        import numpy as np
        B, S, D, H, DOUT, E, K = (4, 256, 128, 128, 128, 8, 2)
        b, s, d = x.shape
        e_cnt, _, h = Wi.shape
        dout = Wo.shape[2]
        xf = x.reshape(-1, d)
        T = xf.shape[0]
        probs = jax.nn.softmax(xf @ Wr, axis=-1)
        topk_p, topk_i = jax.lax.top_k(probs, K)
        mask = topk_i[:, :, None] == jnp.arange(e_cnt)[None, None, :]
        hmix = jnp.zeros((T, K, h), dtype=xf.dtype)
        for e in range(e_cnt):
            he = xf @ Wi[e]
            hmix = hmix + jnp.where(mask[:, :, e][:, :, None], he[:, None, :], 0.0)
        o = jnp.zeros((T, K, dout), dtype=xf.dtype)
        for e in range(e_cnt):
            oe = jnp.einsum('tkh,hd->tkd', hmix, Wo[e])
            o = o + jnp.where(mask[:, :, e][:, :, None], oe, 0.0)
        out = jnp.sum(o * topk_p[:, :, None], axis=1)
        return out.reshape(b, s, dout)

    def _L3_attn_ref(x, W_q, W_k, W_v, W_o, W_down_kv, W_up_k, W_up_v):
        import jax, jax.numpy as jnp
        import numpy as np
        import math
        B, S, D = (4, 256, 128)
        H = 16
        HD = D // H
        DL = 32
        LAMBDA_DECAY = 0.01
        b, s, d = x.shape
        q = x @ W_q
        k = x @ W_k
        v = x @ W_v
        latent_kv = (k + v) @ W_down_kv
        k_rec = (latent_kv @ W_up_k).reshape(b, s, H, HD).transpose(0, 2, 1, 3)
        v_rec = (latent_kv @ W_up_v).reshape(b, s, H, HD).transpose(0, 2, 1, 3)
        qh = q.reshape(b, s, H, HD).transpose(0, 2, 1, 3)
        scores = jnp.einsum('bhqd,bhkd->bhqk', qh, k_rec) / math.sqrt(d)
        t = jnp.arange(s, dtype=jnp.float32)
        decay = jnp.exp(-LAMBDA_DECAY * jnp.abs(t[:, None] - t[None, :]))
        scores = scores * decay[None, None, :, :]
        attn = jax.nn.softmax(scores, axis=-1)
        out = jnp.einsum('bhqk,bhkd->bhqd', attn, v_rec)
        out = out.transpose(0, 2, 1, 3).reshape(b, s, d)
        return out @ W_o

    def _L3_xattn_ref(x, vision, ln_w, ln_b, Wq, Wkv, Wout, attention_mask, num_support):
        import jax, jax.numpy as jnp
        import numpy as np
        B, T, V, C = (32, 32, 125, 128)
        H, DH = (8, 64)
        INNER = H * DH
        K = 5
        SCALE = DH ** (-0.5)

        def layer_norm(x, w, b, eps=1e-05):
            mu = jnp.mean(x, axis=-1, keepdims=True)
            var = jnp.mean(jnp.square(x - mu), axis=-1, keepdims=True)
            return (x - mu) * jax.lax.rsqrt(var + eps) * w + b
        Bb, Tt, Cc = x.shape
        Vv = vision.shape[1]
        am_t = jnp.transpose(attention_mask, (0, 2, 1))
        idxs = jnp.where(am_t != 0, jnp.arange(Vv, dtype=jnp.int32), Vv)
        padded = -jax.lax.top_k(-idxs, num_support)[0]
        vision_pad = jnp.concatenate([vision, jnp.zeros((Bb, 1, Cc), vision.dtype)], axis=1)
        vg = vision_pad[jnp.arange(Bb)[:, None, None], padded]
        valid = padded != Vv
        xn = layer_norm(x, ln_w, ln_b)
        q = jnp.einsum('btc,ce->bte', xn, Wq) * SCALE
        kv = jnp.einsum('btkc,ce->btke', vg, Wkv)
        k, v = jnp.split(kv, 2, axis=-1)
        qh = q.reshape(Bb, Tt, H, DH)
        kh = k.reshape(Bb, Tt, num_support, H, DH)
        vh = v.reshape(Bb, Tt, num_support, H, DH)
        sim = jnp.einsum('bthd,btkhd->bthk', qh, kh)
        sim = sim + jnp.where(valid, 0.0, -10000.0)[:, :, None, :]
        attn = jax.nn.softmax(sim, axis=-1)
        attn = attn * valid[:, :, None, :].astype(attn.dtype)
        out = jnp.einsum('bthk,btkhd->bthd', attn, vh).reshape(Bb, Tt, INNER)
        return jnp.einsum('bte,ec->btc', out, Wout)

    def _L3_ffn_ref(x, w1, b1, w2, b2):
        import jax, jax.numpy as jnp
        import numpy as np
        EPS = 1e-05

        def rmsnorm(x):
            var = jnp.mean(jnp.square(x), axis=-1, keepdims=True)
            return x * jax.lax.rsqrt(var + 1e-06)

        def activation_quant(x):
            scale = 127.0 / jnp.clip(jnp.max(jnp.abs(x), axis=-1, keepdims=True), EPS, None)
            return jnp.clip(jnp.round(x * scale), -128, 127) / scale

        def weight_quant(w):
            scale = 1.0 / jnp.clip(jnp.mean(jnp.abs(w)), EPS, None)
            return jnp.clip(jnp.round(w * scale), -1, 1) / scale

        def bitlinear(x, w, b):
            xn = rmsnorm(x)
            xq = xn + jax.lax.stop_gradient(activation_quant(xn) - xn)
            wq = w + jax.lax.stop_gradient(weight_quant(w) - w)
            return jnp.einsum('bsi,oi->bso', xq, wq) + b
        h = bitlinear(x, w1, b1)
        h = jax.nn.gelu(h, approximate=False)
        return bitlinear(h, w2, b2)
    x = x + _L0_attn_ref(_layernorm(x, axis=-1), L0_attn_WQ, L0_attn_WK, L0_attn_WV, L0_attn_WO)
    x = x + _L0_xattn_ref(_layernorm(x, axis=-1), ctx_1024, ctx_1024, mask_Bx1xSxS2_if1, L0_xattn_w_q, L0_xattn_b_q, L0_xattn_w_k, L0_xattn_b_k, L0_xattn_w_v, L0_xattn_b_v, L0_xattn_w_o, L0_xattn_b_o)
    x = x + _L0_ffn_ref(_layernorm(x, axis=-1), L0_ffn_Wg, L0_ffn_W1, L0_ffn_W2)
    x = x + _L1_attn_ref(_layernorm(x, axis=-1), L1_attn_slope_rate, L1_attn_qkvu_w, L1_attn_qkvu_b, L1_attn_out_w, L1_attn_out_b, L1_attn_theta)
    x = x + _L1_xattn_ref(_layernorm(x, axis=-1), ctx_1024, ctx_1024)
    x = x + _L1_ffn_ref(_layernorm(x, axis=-1), L1_ffn_expert_sel, L1_ffn_keys, L1_ffn_values)
    x = x + _L2_attn_ref(_layernorm(x, axis=-1), L2_attn_Wq, L2_attn_bq, L2_attn_Wk, L2_attn_bk, L2_attn_Wv, L2_attn_bv, L2_attn_temperature)
    x = x + _L2_xattn_ref(_layernorm(x, axis=-1), ctx_1024, ctx_1024, mask_BxS2_ik0, L2_xattn_Wq, L2_xattn_bq, L2_xattn_Wk, L2_xattn_bk, L2_xattn_Wv, L2_xattn_bv)
    x = x + _L2_ffn_ref(_layernorm(x, axis=-1), L2_ffn_Wr, L2_ffn_Wi, L2_ffn_Wo)
    x = x + _L3_attn_ref(_layernorm(x, axis=-1), L3_attn_W_q, L3_attn_W_k, L3_attn_W_v, L3_attn_W_o, L3_attn_W_down_kv, L3_attn_W_up_k, L3_attn_W_up_v)
    x = x + _L3_xattn_ref(_layernorm(x, axis=-1), ctx_1024, L3_xattn_ln_w, L3_xattn_ln_b, L3_xattn_Wq, L3_xattn_Wkv, L3_xattn_Wout, mask_BxS2xS_ik0, 5)
    x = x + _L3_ffn_ref(_layernorm(x, axis=-1), L3_ffn_w1, L3_ffn_b1, L3_ffn_w2, L3_ffn_b2)
    return x

_drawn_inputs = setup_inputs


def setup_inputs(seed=0):
    import zlib

    import numpy as np

    out = dict(_drawn_inputs(seed))
    spreads = {'L0_xattn_b_q': (0.0, 0.278),
     'L0_xattn_b_k': (0.0, 0.8),
     'L0_xattn_b_v': (0.0, 0.1),
     'L0_xattn_b_o': (0.0, 0.1),
     'L1_attn_qkvu_b': (0.0, 0.1),
     'L1_attn_out_b': (0.0, 0.1),
     'L2_attn_temperature': (1.0, 0.6),
     'L2_xattn_bq': (0.0, 0.1),
     'L2_xattn_bk': (0.0, 0.8),
     'L2_xattn_bv': (0.0, 0.1),
     'L3_xattn_ln_w': (1.0, 0.6),
     'L3_xattn_ln_b': (0.0, 0.8),
     'L3_ffn_b1': (0.0, 0.1),
     'L3_ffn_b2': (0.0, 0.1)}
    factors = {'L0_ffn_Wg': 3.72,
     'L0_ffn_W1': 3.619,
     'L0_ffn_W2': 3.356,
     'L1_attn_slope_rate': 6.202,
     'L2_attn_Wq': 5.185,
     'L2_attn_bq': 8.0,
     'L2_attn_Wk': 8.0,
     'L2_attn_bk': 8.0,
     'L2_attn_Wv': 8.0,
     'L2_attn_bv': 8.0,
     'L2_ffn_Wr': 8.0,
     'L2_ffn_Wi': 7.914,
     'L2_ffn_Wo': 7.974,
     'L3_xattn_Wq': 8.0,
     'L3_xattn_Wkv': 5.174,
     'L3_xattn_Wout': 4.967}
    for name, (base, spread) in spreads.items():
        noise = np.random.default_rng([zlib.crc32(name.encode()), seed]).standard_normal(out[name].shape)
        drawn = base * np.exp(spread * noise) if base else spread * noise
        out[name] = jnp.asarray(drawn.astype(out[name].dtype))
    for name, factor in factors.items():
        out[name] = (out[name] * factor).astype(out[name].dtype)
    return out
```

```python
import numpy as np
from contextlib import ExitStack

import concourse.bass as bass
import concourse.mybir as mybir

F32 = mybir.dt.float32
BF16 = mybir.dt.bfloat16
I32 = mybir.dt.int32
U32 = mybir.dt.uint32
ALU = mybir.AluOpType
ACT = mybir.ActivationFunctionType
AX = mybir.AxisListType.X

B, S, D = 32, 128, 128
G = 4
NG = B // G
GT = G * S
H, HD = 16, 8
QUADS, PER = 4, 4
LN_EPS = 1e-5
MASKED = -2.0 ** 100
ds = bass.ds


class Count:

    def __init__(self, sem):
        self.sem, self.base, self.per = sem, 0, 0

    def at(self, g, n):
        return self.sem, g * self.per + (self.base + n)


class Program:

    def __init__(self, nc, ctx, inputs):
        self.nc, self.ctx, self.inputs = nc, ctx, inputs
        self.counts = {}

    def count_of(self, name):
        if name not in self.counts:
            self.counts[name] = Count(self.ctx.enter_context(self.nc.semaphore(name)))
        return self.counts[name]

    def plan(self, **per):
        for name, n in per.items():
            self.count_of(name).per = n
        return [self.count_of(name) for name in per]

    def passed(self, passes):
        for s in self.counts.values():
            s.base += s.per * passes
            s.per = 0


def sb(p, ctx, name, shape, dt=F32):
    return ctx.enter_context(p.nc.sbuf_tensor(name, shape, dt))


class Chain:

    def __init__(self, eng, steps, g=0):
        self.eng, self.steps, self.g, self.n = eng, steps, g, 0

    def __call__(self, instruction):
        self.n += 1
        instruction.then_inc(self.steps.sem, 1)
        self.eng.wait_ge(*self.steps.at(self.g, self.n))

    def ends(self):
        assert self.n == self.steps.per, (self.steps.sem, self.n, self.steps.per)



def load_all(p):
    nc, ctx, ins = p.nc, p.ctx, p.inputs
    p.x = sb(p, ctx, "x_res", [128, B * D])
    p.stats = sb(p, ctx, "row_stats", [128, B, 6])
    p.rstd = sb(p, ctx, "ln_scale", [128, B])
    p.shift = sb(p, ctx, "ln_shift", [128, B])
    p.ident = sb(p, ctx, "ident", [128, 128])
    p.ident_bf = sb(p, ctx, "ident_bf", [128, 128], BF16)
    p.head_mask = sb(p, ctx, "head_mask", [128, PER])
    p.bank = [ctx.enter_context(nc.psum_tensor(f"bank{i}", [128, GT], F32)) for i in range(8)]
    p.w = {}

    def weight(name, shape, src=None):
        p.w[name] = sb(p, ctx, "w_" + name, shape)
        return p.w[name], ins[src or name]

    square = ["L0_attn_WQ", "L0_attn_WK", "L0_attn_WV", "L0_attn_WO", "L0_xattn_w_q", "L0_xattn_w_k",
              "L0_xattn_w_v", "L0_xattn_w_o", "L2_attn_Wq", "L2_attn_Wk", "L2_attn_Wv",
              "L2_xattn_Wq", "L2_xattn_Wk", "L2_xattn_Wv", "L3_attn_W_q", "L3_attn_W_o", "L1_attn_out_w"]
    loads = [weight(n, [128, 128]) for n in square]
    for n in ["L0_xattn_b_q", "L0_xattn_b_k", "L2_attn_bq", "L2_xattn_bq", "L2_xattn_bk",
              "L3_xattn_ln_w", "L3_xattn_ln_b"]:
        t, src = weight(n, [128, 1])
        loads.append((t, src.rearrange("(p a) -> p a", a=1)))
    rows = {"L0_xattn_b_v": 128, "L0_xattn_b_o": 128, "L1_attn_out_b": 128, "L2_attn_bk": 128,
            "L2_attn_bv": 128, "L2_xattn_bv": 128, "L3_ffn_b1": 512, "L3_ffn_b2": 128}
    for n, width in rows.items():
        t, src = weight(n, [128, width])
        loads.append((t, src.rearrange("(a n) -> a n", a=1).to_broadcast([128, width])))
    loads.append(weight("L0_ffn_Wg", [128, 8]))
    loads.append(weight("L2_ffn_Wr", [128, 8]))
    loads.append(weight("L1_ffn_sel", [128, 64]))
    loads.append(weight("L3_xattn_Wq", [128, 512]))
    loads.append(weight("L3_xattn_Wkv", [128, 1024]))
    loads.append(weight("L3_xattn_Wout", [128, 4, 128]))
    loads.append(weight("L1_attn_qk", [128, 4, 128]))
    loads.append(weight("L1_attn_vu", [128, 2, 128]))
    loads.append(weight("L1_attn_qk_b", [128, 4]))
    loads.append(weight("L1_attn_theta", [128, 2]))
    t, src = weight("L1_attn_vb", [128, 128])
    loads.append((t, src.rearrange("(a n) -> a n", a=1).to_broadcast([128, 128])))
    loads.append(weight("L1_attn_ub", [128, 1]))
    t, src = weight("L1_attn_slope", [128, 8])
    loads.append((t, src.rearrange("(a n) -> a n", a=1).to_broadcast([128, 8])))
    loads.append(weight("L2_attn_temp", [128, 1]))
    loads.append(weight("L3_attn_W_k_T", [128, 128]))
    loads.append(weight("L3_attn_W_v_T", [128, 128]))
    loads.append(weight("L3_attn_W_down_kv", [128, 32]))
    loads.append(weight("L3_attn_W_up_k", [32, 128]))
    loads.append(weight("L3_attn_W_up_v", [32, 128]))
    p.w["L2_ffn_M"] = sb(p, ctx, "w_L2_ffn_M", [128, 8, 128])
    p.w["L3_K"] = sb(p, ctx, "w_L3_K", [128, 128])
    p.w["L3_V"] = sb(p, ctx, "w_L3_V", [128, 128])
    p.w["L2_vmask"] = sb(p, ctx, "L2_vmask", [128, PER])

    x_in, w_in, ones_m = (p.count_of(n) for n in ("x_in", "weights_in", "constant_steps"))
    with nc.Block(no_gpsimd_drain=True) as block:
        @block.sync
        def _(sp):
            for i in range(4):
                sp.dma_start(p.x[:, i * 1024:(i + 1) * 1024], ins["x"][:, i * 1024:(i + 1) * 1024]).then_inc(x_in.sem, 16)
            for t, src in loads:
                sp.dma_start(t[:], src).then_inc(w_in.sem, 16)
            sp.wait_ge(w_in.sem, 16 * len(loads))

        @block.gpsimd
        def _(pool):
            then = Chain(pool, ones_m)
            then(nc.gpsimd.memset(p.ident[:], 0.0))
            then(nc.gpsimd.memset(p.head_mask[:], 1.0))
            then(nc.gpsimd.affine_select(out=p.ident[:], in_=p.ident[:], compare_op=ALU.not_equal, fill=1.0, base=0,
                                         pattern=[[-1, 128]], channel_multiplier=1))
            for j in range(QUADS):
                rows = p.head_mask[32 * j:32 * j + 32, :]
                then(nc.gpsimd.affine_select(out=rows, in_=rows, compare_op=ALU.is_ge, fill=0.0, base=0,
                                             pattern=[[-HD, PER]], channel_multiplier=1))
                then(nc.gpsimd.affine_select(out=rows, in_=rows, compare_op=ALU.is_ge, fill=0.0, base=HD - 1,
                                             pattern=[[HD, PER]], channel_multiplier=-1))

        @block.vector
        def _(dve):
            dve.wait_ge(ones_m.sem, 3)
            nc.vector.tensor_copy(p.ident_bf[:], p.ident[:])
            dve.wait_ge(x_in.sem, 64)
            for b in range(B):
                nc.vector.bn_stats(p.stats[:, b, :], p.x[:, b * D:(b + 1) * D])


def norm_rows(p, name, again=None):
    nc = p.nc
    steps, var_ready, root_ready = p.count_of("norm_steps"), p.count_of("variance_ready"), p.count_of("root_ready")
    rounds = 2 if again else 1
    with ExitStack() as ctx:
        a, b, var, y, h, mean, root, veps = (
            sb(p, ctx, f"{name}_norm_{k}", [128, B]) for k in ("a", "b", "var", "y", "h", "mean", "root", "veps"))
        with nc.Block(no_gpsimd_drain=True) as block:
            @block.scalar
            def _(act):
                for r in range(rounds):
                    act.wait_ge(*var_ready.at(0, r + 1))
                    nc.scalar.activation(root[:], veps[:], ACT.Sqrt).then_inc(root_ready.sem, 1)

            @block.vector
            def _(dve):
                then = Chain(dve, steps)
                v = nc.vector

                def inverse_root(out, r):
                    dve.wait_ge(*root_ready.at(0, r + 1))
                    then(v.reciprocal(y[:], root[:]))
                    then(v.tensor_tensor(h[:], y[:], y[:], ALU.mult))
                    then(v.tensor_tensor(h[:], h[:], veps[:], ALU.mult))
                    then(v.tensor_scalar(h[:], h[:], -0.5, 1.5, ALU.mult, ALU.add))
                    then(v.tensor_tensor(out[:], y[:], h[:], ALU.mult))

                me, mo, qe, qo = (p.stats[:, :, i] for i in (1, 4, 2, 5))
                then(v.tensor_tensor(mean[:], me, mo, ALU.add))
                then(v.tensor_tensor(a[:], me, mo, ALU.subtract))
                then(v.tensor_tensor(b[:], qe, qo, ALU.add))
                then(v.tensor_tensor(a[:], a[:], a[:], ALU.mult))
                then(v.tensor_scalar(b[:], b[:], 1.0 / D, None, ALU.mult))
                then(v.scalar_tensor_tensor(var[:], a[:], 0.25, b[:], ALU.mult, ALU.add))
                v.tensor_scalar(veps[:], var[:], LN_EPS, None, ALU.add).then_inc(var_ready.sem, 1)
                inverse_root(p.rstd, 0)
                then(v.tensor_tensor(a[:], mean[:], p.rstd[:], ALU.mult))
                then(v.tensor_scalar(p.shift[:], a[:], -0.5, None, ALU.mult))
                if again:
                    then(v.tensor_tensor(a[:], p.rstd[:], p.rstd[:], ALU.mult))
                    then(v.tensor_tensor(a[:], a[:], var[:], ALU.mult))
                    v.tensor_scalar(veps[:], a[:], again, None, ALU.add).then_inc(var_ready.sem, 1)
                    inverse_root(a, 1)
                    then(v.tensor_tensor(p.rstd[:], p.rstd[:], a[:], ALU.mult))
                    then(v.tensor_tensor(p.shift[:], p.shift[:], a[:], ALU.mult))
                steps.base += then.n
    var_ready.base += rounds
    root_ready.base += rounds



def rows_of_x(p, g, b, n=1):
    return p.x[:, ds(g * (G * D) + b * D, n * D)]


def normalise(p, dve, g, xn, xn_ready):
    for b in range(G):
        one = ds(g * G + b, 1)
        p.nc.vector.tensor_scalar(xn[:, b * D:(b + 1) * D], rows_of_x(p, g, b), p.rstd[:, one], p.shift[:, one],
                                  ALU.mult, ALU.add).then_inc(xn_ready.sem, 1)


def transpose_xn(p, pe, g, xn, xn_ready, bank, xnT_psum):
    for b in range(G):
        pe.wait_ge(*xn_ready.at(g, b + 1))
        last = p.nc.tensor.transpose(bank[:, b * S:(b + 1) * S], xn[:, b * D:(b + 1) * D], p.ident[:])
    last.then_inc(xnT_psum.sem, 1)


def row_statistics(p, dve, g, x_done):
    dve.wait_ge(*x_done.at(g, 1))
    for b in range(G):
        p.nc.vector.bn_stats(p.stats[:, ds(g * G + b, 1), :].rearrange("p a s -> p (a s)"), rows_of_x(p, g, b))


def batch(b):
    return slice(b * S, (b + 1) * S)


UNITS = 4 * G


def all_groups(eng, units):
    units(0, 0, UNITS, True, False)
    with eng.Fori(0, NG // 2 - 1) as i:
        units(i * 2 + 1, 1, UNITS, False, False)
        units(i * 2 + 2, 0, UNITS, False, False)
    units(NG - 1, 1, UNITS, False, True)
    units(NG, 0, 0, False, True)


def before(g, a, u, lag):
    return (g, a, u - lag) if u >= lag else (g - 1, 1 - a, u - lag + UNITS)



def attention16(p, name, w_q, w_k, w_v, w_o=None, cross=False, b_q=None, b_k=None, b_v=None, b_o=None,
                scale=1.0, causal=False, where_mask=False, key_mask=False, decay=False):
    nc, ins = p.nc, p.inputs
    norm_rows(p, name)
    U = UNITS
    (xn_ready, xnT_psum, xnT_ready, q_psum, k_psum, v_psum, q_ready, k_ready, kmask_ready, v_ready, s_psum, max_ready,
     p_ready, t_psum, pt_ready, av_psum, r_ready, rT_psum, rT_ready, oT_ready, y_psum, x_done) = p.plan(
        xn_ready=G, xnT_psum=1, xnT_ready=1, q_psum=1, k_psum=1, v_psum=1, q_ready=1, k_ready=1, kmask_ready=U,
        v_ready=1, s_psum=U, max_ready=U, p_ready=U, t_psum=U, pt_ready=U, av_psum=G, r_ready=G,
        rT_psum=1, rT_ready=1, oT_ready=1, y_psum=1, x_done=1)
    ctx_in, mask_in, mask_ready, prep_ready = p.plan(ctx_in=16 * cross, mask_in=16 * (key_mask + 2 * where_mask),
                                                     mask_ready=(key_mask or 2 * where_mask), stage_prepared=0)
    raw_max, decayed, floor_steps, e_in, e_ready, z_psum, z_ready, ze_ready, sum_ready = p.plan(
        raw_max=U * where_mask, decayed=U * decay, floor_steps=4 * where_mask, masked_shift_ready=G * where_mask,
        masked_exp_ready=G * where_mask, masked_v_psum=where_mask, masked_v_ready=where_mask,
        masked_v_scaled=G * where_mask, masked_sum_steps=G * where_mask)
    r_steps, bias_added = p.plan(reciprocal_steps=G, bias_added=bool(b_o))
    w = p.w
    S_BANK, T_BANK, M_BANK, O_BANK = p.bank[0:4], p.bank[4:6], p.bank[6], p.bank[7]
    masked = causal or where_mask or key_mask

    with ExitStack() as ctx:
        t = lambda k, shape, dt=F32: sb(p, ctx, f"{name}_{k}", shape, dt)
        xn, xnT, qT, kT = t("xn", [128, GT]), t("xnT", [128, GT]), t("qT", [128, 2, GT]), t("kT", [128, 2, GT])
        ctxT = t("ctxT", [128, GT]) if cross else xnT
        kmask = t("kmask", [128, 2, QUADS, PER * S])
        vpad = t("vpad", [128, 2, G * H * 32])
        nmax, rsum, rrec = t("nmax", [128, G, H]), t("rsum", [128, G, H]), t("rrec", [128, G, H])
        probs = t("probs", [128, 4, PER * S])
        probsT = t("probsT", [128, 2, QUADS, PER * S])
        rrep, rT, oT = t("rrep", [128, GT]), t("rT", [128, GT]), t("oT", [128, GT])
        scaled_mask = t("scaled_mask", [128, H])
        spare = t("spare", [128, 1])
        if masked:
            score_bias = t("score_bias", [128, 1 if causal else 2, 1 if causal else G, S], BF16)
        if key_mask or where_mask:
            mask_q = t("mask_q", [128, G, S], I32)
        if where_mask:
            mask_k, masked_k = t("mask_k", [128, G * S], I32), t("masked_k", [128, G * S])
            least, nfloor, count = (t(k, [128, 2, G]) for k in ("least", "nfloor", "count"))
            rowmax, eshift, e = (t(k, [128, G, H]) for k in ("rowmax", "eshift", "e"))
            z, ze = t("masked_v", [128, 2, GT]), t("masked_v_scaled", [128, G, D])
        if decay:
            decay_m, distance = t("decay", [128, S]), t("distance", [128, S])
            scored = t("scored", [128, 4, PER * S])

        def head_slots(a, b=None):
            q = vpad[:, a, :] if b is None else vpad[:, a, b * H * 32:(b + 1) * H * 32]
            return bass.AP(q.tensor, q.offset, [list(q.ap[0]), [128, QUADS * (G if b is None else 1)], [40, PER], [1, HD]])

        with nc.Block(no_gpsimd_drain=True) as block:
            @block.gpsimd
            def _(pool):
                then = Chain(pool, prep_ready)
                then(nc.gpsimd.memset(vpad[:], 0.0))
                then(nc.gpsimd.memset(spare[:], 0.0))
                then(nc.gpsimd.memset(scaled_mask[:], scale))
                then(nc.gpsimd.affine_select(out=scaled_mask[:], in_=scaled_mask[:], compare_op=ALU.is_ge, fill=0.0, base=0,
                                             pattern=[[-HD, H]], channel_multiplier=1))
                then(nc.gpsimd.affine_select(out=scaled_mask[:], in_=scaled_mask[:], compare_op=ALU.is_ge, fill=0.0,
                                             base=HD - 1, pattern=[[HD, H]], channel_multiplier=-1))
                if causal:
                    then(nc.gpsimd.memset(score_bias[:], 0.0))
                    then(nc.gpsimd.affine_select(out=score_bias[:, 0, 0, :], in_=score_bias[:, 0, 0, :], compare_op=ALU.is_ge,
                                                 fill=MASKED, base=0, pattern=[[-1, S]], channel_multiplier=1))
                if decay:
                    then(nc.gpsimd.iota(distance[:], pattern=[[1, S]], base=0, channel_multiplier=-1,
                                        allow_small_or_imprecise_dtypes=True))

            if decay:
                @block.scalar
                def _(act):
                    act.wait_ge(*prep_ready.at(0, 6))
                    nc.scalar.activation(decay_m[:], distance[:], ACT.Abs).then_inc(prep_ready.sem, 1)
                    act.wait_ge(*prep_ready.at(0, 7))
                    nc.scalar.activation(decay_m[:], decay_m[:], ACT.Exp, scale=-0.01)
        prep_ready.base += 5 + 2 * causal + 2 * decay

        AFTER = 6

        with nc.Block(no_gpsimd_drain=True) as block:
            if cross:
                @block.sync
                def _(sp):
                    def load(g):
                        sp.dma_start(ctxT[:], ins["ctx_T"][:, ds(g * GT, GT)]).then_inc(ctx_in.sem, 16)
                        if key_mask:
                            sp.dma_start(mask_q[:], ins["key_mask"].rearrange("(a b) k -> a b k", a=1)[:, ds(g * G, G), :]
                                         .to_broadcast([128, G, S])).then_inc(mask_in.sem, 16)
                        if where_mask:
                            sp.dma_start(mask_q[:].rearrange("p b k -> p (b k)"), ins["mask_qk"][:, ds(g * GT, GT)]).then_inc(mask_in.sem, 16)
                            sp.dma_start(mask_k[:], ins["mask_kq"][:, ds(g * GT, GT)]).then_inc(mask_in.sem, 16)
                    load(0)
                    with sp.Fori(1, NG) as g:
                        sp.wait_ge(*s_psum.at(g - 1, 1))
                        load(g)

            @block.gpsimd
            def _(pool):
                def masks(g, a):
                    if key_mask or where_mask:
                        pool.wait_ge(*mask_in.at(g, mask_in.per))
                        nc.gpsimd.tensor_tensor(spare[:], spare[:], spare[:], ALU.mult)
                        nc.gpsimd.tensor_scalar(score_bias[:, a].rearrange("p b k -> p (b k)"), mask_q[:].rearrange("p b k -> p (b k)"),
                                                0.0, -1e10 if key_mask else MASKED,
                                                ALU.is_equal, ALU.mult).then_inc(mask_ready.sem, 1)
                    if where_mask:
                        nc.gpsimd.tensor_scalar(masked_k[:], mask_k[:], 0.0, None, ALU.is_equal).then_inc(mask_ready.sem, 1)

                def units(g, a, steps, first, last):
                    if first:
                        masks(g, a)
                    for u in range(steps):
                        b, j = u // 4, u % 4
                        if u == 0:
                            pool.wait_ge(*k_ready.at(g, 1))
                        if not (first and u < 8):
                            pool.wait_ge(*s_psum.at(g, u - 7))
                        if u == 11 and not last:
                            masks(g + 1, 1 - a)
                        nc.gpsimd.tensor_tensor(kmask[:, b % 2, j].rearrange("p (c k) -> p c k", c=PER),
                                                kT[:, a, batch(b)].unsqueeze(1).to_broadcast([128, PER, S]),
                                                scaled_mask[:, PER * j:PER * j + PER].unsqueeze(2).to_broadcast([128, PER, S]),
                                                ALU.mult).then_inc(kmask_ready.sem, 1)
                all_groups(pool, units)

            @block.tensor
            def _(pe):
                mm = nc.tensor.matmul

                def scores(g, a, u, first):
                    b, j = u // 4, u % 4
                    pe.wait_ge(*kmask_ready.at(g, u + 1))
                    if u == 0:
                        pe.wait_ge(*q_ready.at(g, 1))
                        if where_mask or key_mask:
                            pe.wait_ge(*mask_ready.at(g, 1))
                    if not (first and u < 4):
                        pe.wait_ge(*(decayed if decay else p_ready).at(g, u - 3))
                    if masked:
                        bias = score_bias[:, 0, 0, :] if causal else score_bias[:, a, b, :]
                        mm(S_BANK[j][:], lhsT=p.ident_bf[:], rhs=bias.unsqueeze(1).to_broadcast([128, PER, S]),
                           start=True, stop=False)
                    mm(S_BANK[j][:], lhsT=qT[:, a, batch(b)], rhs=kmask[:, b % 2, j],
                       start=not masked, stop=True).then_inc(s_psum.sem, 1)

                def transposes(g, a, u, first):
                    pe.wait_ge(*p_ready.at(g, u + 1))
                    if not (first and u < 2):
                        pe.wait_ge(*pt_ready.at(g, u - 1))
                    for c in range(PER):
                        last = nc.tensor.transpose(T_BANK[u % 2][:, batch(c)], probs[:, u % 4, batch(c)], p.ident[:])
                    last.then_inc(t_psum.sem, 1)

                def values(g, a, b, first):
                    pe.wait_ge(*pt_ready.at(g, 4 * b + 4))
                    if b == 0:
                        pe.wait_ge(*v_ready.at(g, 1))
                        if not first:
                            pe.wait_ge(*oT_ready.at(g, 0))
                    if where_mask:
                        pe.wait_ge(*ze_ready.at(g, b + 1))
                        mm(O_BANK[:, batch(b)], lhsT=ze[:, b, :], rhs=p.ident[:], start=True, stop=False,
                           skip_group_check=True)
                    for c in range(PER):
                        for j in range(QUADS):
                            s = (b * H + j * PER + c) * 32
                            last = mm(O_BANK[32 * j:32 * j + 32, batch(b)], lhsT=vpad[:, a, s:s + 32],
                                      rhs=probsT[:, b % 2, j, batch(c)], start=(c == 0 and not where_mask),
                                      stop=(c == PER - 1), tile_position=(0, 32 * j), skip_group_check=True)
                    last.then_inc(av_psum.sem, 1)

                def front(g, a, step):
                    if step == 0:
                        transpose_xn(p, pe, g, xn, xn_ready, M_BANK, xnT_psum)
                    if step == 1:
                        pe.wait_ge(*xnT_ready.at(g, 1))
                        mm(M_BANK[:], lhsT=w[w_q][:], rhs=xnT[:], start=True, stop=True).then_inc(q_psum.sem, 1)
                    if step == 2:
                        if cross:
                            pe.wait_ge(*ctx_in.at(g, 16))
                        pe.wait_ge(*q_ready.at(g, 1))
                        mm(M_BANK[:], lhsT=w[w_k][:], rhs=ctxT[:], start=True, stop=True).then_inc(k_psum.sem, 1)
                    if step == 3:
                        pe.wait_ge(*k_ready.at(g, 1))
                        for b in range(G):
                            last = mm(M_BANK[:, batch(b)], lhsT=ctxT[:, batch(b)], rhs=w[w_v][:], start=True, stop=True)
                        last.then_inc(v_psum.sem, 1)
                    if step == 4 and where_mask:
                        pe.wait_ge(*mask_ready.at(g, 2))
                        pe.wait_ge(*v_ready.at(g, 1))
                        for b in range(G):
                            last = mm(M_BANK[:, batch(b)], lhsT=masked_k[:, batch(b)], rhs=head_slots(a, b),
                                      start=True, stop=True)
                        last.then_inc(z_psum.sem, 1)

                def divisors(g):
                    pe.wait_ge(*r_ready.at(g, G))
                    for b in range(G):
                        last = nc.tensor.transpose(M_BANK[:, batch(b)], rrep[:, batch(b)], p.ident[:])
                    last.then_inc(rT_psum.sem, 1)

                def outputs(g):
                    pe.wait_ge(*oT_ready.at(g, 1))
                    for b in range(G):
                        if w_o:
                            last = mm(M_BANK[:, batch(b)], lhsT=oT[:, batch(b)], rhs=w[w_o][:], start=True, stop=True)
                        else:
                            last = nc.tensor.transpose(M_BANK[:, batch(b)], oT[:, batch(b)], p.ident[:])
                    last.then_inc(y_psum.sem, 1)

                def units(g, a, steps, first, last):
                    if first:
                        for step in range(5):
                            front(g, a, step)
                    for u in range(steps or AFTER):
                        if steps:
                            scores(g, a, u, first)
                        if steps or u < 2:
                            if not (first and u < 2):
                                h, ha, hu = before(g, a, u, 2)
                                transposes(h, ha, hu, first)
                        if u % 4 == 2 and not (first and u < 6) and not (not steps and u > 2):
                            h, ha, hu = before(g, a, u, 6)
                            values(h, ha, hu // 4, first)
                        if u == 2 and not first:
                            if steps:
                                pe.wait_ge(*(z_ready if where_mask else v_ready).at(g, 1))
                            divisors(g - 1)
                        if u == 4 and not first:
                            outputs(g - 1)
                        if not last:
                            if u == 6 and not first:
                                pe.wait_ge(*x_done.at(g - 1, 1))
                            if u == 6 and first:
                                pe.wait_ge(*(z_ready if where_mask else v_ready).at(g, 1))
                            for step, at in enumerate((6, 8, 9, 10, 12)):
                                if u == at:
                                    front(g + 1, 1 - a, step)
                all_groups(pe, units)

            @block.scalar
            def _(act):
                def units(g, a, steps, first, last):
                    def start(g, a):
                        act.wait_ge(*xnT_psum.at(g, 1))
                        nc.scalar.activation(xnT[:], M_BANK[:], ACT.Copy).then_inc(xnT_ready.sem, 1)

                    def masked_values(g, a):
                        act.wait_ge(*z_psum.at(g, 1))
                        nc.scalar.activation(z[:, a, :], M_BANK[:], ACT.Copy).then_inc(z_ready.sem, 1)

                    if first:
                        start(g, a)
                        if where_mask:
                            masked_values(g, a)
                    for u in range(steps or AFTER):
                        if steps:
                            b, j = u // 4, u % 4
                            act.wait_ge(*max_ready.at(g, u + 1))
                            if not (first and u < 4):
                                act.wait_ge(*t_psum.at(g, u - 3))
                            src = scored[:, u % 4, :] if decay else S_BANK[j][:]
                            for c in range(PER):
                                h = 4 * j + c
                                done = nc.scalar.activation(probs[:, u % 4, batch(c)], src[:, batch(c)], ACT.Exp,
                                                            bias=nmax[:, b, h:h + 1], accum_out=rsum[:, b, h:h + 1])
                            done.then_inc(p_ready.sem, 1)
                            if where_mask and j == 3:
                                act.wait_ge(*e_in.at(g, b + 1))
                                nc.scalar.activation(e[:, b, :], eshift[:, b, :], ACT.Exp).then_inc(e_ready.sem, 1)
                        if u == 2 and not first:
                            act.wait_ge(*rT_psum.at(g - 1, 1))
                            nc.scalar.activation(rT[:], M_BANK[:], ACT.Copy).then_inc(rT_ready.sem, 1)
                        if u == 6 and not last:
                            start(g + 1, 1 - a)
                        if u == 12 and not last and where_mask:
                            masked_values(g + 1, 1 - a)
                nc.scalar.preload_act_table(ACT.Exp)
                all_groups(act, units)

            @block.vector
            def _(dve):
                v = nc.vector

                def row_max(g, a, u, first):
                    b, j = u // 4, u % 4
                    dve.wait_ge(*s_psum.at(g, u + 1))
                    heads = slice(4 * j, 4 * j + 4)
                    src = S_BANK[j][:].rearrange("p (c k) -> p c k", c=PER)
                    if decay:
                        if not (first and u < 4):
                            dve.wait_ge(*p_ready.at(g, u - 3))
                        out = scored[:, u % 4, :].rearrange("p (c k) -> p c k", c=PER)
                        v.tensor_tensor(out, src, decay_m[:].unsqueeze(1).to_broadcast([128, PER, S]),
                                        ALU.mult).then_inc(decayed.sem, 1)
                        dve.wait_ge(*decayed.at(g, u + 1))
                        src = out
                    if where_mask:
                        v.tensor_reduce(rowmax[:, b, heads], src, axis=AX, op=ALU.max, negate=True).then_inc(raw_max.sem, 1)
                        dve.wait_ge(*raw_max.at(g, u + 1))
                        v.tensor_scalar(nmax[:, b, heads], rowmax[:, b, heads], nfloor[:, a, b:b + 1], None,
                                        ALU.min).then_inc(max_ready.sem, 1)
                        if j == 3:
                            dve.wait_ge(*max_ready.at(g, u + 1))
                            v.tensor_scalar(eshift[:, b, :], nmax[:, b, :], 1e4, -1e4, ALU.min, ALU.add).then_inc(e_in.sem, 1)
                    else:
                        v.tensor_reduce(nmax[:, b, heads], src, axis=AX, op=ALU.max, negate=True).then_inc(max_ready.sem, 1)

                def copy_out(g, a, u, first):
                    b, j = u // 4, u % 4
                    dve.wait_ge(*t_psum.at(g, u + 1))
                    if j == 0 and not (first and b < 2):
                        dve.wait_ge(*av_psum.at(g, b - 1))
                    v.tensor_copy(probsT[:, b % 2, j, :], T_BANK[u % 2][:]).then_inc(pt_ready.sem, 1)

                def reciprocals(g, b):
                    dve.wait_ge(*p_ready.at(g, 4 * b + 4))
                    if where_mask:
                        dve.wait_ge(*sum_ready.at(g, b + 1))
                    v.reciprocal(rrec[:, b, :], rsum[:, b, :]).then_inc(r_steps.sem, 1)
                    dve.wait_ge(*r_steps.at(g, b + 1))
                    v.tensor_copy(rrep[:, batch(b)].rearrange("p (h d) -> p h d", h=H),
                                  rrec[:, b, :].unsqueeze(2).to_broadcast([128, H, HD])).then_inc(r_ready.sem, 1)

                def masked_terms(g, a, b):
                    dve.wait_ge(*e_ready.at(g, b + 1))
                    if b == 0:
                        dve.wait_ge(*z_ready.at(g, 1))
                    v.tensor_tensor(ze[:, b, :].rearrange("p (h d) -> p h d", h=H),
                                    z[:, a, batch(b)].rearrange("p (h d) -> p h d", h=H),
                                    e[:, b, :].unsqueeze(2).to_broadcast([128, H, HD]), ALU.mult).then_inc(ze_ready.sem, 1)
                    v.scalar_tensor_tensor(rsum[:, b, :], e[:, b, :], count[:, a, b:b + 1], rsum[:, b, :],
                                           ALU.mult, ALU.add).then_inc(sum_ready.sem, 1)

                def floors(g, a):
                    dve.wait_ge(*mask_ready.at(g, 1))
                    v.tensor_reduce(least[:, a], score_bias[:, a], axis=AX, op=ALU.add).then_inc(floor_steps.sem, 1)
                    dve.wait_ge(*floor_steps.at(g, 1))
                    v.tensor_scalar(count[:, a], least[:, a], 1.0 / MASKED, None, ALU.mult).then_inc(floor_steps.sem, 1)
                    v.tensor_scalar(nfloor[:, a], least[:, a], 0.0, -3e38, ALU.is_lt, ALU.mult).then_inc(floor_steps.sem, 1)
                    dve.wait_ge(*floor_steps.at(g, 3))
                    v.tensor_scalar(nfloor[:, a], nfloor[:, a], 3e38, 1e4, ALU.add, ALU.max).then_inc(floor_steps.sem, 1)
                    dve.wait_ge(*floor_steps.at(g, 4))

                def projected(out, bias, psum, ready, g):
                    dve.wait_ge(*psum.at(g, 1))
                    if bias:
                        v.tensor_scalar(out, M_BANK[:], w[bias][:, 0:1], None, ALU.add).then_inc(ready.sem, 1)
                    else:
                        v.tensor_copy(out, M_BANK[:]).then_inc(ready.sem, 1)

                def front(g, a, step):
                    if step == 0:
                        normalise(p, dve, g, xn, xn_ready)
                    if step == 1 and where_mask:
                        floors(g, a)
                    if step == 2:
                        projected(qT[:, a, :], b_q, q_psum, q_ready, g)
                    if step == 3:
                        projected(kT[:, a, :], b_k, k_psum, k_ready, g)
                    if step == 4:
                        dve.wait_ge(*v_psum.at(g, 1))
                        if b_v:
                            for b in range(G):
                                last = v.tensor_tensor(head_slots(a, b), M_BANK[:, batch(b)].rearrange("p (j c d) -> p j c d", j=QUADS, c=PER),
                                                       w[b_v][:].rearrange("p (j c d) -> p j c d", j=QUADS, c=PER), ALU.add)
                        else:
                            last = v.tensor_copy(head_slots(a), M_BANK[:].rearrange("p (j c d) -> p j c d", j=QUADS * G, c=PER))
                        last.then_inc(v_ready.sem, 1)

                def divided(g):
                    dve.wait_ge(*rT_ready.at(g, 1))
                    dve.wait_ge(*av_psum.at(g, G))
                    v.tensor_tensor(oT[:], O_BANK[:], rT[:], ALU.mult).then_inc(oT_ready.sem, 1)

                def output_bias(g):
                    for b in range(G):
                        last = v.tensor_tensor(rows_of_x(p, g, b), rows_of_x(p, g, b), w[b_o][:], ALU.add)
                    last.then_inc(bias_added.sem, 1)

                def add_output(g):
                    if b_o:
                        dve.wait_ge(*bias_added.at(g, 1))
                    dve.wait_ge(*y_psum.at(g, 1))
                    v.tensor_tensor(rows_of_x(p, g, 0, G), rows_of_x(p, g, 0, G), M_BANK[:], ALU.add).then_inc(x_done.sem, 1)

                def units(g, a, steps, first, last):
                    if first:
                        for step in range(5):
                            front(g, a, step)
                    for u in range(steps or AFTER + 1):
                        if steps:
                            row_max(g, a, u, first)
                        if u % 4 == 1 and not (first and u < 5) and (steps or u == 1):
                            h, ha, hu = before(g, a, u, 5)
                            if where_mask:
                                masked_terms(h, ha, hu // 4)
                        if not (first and u < 2) and (steps or u < 2):
                            copy_out(*before(g, a, u, 2), first)
                        if u % 4 == 1 and not (first and u < 5) and (steps or u == 1):
                            reciprocals(h, hu // 4)
                        if not first:
                            if u == 2 and b_o:
                                output_bias(g - 1)
                            if u == 3:
                                divided(g - 1)
                            if u == 5:
                                add_output(g - 1)
                            if u == 6:
                                row_statistics(p, dve, g - 1, x_done)
                        if not last:
                            for step, at in enumerate((4, 8, 9, 10, 11)):
                                if u == at:
                                    front(g + 1, 1 - a, step)
                all_groups(dve, units)
        p.passed(NG)


def front(p, name, ctx):
    return sb(p, ctx, f"{name}_xn", [128, GT]), sb(p, ctx, f"{name}_xnT", [128, GT])


class Router:

    def __init__(self, p, ctx, name, experts, kept, sigmoid=False, renormalise=False):
        t = lambda k, shape, dt=F32: sb(p, ctx, f"{name}_{k}", shape, dt)
        self.p, self.experts, self.kept, self.sigmoid, self.renormalise = p, experts, kept, sigmoid, renormalise
        self.logits, self.scores = t("logits", [128, G, experts]), t("scores", [128, G, experts])
        self.spare = t("spare", [128, 1])
        self.most, self.total = t("most", [128, G]), t("total", [128, G])
        self.top, self.where, self.where_f = t("top", [128, G, 8]), t("where", [128, G, 8], U32), t("where_f", [128, G, 8])
        self.number, self.part = t("number", [128, experts]), t("part", [128, G, experts])
        self.steps, self.logits_psum, self.logits_ready, self.scores_ready = p.plan(
            route_steps=(0 if sigmoid else 4) + G + G + 1 + (4 if renormalise else 0) + 2 * kept + kept - 2,
            logits_psum=1, logits_ready=1, scores_ready=1)

    def prepare(self, pool, prep_ready):
        return self.p.nc.gpsimd.iota(self.number[:], pattern=[[1, self.experts]], base=0, channel_multiplier=0,
                                     allow_small_or_imprecise_dtypes=True)

    def tensor(self, pe, g, xnT, w, bank):
        for b in range(G):
            last = self.p.nc.tensor.matmul(bank[:, b * self.experts:(b + 1) * self.experts], lhsT=xnT[:, batch(b)],
                                           rhs=w[:], start=True, stop=True)
        last.then_inc(self.logits_psum.sem, 1)

    def scalar(self, act, g):
        act.wait_ge(*self.logits_ready.at(g, 1))
        self.p.nc.scalar.activation(self.scores[:], self.logits[:], ACT.Sigmoid if self.sigmoid else ACT.Exp)\
            .then_inc(self.scores_ready.sem, 1)

    def vector(self, dve, g, bank, gates, gates_ready):
        v, n, k = self.p.nc.vector, self.experts, self.kept
        then = Chain(dve, self.steps, g)
        wide = lambda x, m: x.unsqueeze(2).to_broadcast([128, G, m])
        dve.wait_ge(*self.logits_psum.at(g, 1))
        src = bank[:, 0:G * n].rearrange("p (b e) -> p b e", b=G)
        if self.sigmoid:
            v.tensor_copy(self.logits[:], src).then_inc(self.logits_ready.sem, 1)
            dve.wait_ge(*self.scores_ready.at(g, 1))
        else:
            then(v.tensor_reduce(self.most[:], src, axis=AX, op=ALU.max))
            v.tensor_tensor(self.logits[:], src, wide(self.most[:], n), ALU.subtract).then_inc(self.logits_ready.sem, 1)
            dve.wait_ge(*self.scores_ready.at(g, 1))
            then(v.tensor_reduce(self.total[:], self.scores[:], axis=AX, op=ALU.add))
            then(v.reciprocal(self.most[:], self.total[:]))
            then(v.tensor_tensor(self.scores[:], self.scores[:], wide(self.most[:], n), ALU.mult))
        v.memset(self.spare[:], 0.0)
        for b in range(G):
            v.max(self.top[:, b, :], self.scores[:, b, :]).then_inc(self.steps.sem, 1)
        then.n += G
        dve.wait_ge(*self.steps.at(g, then.n))
        v.memset(self.spare[:], 0.0)
        for b in range(G):
            v.max_index(self.where[:, b, :], self.top[:, b, :], self.scores[:, b, :]).then_inc(self.steps.sem, 1)
        then.n += G
        dve.wait_ge(*self.steps.at(g, then.n))
        then(v.tensor_copy(self.where_f[:], self.where[:]))
        if self.renormalise:
            then(v.tensor_reduce(self.total[:], self.top[:, :, 0:k], axis=AX, op=ALU.add))
            then(v.tensor_scalar(self.total[:], self.total[:], 1e-8, None, ALU.add))
            then(v.reciprocal(self.most[:], self.total[:]))
            then(v.tensor_tensor(self.top[:, :, 0:k], self.top[:, :, 0:k], wide(self.most[:], k), ALU.mult))
        number = self.number[:].unsqueeze(1).to_broadcast([128, G, n])
        for i in range(k):
            out = gates if i == 0 else self.part
            then(v.tensor_tensor(out[:], number, wide(self.where_f[:, :, i], n), ALU.is_equal))
            if i == 0:
                then(v.tensor_tensor(gates[:], gates[:], wide(self.top[:, :, 0], n), ALU.mult))
            else:
                then(v.tensor_tensor(self.part[:], self.part[:], wide(self.top[:, :, i], n), ALU.mult))
                last = v.tensor_tensor(gates[:], gates[:], self.part[:], ALU.add)
                if i < k - 1:
                    then(last)
        last.then_inc(gates_ready.sem, 1)
        then.ends()


def ffn_squared_relu(p, name):
    nc, ins, w = p.nc, p.inputs, p.w
    E, HALVES = 8, 2
    norm_rows(p, name)
    (xn_ready, xnT_psum, xnT_ready, h_psum, relu_ready, h_ready, y_psum, added, gates_ready, x_done) = p.plan(
        xn_ready=G, xnT_psum=1, xnT_ready=1, h_psum=E * HALVES, relu_ready=E * HALVES, h_ready=E * HALVES,
        y_psum=E, expert_added=E, gates_ready=1, x_done=1)
    w_in, prep = p.plan(expert_weights_in=0, stage_prepared=0)
    H_BANK, Y_BANK, L_BANK, M_BANK = p.bank[0:4], p.bank[4:6], p.bank[7], p.bank[6]
    with ExitStack() as ctx:
        t = lambda k, shape, dt=F32: sb(p, ctx, f"{name}_{k}", shape, dt)
        xn, xnT = front(p, name, ctx)
        w1, w2 = t("w1", [128, E, HALVES * 128]), t("w2", [128, E, HALVES, D])
        relu, h = t("relu", [128, 2, GT]), t("h", [128, 4, GT])
        gates = t("gates", [128, G, E])
        router = Router(p, ctx, name, E, 2, renormalise=True)
        with nc.Block(no_gpsimd_drain=True) as block:
            @block.sync
            def _(sp):
                sp.dma_start(w1[:], ins["L0_ffn_W1"]).then_inc(w_in.sem, 16)
                sp.dma_start(w2[:], ins["L0_ffn_W2"]).then_inc(w_in.sem, 16)

            @block.gpsimd
            def _(pool):
                Chain(pool, prep)(router.prepare(pool, prep))
                pool.wait_ge(*w_in.at(0, 32))
        prep.base += 1
        w_in.base += 32

        with nc.Block(no_gpsimd_drain=True) as block:
            @block.tensor
            def _(pe):
                mm = nc.tensor.matmul

                def up(g, e, a):
                    n = 2 * e + a
                    if n >= 4:
                        pe.wait_ge(*relu_ready.at(g, n - 3))
                    mm(H_BANK[n % 4][:], lhsT=w1[:, e, 128 * a:128 * a + 128], rhs=xnT[:], start=True, stop=True)\
                        .then_inc(h_psum.sem, 1)

                def down(g, e):
                    pe.wait_ge(*h_ready.at(g, 2 * e + 2))
                    if e >= 2:
                        pe.wait_ge(*added.at(g, e - 1))
                    for b in range(G):
                        for a in range(HALVES):
                            last = mm(Y_BANK[e % 2][:, batch(b)], lhsT=h[:, (2 * e + a) % 4, batch(b)], rhs=w2[:, e, a, :],
                                      start=(a == 0), stop=(a == 1))
                    last.then_inc(y_psum.sem, 1)

                with pe.Fori(0, NG) as g:
                    transpose_xn(p, pe, g, xn, xn_ready, M_BANK, xnT_psum)
                    pe.wait_ge(*xnT_ready.at(g, 1))
                    router.tensor(pe, g, xnT, w["L0_ffn_Wg"], L_BANK)
                    for e in range(E):
                        up(g, e, 0)
                        up(g, e, 1)
                        if e:
                            down(g, e - 1)
                    down(g, E - 1)

            @block.scalar
            def _(act):
                nc.scalar.preload_act_table(ACT.Exp)
                with act.Fori(0, NG) as g:
                    act.wait_ge(*xnT_psum.at(g, 1))
                    nc.scalar.activation(xnT[:], M_BANK[:], ACT.Copy).then_inc(xnT_ready.sem, 1)
                    router.scalar(act, g)
                    for n in range(E * HALVES):
                        act.wait_ge(*h_psum.at(g, n + 1))
                        if n >= 2:
                            act.wait_ge(*h_ready.at(g, n - 1))
                        nc.scalar.activation(relu[:, n % 2, :], H_BANK[n % 4][:], ACT.Relu).then_inc(relu_ready.sem, 1)

            @block.vector
            def _(dve):
                v = nc.vector

                def add_expert(g, e):
                    dve.wait_ge(*y_psum.at(g, e + 1))
                    if e:
                        dve.wait_ge(*added.at(g, e))
                    for b in range(G):
                        last = v.scalar_tensor_tensor(rows_of_x(p, g, b), Y_BANK[e % 2][:, batch(b)], gates[:, b, e:e + 1],
                                                      rows_of_x(p, g, b), ALU.mult, ALU.add)
                    last.then_inc(added.sem, 1)
                    if e == E - 1:
                        dve.wait_ge(*added.at(g, E))
                        v.tensor_copy(gates[:, 0, 0:1], gates[:, 0, 0:1]).then_inc(x_done.sem, 1)

                with dve.Fori(0, NG) as g:
                    normalise(p, dve, g, xn, xn_ready)
                    router.vector(dve, g, L_BANK, gates, gates_ready)
                    dve.wait_ge(*gates_ready.at(g, 1))
                    for n in range(E * HALVES):
                        dve.wait_ge(*relu_ready.at(g, n + 1))
                        if n >= 4:
                            dve.wait_ge(*y_psum.at(g, n // 2 - 1))
                        v.tensor_tensor(h[:, n % 4, :], relu[:, n % 2, :], relu[:, n % 2, :], ALU.mult).then_inc(h_ready.sem, 1)
                        if n % 2 and n > 1:
                            add_expert(g, n // 2 - 1)
                    add_expert(g, E - 1)
                    row_statistics(p, dve, g, x_done)
        p.passed(NG)


def ffn_linear_experts(p, name):
    nc, ins, w = p.nc, p.inputs, p.w
    E = 8
    norm_rows(p, name)
    xn_ready, xnT_psum, xnT_ready, y_psum, added, gates_ready, x_done = p.plan(
        xn_ready=G, xnT_psum=1, xnT_ready=1, y_psum=2 * G, expert_added=2 * G * 4, gates_ready=1, x_done=1)
    w_in, prep, product, copied = p.plan(expert_weights_in=0, stage_prepared=0, product_psum=0, product_ready=0)
    Y_BANK, L_BANK, M_BANK = p.bank[0:4], p.bank[7], p.bank[6]
    ORDER = [(0, 0), (1, 0), (0, 1), (1, 1), (2, 0), (3, 0), (2, 1), (3, 1)]
    with ExitStack() as ctx:
        t = lambda k, shape, dt=F32: sb(p, ctx, f"{name}_{k}", shape, dt)
        xn, xnT = front(p, name, ctx)
        wi, wo, wio = t("wiT", [128, E, 128]), t("wo", [128, E, D]), t("wio", [128, E, D])
        gates = t("gates", [128, G, E])
        router = Router(p, ctx, name, E, 2)
        with nc.Block(no_gpsimd_drain=True) as block:
            @block.sync
            def _(sp):
                sp.dma_start(wi[:], ins["L2_ffn_WiT"]).then_inc(w_in.sem, 16)
                sp.dma_start(wo[:], ins["L2_ffn_Wo"]).then_inc(w_in.sem, 16)

            @block.gpsimd
            def _(pool):
                Chain(pool, prep)(router.prepare(pool, prep))

            @block.tensor
            def _(pe):
                pe.wait_ge(*w_in.at(0, 32))
                for e in range(E):
                    last = nc.tensor.matmul(p.bank[e // 4][:, batch(e % 4)], lhsT=wi[:, e, :], rhs=wo[:, e, :], start=True, stop=True)
                last.then_inc(product.sem, 1)

            @block.scalar
            def _(act):
                act.wait_ge(*product.at(0, 1))
                for i in range(2):
                    nc.scalar.activation(wio[:, 4 * i:4 * i + 4, :].rearrange("p e d -> p (e d)"), p.bank[i][:], ACT.Copy)
        prep.base += 1
        w_in.base += 32
        product.base += 1

        with nc.Block(no_gpsimd_drain=True) as block:
            @block.tensor
            def _(pe):
                with pe.Fori(0, NG) as g:
                    transpose_xn(p, pe, g, xn, xn_ready, M_BANK, xnT_psum)
                    pe.wait_ge(*xnT_ready.at(g, 1))
                    router.tensor(pe, g, xnT, w["L2_ffn_Wr"], L_BANK)
                    for n in range(2 * G):
                        b, i = ORDER[n]
                        if n >= 4:
                            pe.wait_ge(*added.at(g, 8 * ((n - 4) // 2) + 8))
                        nc.tensor.matmul(Y_BANK[(2 * b + i) % 4][:], lhsT=xnT[:, batch(b)],
                                         rhs=wio[:, 4 * i:4 * i + 4, :].rearrange("p e d -> p (e d)"),
                                         start=True, stop=True).then_inc(y_psum.sem, 1)

            @block.scalar
            def _(act):
                nc.scalar.preload_act_table(ACT.Exp)
                with act.Fori(0, NG) as g:
                    act.wait_ge(*xnT_psum.at(g, 1))
                    nc.scalar.activation(xnT[:], M_BANK[:], ACT.Copy).then_inc(xnT_ready.sem, 1)
                    router.scalar(act, g)

            @block.vector
            def _(dve):
                v = nc.vector
                with dve.Fori(0, NG) as g:
                    normalise(p, dve, g, xn, xn_ready)
                    router.vector(dve, g, L_BANK, gates, gates_ready)
                    dve.wait_ge(*gates_ready.at(g, 1))
                    n = 0
                    for n0 in (0, 4):
                        for i in range(2):
                            for e in range(4):
                                for b in (n0 // 2, n0 // 2 + 1):
                                    y = 2 * b + i
                                    if e == 0:
                                        dve.wait_ge(*y_psum.at(g, ORDER.index((b, i)) + 1))
                                    if n >= 2:
                                        dve.wait_ge(*added.at(g, n - 1))
                                    v.scalar_tensor_tensor(rows_of_x(p, g, b), Y_BANK[y % 4][:, batch(e)],
                                                           gates[:, b, 4 * i + e:4 * i + e + 1], rows_of_x(p, g, b),
                                                           ALU.mult, ALU.add).then_inc(added.sem, 1)
                                    n += 1
                    dve.wait_ge(*added.at(g, n))
                    v.tensor_copy(gates[:, 0, 0:1], gates[:, 0, 0:1]).then_inc(x_done.sem, 1)
                    row_statistics(p, dve, g, x_done)
        p.passed(NG)


def ffn_sigmoid_experts(p, name):
    nc, ins, w = p.nc, p.inputs, p.w
    E = 64
    norm_rows(p, name)
    xn_ready, xnT_psum, xnT_ready, gates_ready = p.plan(xn_ready=G, xnT_psum=1, xnT_ready=1, gates_ready=1)
    prep, = p.plan(stage_prepared=0)
    H_BANK, Y_BANK, L_BANK, M_BANK = p.bank[0:4], p.bank[4:8], p.bank[7], p.bank[6]
    with ExitStack() as ctx:
        t = lambda k, shape, dt=F32: sb(p, ctx, f"{name}_{k}", shape, dt)
        xn, xnT_now = front(p, name, ctx)
        gates_now = t("gates_now", [128, G, E])
        xnT, gates = t("xnT_all", [128, B * S]), t("gates", [128, B, E])
        keys, values = t("keys", [128, 2, 128]), t("values", [128, 2, D])
        relu = t("relu", [128, 4, GT])
        gate_now = t("gate_pair", [128, 2, B])
        router = Router(p, ctx, name, E, 4, sigmoid=True)
        with nc.Block(no_gpsimd_drain=True) as block:
            @block.gpsimd
            def _(pool):
                Chain(pool, prep)(router.prepare(pool, prep))
        prep.base += 1

        with nc.Block(no_gpsimd_drain=True) as block:
            @block.tensor
            def _(pe):
                with pe.Fori(0, NG) as g:
                    transpose_xn(p, pe, g, xn, xn_ready, M_BANK, xnT_psum)
                    pe.wait_ge(*xnT_ready.at(g, 1))
                    router.tensor(pe, g, xnT_now, w["L1_ffn_sel"], L_BANK)

            @block.scalar
            def _(act):
                nc.scalar.preload_act_table(ACT.Sigmoid)
                with act.Fori(0, NG) as g:
                    act.wait_ge(*xnT_psum.at(g, 1))
                    nc.scalar.activation(xnT_now[:], M_BANK[:], ACT.Copy).then_inc(xnT_ready.sem, 1)
                    nc.scalar.activation(xnT[:, ds(g * GT, GT)], M_BANK[:], ACT.Copy)
                    router.scalar(act, g)

            @block.vector
            def _(dve):
                with dve.Fori(0, NG) as g:
                    normalise(p, dve, g, xn, xn_ready)
                    router.vector(dve, g, L_BANK, gates_now, gates_ready)
                    dve.wait_ge(*gates_ready.at(g, 1))
                    nc.vector.tensor_copy(gates[:, ds(g * G, G), :], gates_now[:])
        p.passed(NG)

        *w_in, h_psum, relu_ready, y_psum, added, gate_ready = p.plan(
            even_expert_weights_in=32, odd_expert_weights_in=32, h_psum=2 * NG, relu_ready=2 * NG, y_psum=2 * NG, expert_added=2 * NG, gates_ready=2)

        def passes(eng, run):
            run(0, True)
            with eng.Fori(1, E // 2) as i:
                run(i, False)

        with nc.Block(no_gpsimd_drain=True) as block:
            @block.sync
            def _(sp):
                def run(i, first):
                    for a in range(2):
                        if not first:
                            sp.wait_ge(*y_psum.at(i - 1, NG * (a + 1)))
                        sp.dma_start(keys[:, a, :], ins["L1_ffn_keys"][:, ds((2 * i + a) * 128, 128)]).then_inc(w_in[a].sem, 16)
                        sp.dma_start(values[:, a, :], ins["L1_ffn_values"][:, ds((2 * i + a) * D, D)]).then_inc(w_in[a].sem, 16)
                passes(sp, run)

            @block.tensor
            def _(pe):
                mm = nc.tensor.matmul

                def up(i, n, first):
                    if n % NG == 0:
                        pe.wait_ge(*w_in[n // NG].at(i, 32))
                    if not (first and n < 4):
                        pe.wait_ge(*relu_ready.at(i, n - 3))
                    mm(H_BANK[n % 4][:], lhsT=keys[:, n // NG, :], rhs=xnT[:, (n % NG) * GT:(n % NG + 1) * GT],
                       start=True, stop=True).then_inc(h_psum.sem, 1)

                def down(i, n, first):
                    pe.wait_ge(*relu_ready.at(i, n + 1))
                    if not (first and n < 4):
                        pe.wait_ge(*added.at(i, n - 3))
                    for b in range(G):
                        last = mm(Y_BANK[n % 4][:, batch(b)], lhsT=relu[:, n % 4, batch(b)], rhs=values[:, n // NG, :],
                                  start=True, stop=True)
                    last.then_inc(y_psum.sem, 1)

                def run(i, first):
                    for n in range(2 * NG):
                        up(i, n, first)
                        if n >= 2:
                            down(i, n - 2, first)
                    down(i, 2 * NG - 2, first)
                    down(i, 2 * NG - 1, first)
                passes(pe, run)

            @block.scalar
            def _(act):
                def run(i, first):
                    for n in range(2 * NG):
                        act.wait_ge(*h_psum.at(i, n + 1))
                        if not (first and n < 4):
                            act.wait_ge(*y_psum.at(i, n - 3))
                        nc.scalar.activation(relu[:, n % 4, :], H_BANK[n % 4][:], ACT.Relu).then_inc(relu_ready.sem, 1)
                passes(act, run)

            @block.vector
            def _(dve):
                v = nc.vector

                def run(i, first):
                    for n in range(2 * NG):
                        a = n // NG
                        if n % NG == 0:
                            if not first:
                                dve.wait_ge(*added.at(i - 1, NG * (a + 1)))
                            v.tensor_copy(gate_now[:, a, :], gates[:, :, ds(2 * i + a, 1)].rearrange("p b a -> p (b a)"))\
                                .then_inc(gate_ready.sem, 1)
                            dve.wait_ge(*gate_ready.at(i, a + 1))
                        dve.wait_ge(*y_psum.at(i, n + 1))
                        if not (first and n < NG):
                            dve.wait_ge(*added.at(i, n - NG + 1))
                        for b in range(G):
                            k = (n % NG) * G + b
                            rows = p.x[:, k * D:(k + 1) * D]
                            last = v.scalar_tensor_tensor(rows, Y_BANK[n % 4][:, batch(b)], gate_now[:, a, k:k + 1],
                                                          rows, ALU.mult, ALU.add)
                        last.then_inc(added.sem, 1)
                passes(dve, run)
        p.passed(E // 2)
        all_statistics(p)


def all_statistics(p):
    with p.nc.Block(no_gpsimd_drain=True) as block:
        @block.vector
        def _(dve):
            for b in range(B):
                p.nc.vector.bn_stats(p.stats[:, b, :], p.x[:, b * D:(b + 1) * D])



def linear_attention(p, name):
    nc, ins, w = p.nc, p.inputs, p.w
    C1 = 6.28125
    C2 = float(np.round((2 * np.pi - C1) * 2 ** 20) / 2 ** 20)
    C3 = 2 * np.pi - C1 - C2
    ROUND = 1.5 * 2 ** 23
    norm_rows(p, name)
    (xn_ready, xnT_psum, xnT_ready, qk_psum, v_psum, u_psum, act_ready, turned, v_ready, u_ready, s_psum, e_ready, o_psum,
     uo_ready, sq_ready, ms_psum, y_psum, ms_in, root_ready, bias_added, tail, x_done) = p.plan(
        xn_ready=G, xnT_psum=1, xnT_ready=1, qk_psum=4, v_psum=1, u_psum=1, silu_ready=4, turned_ready=4, v_ready=G,
        u_ready=1, s_psum=16, masked_ready=16, av_psum=G, gated_ready=1, squares_ready=1, mean_square_psum=1, y_psum=1,
        variance_ready=1, root_ready=1, bias_added=1, tail_steps=1, x_done=1)
    prep, angle, sines = p.plan(stage_prepared=0, angle_steps=0, table_ready=0)
    M_BANK, Y_BANK, O_BANK = p.bank[6], p.bank[5], p.bank[7]
    V_BANK, U_BANK = p.bank[4], p.bank[5]
    with ExitStack() as ctx:
        t = lambda k, shape, dt=F32: sb(p, ctx, f"{name}_{k}", shape, dt)
        xn, xnT = front(p, name, ctx)
        silu, qk = t("silu", [128, 2, GT]), t("qk", [128, 4, GT])
        uT, uo, sq = t("uT", [128, GT]), t("uo", [128, GT]), t("sq", [128, GT])
        vpad = t("vpad", [128, G, 8 * 32])
        energy = t("energy", [128, 2, 8, S])
        keep = t("keep", [128, 8, S])
        table, pos, th, turns, whole = (t(k, [128, 2, S]) for k in ("table", "pos", "th", "turns", "whole"))
        quarter = t("quarter", [128, 1])
        ones = t("ones", [128, 1])
        veps, root, rs = t("veps", [128, G]), t("root", [128, G]), t("rs", [128, G])

        with nc.Block(no_gpsimd_drain=True) as block:
            @block.gpsimd
            def _(pool):
                then = Chain(pool, prep)
                then(nc.gpsimd.iota(pos[:], pattern=[[0, 2], [1, S]], base=0, channel_multiplier=0,
                                    allow_small_or_imprecise_dtypes=True))
                then(nc.gpsimd.memset(quarter[:], 1.0))
                for j in range(4):
                    rows = quarter[32 * j:32 * j + 32, :]
                    then(nc.gpsimd.affine_select(out=rows, in_=rows, compare_op=ALU.is_ge, fill=0.0, base=15,
                                                 pattern=[[0, 1]], channel_multiplier=-1))
                then(nc.gpsimd.memset(keep[:], 1.0))
                then(nc.gpsimd.affine_select(out=keep[:], in_=keep[:], compare_op=ALU.is_ge, fill=0.0, base=0,
                                             pattern=[[0, 8], [1, S]], channel_multiplier=-1))
                then(nc.gpsimd.memset(vpad[:], 0.0))
                then(nc.gpsimd.memset(ones[:], 1.0))

            @block.vector
            def _(dve):
                v = nc.vector
                then = Chain(dve, angle)
                dve.wait_ge(*prep.at(0, 8))
                for i in range(2):
                    then(v.tensor_scalar(th[:, i, :], pos[:, i, :], w["L1_attn_theta"][:, i:i + 1], None, ALU.mult))
                then(v.tensor_scalar(quarter[:], quarter[:], 0.25, None, ALU.mult))
                then(v.tensor_scalar(turns[:], th[:], 1 / (2 * np.pi), quarter[:], ALU.mult, ALU.add))
                then(v.tensor_scalar(whole[:], turns[:], ROUND, ROUND, ALU.add, ALU.subtract))
                for c in (C1, C2, C3):
                    then(v.scalar_tensor_tensor(th[:], whole[:], -c, th[:], ALU.mult, ALU.add))
                then(v.tensor_scalar(quarter[:], quarter[:], 2 * np.pi, None, ALU.mult))
                then(v.tensor_scalar(th[:], th[:], quarter[:], 3.1415925, ALU.add, ALU.min))
                then(v.tensor_scalar(th[:], th[:], -3.1415925, None, ALU.max))
                for h in range(8):
                    at = keep[:, 2 * (h % 4) + h // 4, :]
                    then(v.tensor_scalar(at, at, w["L1_attn_slope"][:, h:h + 1], None, ALU.mult))

            @block.scalar
            def _(act):
                act.wait_ge(*angle.at(0, 19))
                nc.scalar.activation(table[:], th[:], ACT.Sin)
                nc.scalar.activation(keep[:], keep[:], ACT.Exp)
        prep.base += 10
        angle.base += 19

        with nc.Block(no_gpsimd_drain=True) as block:
            @block.tensor
            def _(pe):
                mm = nc.tensor.matmul

                def scores(g, b, r):
                    u = 4 * b + r
                    if b > 0:
                        pe.wait_ge(*e_ready.at(g, u - 3))
                    rows = slice(32 * r, 32 * r + 32)
                    for i in range(2):
                        last = mm(p.bank[r][:, batch(i)], lhsT=qk[rows, 2 + i, batch(b)], rhs=qk[rows, i, batch(b)],
                                  start=True, stop=True)
                    last.then_inc(s_psum.sem, 1)

                def values(g, b):
                    pe.wait_ge(*e_ready.at(g, 4 * b + 4))
                    for c in range(2):
                        for j in range(4):
                            h = 2 * j + c
                            last = mm(O_BANK[32 * j:32 * j + 32, batch(b)], lhsT=vpad[:, b, 32 * h:32 * h + 32],
                                      rhs=energy[:, b % 2, 2 * (h % 4) + h // 4, :], start=(c == 0), stop=(c == 1),
                                      tile_position=(0, 32 * j), skip_group_check=True)
                    last.then_inc(o_psum.sem, 1)

                with pe.Fori(0, NG) as g:
                    transpose_xn(p, pe, g, xn, xn_ready, M_BANK, xnT_psum)
                    pe.wait_ge(*xnT_ready.at(g, 1))
                    for i in range(4):
                        mm(p.bank[i][:], lhsT=w["L1_attn_qk"][:, i, :], rhs=xnT[:], start=True, stop=True).then_inc(qk_psum.sem, 1)
                    for b in range(G):
                        last = mm(V_BANK[:, batch(b)], lhsT=xnT[:, batch(b)], rhs=w["L1_attn_vu"][:, 0, :], start=True, stop=True)
                    last.then_inc(v_psum.sem, 1)
                    mm(U_BANK[:], lhsT=w["L1_attn_vu"][:, 1, :], rhs=xnT[:], start=True, stop=True).then_inc(u_psum.sem, 1)
                    pe.wait_ge(*turned.at(g, 4))
                    pe.wait_ge(*v_ready.at(g, G))
                    for u in range(16):
                        scores(g, u // 4, u % 4)
                        if u % 4 == 3 and u > 3:
                            values(g, u // 4 - 1)
                    values(g, 3)
                    pe.wait_ge(*sq_ready.at(g, 1))
                    for b in range(G):
                        last = mm(M_BANK[:, b:b + 1], lhsT=sq[:, batch(b)], rhs=ones[:], start=True, stop=True)
                    last.then_inc(ms_psum.sem, 1)
                    pe.wait_ge(*uo_ready.at(g, 1))
                    for b in range(G):
                        last = mm(Y_BANK[:, batch(b)], lhsT=uo[:, batch(b)], rhs=w["L1_attn_out_w"][:], start=True, stop=True)
                    last.then_inc(y_psum.sem, 1)

            @block.scalar
            def _(act):
                with act.Fori(0, NG) as g:
                    act.wait_ge(*xnT_psum.at(g, 1))
                    nc.scalar.activation(xnT[:], M_BANK[:], ACT.Copy).then_inc(xnT_ready.sem, 1)
                    for i in range(4):
                        act.wait_ge(*qk_psum.at(g, i + 1))
                        if i >= 2:
                            act.wait_ge(*turned.at(g, i - 1))
                        nc.scalar.activation(silu[:, i % 2, :], p.bank[i][:], ACT.Silu, bias=w["L1_attn_qk_b"][:, i:i + 1])\
                            .then_inc(act_ready.sem, 1)
                    act.wait_ge(*u_psum.at(g, 1))
                    nc.scalar.activation(uT[:], U_BANK[:], ACT.Identity, bias=w["L1_attn_ub"][:, 0:1]).then_inc(u_ready.sem, 1)
                    act.wait_ge(*o_psum.at(g, G))
                    nc.scalar.activation(sq[:], O_BANK[:], ACT.Square).then_inc(sq_ready.sem, 1)
                    act.wait_ge(*ms_in.at(g, 1))
                    nc.scalar.activation(root[:], veps[:], ACT.Sqrt).then_inc(root_ready.sem, 1)

            @block.vector
            def _(dve):
                v = nc.vector
                with dve.Fori(0, NG) as g:
                    normalise(p, dve, g, xn, xn_ready)
                    for i in range(4):
                        dve.wait_ge(*act_ready.at(g, i + 1))
                        v.tensor_tensor(qk[:, i, :].rearrange("p (b n) -> p b n", b=G), silu[:, i % 2, :].rearrange("p (b n) -> p b n", b=G),
                                        table[:, i % 2, :].unsqueeze(1).to_broadcast([128, G, S]), ALU.mult).then_inc(turned.sem, 1)
                    dve.wait_ge(*v_psum.at(g, 1))
                    for b in range(G):
                        q = vpad[:, b, 0:256]
                        slots = bass.AP(q.tensor, q.offset, [list(q.ap[0]), [64, 4], [48, 2], [1, 16]])
                        v.tensor_tensor(slots, V_BANK[:, batch(b)].rearrange("p (j c d) -> p j c d", j=4, c=2),
                                        w["L1_attn_vb"][:].rearrange("p (j c d) -> p j c d", j=4, c=2), ALU.add).then_inc(v_ready.sem, 1)
                    for u in range(16):
                        b, r = u // 4, u % 4
                        dve.wait_ge(*s_psum.at(g, u + 1))
                        if b >= 2 and r == 0:
                            dve.wait_ge(*o_psum.at(g, b - 1))
                        v.tensor_tensor(energy[:, b % 2, 2 * r:2 * r + 2, :], p.bank[r][:, 0:2 * S].rearrange("p (t n) -> p t n", t=2),
                                        keep[:, 2 * r:2 * r + 2, :], ALU.mult).then_inc(e_ready.sem, 1)
                    dve.wait_ge(*sq_ready.at(g, 1))
                    dve.wait_ge(*u_ready.at(g, 1))
                    v.tensor_tensor(uo[:], O_BANK[:], uT[:], ALU.mult).then_inc(uo_ready.sem, 1)
                    dve.wait_ge(*ms_psum.at(g, 1))
                    v.tensor_scalar(veps[:], M_BANK[:, 0:G], 1.0 / D, 1e-6, ALU.mult, ALU.add).then_inc(ms_in.sem, 1)
                    for b in range(G):
                        last = v.tensor_tensor(rows_of_x(p, g, b), rows_of_x(p, g, b), w["L1_attn_out_b"][:], ALU.add)
                    last.then_inc(bias_added.sem, 1)
                    dve.wait_ge(*root_ready.at(g, 1))
                    v.reciprocal(rs[:], root[:]).then_inc(tail.sem, 1)
                    dve.wait_ge(*tail.at(g, 1))
                    dve.wait_ge(*bias_added.at(g, 1))
                    dve.wait_ge(*y_psum.at(g, 1))
                    for b in range(G):
                        last = v.scalar_tensor_tensor(rows_of_x(p, g, b), Y_BANK[:, batch(b)], rs[:, b:b + 1], rows_of_x(p, g, b),
                                                      ALU.mult, ALU.add)
                    last.then_inc(x_done.sem, 1)
                    row_statistics(p, dve, g, x_done)
        p.passed(NG)



def single_head(p, name):
    nc, ins = p.nc, p.inputs
    norm_rows(p, name)
    (ctx_in, rows_in, xn_ready, xnT_psum, xnT_ready, s_psum, max_ready, p_ready, t_psum, pt_ready, y_psum, r_steps, x_done) = p.plan(
        ctx_in=16, ctx_rows_in=16, xn_ready=G, xnT_psum=1, xnT_ready=1, s_psum=1, max_ready=1, p_ready=1, t_psum=1,
        pt_ready=1, y_psum=1, reciprocal_steps=1, x_done=1)
    with ExitStack() as ctx:
        t = lambda k, shape, dt=F32: sb(p, ctx, f"{name}_{k}", shape, dt)
        xn, xnT = front(p, name, ctx)
        ctxT, rows, probs, probsT = (t(k, [128, GT]) for k in ("ctxT", "ctx_rows", "probs", "probsT"))
        nmax, rsum, rrec = t("nmax", [128, G]), t("rsum", [128, G]), t("rrec", [128, G])
        with nc.Block(no_gpsimd_drain=True) as block:
            @block.sync
            def _(sp):
                def load(g):
                    sp.dma_start(ctxT[:], ins["ctx_T"][:, ds(g * GT, GT)]).then_inc(ctx_in.sem, 16)
                    sp.dma_start(rows[:], ins["ctx_rows"][:, ds(g * GT, GT)]).then_inc(rows_in.sem, 16)
                load(0)
                with sp.Fori(1, NG) as g:
                    sp.wait_ge(*y_psum.at(g - 1, 1))
                    load(g)

            @block.tensor
            def _(pe):
                with pe.Fori(0, NG) as g:
                    transpose_xn(p, pe, g, xn, xn_ready, p.bank[6], xnT_psum)
                    pe.wait_ge(*xnT_ready.at(g, 1))
                    pe.wait_ge(*ctx_in.at(g, 16))
                    for b in range(G):
                        last = nc.tensor.matmul(p.bank[0][:, batch(b)], lhsT=xnT[:, batch(b)], rhs=ctxT[:, batch(b)], start=True, stop=True)
                    last.then_inc(s_psum.sem, 1)
                    pe.wait_ge(*p_ready.at(g, 1))
                    for b in range(G):
                        last = nc.tensor.transpose(p.bank[1][:, batch(b)], probs[:, batch(b)], p.ident[:])
                    last.then_inc(t_psum.sem, 1)
                    pe.wait_ge(*pt_ready.at(g, 1))
                    pe.wait_ge(*rows_in.at(g, 16))
                    for b in range(G):
                        last = nc.tensor.matmul(p.bank[2][:, batch(b)], lhsT=probsT[:, batch(b)], rhs=rows[:, batch(b)], start=True, stop=True)
                    last.then_inc(y_psum.sem, 1)

            @block.scalar
            def _(act):
                nc.scalar.preload_act_table(ACT.Exp)
                with act.Fori(0, NG) as g:
                    act.wait_ge(*xnT_psum.at(g, 1))
                    nc.scalar.activation(xnT[:], p.bank[6][:], ACT.Copy, scale=HD ** -0.5).then_inc(xnT_ready.sem, 1)
                    act.wait_ge(*max_ready.at(g, 1))
                    for b in range(G):
                        last = nc.scalar.activation(probs[:, batch(b)], p.bank[0][:, batch(b)], ACT.Exp, bias=nmax[:, b:b + 1],
                                                    accum_out=rsum[:, b:b + 1])
                    last.then_inc(p_ready.sem, 1)

            @block.vector
            def _(dve):
                v = nc.vector
                with dve.Fori(0, NG) as g:
                    normalise(p, dve, g, xn, xn_ready)
                    dve.wait_ge(*s_psum.at(g, 1))
                    v.tensor_reduce(nmax[:], p.bank[0][:].rearrange("p (b k) -> p b k", b=G), axis=AX, op=ALU.max, negate=True)\
                        .then_inc(max_ready.sem, 1)
                    dve.wait_ge(*p_ready.at(g, 1))
                    v.reciprocal(rrec[:], rsum[:]).then_inc(r_steps.sem, 1)
                    dve.wait_ge(*t_psum.at(g, 1))
                    v.tensor_copy(probsT[:], p.bank[1][:]).then_inc(pt_ready.sem, 1)
                    dve.wait_ge(*r_steps.at(g, 1))
                    dve.wait_ge(*y_psum.at(g, 1))
                    for b in range(G):
                        last = v.scalar_tensor_tensor(rows_of_x(p, g, b), p.bank[2][:, batch(b)], rrec[:, b:b + 1], rows_of_x(p, g, b),
                                                      ALU.mult, ALU.add)
                    last.then_inc(x_done.sem, 1)
                    row_statistics(p, dve, g, x_done)
        p.passed(NG)



def channel_attention(p, name):
    nc, ins, w = p.nc, p.inputs, p.w
    norm_rows(p, name)
    (xn_ready, xnT_psum, xnT_ready, q_psum, k_psum, v_psum, q_ready, k_ready, v_ready, vmask_ready, s_psum, max_ready,
     p_ready, r_steps, qpad_ready, av_psum, x_done) = p.plan(
        xn_ready=G, xnT_psum=1, xnT_ready=1, q_psum=1, k_psum=1, v_psum=1, q_ready=1, k_ready=1, v_ready=1,
        kmask_ready=UNITS, s_psum=UNITS, max_ready=UNITS, p_ready=UNITS, reciprocal_steps=G, qpad_ready=G, av_psum=G, x_done=1)
    prep, = p.plan(stage_prepared=0)
    S_BANK, M_BANK, O_BANK = p.bank[0:4], p.bank[6], p.bank[7]
    with ExitStack() as ctx:
        t = lambda k, shape, dt=F32: sb(p, ctx, f"{name}_{k}", shape, dt)
        xn, xnT = front(p, name, ctx)
        qT, k, vv = t("qT", [128, 2, GT]), t("k", [128, 2, GT]), t("v", [128, 2, GT])
        vmask, qpad = t("vmask", [128, 2, QUADS, PER * S]), t("qpad", [128, 2, H * 32])
        probs = t("probs", [128, 2, QUADS, PER * S])
        nmax, rsum, rrec = t("nmax", [128, G, H]), t("rsum", [128, G, H]), t("rrec", [128, G, H])
        temperature = t("temperature", [128, H])
        with nc.Block(no_gpsimd_drain=True) as block:
            @block.gpsimd
            def _(pool):
                then = Chain(pool, prep)
                then(nc.gpsimd.memset(qpad[:], 0.0))
                then(nc.gpsimd.memset(temperature[:], 1.0))
                then(nc.gpsimd.affine_select(out=temperature[:], in_=temperature[:], compare_op=ALU.is_ge, fill=0.0, base=0,
                                             pattern=[[-HD, H]], channel_multiplier=1))
                then(nc.gpsimd.affine_select(out=temperature[:], in_=temperature[:], compare_op=ALU.is_ge, fill=0.0,
                                             base=HD - 1, pattern=[[HD, H]], channel_multiplier=-1))
                then(nc.gpsimd.tensor_tensor(temperature[:], temperature[:], w["L2_attn_temp"][:].to_broadcast([128, H]), ALU.mult))
        prep.base += 5
        AFTER = 4

        with nc.Block(no_gpsimd_drain=True) as block:
            @block.gpsimd
            def _(pool):
                def units(g, a, steps, first, last):
                    for u in range(steps):
                        b, j = u // 4, u % 4
                        if u == 0:
                            pool.wait_ge(*v_ready.at(g, 1))
                        if not (first and u < 8):
                            pool.wait_ge(*s_psum.at(g, u - 7))
                        nc.gpsimd.tensor_tensor(vmask[:, b % 2, j].rearrange("p (c k) -> p c k", c=PER),
                                                vv[:, a, batch(b)].unsqueeze(1).to_broadcast([128, PER, S]),
                                                temperature[:, PER * j:PER * j + PER].unsqueeze(2).to_broadcast([128, PER, S]),
                                                ALU.mult).then_inc(vmask_ready.sem, 1)
                all_groups(pool, units)

            @block.tensor
            def _(pe):
                mm = nc.tensor.matmul

                def scores(g, a, u, first):
                    b, j = u // 4, u % 4
                    pe.wait_ge(*vmask_ready.at(g, u + 1))
                    if u == 0:
                        pe.wait_ge(*k_ready.at(g, 1))
                    if not (first and u < 4):
                        pe.wait_ge(*p_ready.at(g, u - 3))
                    mm(S_BANK[j][:], lhsT=k[:, a, batch(b)], rhs=vmask[:, b % 2, j], start=True, stop=True).then_inc(s_psum.sem, 1)

                def values(g, b, first):
                    pe.wait_ge(*qpad_ready.at(g, b + 1))
                    if b == 0 and not first:
                        pe.wait_ge(*x_done.at(g, 0))
                    for c in range(PER):
                        for j in range(QUADS):
                            h = j * PER + c
                            last = mm(O_BANK[32 * j:32 * j + 32, batch(b)], lhsT=qpad[:, b % 2, 32 * h:32 * h + 32],
                                      rhs=probs[:, b % 2, j, batch(c)], start=(c == 0), stop=(c == PER - 1),
                                      tile_position=(0, 32 * j), skip_group_check=True)
                    last.then_inc(av_psum.sem, 1)

                def front(g, a, step):
                    if step == 0:
                        transpose_xn(p, pe, g, xn, xn_ready, M_BANK, xnT_psum)
                    if step == 1:
                        pe.wait_ge(*xnT_ready.at(g, 1))
                        for b in range(G):
                            last = mm(M_BANK[:, batch(b)], lhsT=xnT[:, batch(b)], rhs=w["L2_attn_Wv"][:], start=True, stop=True)
                        last.then_inc(v_psum.sem, 1)
                    if step == 2:
                        pe.wait_ge(*v_ready.at(g, 1))
                        for b in range(G):
                            last = mm(M_BANK[:, batch(b)], lhsT=xnT[:, batch(b)], rhs=w["L2_attn_Wk"][:], start=True, stop=True)
                        last.then_inc(k_psum.sem, 1)
                    if step == 3:
                        pe.wait_ge(*k_ready.at(g, 1))
                        mm(M_BANK[:], lhsT=w["L2_attn_Wq"][:], rhs=xnT[:], start=True, stop=True).then_inc(q_psum.sem, 1)

                def units(g, a, steps, first, last):
                    if first:
                        for step in range(4):
                            front(g, a, step)
                    for u in range(steps or AFTER):
                        if steps:
                            scores(g, a, u, first)
                        if u % 4 == 2 and not (first and u < 6):
                            h, ha, hu = before(g, a, u, 6)
                            values(h, hu // 4, first)
                        if not last:
                            if u == 4:
                                pe.wait_ge(*q_ready.at(g, 1))
                            for step, at in enumerate((4, 6, 8, 10)):
                                if u == at:
                                    front(g + 1, 1 - a, step)
                all_groups(pe, units)

            @block.scalar
            def _(act):
                nc.scalar.preload_act_table(ACT.Exp)

                def start(g):
                    act.wait_ge(*xnT_psum.at(g, 1))
                    nc.scalar.activation(xnT[:], M_BANK[:], ACT.Copy).then_inc(xnT_ready.sem, 1)

                def units(g, a, steps, first, last):
                    if first:
                        start(g)
                    for u in range(steps):
                        b, j = u // 4, u % 4
                        act.wait_ge(*max_ready.at(g, u + 1))
                        if j == 0 and not (first and b < 2):
                            act.wait_ge(*av_psum.at(g, b - 1))
                        for c in range(PER):
                            h = 4 * j + c
                            done = nc.scalar.activation(probs[:, b % 2, j, batch(c)], S_BANK[j][:, batch(c)], ACT.Exp,
                                                        bias=nmax[:, b, h:h + 1], accum_out=rsum[:, b, h:h + 1])
                        done.then_inc(p_ready.sem, 1)
                        if u == 4 and not last:
                            start(g + 1)
                all_groups(act, units)

            @block.vector
            def _(dve):
                v = nc.vector

                def scaled_q(g, a, b, first):
                    dve.wait_ge(*p_ready.at(g, 4 * b + 4))
                    v.reciprocal(rrec[:, b, :], rsum[:, b, :]).then_inc(r_steps.sem, 1)
                    dve.wait_ge(*r_steps.at(g, b + 1))
                    if not (first and b < 2):
                        dve.wait_ge(*av_psum.at(g, b - 1))
                    q = qpad[:, b % 2, :]
                    slots = bass.AP(q.tensor, q.offset, [list(q.ap[0]), [128, QUADS], [40, PER], [1, HD]])
                    v.tensor_tensor(slots, qT[:, a, batch(b)].rearrange("p (j c d) -> p j c d", j=QUADS, c=PER),
                                    rrec[:, b, :].rearrange("p (j c) -> p j c", j=QUADS).unsqueeze(3).to_broadcast([128, QUADS, PER, HD]),
                                    ALU.mult).then_inc(qpad_ready.sem, 1)

                def front(g, a, step):
                    if step == 0:
                        normalise(p, dve, g, xn, xn_ready)
                    for i, out, bias, psum, ready in ((1, vv, "L2_attn_bv", v_psum, v_ready), (2, k, "L2_attn_bk", k_psum, k_ready)):
                        if step == i:
                            dve.wait_ge(*psum.at(g, 1))
                            v.tensor_tensor(out[:, a, :].rearrange("p (b c) -> p b c", b=G), M_BANK[:].rearrange("p (b c) -> p b c", b=G),
                                            w[bias][:].unsqueeze(1).to_broadcast([128, G, D]), ALU.add).then_inc(ready.sem, 1)
                    if step == 3:
                        dve.wait_ge(*q_psum.at(g, 1))
                        v.tensor_scalar(qT[:, a, :], M_BANK[:], w["L2_attn_bq"][:, 0:1], None, ALU.add).then_inc(q_ready.sem, 1)

                def units(g, a, steps, first, last):
                    if first:
                        for step in range(4):
                            front(g, a, step)
                    for u in range(steps or AFTER):
                        if steps:
                            dve.wait_ge(*s_psum.at(g, u + 1))
                            v.tensor_reduce(nmax[:, u // 4, 4 * (u % 4):4 * (u % 4) + 4], S_BANK[u % 4][:].rearrange("p (c k) -> p c k", c=PER),
                                            axis=AX, op=ALU.max, negate=True).then_inc(max_ready.sem, 1)
                        if u % 4 == 1 and not (first and u < 5):
                            h, ha, hu = before(g, a, u, 5)
                            scaled_q(h, ha, hu // 4, first)
                        if u == 3 and not first:
                            dve.wait_ge(*av_psum.at(g - 1, G))
                            v.tensor_tensor(rows_of_x(p, g - 1, 0, G), rows_of_x(p, g - 1, 0, G), O_BANK[:], ALU.add).then_inc(x_done.sem, 1)
                            row_statistics(p, dve, g - 1, x_done)
                        if not last:
                            for step, at in enumerate((2, 7, 9, 11)):
                                if u == at:
                                    front(g + 1, 1 - a, step)
                all_groups(dve, units)
        p.passed(NG)


def latent_weights(p):
    nc, w = p.nc, p.w
    sum_ready, down_psum, down_ready, up_psum = p.plan(latent_sum_ready=0, latent_psum=0, latent_ready=0, latent_up_psum=0)
    with ExitStack() as ctx:
        both, down = sb(p, ctx, "latent_both", [128, 128]), sb(p, ctx, "latent_down", [32, 128])
        with nc.Block(no_gpsimd_drain=True) as block:
            @block.vector
            def _(dve):
                nc.vector.tensor_tensor(both[:], w["L3_attn_W_k_T"][:], w["L3_attn_W_v_T"][:], ALU.add).then_inc(sum_ready.sem, 1)

            @block.tensor
            def _(pe):
                pe.wait_ge(*sum_ready.at(0, 1))
                nc.tensor.matmul(p.bank[0][0:32, 0:128], lhsT=w["L3_attn_W_down_kv"][:], rhs=both[:], start=True, stop=True)\
                    .then_inc(down_psum.sem, 1)
                pe.wait_ge(*down_ready.at(0, 1))
                for i, n in enumerate(("L3_attn_W_up_k", "L3_attn_W_up_v")):
                    last = nc.tensor.matmul(p.bank[1][:, batch(i)], lhsT=down[:], rhs=w[n][:], start=True, stop=True)
                last.then_inc(up_psum.sem, 1)

            @block.scalar
            def _(act):
                act.wait_ge(*down_psum.at(0, 1))
                nc.scalar.activation(down[:], p.bank[0][0:32, 0:128], ACT.Copy).then_inc(down_ready.sem, 1)
                act.wait_ge(*up_psum.at(0, 1))
                nc.scalar.activation(w["L3_K"][:], p.bank[1][:, batch(0)], ACT.Copy)
                nc.scalar.activation(w["L3_V"][:], p.bank[1][:, batch(1)], ACT.Copy)
    for s in (sum_ready, down_psum, down_ready, up_psum):
        s.base += 1



SUPPORT = 5


def support_attention(p, name):
    nc, ins, w = p.nc, p.inputs, p.w
    HEADS, HD3, CH = 8, 64, 4
    norm_rows(p, name, again=1e-5)
    (ctx_in, mask_in, xn_ready, xnT_psum, xnT_ready, q_psum, q_ready, k_psum, k_ready, v_psum, v_ready, named, order_psum,
     bias_ready, floor_steps, s_psum, raw_max, max_ready, shift_ready, e_ready, p_ready, t_psum, pt_ready, av_psum,
     r_steps, sum_ready, o_ready, oT_psum, oT_ready, y_psum, x_part, x_done) = p.plan(
        ctx_in=16, mask_in=16, xn_ready=G, xnT_psum=1, xnT_ready=1, q_psum=4, q_ready=4, k_psum=4, k_ready=4, v_psum=4,
        v_ready=4, mask_named=1, mask_order_psum=1, mask_ready=1, floor_steps=4, s_psum=G, raw_max=G, max_ready=G,
        masked_shift_ready=G, masked_exp_ready=G, p_ready=G, t_psum=G, pt_ready=G, av_psum=G, reciprocal_steps=G,
        masked_sum_steps=G, o_ready=G, oT_psum=G, oT_ready=G, y_psum=G, expert_added=G, x_done=1)
    prep, = p.plan(stage_prepared=0)
    T_BANK, O_BANK, M_BANK = p.bank[4:6], p.bank[6], p.bank[7]
    with ExitStack() as ctx:
        t = lambda k, shape, dt=F32: sb(p, ctx, f"{name}_{k}", shape, dt)
        xn, xnT = front(p, name, ctx)
        ctxT, mask = t("ctxT", [128, GT]), t("mask", [128, GT], I32)
        named_bf, ones, order = t("named", [128, GT], BF16), t("ones", [128, S], BF16), t("order", [128, S], BF16)
        score_bias = t("score_bias", [128, G, S], BF16)
        qT, kT, vv = t("qT", [128, CH, GT]), t("kT", [128, CH, GT]), t("v", [128, G, HEADS * HD3])
        probs, probsT = t("probs", [128, 2, 2, CH * S]), t("probsT", [128, 2, 2, CH * S])
        nmax, rsum, rrec, rowmax, eshift, e = (t(k, [128, G, HEADS]) for k in ("nmax", "rsum", "rrec", "rowmax", "eshift", "e"))
        pads, nfloor = t("pads", [128, G]), t("nfloor", [128, G])
        o, oT = t("o", [128, 2, HEADS * HD3]), t("oT", [128, 2, CH * S])

        with nc.Block(no_gpsimd_drain=True) as block:
            @block.gpsimd
            def _(pool):
                then = Chain(pool, prep)
                then(nc.gpsimd.memset(order[:], 1.0))
                then(nc.gpsimd.affine_select(out=order[:], in_=order[:], compare_op=ALU.is_ge, fill=0.0, base=0,
                                             pattern=[[1, S]], channel_multiplier=-1))
                then(nc.gpsimd.affine_select(out=order[:], in_=order[:], compare_op=ALU.not_equal, fill=-1024.0, base=0,
                                             pattern=[[1, S]], channel_multiplier=-1))
        prep.base += 3

        with nc.Block(no_gpsimd_drain=True) as block:
            @block.sync
            def _(sp):
                def load(g):
                    sp.dma_start(ctxT[:], ins["ctx_T"][:, ds(g * GT, GT)]).then_inc(ctx_in.sem, 16)
                    sp.dma_start(mask[:], ins["visible"][:, ds(g * GT, GT)]).then_inc(mask_in.sem, 16)
                load(0)
                with sp.Fori(1, NG) as g:
                    sp.wait_ge(*v_psum.at(g - 1, 4))
                    sp.wait_ge(*named.at(g - 1, 1))
                    load(g)

            @block.tensor
            def _(pe):
                mm = nc.tensor.matmul

                def scores(g, b):
                    banks = p.bank[2 * (b % 2):2 * (b % 2) + 2]
                    if b >= 2:
                        pe.wait_ge(*x_part.at(g, b - 1))
                    for r in range(2):
                        mm(banks[r][:], lhsT=p.ident_bf[:], rhs=score_bias[:, b, :].unsqueeze(1).to_broadcast([128, CH, S]),
                           start=True, stop=False, skip_group_check=True)
                    for ch in range(CH):
                        for r in range(2):
                            rows = slice(64 * r, 64 * r + 64)
                            last = mm(banks[r][:, batch(ch)], lhsT=qT[rows, ch, batch(b)], rhs=kT[rows, ch, batch(b)],
                                      start=False, stop=(ch == CH - 1), skip_group_check=True)
                    last.then_inc(s_psum.sem, 1)

                def output(g, b):
                    pe.wait_ge(*p_ready.at(g, b + 1))
                    if b:
                        pe.wait_ge(*pt_ready.at(g, b))
                    for r in range(2):
                        for ch in range(CH):
                            last = nc.tensor.transpose(T_BANK[r][:, batch(ch)], probs[:, b % 2, r, batch(ch)], p.ident[:])
                    last.then_inc(t_psum.sem, 1)
                    pe.wait_ge(*pt_ready.at(g, b + 1))
                    if b:
                        pe.wait_ge(*o_ready.at(g, b))
                    for h in range(HEADS):
                        last = mm(O_BANK[:, h * HD3:(h + 1) * HD3], lhsT=probsT[:, b % 2, h % 2, batch(h // 2)],
                                  rhs=vv[:, b, h * HD3:(h + 1) * HD3], start=True, stop=True)
                    last.then_inc(av_psum.sem, 1)
                    pe.wait_ge(*o_ready.at(g, b + 1))
                    if b:
                        pe.wait_ge(*oT_ready.at(g, b))
                    for ch in range(CH):
                        last = nc.tensor.transpose(M_BANK[:, batch(ch)], o[:, b % 2, batch(ch)], p.ident[:])
                    last.then_inc(oT_psum.sem, 1)
                    pe.wait_ge(*oT_ready.at(g, b + 1))
                    for ch in range(CH):
                        last = mm(p.bank[2 * (b % 2)][:, 0:D], lhsT=oT[:, b % 2, batch(ch)], rhs=w["L3_xattn_Wout"][:, ch, :],
                                  start=(ch == 0), stop=(ch == CH - 1))
                    last.then_inc(y_psum.sem, 1)

                with pe.Fori(0, NG) as g:
                    transpose_xn(p, pe, g, xn, xn_ready, M_BANK, xnT_psum)
                    pe.wait_ge(*named.at(g, 1))
                    for b in range(G):
                        last = mm(O_BANK[:, batch(b)], lhsT=named_bf[:, batch(b)], rhs=order[:], start=True, stop=True)
                    last.then_inc(order_psum.sem, 1)
                    pe.wait_ge(*ctx_in.at(g, 16))
                    for ch in range(CH):
                        mm(p.bank[ch][:], lhsT=w["L3_xattn_Wkv"][:, batch(ch)], rhs=ctxT[:], start=True, stop=True).then_inc(k_psum.sem, 1)
                    pe.wait_ge(*xnT_ready.at(g, 1))
                    for ch in range(CH):
                        pe.wait_ge(*k_ready.at(g, ch + 1))
                        mm(p.bank[ch][:], lhsT=w["L3_xattn_Wq"][:, batch(ch)], rhs=xnT[:], start=True, stop=True).then_inc(q_psum.sem, 1)
                    for b in range(G):
                        if b >= 2:
                            pe.wait_ge(*v_ready.at(g, b - 1))
                        mm(T_BANK[b % 2][:], lhsT=ctxT[:, batch(b)], rhs=w["L3_xattn_Wkv"][:, 512:1024], start=True, stop=True)\
                            .then_inc(v_psum.sem, 1)
                    pe.wait_ge(*q_ready.at(g, 4))
                    pe.wait_ge(*bias_ready.at(g, 1))
                    scores(g, 0)
                    scores(g, 1)
                    pe.wait_ge(*v_ready.at(g, 4))
                    output(g, 0)
                    for b in range(2, G):
                        scores(g, b)
                        output(g, b - 1)
                    output(g, G - 1)

            @block.scalar
            def _(act):
                nc.scalar.preload_act_table(ACT.Exp)
                with act.Fori(0, NG) as g:
                    act.wait_ge(*xnT_psum.at(g, 1))
                    nc.scalar.activation(xnT[:], M_BANK[:], ACT.Identity, scale=w["L3_xattn_ln_w"][:, 0:1],
                                         bias=w["L3_xattn_ln_b"][:, 0:1]).then_inc(xnT_ready.sem, 1)
                    for ch in range(CH):
                        act.wait_ge(*k_psum.at(g, ch + 1))
                        nc.scalar.activation(kT[:, ch, :], p.bank[ch][:], ACT.Copy).then_inc(k_ready.sem, 1)
                    for ch in range(CH):
                        act.wait_ge(*q_psum.at(g, ch + 1))
                        nc.scalar.activation(qT[:, ch, :], p.bank[ch][:], ACT.Copy, scale=HD3 ** -0.5).then_inc(q_ready.sem, 1)

                    def exps(b):
                        act.wait_ge(*max_ready.at(g, b + 1))
                        if b >= 2:
                            act.wait_ge(*t_psum.at(g, b - 1))
                        for r in range(2):
                            for ch in range(CH):
                                i = CH * r + ch
                                last = nc.scalar.activation(probs[:, b % 2, r, batch(ch)], p.bank[2 * (b % 2) + r][:, batch(ch)], ACT.Exp,
                                                            bias=nmax[:, b, i:i + 1], accum_out=rsum[:, b, i:i + 1])
                        last.then_inc(p_ready.sem, 1)
                        act.wait_ge(*shift_ready.at(g, b + 1))
                        nc.scalar.activation(e[:, b, :], eshift[:, b, :], ACT.Exp).then_inc(e_ready.sem, 1)

                    def out_copy(b):
                        act.wait_ge(*oT_psum.at(g, b + 1))
                        nc.scalar.activation(oT[:, b % 2, :], M_BANK[:], ACT.Copy).then_inc(oT_ready.sem, 1)

                    exps(0)
                    exps(1)
                    out_copy(0)
                    for b in range(2, G):
                        exps(b)
                        out_copy(b - 1)
                    out_copy(G - 1)

            @block.vector
            def _(dve):
                v = nc.vector

                def maxima(g, b):
                    dve.wait_ge(*s_psum.at(g, b + 1))
                    for r in range(2):
                        last = v.tensor_reduce(rowmax[:, b, CH * r:CH * r + CH], p.bank[2 * (b % 2) + r][:].rearrange("p (c k) -> p c k", c=CH),
                                               axis=AX, op=ALU.max, negate=True)
                    last.then_inc(raw_max.sem, 1)
                    dve.wait_ge(*raw_max.at(g, b + 1))
                    v.tensor_scalar(nmax[:, b, :], rowmax[:, b, :], nfloor[:, b:b + 1], None, ALU.min).then_inc(max_ready.sem, 1)
                    dve.wait_ge(*max_ready.at(g, b + 1))
                    v.tensor_scalar(eshift[:, b, :], nmax[:, b, :], 1e4, -1e4, ALU.min, ALU.add).then_inc(shift_ready.sem, 1)

                def output(g, b):
                    dve.wait_ge(*t_psum.at(g, b + 1))
                    for r in range(2):
                        last = v.tensor_copy(probsT[:, b % 2, r, :], T_BANK[r][:])
                    last.then_inc(pt_ready.sem, 1)
                    dve.wait_ge(*e_ready.at(g, b + 1))
                    v.scalar_tensor_tensor(rsum[:, b, :], e[:, b, :], pads[:, b:b + 1], rsum[:, b, :], ALU.mult, ALU.add)\
                        .then_inc(sum_ready.sem, 1)
                    dve.wait_ge(*sum_ready.at(g, b + 1))
                    v.reciprocal(rrec[:, b, :], rsum[:, b, :]).then_inc(r_steps.sem, 1)
                    dve.wait_ge(*r_steps.at(g, b + 1))
                    dve.wait_ge(*av_psum.at(g, b + 1))
                    v.tensor_tensor(o[:, b % 2, :].rearrange("p (c r d) -> p c r d", c=CH, r=2), O_BANK[:].rearrange("p (c r d) -> p c r d", c=CH, r=2),
                                    rrec[:, b, :].rearrange("p (r c) -> p c r", r=2).unsqueeze(3).to_broadcast([128, CH, 2, HD3]),
                                    ALU.mult).then_inc(o_ready.sem, 1)
                    dve.wait_ge(*y_psum.at(g, b + 1))
                    v.tensor_tensor(rows_of_x(p, g, b), rows_of_x(p, g, b), p.bank[2 * (b % 2)][:, 0:D], ALU.add).then_inc(x_part.sem, 1)

                with dve.Fori(0, NG) as g:
                    dve.wait_ge(*mask_in.at(g, 16))
                    v.tensor_scalar(named_bf[:], mask[:], 0.0, None, ALU.not_equal).then_inc(named.sem, 1)
                    normalise(p, dve, g, xn, xn_ready)
                    dve.wait_ge(*order_psum.at(g, 1))
                    v.tensor_scalar(score_bias[:].rearrange("p b k -> p (b k)"), O_BANK[:], -1024.0 + SUPPORT - 0.5, MASKED,
                                    ALU.is_gt, ALU.mult).then_inc(bias_ready.sem, 1)
                    dve.wait_ge(*bias_ready.at(g, 1))
                    v.tensor_reduce(pads[:], score_bias[:], axis=AX, op=ALU.add).then_inc(floor_steps.sem, 1)
                    dve.wait_ge(*floor_steps.at(g, 1))
                    v.tensor_scalar(pads[:], pads[:], 1.0 / MASKED, SUPPORT - S, ALU.mult, ALU.add).then_inc(floor_steps.sem, 1)
                    dve.wait_ge(*floor_steps.at(g, 2))
                    v.tensor_scalar(nfloor[:], pads[:], 0.5, -3e38, ALU.is_gt, ALU.mult).then_inc(floor_steps.sem, 1)
                    dve.wait_ge(*floor_steps.at(g, 3))
                    v.tensor_scalar(nfloor[:], nfloor[:], 3e38, 1e4, ALU.add, ALU.max).then_inc(floor_steps.sem, 1)
                    dve.wait_ge(*floor_steps.at(g, 4))
                    for b in range(G):
                        dve.wait_ge(*v_psum.at(g, b + 1))
                        v.tensor_copy(vv[:, b, :], T_BANK[b % 2][:]).then_inc(v_ready.sem, 1)
                    maxima(g, 0)
                    maxima(g, 1)
                    output(g, 0)
                    for b in range(2, G):
                        maxima(g, b)
                        output(g, b - 1)
                    output(g, G - 1)
                    dve.wait_ge(*x_part.at(g, G))
                    v.tensor_copy(pads[:, 0:1], pads[:, 0:1]).then_inc(x_done.sem, 1)
                    row_statistics(p, dve, g, x_done)
        p.passed(NG)



def quantised_ffn(p, name):
    nc, ins, w = p.nc, p.inputs, p.w
    F, CH = 512, 4
    ROUND = 1.5 * 2 ** 23
    norm_rows(p, name, again=1e-6)
    (xn_ready, q_steps, qT_psum, qT_ready, h_psum, h_in, h_ready, sums_ready, am_ready, ms_in, root_ready, tail, q2_steps,
     t_psum, t_ready, y_psum, x_done, added_steps) = p.plan(
        xn_ready=G, quantise_steps=5 + G + 1, xnT_psum=1, xnT_ready=1, h_psum=G, relu_ready=G, h_ready=G, squares_ready=G,
        max_ready=G, variance_ready=1, root_ready=1, tail_steps=5, quantise_2_steps=2 * G, t_psum=G, pt_ready=G, y_psum=1,
        x_done=1, added_steps=G)
    w_in, prep, prep_sum, prep_psum, prep_steps = p.plan(expert_weights_in=0, stage_prepared=0, weight_sums_ready=0, product_psum=0, angle_steps=0)
    M_BANK, T_BANK, Y_BANK = p.bank[6], p.bank[4:6], p.bank[7]
    with ExitStack() as ctx:
        t = lambda k, shape, dt=F32: sb(p, ctx, f"{name}_{k}", shape, dt)
        xn = t("xn", [128, GT])
        w1, w2, q1, q2 = t("w1", [128, F]), t("w2", [128, CH * D]), t("q1", [128, F], BF16), t("q2", [128, CH * D], BF16)
        ones, sums, mean, wscale = t("ones", [128, 128]), t("sums", [128, 2]), t("mean", [128, 2]), t("wscale", [128, 2])
        most, scale, back = t("most", [128, G]), t("scale", [128, G]), t("back", [128, G])
        xqT = t("xqT", [128, GT], BF16)
        pre, h, junk = t("pre", [128, 2, F]), t("h", [128, G, F]), t("junk", [128, F])
        ss, most2, veps, root, rs, scale2, back2 = (t(k, [128, G]) for k in ("ss", "most2", "veps", "root", "rs", "scale2", "back2"))
        hqT = t("hqT", [128, 2, CH * S], BF16)

        with nc.Block(no_gpsimd_drain=True) as block:
            @block.sync
            def _(sp):
                sp.dma_start(w1[:], ins["L3_ffn_w1T"]).then_inc(w_in.sem, 16)
                sp.dma_start(w2[:], ins["L3_ffn_w2T"]).then_inc(w_in.sem, 16)

            @block.gpsimd
            def _(pool):
                Chain(pool, prep)(nc.gpsimd.memset(ones[:], 1.0))

            @block.tensor
            def _(pe):
                pe.wait_ge(*prep.at(0, 1))
                pe.wait_ge(*prep_sum.at(0, 2))
                nc.tensor.matmul(M_BANK[:, 0:2], lhsT=ones[:], rhs=sums[:], start=True, stop=True).then_inc(prep_psum.sem, 1)

            @block.vector
            def _(dve):
                v = nc.vector
                then = Chain(dve, prep_steps)
                dve.wait_ge(*w_in.at(0, 32))
                for i, m in enumerate((w1, w2)):
                    v.tensor_reduce(sums[:, i:i + 1], m[:], axis=AX, op=ALU.add, apply_absolute_value=True).then_inc(prep_sum.sem, 1)
                dve.wait_ge(*prep_psum.at(0, 1))
                then(v.tensor_scalar(mean[:], M_BANK[:, 0:2], 1.0 / (F * D), 1e-5, ALU.mult, ALU.max))
                then(v.reciprocal(wscale[:], mean[:]))
                for i, (m, q) in enumerate(((w1, q1), (w2, q2))):
                    then(v.tensor_scalar(m[:], m[:], wscale[:, i:i + 1], ROUND, ALU.mult, ALU.add))
                    then(v.tensor_scalar(m[:], m[:], ROUND, -1.0, ALU.subtract, ALU.max))
                    then(v.tensor_scalar(q[:], m[:], 1.0, None, ALU.min))
                then(v.tensor_scalar(mean[:], mean[:], 1.0 / 127.0, None, ALU.mult))
        for s, n in ((w_in, 32), (prep, 1), (prep_sum, 2), (prep_psum, 1), (prep_steps, 9)):
            s.base += n

        with nc.Block(no_gpsimd_drain=True) as block:
            @block.tensor
            def _(pe):
                mm = nc.tensor.matmul
                with pe.Fori(0, NG) as g:
                    pe.wait_ge(*q_steps.at(g, q_steps.per))
                    for b in range(G):
                        last = nc.tensor.transpose(M_BANK[:, batch(b)], xn[:, batch(b)], p.ident[:])
                    last.then_inc(qT_psum.sem, 1)
                    pe.wait_ge(*qT_ready.at(g, 1))
                    for b in range(G):
                        mm(p.bank[b][:], lhsT=xqT[:, batch(b)], rhs=q1[:], start=True, stop=True).then_inc(h_psum.sem, 1)

                    def second(b):
                        pe.wait_ge(*t_ready.at(g, b + 1))
                        for ch in range(CH):
                            last = mm(Y_BANK[:, batch(b)], lhsT=hqT[:, b % 2, batch(ch)], rhs=q2[:, batch(ch)],
                                      start=(ch == 0), stop=(ch == CH - 1))
                        return last

                    for b in range(G):
                        pe.wait_ge(*q2_steps.at(g, 2 * b + 2))
                        if b >= 2:
                            pe.wait_ge(*t_ready.at(g, b - 1))
                        for ch in range(CH):
                            last = nc.tensor.transpose(T_BANK[b % 2][:, batch(ch)], h[:, b, batch(ch)], p.ident[:])
                        last.then_inc(t_psum.sem, 1)
                        if b:
                            second(b - 1)
                    second(G - 1).then_inc(y_psum.sem, 1)

            @block.scalar
            def _(act):
                with act.Fori(0, NG) as g:
                    act.wait_ge(*qT_psum.at(g, 1))
                    nc.scalar.activation(xqT[:], M_BANK[:], ACT.Copy).then_inc(qT_ready.sem, 1)
                    for b in range(G):
                        act.wait_ge(*h_in.at(g, b + 1))
                        nc.scalar.activation(h[:, b, :], pre[:, b % 2, :], ACT.Gelu).then_inc(h_ready.sem, 1)
                        act.wait_ge(*h_ready.at(g, b + 1))
                        nc.scalar.activation(junk[:], h[:, b, :], ACT.Square, accum_out=ss[:, b:b + 1]).then_inc(sums_ready.sem, 1)
                    act.wait_ge(*ms_in.at(g, 1))
                    nc.scalar.activation(root[:], veps[:], ACT.Sqrt).then_inc(root_ready.sem, 1)
                    for b in range(G):
                        act.wait_ge(*t_psum.at(g, b + 1))
                        nc.scalar.activation(hqT[:, b % 2, :], T_BANK[b % 2][:], ACT.Copy).then_inc(t_ready.sem, 1)

            @block.vector
            def _(dve):
                v = nc.vector
                with dve.Fori(0, NG) as g:
                    normalise(p, dve, g, xn, xn_ready)
                    dve.wait_ge(*xn_ready.at(g, G))
                    then = Chain(dve, q_steps, g)
                    then(v.tensor_reduce(most[:], xn[:].rearrange("p (b d) -> p b d", b=G), axis=AX, op=ALU.max, apply_absolute_value=True))
                    then(v.tensor_scalar(most[:], most[:], 1e-5, None, ALU.max))
                    then(v.reciprocal(scale[:], most[:]))
                    then(v.tensor_scalar(scale[:], scale[:], 127.0, None, ALU.mult))
                    then(v.tensor_scalar(back[:], most[:], mean[:, 0:1], None, ALU.mult))
                    for b in range(G):
                        v.tensor_scalar(xn[:, batch(b)], xn[:, batch(b)], scale[:, b:b + 1], ROUND, ALU.mult, ALU.add).then_inc(q_steps.sem, 1)
                    then.n += G
                    dve.wait_ge(*q_steps.at(g, then.n))
                    then(v.tensor_scalar(xn[:], xn[:], ROUND, None, ALU.subtract))
                    then.ends()
                    for b in range(G):
                        dve.wait_ge(*h_psum.at(g, b + 1))
                        if b >= 2:
                            dve.wait_ge(*h_ready.at(g, b - 1))
                        v.scalar_tensor_tensor(pre[:, b % 2, :], p.bank[b][:], back[:, b:b + 1], w["L3_ffn_b1"][:], ALU.mult, ALU.add)\
                            .then_inc(h_in.sem, 1)
                    for b in range(G):
                        dve.wait_ge(*h_ready.at(g, b + 1))
                        v.tensor_reduce(most2[:, b:b + 1], h[:, b, :], axis=AX, op=ALU.max, apply_absolute_value=True).then_inc(am_ready.sem, 1)
                    dve.wait_ge(*sums_ready.at(g, G))
                    v.tensor_scalar(veps[:], ss[:], 1.0 / F, 1e-6, ALU.mult, ALU.add).then_inc(ms_in.sem, 1)
                    dve.wait_ge(*root_ready.at(g, 1))
                    then = Chain(dve, tail, g)
                    dve.wait_ge(*am_ready.at(g, G))
                    then(v.reciprocal(rs[:], root[:]))
                    then(v.tensor_tensor(most2[:], most2[:], rs[:], ALU.mult))
                    then(v.tensor_scalar(most2[:], most2[:], 1e-5, None, ALU.max))
                    then(v.reciprocal(scale2[:], most2[:]))
                    v.tensor_scalar(back2[:], most2[:], mean[:, 1:2], None, ALU.mult)
                    then(v.scalar_tensor_tensor(scale2[:], scale2[:], 127.0, rs[:], ALU.mult, ALU.mult))
                    then.ends()
                    for b in range(G):
                        v.tensor_scalar(h[:, b, :], h[:, b, :], scale2[:, b:b + 1], ROUND, ALU.mult, ALU.add).then_inc(q2_steps.sem, 1)
                        dve.wait_ge(*q2_steps.at(g, 2 * b + 1))
                        v.tensor_scalar(h[:, b, :], h[:, b, :], ROUND, None, ALU.subtract).then_inc(q2_steps.sem, 1)
                    dve.wait_ge(*y_psum.at(g, 1))
                    for b in range(G):
                        v.scalar_tensor_tensor(xn[:, batch(b)], Y_BANK[:, batch(b)], back2[:, b:b + 1], w["L3_ffn_b2"][:], ALU.mult, ALU.add)\
                            .then_inc(added_steps.sem, 1)
                    dve.wait_ge(*added_steps.at(g, G))
                    v.tensor_tensor(rows_of_x(p, g, 0, G), rows_of_x(p, g, 0, G), xn[:], ALU.add).then_inc(x_done.sem, 1)
                    dve.wait_ge(*x_done.at(g, 1))
        p.passed(NG)


def store_out(p, out):
    nc, stored = p.nc, p.count_of("out_stored")
    with nc.Block(no_gpsimd_drain=True) as block:
        @block.sync
        def _(sp):
            for i in range(4):
                sp.dma_start(out[:, i * 1024:(i + 1) * 1024], p.x[:, i * 1024:(i + 1) * 1024]).then_inc(stored.sem, 16)
            sp.wait_ge(stored.sem, 64)


def build(nc, inputs, out, stages=12):
    with ExitStack() as ctx:
        p = Program(nc, ctx, inputs)
        load_all(p)
        for stage in STAGES[:stages]:
            stage(p)
        store_out(p, out)


STAGES = [
    lambda p: attention16(p, "L0a", "L0_attn_WQ", "L0_attn_WK", "L0_attn_WV", "L0_attn_WO", scale=HD ** -0.5, causal=True),
    lambda p: attention16(p, "L0x", "L0_xattn_w_q", "L0_xattn_w_k", "L0_xattn_w_v", "L0_xattn_w_o", cross=True,
                          b_q="L0_xattn_b_q", b_k="L0_xattn_b_k", b_v="L0_xattn_b_v", b_o="L0_xattn_b_o",
                          scale=HD ** -0.5, where_mask=True),
    lambda p: ffn_squared_relu(p, "L0f"),
    lambda p: linear_attention(p, "L1a"),
    lambda p: single_head(p, "L1x"),
    lambda p: ffn_sigmoid_experts(p, "L1f"),
    lambda p: channel_attention(p, "L2a"),
    lambda p: attention16(p, "L2x", "L2_xattn_Wq", "L2_xattn_Wk", "L2_xattn_Wv", cross=True, b_q="L2_xattn_bq",
                          b_k="L2_xattn_bk", b_v="L2_xattn_bv", key_mask=True),
    lambda p: ffn_linear_experts(p, "L2f"),
    lambda p: (latent_weights(p), attention16(p, "L3a", "L3_attn_W_q", "L3_K", "L3_V", "L3_attn_W_o", scale=D ** -0.5, decay=True)),
    lambda p: support_attention(p, "L3x"),
    lambda p: quantised_ffn(p, "L3f"),
]



def layouts(i):
    a = {k: np.asarray(v) for k, v in i.items()}
    T = lambda m: np.ascontiguousarray(m.T)
    rows = lambda m: np.ascontiguousarray(m.transpose(1, 0, 2)).reshape(128, -1)
    cols = lambda m: np.ascontiguousarray(m.transpose(2, 0, 1)).reshape(128, -1)
    o = {"x": rows(a["x"]), "ctx_T": cols(a["ctx_1024"]), "ctx_rows": rows(a["ctx_1024"])}
    m = a["mask_Bx1xSxS2_if1"][:, 0]
    o["mask_qk"], o["mask_kq"] = rows(m), cols(m)
    o["key_mask"] = a["mask_BxS2_ik0"]
    o["visible"] = rows(a["mask_BxS2xS_ik0"])
    for n in ["L0_attn_WQ", "L0_attn_WK", "L0_attn_WV", "L0_attn_WO", "L2_xattn_Wq", "L2_xattn_Wk", "L2_xattn_Wv",
              "L1_attn_out_w"]:
        o[n] = T(a[n])
    for n in ["L0_xattn_w_q", "L0_xattn_w_k", "L0_xattn_w_v", "L0_xattn_w_o", "L2_attn_Wq", "L2_attn_Wk",
              "L2_attn_Wv", "L3_attn_W_q", "L3_attn_W_o", "L0_xattn_b_q", "L0_xattn_b_k", "L2_attn_bq",
              "L2_xattn_bq", "L2_xattn_bk", "L3_xattn_ln_w", "L3_xattn_ln_b", "L0_xattn_b_v", "L0_xattn_b_o",
              "L1_attn_out_b", "L2_attn_bk", "L2_attn_bv", "L2_xattn_bv", "L3_ffn_b1", "L3_ffn_b2", "L0_ffn_Wg",
              "L2_ffn_Wr", "L3_xattn_Wq", "L3_xattn_Wkv", "L3_attn_W_down_kv", "L3_attn_W_up_k", "L3_attn_W_up_v"]:
        o[n] = a[n]
    o["L0_ffn_W1"] = np.ascontiguousarray(a["L0_ffn_W1"].transpose(1, 0, 2))
    o["L0_ffn_W2"] = np.ascontiguousarray(a["L0_ffn_W2"].reshape(8, 2, 128, 128).transpose(2, 0, 1, 3))
    o["L2_ffn_WiT"] = np.ascontiguousarray(a["L2_ffn_Wi"].transpose(2, 0, 1))
    o["L2_ffn_Wo"] = np.ascontiguousarray(a["L2_ffn_Wo"].transpose(1, 0, 2))
    o["L1_ffn_keys"] = cols(a["L1_ffn_keys"].transpose(0, 2, 1))
    o["L1_ffn_values"] = rows(a["L1_ffn_values"])
    o["L3_ffn_w1T"] = T(a["L3_ffn_w1"])
    o["L3_ffn_w2T"] = rows(np.ascontiguousarray(a["L3_ffn_w2"].T).reshape(4, 128, 128))
    o["L1_ffn_sel"] = T(a["L1_ffn_expert_sel"])
    o["L3_attn_W_k_T"], o["L3_attn_W_v_T"] = T(a["L3_attn_W_k"]), T(a["L3_attn_W_v"])
    o["L3_xattn_Wout"] = np.ascontiguousarray(a["L3_xattn_Wout"].reshape(4, 128, 128).transpose(1, 0, 2))
    w, bias = a["L1_attn_qkvu_w"], a["L1_attn_qkvu_b"]
    twice = np.concatenate([np.r_[16 * h:16 * h + 16, 16 * h:16 * h + 16] for h in range(8)])
    order = np.concatenate([twice, 128 + twice])
    o["L1_attn_qk"] = np.ascontiguousarray(w[order].reshape(4, 128, 128).transpose(2, 0, 1))
    o["L1_attn_qk_b"] = np.ascontiguousarray(bias[order].reshape(4, 128).T)
    o["L1_attn_vu"] = np.ascontiguousarray(w[256:].reshape(2, 128, 128).transpose(2, 0, 1))
    o["L1_attn_vb"] = bias[256:384].copy()
    o["L1_attn_ub"] = bias[384:].reshape(128, 1).copy()
    th = a["L1_attn_theta"].reshape(128)[twice]
    o["L1_attn_theta"] = np.ascontiguousarray(th.reshape(2, 128).T)
    o["L1_attn_slope"] = a["L1_attn_slope_rate"].reshape(8)
    o["L2_attn_temp"] = np.repeat(a["L2_attn_temperature"].reshape(16), 8).reshape(128, 1)
    return o


def kernel(**inputs):
    import concourse.bacc as bacc
    from concourse.bass_utils import run_bass_kernel_spmd

    nc = bacc.Bacc("TRN2", target_bir_lowering=False, num_devices=1)
    arrays = layouts(inputs)
    aps = {n: nc.dram_tensor(n, a.shape, mybir.dt.from_np(a.dtype), kind="ExternalInput").ap() for n, a in arrays.items()}
    out = nc.dram_tensor("out", (128, B * D), F32, kind="ExternalOutput").ap()
    build(nc, aps, out)
    got = run_bass_kernel_spmd(nc, [arrays], core_ids=[0]).results[0]["out"]
    return np.ascontiguousarray(got.reshape(128, B, D).transpose(1, 0, 2))
```

```python
import numpy as np
from contextlib import ExitStack

import concourse.bass as bass
import concourse.mybir as mybir

F32 = mybir.dt.float32
BF16 = mybir.dt.bfloat16
I32 = mybir.dt.int32
U32 = mybir.dt.uint32
ALU = mybir.AluOpType
ACT = mybir.ActivationFunctionType
AX = mybir.AxisListType.X

B, S, D = 32, 128, 128
G = 4
NG = B // G
GT = G * S
H, HD = 16, 8
QUADS, PER = 4, 4
LN_EPS = 1e-5
MASKED = -2.0 ** 100
ds = bass.ds


class Count:

    def __init__(self, sem):
        self.sem, self.base, self.per = sem, 0, 0

    def at(self, g, n):
        return self.sem, g * self.per + (self.base + n)


class Program:

    def __init__(self, nc, ctx, inputs):
        self.nc, self.ctx, self.inputs = nc, ctx, inputs
        self.counts = {}

    def count_of(self, name):
        if name not in self.counts:
            self.counts[name] = Count(self.ctx.enter_context(self.nc.semaphore(name)))
        return self.counts[name]

    def plan(self, **per):
        for name, n in per.items():
            self.count_of(name).per = n
        return [self.count_of(name) for name in per]

    def passed(self, passes):
        for s in self.counts.values():
            s.base += s.per * passes
            s.per = 0


def sb(p, ctx, name, shape, dt=F32):
    return ctx.enter_context(p.nc.sbuf_tensor(name, shape, dt))


class Chain:

    def __init__(self, eng, steps, g=0):
        self.eng, self.steps, self.g, self.n = eng, steps, g, 0

    def __call__(self, instruction):
        self.n += 1
        instruction.then_inc(self.steps.sem, 1)
        self.eng.wait_ge(*self.steps.at(self.g, self.n))

    def ends(self):
        assert self.n == self.steps.per, (self.steps.sem, self.n, self.steps.per)



def load_all(p):
    nc, ctx, ins = p.nc, p.ctx, p.inputs
    p.x = sb(p, ctx, "x_res", [128, B * D])
    p.stats = sb(p, ctx, "row_stats", [128, B, 6])
    p.rstd = sb(p, ctx, "ln_scale", [128, B])
    p.shift = sb(p, ctx, "ln_shift", [128, B])
    p.ident = sb(p, ctx, "ident", [128, 128])
    p.ident_bf = sb(p, ctx, "ident_bf", [128, 128], BF16)
    p.head_mask = sb(p, ctx, "head_mask", [128, PER])
    p.bank = [ctx.enter_context(nc.psum_tensor(f"bank{i}", [128, GT], F32)) for i in range(8)]
    p.w = {}

    def weight(name, shape, src=None):
        p.w[name] = sb(p, ctx, "w_" + name, shape)
        return p.w[name], ins[src or name]

    square = ["L0_attn_WQ", "L0_attn_WK", "L0_attn_WV", "L0_attn_WO", "L0_xattn_w_q", "L0_xattn_w_k",
              "L0_xattn_w_v", "L0_xattn_w_o", "L2_attn_Wq", "L2_attn_Wk", "L2_attn_Wv",
              "L2_xattn_Wq", "L2_xattn_Wk", "L2_xattn_Wv", "L3_attn_W_q", "L3_attn_W_o", "L1_attn_out_w"]
    loads = [weight(n, [128, 128]) for n in square]
    for n in ["L0_xattn_b_q", "L0_xattn_b_k", "L2_attn_bq", "L2_xattn_bq", "L2_xattn_bk",
              "L3_xattn_ln_w", "L3_xattn_ln_b"]:
        t, src = weight(n, [128, 1])
        loads.append((t, src.rearrange("(p a) -> p a", a=1)))
    rows = {"L0_xattn_b_v": 128, "L0_xattn_b_o": 128, "L1_attn_out_b": 128, "L2_attn_bk": 128,
            "L2_attn_bv": 128, "L2_xattn_bv": 128, "L3_ffn_b1": 512, "L3_ffn_b2": 128}
    for n, width in rows.items():
        t, src = weight(n, [128, width])
        loads.append((t, src.rearrange("(a n) -> a n", a=1).to_broadcast([128, width])))
    loads.append(weight("L0_ffn_Wg", [128, 8]))
    loads.append(weight("L2_ffn_Wr", [128, 8]))
    loads.append(weight("L1_ffn_sel", [128, 64]))
    loads.append(weight("L3_xattn_Wq", [128, 512]))
    loads.append(weight("L3_xattn_Wkv", [128, 1024]))
    loads.append(weight("L3_xattn_Wout", [128, 4, 128]))
    loads.append(weight("L1_attn_qk", [128, 4, 128]))
    loads.append(weight("L1_attn_vu", [128, 2, 128]))
    loads.append(weight("L1_attn_qk_b", [128, 4]))
    loads.append(weight("L1_attn_theta", [128, 2]))
    t, src = weight("L1_attn_vb", [128, 128])
    loads.append((t, src.rearrange("(a n) -> a n", a=1).to_broadcast([128, 128])))
    loads.append(weight("L1_attn_ub", [128, 1]))
    t, src = weight("L1_attn_slope", [128, 8])
    loads.append((t, src.rearrange("(a n) -> a n", a=1).to_broadcast([128, 8])))
    loads.append(weight("L2_attn_temp", [128, 1]))
    loads.append(weight("L3_attn_W_k_T", [128, 128]))
    loads.append(weight("L3_attn_W_v_T", [128, 128]))
    loads.append(weight("L3_attn_W_down_kv", [128, 32]))
    loads.append(weight("L3_attn_W_up_k", [32, 128]))
    loads.append(weight("L3_attn_W_up_v", [32, 128]))
    p.w["L2_ffn_M"] = sb(p, ctx, "w_L2_ffn_M", [128, 8, 128])
    p.w["L3_K"] = sb(p, ctx, "w_L3_K", [128, 128])
    p.w["L3_V"] = sb(p, ctx, "w_L3_V", [128, 128])
    p.w["L2_vmask"] = sb(p, ctx, "L2_vmask", [128, PER])

    x_in, w_in, ones_m = (p.count_of(n) for n in ("x_in", "weights_in", "constant_steps"))
    with nc.Block(no_gpsimd_drain=True) as block:
        @block.sync
        def _(sp):
            for i in range(4):
                sp.dma_start(p.x[:, i * 1024:(i + 1) * 1024], ins["x"][:, i * 1024:(i + 1) * 1024]).then_inc(x_in.sem, 16)
            for t, src in loads:
                sp.dma_start(t[:], src).then_inc(w_in.sem, 16)
            sp.wait_ge(w_in.sem, 16 * len(loads))

        @block.gpsimd
        def _(pool):
            then = Chain(pool, ones_m)
            then(nc.gpsimd.memset(p.ident[:], 0.0))
            then(nc.gpsimd.memset(p.head_mask[:], 1.0))
            then(nc.gpsimd.affine_select(out=p.ident[:], in_=p.ident[:], compare_op=ALU.not_equal, fill=1.0, base=0,
                                         pattern=[[-1, 128]], channel_multiplier=1))
            for j in range(QUADS):
                rows = p.head_mask[32 * j:32 * j + 32, :]
                then(nc.gpsimd.affine_select(out=rows, in_=rows, compare_op=ALU.is_ge, fill=0.0, base=0,
                                             pattern=[[-HD, PER]], channel_multiplier=1))
                then(nc.gpsimd.affine_select(out=rows, in_=rows, compare_op=ALU.is_ge, fill=0.0, base=HD - 1,
                                             pattern=[[HD, PER]], channel_multiplier=-1))

        @block.vector
        def _(dve):
            dve.wait_ge(ones_m.sem, 3)
            nc.vector.tensor_copy(p.ident_bf[:], p.ident[:])
            dve.wait_ge(x_in.sem, 64)
            for b in range(B):
                nc.vector.bn_stats(p.stats[:, b, :], p.x[:, b * D:(b + 1) * D])


def norm_rows(p, name, again=None):
    nc = p.nc
    steps, var_ready, root_ready = p.count_of("norm_steps"), p.count_of("variance_ready"), p.count_of("root_ready")
    rounds = 2 if again else 1
    with ExitStack() as ctx:
        a, b, var, y, h, mean, root, veps = (
            sb(p, ctx, f"{name}_norm_{k}", [128, B]) for k in ("a", "b", "var", "y", "h", "mean", "root", "veps"))
        with nc.Block(no_gpsimd_drain=True) as block:
            @block.scalar
            def _(act):
                for r in range(rounds):
                    act.wait_ge(*var_ready.at(0, r + 1))
                    nc.scalar.activation(root[:], veps[:], ACT.Sqrt).then_inc(root_ready.sem, 1)

            @block.vector
            def _(dve):
                then = Chain(dve, steps)
                v = nc.vector

                def inverse_root(out, r):
                    dve.wait_ge(*root_ready.at(0, r + 1))
                    then(v.reciprocal(y[:], root[:]))
                    then(v.tensor_tensor(h[:], y[:], y[:], ALU.mult))
                    then(v.tensor_tensor(h[:], h[:], veps[:], ALU.mult))
                    then(v.tensor_scalar(h[:], h[:], -0.5, 1.5, ALU.mult, ALU.add))
                    then(v.tensor_tensor(out[:], y[:], h[:], ALU.mult))

                me, mo, qe, qo = (p.stats[:, :, i] for i in (1, 4, 2, 5))
                then(v.tensor_tensor(mean[:], me, mo, ALU.add))
                then(v.tensor_tensor(a[:], me, mo, ALU.subtract))
                then(v.tensor_tensor(b[:], qe, qo, ALU.add))
                then(v.tensor_tensor(a[:], a[:], a[:], ALU.mult))
                then(v.tensor_scalar(b[:], b[:], 1.0 / D, None, ALU.mult))
                then(v.scalar_tensor_tensor(var[:], a[:], 0.25, b[:], ALU.mult, ALU.add))
                v.tensor_scalar(veps[:], var[:], LN_EPS, None, ALU.add).then_inc(var_ready.sem, 1)
                inverse_root(p.rstd, 0)
                then(v.tensor_tensor(a[:], mean[:], p.rstd[:], ALU.mult))
                then(v.tensor_scalar(p.shift[:], a[:], -0.5, None, ALU.mult))
                if again:
                    then(v.tensor_tensor(a[:], p.rstd[:], p.rstd[:], ALU.mult))
                    then(v.tensor_tensor(a[:], a[:], var[:], ALU.mult))
                    v.tensor_scalar(veps[:], a[:], again, None, ALU.add).then_inc(var_ready.sem, 1)
                    inverse_root(a, 1)
                    then(v.tensor_tensor(p.rstd[:], p.rstd[:], a[:], ALU.mult))
                    then(v.tensor_tensor(p.shift[:], p.shift[:], a[:], ALU.mult))
                steps.base += then.n
    var_ready.base += rounds
    root_ready.base += rounds



def rows_of_x(p, g, b, n=1):
    return p.x[:, ds(g * (G * D) + b * D, n * D)]


def normalise(p, dve, g, xn, xn_ready):
    for b in range(G):
        one = ds(g * G + b, 1)
        p.nc.vector.tensor_scalar(xn[:, b * D:(b + 1) * D], rows_of_x(p, g, b), p.rstd[:, one], p.shift[:, one],
                                  ALU.mult, ALU.add).then_inc(xn_ready.sem, 1)


def transpose_xn(p, pe, g, xn, xn_ready, bank, xnT_psum):
    for b in range(G):
        pe.wait_ge(*xn_ready.at(g, b + 1))
        last = p.nc.tensor.transpose(bank[:, b * S:(b + 1) * S], xn[:, b * D:(b + 1) * D], p.ident[:])
    last.then_inc(xnT_psum.sem, 1)


def row_statistics(p, dve, g, x_done, n=1):
    dve.wait_ge(*x_done.at(g, n))
    for b in range(G):
        p.nc.vector.bn_stats(p.stats[:, ds(g * G + b, 1), :].rearrange("p a s -> p (a s)"), rows_of_x(p, g, b))


def batch(b):
    return slice(b * S, (b + 1) * S)


UNITS = 4 * G


def all_groups(eng, units, n=UNITS):
    units(0, 0, n, True, False)
    with eng.Fori(0, NG // 2 - 1) as i:
        units(i * 2 + 1, 1, n, False, False)
        units(i * 2 + 2, 0, n, False, False)
    units(NG - 1, 1, n, False, True)
    units(NG, 0, 0, False, True)


def before(g, a, u, lag, n=UNITS):
    return (g, a, u - lag) if u >= lag else (g - 1, 1 - a, u - lag + n)



def attention16(p, name, w_q, w_k, w_v, w_o=None, cross=False, b_q=None, b_k=None, b_v=None, b_o=None,
                scale=1.0, causal=False, where_mask=False, key_mask=False, decay=False):
    nc, ins = p.nc, p.inputs
    norm_rows(p, name)
    U = UNITS
    (xn_ready, xnT_psum, xnT_ready, q_psum, k_psum, v_psum, q_ready, k_ready, kmask_ready, v_ready, s_psum, max_ready,
     p_ready, t_psum, pt_ready, av_psum, r_ready, rT_psum, rT_ready, oT_ready, y_psum, x_done) = p.plan(
        xn_ready=G, xnT_psum=1, xnT_ready=1, q_psum=1, k_psum=1, v_psum=1, q_ready=1, k_ready=1, kmask_ready=U,
        v_ready=1, s_psum=U, max_ready=U, p_ready=U, t_psum=U, pt_ready=U, av_psum=G, r_ready=G,
        rT_psum=1, rT_ready=1, oT_ready=1, y_psum=1, x_done=1)
    ctx_in, mask_in, mask_ready, prep_ready = p.plan(ctx_in=16 * cross, mask_in=16 * (key_mask + 2 * where_mask),
                                                     mask_ready=(key_mask or 2 * where_mask), stage_prepared=0)
    raw_max, decayed, floor_steps, e_in, e_ready, z_psum, z_ready, ze_ready, sum_ready = p.plan(
        raw_max=U * where_mask, decayed=U * decay, floor_steps=4 * where_mask, masked_shift_ready=G * where_mask,
        masked_exp_ready=G * where_mask, masked_v_psum=where_mask, masked_v_ready=where_mask,
        masked_v_scaled=G * where_mask, masked_sum_steps=G * where_mask)
    r_steps, bias_added = p.plan(reciprocal_steps=G, bias_added=bool(b_o))
    w = p.w
    S_BANK, T_BANK, M_BANK, O_BANK = p.bank[0:4], p.bank[4:6], p.bank[6], p.bank[7]
    masked = causal or where_mask or key_mask

    with ExitStack() as ctx:
        t = lambda k, shape, dt=F32: sb(p, ctx, f"{name}_{k}", shape, dt)
        xn, xnT, qT, kT = t("xn", [128, GT]), t("xnT", [128, GT]), t("qT", [128, 2, GT]), t("kT", [128, 2, GT])
        ctxT = t("ctxT", [128, GT]) if cross else xnT
        kmask = t("kmask", [128, 2, QUADS, PER * S])
        vpad = t("vpad", [128, 2, G * H * 32])
        nmax, rsum, rrec = t("nmax", [128, G, H]), t("rsum", [128, G, H]), t("rrec", [128, G, H])
        probs = t("probs", [128, 4, PER * S])
        probsT = t("probsT", [128, 2, QUADS, PER * S])
        rrep, rT, oT = t("rrep", [128, GT]), t("rT", [128, GT]), t("oT", [128, GT])
        scaled_mask = t("scaled_mask", [128, H])
        spare = t("spare", [128, 1])
        if masked:
            score_bias = t("score_bias", [128, 1 if causal else 2, 1 if causal else G, S], BF16)
        if key_mask or where_mask:
            mask_q = t("mask_q", [128, G, S], I32)
        if where_mask:
            mask_k, masked_k = t("mask_k", [128, G * S], I32), t("masked_k", [128, G * S])
            least, nfloor, count = (t(k, [128, 2, G]) for k in ("least", "nfloor", "count"))
            rowmax, eshift, e = (t(k, [128, G, H]) for k in ("rowmax", "eshift", "e"))
            z, ze = t("masked_v", [128, 2, GT]), t("masked_v_scaled", [128, G, D])
        if decay:
            decay_m, distance = t("decay", [128, S]), t("distance", [128, S])
            scored = t("scored", [128, 4, PER * S])

        def head_slots(a, b=None):
            q = vpad[:, a, :] if b is None else vpad[:, a, b * H * 32:(b + 1) * H * 32]
            return bass.AP(q.tensor, q.offset, [list(q.ap[0]), [128, QUADS * (G if b is None else 1)], [40, PER], [1, HD]])

        with nc.Block(no_gpsimd_drain=True) as block:
            @block.gpsimd
            def _(pool):
                then = Chain(pool, prep_ready)
                then(nc.gpsimd.memset(vpad[:], 0.0))
                then(nc.gpsimd.memset(spare[:], 0.0))
                then(nc.gpsimd.memset(scaled_mask[:], scale))
                then(nc.gpsimd.affine_select(out=scaled_mask[:], in_=scaled_mask[:], compare_op=ALU.is_ge, fill=0.0, base=0,
                                             pattern=[[-HD, H]], channel_multiplier=1))
                then(nc.gpsimd.affine_select(out=scaled_mask[:], in_=scaled_mask[:], compare_op=ALU.is_ge, fill=0.0,
                                             base=HD - 1, pattern=[[HD, H]], channel_multiplier=-1))
                if causal:
                    then(nc.gpsimd.memset(score_bias[:], 0.0))
                    then(nc.gpsimd.affine_select(out=score_bias[:, 0, 0, :], in_=score_bias[:, 0, 0, :], compare_op=ALU.is_ge,
                                                 fill=MASKED, base=0, pattern=[[-1, S]], channel_multiplier=1))
                if decay:
                    then(nc.gpsimd.iota(distance[:], pattern=[[1, S]], base=0, channel_multiplier=-1,
                                        allow_small_or_imprecise_dtypes=True))

            if decay:
                @block.scalar
                def _(act):
                    act.wait_ge(*prep_ready.at(0, 6))
                    nc.scalar.activation(decay_m[:], distance[:], ACT.Abs).then_inc(prep_ready.sem, 1)
                    act.wait_ge(*prep_ready.at(0, 7))
                    nc.scalar.activation(decay_m[:], decay_m[:], ACT.Exp, scale=-0.01)
        prep_ready.base += 5 + 2 * causal + 2 * decay

        LAG = 3
        AFTER = LAG + 4

        with nc.Block(no_gpsimd_drain=True) as block:
            if cross:
                @block.sync
                def _(sp):
                    def load(g):
                        sp.dma_start(ctxT[:], ins["ctx_T"][:, ds(g * GT, GT)]).then_inc(ctx_in.sem, 16)
                        if key_mask:
                            sp.dma_start(mask_q[:], ins["key_mask"].rearrange("(a b) k -> a b k", a=1)[:, ds(g * G, G), :]
                                         .to_broadcast([128, G, S])).then_inc(mask_in.sem, 16)
                        if where_mask:
                            sp.dma_start(mask_q[:].rearrange("p b k -> p (b k)"), ins["mask_qk"][:, ds(g * GT, GT)]).then_inc(mask_in.sem, 16)
                            sp.dma_start(mask_k[:], ins["mask_kq"][:, ds(g * GT, GT)]).then_inc(mask_in.sem, 16)
                    load(0)
                    with sp.Fori(1, NG) as g:
                        sp.wait_ge(*s_psum.at(g - 1, 1))
                        load(g)

            @block.gpsimd
            def _(pool):
                def masks(g, a):
                    if key_mask or where_mask:
                        pool.wait_ge(*mask_in.at(g, mask_in.per))
                        nc.gpsimd.tensor_tensor(spare[:], spare[:], spare[:], ALU.mult)
                        nc.gpsimd.tensor_scalar(score_bias[:, a].rearrange("p b k -> p (b k)"), mask_q[:].rearrange("p b k -> p (b k)"),
                                                0.0, -1e10 if key_mask else MASKED,
                                                ALU.is_equal, ALU.mult).then_inc(mask_ready.sem, 1)
                    if where_mask:
                        nc.gpsimd.tensor_scalar(masked_k[:], mask_k[:], 0.0, None, ALU.is_equal).then_inc(mask_ready.sem, 1)

                def units(g, a, steps, first, last):
                    if first:
                        masks(g, a)
                    for u in range(steps):
                        b, j = u // 4, u % 4
                        if u == 0:
                            pool.wait_ge(*k_ready.at(g, 1))
                        if not (first and u < 8):
                            pool.wait_ge(*s_psum.at(g, u - 7))
                        if u == 11 and not last:
                            masks(g + 1, 1 - a)
                        nc.gpsimd.tensor_tensor(kmask[:, b % 2, j].rearrange("p (c k) -> p c k", c=PER),
                                                kT[:, a, batch(b)].unsqueeze(1).to_broadcast([128, PER, S]),
                                                scaled_mask[:, PER * j:PER * j + PER].unsqueeze(2).to_broadcast([128, PER, S]),
                                                ALU.mult).then_inc(kmask_ready.sem, 1)
                all_groups(pool, units)

            @block.tensor
            def _(pe):
                mm = nc.tensor.matmul

                def scores(g, a, u, first):
                    b, j = u // 4, u % 4
                    pe.wait_ge(*kmask_ready.at(g, u + 1))
                    if u == 0:
                        pe.wait_ge(*q_ready.at(g, 1))
                        if where_mask or key_mask:
                            pe.wait_ge(*mask_ready.at(g, 1))
                    if not (first and u < 4):
                        pe.wait_ge(*(decayed if decay else p_ready).at(g, u - 3))
                    if masked:
                        bias = score_bias[:, 0, 0, :] if causal else score_bias[:, a, b, :]
                        mm(S_BANK[j][:], lhsT=p.ident_bf[:], rhs=bias.unsqueeze(1).to_broadcast([128, PER, S]),
                           start=True, stop=False)
                    mm(S_BANK[j][:], lhsT=qT[:, a, batch(b)], rhs=kmask[:, b % 2, j],
                       start=not masked, stop=True).then_inc(s_psum.sem, 1)

                def transposes(g, a, u, first):
                    pe.wait_ge(*p_ready.at(g, u + 1))
                    if not (first and u < 2):
                        pe.wait_ge(*pt_ready.at(g, u - 1))
                    for c in range(PER):
                        last = nc.tensor.transpose(T_BANK[u % 2][:, batch(c)], probs[:, u % 4, batch(c)], p.ident[:])
                    last.then_inc(t_psum.sem, 1)

                def values(g, a, b, first):
                    pe.wait_ge(*pt_ready.at(g, 4 * b + 4))
                    if b == 0:
                        pe.wait_ge(*v_ready.at(g, 1))
                        if not first:
                            pe.wait_ge(*oT_ready.at(g, 0))
                    if where_mask:
                        pe.wait_ge(*ze_ready.at(g, b + 1))
                        mm(O_BANK[:, batch(b)], lhsT=ze[:, b, :], rhs=p.ident[:], start=True, stop=False,
                           skip_group_check=True)
                    for c in range(PER):
                        for j in range(QUADS):
                            s = (b * H + j * PER + c) * 32
                            last = mm(O_BANK[32 * j:32 * j + 32, batch(b)], lhsT=vpad[:, a, s:s + 32],
                                      rhs=probsT[:, b % 2, j, batch(c)], start=(c == 0 and not where_mask),
                                      stop=(c == PER - 1), tile_position=(0, 32 * j), skip_group_check=True)
                    last.then_inc(av_psum.sem, 1)

                def front(g, a, step):
                    if step == 0:
                        transpose_xn(p, pe, g, xn, xn_ready, M_BANK, xnT_psum)
                    if step == 1:
                        pe.wait_ge(*xnT_ready.at(g, 1))
                        mm(M_BANK[:], lhsT=w[w_q][:], rhs=xnT[:], start=True, stop=True).then_inc(q_psum.sem, 1)
                    if step == 2:
                        if cross:
                            pe.wait_ge(*ctx_in.at(g, 16))
                        pe.wait_ge(*q_ready.at(g, 1))
                        mm(M_BANK[:], lhsT=w[w_k][:], rhs=ctxT[:], start=True, stop=True).then_inc(k_psum.sem, 1)
                    if step == 3:
                        pe.wait_ge(*k_ready.at(g, 1))
                        for b in range(G):
                            last = mm(M_BANK[:, batch(b)], lhsT=ctxT[:, batch(b)], rhs=w[w_v][:], start=True, stop=True)
                        last.then_inc(v_psum.sem, 1)
                    if step == 4 and where_mask:
                        pe.wait_ge(*mask_ready.at(g, 2))
                        pe.wait_ge(*v_ready.at(g, 1))
                        for b in range(G):
                            last = mm(M_BANK[:, batch(b)], lhsT=masked_k[:, batch(b)], rhs=head_slots(a, b),
                                      start=True, stop=True)
                        last.then_inc(z_psum.sem, 1)

                def divisors(g):
                    pe.wait_ge(*r_ready.at(g, G))
                    for b in range(G):
                        last = nc.tensor.transpose(M_BANK[:, batch(b)], rrep[:, batch(b)], p.ident[:])
                    last.then_inc(rT_psum.sem, 1)

                def outputs(g):
                    pe.wait_ge(*oT_ready.at(g, 1))
                    for b in range(G):
                        if w_o:
                            last = mm(M_BANK[:, batch(b)], lhsT=oT[:, batch(b)], rhs=w[w_o][:], start=True, stop=True)
                        else:
                            last = nc.tensor.transpose(M_BANK[:, batch(b)], oT[:, batch(b)], p.ident[:])
                    last.then_inc(y_psum.sem, 1)

                def units(g, a, steps, first, last):
                    if first:
                        for step in range(5):
                            front(g, a, step)
                    for u in range(steps or AFTER):
                        if steps:
                            scores(g, a, u, first)
                        if (steps or u < LAG) and not (first and u < LAG):
                            h, ha, hu = before(g, a, u, LAG)
                            transposes(h, ha, hu, first)
                        if u % 4 == LAG and not (first and u < LAG + 4) and (steps or u == LAG):
                            h, ha, hu = before(g, a, u, LAG + 4)
                            values(h, ha, hu // 4, first)
                        if u == LAG and not first:
                            if steps:
                                pe.wait_ge(*(z_ready if where_mask else v_ready).at(g, 1))
                            divisors(g - 1)
                        if u == LAG + 2 and not first:
                            outputs(g - 1)
                        if not last:
                            if u == LAG + 4 and not first:
                                pe.wait_ge(*x_done.at(g - 1, 1))
                            if u == LAG + 4 and first:
                                pe.wait_ge(*(z_ready if where_mask else v_ready).at(g, 1))
                            for step, at in enumerate((4, 6, 8, 10, 12)):
                                if u == LAG + at:
                                    front(g + 1, 1 - a, step)
                all_groups(pe, units)

            @block.scalar
            def _(act):
                def units(g, a, steps, first, last):
                    def start(g, a):
                        act.wait_ge(*xnT_psum.at(g, 1))
                        nc.scalar.activation(xnT[:], M_BANK[:], ACT.Copy).then_inc(xnT_ready.sem, 1)

                    def masked_values(g, a):
                        act.wait_ge(*z_psum.at(g, 1))
                        nc.scalar.activation(z[:, a, :], M_BANK[:], ACT.Copy).then_inc(z_ready.sem, 1)

                    if first:
                        start(g, a)
                        if where_mask:
                            masked_values(g, a)
                    for u in range(steps or AFTER):
                        if steps:
                            b, j = u // 4, u % 4
                            act.wait_ge(*max_ready.at(g, u + 1))
                            if not (first and u < 4):
                                act.wait_ge(*t_psum.at(g, u - 3))
                            src = scored[:, u % 4, :] if decay else S_BANK[j][:]
                            for c in range(PER):
                                h = 4 * j + c
                                done = nc.scalar.activation(probs[:, u % 4, batch(c)], src[:, batch(c)], ACT.Exp,
                                                            bias=nmax[:, b, h:h + 1], accum_out=rsum[:, b, h:h + 1])
                            done.then_inc(p_ready.sem, 1)
                            if where_mask and j == 3:
                                act.wait_ge(*e_in.at(g, b + 1))
                                nc.scalar.activation(e[:, b, :], eshift[:, b, :], ACT.Exp).then_inc(e_ready.sem, 1)
                        if u == LAG and not first:
                            act.wait_ge(*rT_psum.at(g - 1, 1))
                            nc.scalar.activation(rT[:], M_BANK[:], ACT.Copy).then_inc(rT_ready.sem, 1)
                        if u == LAG + 4 and not last:
                            start(g + 1, 1 - a)
                        if u == LAG + 12 and not last and where_mask:
                            masked_values(g + 1, 1 - a)
                nc.scalar.preload_act_table(ACT.Exp)
                all_groups(act, units)

            @block.vector
            def _(dve):
                v = nc.vector

                def row_max(g, a, u, first):
                    b, j = u // 4, u % 4
                    dve.wait_ge(*s_psum.at(g, u + 1))
                    heads = slice(4 * j, 4 * j + 4)
                    src = S_BANK[j][:].rearrange("p (c k) -> p c k", c=PER)
                    if decay:
                        if not (first and u < 4):
                            dve.wait_ge(*p_ready.at(g, u - 3))
                        out = scored[:, u % 4, :].rearrange("p (c k) -> p c k", c=PER)
                        v.tensor_tensor(out, src, decay_m[:].unsqueeze(1).to_broadcast([128, PER, S]),
                                        ALU.mult).then_inc(decayed.sem, 1)
                        dve.wait_ge(*decayed.at(g, u + 1))
                        src = out
                    if where_mask:
                        v.tensor_reduce(rowmax[:, b, heads], src, axis=AX, op=ALU.max, negate=True).then_inc(raw_max.sem, 1)
                        dve.wait_ge(*raw_max.at(g, u + 1))
                        v.tensor_scalar(nmax[:, b, heads], rowmax[:, b, heads], nfloor[:, a, b:b + 1], None,
                                        ALU.min).then_inc(max_ready.sem, 1)
                        if j == 3:
                            dve.wait_ge(*max_ready.at(g, u + 1))
                            v.tensor_scalar(eshift[:, b, :], nmax[:, b, :], 1e4, -1e4, ALU.min, ALU.add).then_inc(e_in.sem, 1)
                    else:
                        v.tensor_reduce(nmax[:, b, heads], src, axis=AX, op=ALU.max, negate=True).then_inc(max_ready.sem, 1)

                def copy_out(g, a, u, first):
                    b, j = u // 4, u % 4
                    dve.wait_ge(*t_psum.at(g, u + 1))
                    if j == 0 and not (first and b < 2):
                        dve.wait_ge(*av_psum.at(g, b - 1))
                    v.tensor_copy(probsT[:, b % 2, j, :], T_BANK[u % 2][:]).then_inc(pt_ready.sem, 1)

                def reciprocals(g, b):
                    dve.wait_ge(*p_ready.at(g, 4 * b + 4))
                    if where_mask:
                        dve.wait_ge(*sum_ready.at(g, b + 1))
                    v.reciprocal(rrec[:, b, :], rsum[:, b, :]).then_inc(r_steps.sem, 1)
                    dve.wait_ge(*r_steps.at(g, b + 1))
                    v.tensor_copy(rrep[:, batch(b)].rearrange("p (h d) -> p h d", h=H),
                                  rrec[:, b, :].unsqueeze(2).to_broadcast([128, H, HD])).then_inc(r_ready.sem, 1)

                def masked_terms(g, a, b):
                    dve.wait_ge(*e_ready.at(g, b + 1))
                    if b == 0:
                        dve.wait_ge(*z_ready.at(g, 1))
                    v.tensor_tensor(ze[:, b, :].rearrange("p (h d) -> p h d", h=H),
                                    z[:, a, batch(b)].rearrange("p (h d) -> p h d", h=H),
                                    e[:, b, :].unsqueeze(2).to_broadcast([128, H, HD]), ALU.mult).then_inc(ze_ready.sem, 1)
                    v.scalar_tensor_tensor(rsum[:, b, :], e[:, b, :], count[:, a, b:b + 1], rsum[:, b, :],
                                           ALU.mult, ALU.add).then_inc(sum_ready.sem, 1)

                def floors(g, a):
                    dve.wait_ge(*mask_ready.at(g, 1))
                    v.tensor_reduce(least[:, a], score_bias[:, a], axis=AX, op=ALU.add).then_inc(floor_steps.sem, 1)
                    dve.wait_ge(*floor_steps.at(g, 1))
                    v.tensor_scalar(count[:, a], least[:, a], 1.0 / MASKED, None, ALU.mult).then_inc(floor_steps.sem, 1)
                    v.tensor_scalar(nfloor[:, a], least[:, a], 0.0, -3e38, ALU.is_lt, ALU.mult).then_inc(floor_steps.sem, 1)
                    dve.wait_ge(*floor_steps.at(g, 3))
                    v.tensor_scalar(nfloor[:, a], nfloor[:, a], 3e38, 1e4, ALU.add, ALU.max).then_inc(floor_steps.sem, 1)
                    dve.wait_ge(*floor_steps.at(g, 4))

                def projected(out, bias, psum, ready, g):
                    dve.wait_ge(*psum.at(g, 1))
                    if bias:
                        v.tensor_scalar(out, M_BANK[:], w[bias][:, 0:1], None, ALU.add).then_inc(ready.sem, 1)
                    else:
                        v.tensor_copy(out, M_BANK[:]).then_inc(ready.sem, 1)

                def front(g, a, step):
                    if step == 0:
                        normalise(p, dve, g, xn, xn_ready)
                    if step == 1 and where_mask:
                        floors(g, a)
                    if step == 2:
                        projected(qT[:, a, :], b_q, q_psum, q_ready, g)
                    if step == 3:
                        projected(kT[:, a, :], b_k, k_psum, k_ready, g)
                    if step == 4:
                        dve.wait_ge(*v_psum.at(g, 1))
                        if b_v:
                            for b in range(G):
                                last = v.tensor_tensor(head_slots(a, b), M_BANK[:, batch(b)].rearrange("p (j c d) -> p j c d", j=QUADS, c=PER),
                                                       w[b_v][:].rearrange("p (j c d) -> p j c d", j=QUADS, c=PER), ALU.add)
                        else:
                            last = v.tensor_copy(head_slots(a), M_BANK[:].rearrange("p (j c d) -> p j c d", j=QUADS * G, c=PER))
                        last.then_inc(v_ready.sem, 1)

                def divided(g):
                    dve.wait_ge(*rT_ready.at(g, 1))
                    dve.wait_ge(*av_psum.at(g, G))
                    v.tensor_tensor(oT[:], O_BANK[:], rT[:], ALU.mult).then_inc(oT_ready.sem, 1)

                def output_bias(g):
                    for b in range(G):
                        last = v.tensor_tensor(rows_of_x(p, g, b), rows_of_x(p, g, b), w[b_o][:], ALU.add)
                    last.then_inc(bias_added.sem, 1)

                def add_output(g):
                    if b_o:
                        dve.wait_ge(*bias_added.at(g, 1))
                    dve.wait_ge(*y_psum.at(g, 1))
                    v.tensor_tensor(rows_of_x(p, g, 0, G), rows_of_x(p, g, 0, G), M_BANK[:], ALU.add).then_inc(x_done.sem, 1)

                def units(g, a, steps, first, last):
                    if first:
                        for step in range(5):
                            front(g, a, step)
                    for u in range(steps or AFTER + 1):
                        if steps:
                            row_max(g, a, u, first)
                        if u % 4 == LAG - 1 and not (first and u < LAG + 3) and (steps or u == LAG - 1):
                            h, ha, hu = before(g, a, u, LAG + 3)
                            if where_mask:
                                masked_terms(h, ha, hu // 4)
                        if not (first and u < LAG) and (steps or u < LAG):
                            copy_out(*before(g, a, u, LAG), first)
                        if u % 4 == LAG - 1 and not (first and u < LAG + 3) and (steps or u == LAG - 1):
                            reciprocals(h, hu // 4)
                        if not first:
                            if u == LAG and b_o:
                                output_bias(g - 1)
                            if u == LAG + 1:
                                divided(g - 1)
                            if u == LAG + 3:
                                add_output(g - 1)
                            if u == LAG + 4:
                                row_statistics(p, dve, g - 1, x_done)
                        if not last:
                            for step, at in enumerate((2, 6, 7, 9, 11)):
                                if u == LAG + at:
                                    front(g + 1, 1 - a, step)
                all_groups(dve, units)
        p.passed(NG)


def front(p, name, ctx):
    return sb(p, ctx, f"{name}_xn", [128, GT]), sb(p, ctx, f"{name}_xnT", [128, GT])


class Router:

    def __init__(self, p, ctx, name, experts, kept, sigmoid=False, renormalise=False):
        t = lambda k, shape, dt=F32: sb(p, ctx, f"{name}_{k}", shape, dt)
        self.p, self.experts, self.kept, self.sigmoid, self.renormalise = p, experts, kept, sigmoid, renormalise
        self.logits, self.scores = t("logits", [128, G, experts]), t("scores", [128, G, experts])
        self.spare = t("spare", [128, 1])
        self.most, self.total = t("most", [128, G]), t("total", [128, G])
        self.top, self.where, self.where_f = t("top", [128, G, 8]), t("where", [128, G, 8], U32), t("where_f", [128, G, 8])
        self.number, self.part = t("number", [128, experts]), t("part", [128, G, experts])
        self.steps, self.logits_psum, self.logits_ready, self.scores_ready = p.plan(
            route_steps=(0 if sigmoid else 4) + G + G + 1 + (4 if renormalise else 0) + 2 * kept + kept - 2,
            logits_psum=1, logits_ready=1, scores_ready=1)

    def prepare(self, pool, prep_ready):
        return self.p.nc.gpsimd.iota(self.number[:], pattern=[[1, self.experts]], base=0, channel_multiplier=0,
                                     allow_small_or_imprecise_dtypes=True)

    def tensor(self, pe, g, xnT, w, bank):
        for b in range(G):
            last = self.p.nc.tensor.matmul(bank[:, b * self.experts:(b + 1) * self.experts], lhsT=xnT[:, batch(b)],
                                           rhs=w[:], start=True, stop=True)
        last.then_inc(self.logits_psum.sem, 1)

    def wide(self, x, m):
        return x.unsqueeze(2).to_broadcast([128, G, m])

    def scalar(self, act, g):
        act.wait_ge(*self.logits_ready.at(g, 1))
        self.p.nc.scalar.activation(self.scores[:], self.logits[:], ACT.Sigmoid if self.sigmoid else ACT.Exp)\
            .then_inc(self.scores_ready.sem, 1)

    def vector(self, dve, g, bank, gates, gates_ready):
        self.finish(dve, g, self.begin(dve, g, bank), gates, gates_ready)

    def begin(self, dve, g, bank):
        v, n = self.p.nc.vector, self.experts
        then = Chain(dve, self.steps, g)
        dve.wait_ge(*self.logits_psum.at(g, 1))
        src = bank[:, 0:G * n].rearrange("p (b e) -> p b e", b=G)
        if self.sigmoid:
            v.tensor_copy(self.logits[:], src).then_inc(self.logits_ready.sem, 1)
        else:
            then(v.tensor_reduce(self.most[:], src, axis=AX, op=ALU.max))
            v.tensor_tensor(self.logits[:], src, self.wide(self.most[:], n), ALU.subtract).then_inc(self.logits_ready.sem, 1)
        return then

    def chain(self, dve, g):
        then = Chain(dve, self.steps, g)
        then.n = 0 if self.sigmoid else 1
        return then

    def finish(self, dve, g, then, gates, gates_ready):
        v, n, k, wide = self.p.nc.vector, self.experts, self.kept, self.wide
        dve.wait_ge(*self.scores_ready.at(g, 1))
        if not self.sigmoid:
            then(v.tensor_reduce(self.total[:], self.scores[:], axis=AX, op=ALU.add))
            then(v.reciprocal(self.most[:], self.total[:]))
            then(v.tensor_tensor(self.scores[:], self.scores[:], wide(self.most[:], n), ALU.mult))
        v.memset(self.spare[:], 0.0)
        for b in range(G):
            v.max(self.top[:, b, :], self.scores[:, b, :]).then_inc(self.steps.sem, 1)
        then.n += G
        dve.wait_ge(*self.steps.at(g, then.n))
        v.memset(self.spare[:], 0.0)
        for b in range(G):
            v.max_index(self.where[:, b, :], self.top[:, b, :], self.scores[:, b, :]).then_inc(self.steps.sem, 1)
        then.n += G
        dve.wait_ge(*self.steps.at(g, then.n))
        then(v.tensor_copy(self.where_f[:], self.where[:]))
        if self.renormalise:
            then(v.tensor_reduce(self.total[:], self.top[:, :, 0:k], axis=AX, op=ALU.add))
            then(v.tensor_scalar(self.total[:], self.total[:], 1e-8, None, ALU.add))
            then(v.reciprocal(self.most[:], self.total[:]))
            then(v.tensor_tensor(self.top[:, :, 0:k], self.top[:, :, 0:k], wide(self.most[:], k), ALU.mult))
        number = self.number[:].unsqueeze(1).to_broadcast([128, G, n])
        for i in range(k):
            out = gates if i == 0 else self.part[:]
            then(v.tensor_tensor(out, number, wide(self.where_f[:, :, i], n), ALU.is_equal))
            if i == 0:
                then(v.tensor_tensor(gates, gates, wide(self.top[:, :, 0], n), ALU.mult))
            else:
                then(v.tensor_tensor(self.part[:], self.part[:], wide(self.top[:, :, i], n), ALU.mult))
                last = v.tensor_tensor(gates, gates, self.part[:], ALU.add)
                if i < k - 1:
                    then(last)
        last.then_inc(gates_ready.sem, 1)
        then.ends()


def ffn_squared_relu(p, name):
    nc, ins, w = p.nc, p.inputs, p.w
    E, HALVES = 8, 2
    norm_rows(p, name)
    (xn_ready, xnT_psum, xnT_ready, h_psum, relu_ready, h_ready, y_psum, added, gates_ready) = p.plan(
        xn_ready=G, xnT_psum=1, xnT_ready=1, h_psum=E * HALVES, relu_ready=E * HALVES, h_ready=E * HALVES,
        y_psum=E, expert_added=E, gates_ready=1)
    w_in, prep = p.plan(expert_weights_in=0, stage_prepared=0)
    H_BANK, Y_BANK, L_BANK, M_BANK = p.bank[0:4], p.bank[4:6], p.bank[7], p.bank[6]
    with ExitStack() as ctx:
        t = lambda k, shape, dt=F32: sb(p, ctx, f"{name}_{k}", shape, dt)
        xn, xnT = t("xn", [128, GT]), t("xnT", [128, 2, GT])
        w1, w2 = t("w1", [128, E, HALVES * 128]), t("w2", [128, E, HALVES, D])
        relu, h = t("relu", [128, 4, GT]), t("h", [128, 8, GT])
        gates = t("gates", [128, 2, G, E])
        router = Router(p, ctx, name, E, 2, renormalise=True)
        with nc.Block(no_gpsimd_drain=True) as block:
            @block.sync
            def _(sp):
                sp.dma_start(w1[:], ins["L0_ffn_W1"]).then_inc(w_in.sem, 16)
                sp.dma_start(w2[:], ins["L0_ffn_W2"]).then_inc(w_in.sem, 16)

            @block.gpsimd
            def _(pool):
                Chain(pool, prep)(router.prepare(pool, prep))
                pool.wait_ge(*w_in.at(0, 32))
        prep.base += 1
        w_in.base += 32

        with nc.Block(no_gpsimd_drain=True) as block:
            @block.tensor
            def _(pe):
                mm = nc.tensor.matmul

                def up(g, a, e, half, first):
                    n = 2 * e + half
                    if n == 0:
                        pe.wait_ge(*xnT_ready.at(g, 1))
                    if not (first and n < 4):
                        pe.wait_ge(*relu_ready.at(g, n - 3))
                    mm(H_BANK[n % 4][:], lhsT=w1[:, e, 128 * half:128 * half + 128], rhs=xnT[:, a, :], start=True, stop=True)\
                        .then_inc(h_psum.sem, 1)

                def down(g, e, first):
                    pe.wait_ge(*h_ready.at(g, 2 * e + 2))
                    if not (first and e < 2):
                        pe.wait_ge(*added.at(g, e - 1))
                    for b in range(G):
                        for half in range(HALVES):
                            last = mm(Y_BANK[e % 2][:, batch(b)], lhsT=h[:, (2 * e + half) % 8, batch(b)], rhs=w2[:, e, half, :],
                                      start=(half == 0), stop=(half == 1))
                    last.then_inc(y_psum.sem, 1)

                def units(g, a, steps, first, last):
                    if first:
                        transpose_xn(p, pe, g, xn, xn_ready, M_BANK, xnT_psum)
                        pe.wait_ge(*xnT_ready.at(g, 1))
                        router.tensor(pe, g, xnT[:, a, :], w["L0_ffn_Wg"], L_BANK)
                    for e in range(steps or 2):
                        if steps:
                            up(g, a, e, 0, first)
                            up(g, a, e, 1, first)
                        if not (first and e < 2):
                            h_, _, he = before(g, a, e, 2, E)
                            down(h_, he, first)
                        if e == 1 and not last:
                            transpose_xn(p, pe, g + 1, xn, xn_ready, M_BANK, xnT_psum)
                        if e == 2 and not last:
                            pe.wait_ge(*xnT_ready.at(g + 1, 1))
                            router.tensor(pe, g + 1, xnT[:, 1 - a, :], w["L0_ffn_Wg"], L_BANK)
                all_groups(pe, units, E)

            @block.scalar
            def _(act):
                def copy(g, a):
                    act.wait_ge(*xnT_psum.at(g, 1))
                    nc.scalar.activation(xnT[:, a, :], M_BANK[:], ACT.Copy).then_inc(xnT_ready.sem, 1)

                def units(g, a, steps, first, last):
                    if first:
                        copy(g, a)
                        router.scalar(act, g)
                    for n in range(2 * steps):
                        act.wait_ge(*h_psum.at(g, n + 1))
                        if not (first and n < 4):
                            act.wait_ge(*h_ready.at(g, n - 3))
                        nc.scalar.activation(relu[:, n % 4, :], H_BANK[n % 4][:], ACT.Relu).then_inc(relu_ready.sem, 1)
                        if n == 3 and not last:
                            copy(g + 1, 1 - a)
                        if n == 7 and not last:
                            router.scalar(act, g + 1)
                nc.scalar.preload_act_table(ACT.Exp)
                all_groups(act, units, E)

            @block.vector
            def _(dve):
                v = nc.vector

                def add_expert(g, a, e):
                    dve.wait_ge(*y_psum.at(g, e + 1))
                    if e:
                        dve.wait_ge(*added.at(g, e))
                    else:
                        dve.wait_ge(*gates_ready.at(g, 1))
                    for b in range(G):
                        last = v.scalar_tensor_tensor(rows_of_x(p, g, b), Y_BANK[e % 2][:, batch(b)], gates[:, a, b, e:e + 1],
                                                      rows_of_x(p, g, b), ALU.mult, ALU.add)
                    last.then_inc(added.sem, 1)
                    if e == E - 1:
                        row_statistics(p, dve, g, added, E)

                def units(g, a, steps, first, last):
                    if first:
                        normalise(p, dve, g, xn, xn_ready)
                        router.vector(dve, g, L_BANK, gates[:, a], gates_ready)
                    for e in range(steps or 2):
                        if e == 0 and not last:
                            normalise(p, dve, g + 1, xn, xn_ready)
                        for n in (2 * e, 2 * e + 1) if steps else ():
                            dve.wait_ge(*relu_ready.at(g, n + 1))
                            if not (first and n < 8) and n % 2 == 0:
                                dve.wait_ge(*y_psum.at(g, e - 3))
                            v.tensor_tensor(h[:, n % 8, :], relu[:, n % 4, :], relu[:, n % 4, :], ALU.mult).then_inc(h_ready.sem, 1)
                        if not (first and e < 2):
                            add_expert(*before(g, a, e, 2, E))
                        if e == 3 and not last:
                            chain = router.begin(dve, g + 1, L_BANK)
                        if e == 4 and not last:
                            router.finish(dve, g + 1, chain, gates[:, 1 - a], gates_ready)
                all_groups(dve, units, E)
        p.passed(NG)


def ffn_linear_experts(p, name):
    nc, ins, w = p.nc, p.inputs, p.w
    E = 8
    norm_rows(p, name)
    xn_ready, xnT_psum, xnT_ready, y_psum, added, gates_ready = p.plan(
        xn_ready=G, xnT_psum=1, xnT_ready=1, y_psum=2 * G, expert_added=2 * G * 4, gates_ready=1)
    w_in, prep, product, copied = p.plan(expert_weights_in=0, stage_prepared=0, product_psum=0, product_ready=0)
    Y_BANK, L_BANK, M_BANK = p.bank[0:4], p.bank[7], p.bank[6]
    ORDER = [(0, 0), (1, 0), (0, 1), (1, 1), (2, 0), (3, 0), (2, 1), (3, 1)]
    with ExitStack() as ctx:
        t = lambda k, shape, dt=F32: sb(p, ctx, f"{name}_{k}", shape, dt)
        xn, xnT = t("xn", [128, GT]), t("xnT", [128, 2, GT])
        wi, wo, wio = t("wiT", [128, E, 128]), t("wo", [128, E, D]), t("wio", [128, E, D])
        gates = t("gates", [128, G, E])
        router = Router(p, ctx, name, E, 2)
        with nc.Block(no_gpsimd_drain=True) as block:
            @block.sync
            def _(sp):
                sp.dma_start(wi[:], ins["L2_ffn_WiT"]).then_inc(w_in.sem, 16)
                sp.dma_start(wo[:], ins["L2_ffn_Wo"]).then_inc(w_in.sem, 16)

            @block.gpsimd
            def _(pool):
                Chain(pool, prep)(router.prepare(pool, prep))

            @block.tensor
            def _(pe):
                pe.wait_ge(*w_in.at(0, 32))
                for e in range(E):
                    last = nc.tensor.matmul(p.bank[e // 4][:, batch(e % 4)], lhsT=wi[:, e, :], rhs=wo[:, e, :], start=True, stop=True)
                last.then_inc(product.sem, 1)

            @block.scalar
            def _(act):
                act.wait_ge(*product.at(0, 1))
                for i in range(2):
                    nc.scalar.activation(wio[:, 4 * i:4 * i + 4, :].rearrange("p e d -> p (e d)"), p.bank[i][:], ACT.Copy)
        prep.base += 1
        w_in.base += 32
        product.base += 1

        with nc.Block(no_gpsimd_drain=True) as block:
            @block.tensor
            def _(pe):
                def front(g, a, first):
                    transpose_xn(p, pe, g, xn, xn_ready, M_BANK, xnT_psum)
                    pe.wait_ge(*xnT_ready.at(g, 1))
                    router.tensor(pe, g, xnT[:, a, :], w["L2_ffn_Wr"], L_BANK)

                def units(g, a, steps, first, last):
                    if first:
                        front(g, a, True)
                    for n in range(2 * G if steps else 0):
                        b, i = ORDER[n]
                        if n == 4 and not last:
                            front(g + 1, 1 - a, False)
                        if not (first and n < 4):
                            pe.wait_ge(*added.at(g, 8 * ((n - 4) // 2) + 8))
                        nc.tensor.matmul(Y_BANK[(2 * b + i) % 4][:], lhsT=xnT[:, a, batch(b)],
                                         rhs=wio[:, 4 * i:4 * i + 4, :].rearrange("p e d -> p (e d)"),
                                         start=True, stop=True).then_inc(y_psum.sem, 1)
                all_groups(pe, units, 1)

            @block.scalar
            def _(act):
                def units(g, a, steps, first, last):
                    def front(g, a):
                        act.wait_ge(*xnT_psum.at(g, 1))
                        nc.scalar.activation(xnT[:, a, :], M_BANK[:], ACT.Copy).then_inc(xnT_ready.sem, 1)
                        router.scalar(act, g)
                    if first:
                        front(g, a)
                    if not last:
                        front(g + 1, 1 - a)
                nc.scalar.preload_act_table(ACT.Exp)
                all_groups(act, units, 1)

            @block.vector
            def _(dve):
                v = nc.vector

                def add_experts(g, n0):
                    n = 8 * n0 // 2
                    for i in range(2):
                        for e in range(4):
                            for b in (n0 // 2, n0 // 2 + 1):
                                y = 2 * b + i
                                if e == 0:
                                    dve.wait_ge(*y_psum.at(g, ORDER.index((b, i)) + 1))
                                if n % 16 >= 2:
                                    dve.wait_ge(*added.at(g, n - 1))
                                v.scalar_tensor_tensor(rows_of_x(p, g, b), Y_BANK[y % 4][:, batch(e)],
                                                       gates[:, b, 4 * i + e:4 * i + e + 1], rows_of_x(p, g, b),
                                                       ALU.mult, ALU.add).then_inc(added.sem, 1)
                                n += 1

                def units(g, a, steps, first, last):
                    if first:
                        normalise(p, dve, g, xn, xn_ready)
                        router.vector(dve, g, L_BANK, gates[:], gates_ready)
                        dve.wait_ge(*gates_ready.at(g, 1))
                    if steps:
                        if not last:
                            normalise(p, dve, g + 1, xn, xn_ready)
                        add_experts(g, 0)
                        add_experts(g, 4)
                        if not last:
                            chain = router.begin(dve, g + 1, L_BANK)
                        row_statistics(p, dve, g, added, 8 * G)
                        if not last:
                            router.finish(dve, g + 1, chain, gates[:], gates_ready)
                            dve.wait_ge(*gates_ready.at(g + 1, 1))
                all_groups(dve, units, 1)
        p.passed(NG)


def ffn_sigmoid_experts(p, name):
    nc, ins, w = p.nc, p.inputs, p.w
    E = 64
    norm_rows(p, name)
    xn_ready, xnT_psum, xnT_ready, gates_ready = p.plan(xn_ready=G, xnT_psum=1, xnT_ready=1, gates_ready=1)
    prep, = p.plan(stage_prepared=0)
    H_BANK, Y_BANK, L_BANK, M_BANK = p.bank[0:4], p.bank[4:8], p.bank[7], p.bank[6]
    with ExitStack() as ctx:
        t = lambda k, shape, dt=F32: sb(p, ctx, f"{name}_{k}", shape, dt)
        xn, xnT_now = front(p, name, ctx)
        gates_now = t("gates_now", [128, G, E])
        xnT, gates = t("xnT_all", [128, B * S]), t("gates", [128, B, E])
        keys, values = t("keys", [128, 2, 128]), t("values", [128, 2, D])
        relu = t("relu", [128, 4, GT])
        gate_now = t("gate_pair", [128, 2, B])
        router = Router(p, ctx, name, E, 4, sigmoid=True)
        with nc.Block(no_gpsimd_drain=True) as block:
            @block.gpsimd
            def _(pool):
                Chain(pool, prep)(router.prepare(pool, prep))
        prep.base += 1

        with nc.Block(no_gpsimd_drain=True) as block:
            @block.tensor
            def _(pe):
                with pe.Fori(0, NG) as g:
                    transpose_xn(p, pe, g, xn, xn_ready, M_BANK, xnT_psum)
                    pe.wait_ge(*xnT_ready.at(g, 1))
                    router.tensor(pe, g, xnT_now, w["L1_ffn_sel"], L_BANK)

            @block.scalar
            def _(act):
                nc.scalar.preload_act_table(ACT.Sigmoid)
                with act.Fori(0, NG) as g:
                    act.wait_ge(*xnT_psum.at(g, 1))
                    nc.scalar.activation(xnT_now[:], M_BANK[:], ACT.Copy)
                    nc.scalar.activation(xnT[:, ds(g * GT, GT)], M_BANK[:], ACT.Copy).then_inc(xnT_ready.sem, 1)
                    router.scalar(act, g)

            @block.vector
            def _(dve):
                def finish(g, chain):
                    router.finish(dve, g, chain, gates_now[:], gates_ready)
                    dve.wait_ge(*gates_ready.at(g, 1))
                    nc.vector.tensor_copy(gates[:, ds(g * G, G), :], gates_now[:])

                normalise(p, dve, 0, xn, xn_ready)
                router.begin(dve, 0, L_BANK)
                with dve.Fori(1, NG) as g:
                    normalise(p, dve, g, xn, xn_ready)
                    finish(g - 1, router.chain(dve, g - 1))
                    router.begin(dve, g, L_BANK)
                finish(NG - 1, router.chain(dve, NG - 1))
        p.passed(NG)

        *w_in, h_psum, relu_ready, y_psum, added, gate_ready = p.plan(
            even_expert_weights_in=32, odd_expert_weights_in=32, h_psum=2 * NG, relu_ready=2 * NG, y_psum=2 * NG, expert_added=2 * NG, gates_ready=2)

        def passes(eng, run):
            run(0, True)
            with eng.Fori(1, E // 2) as i:
                run(i, False)

        with nc.Block(no_gpsimd_drain=True) as block:
            @block.sync
            def _(sp):
                def run(i, first):
                    for a in range(2):
                        if not first:
                            sp.wait_ge(*y_psum.at(i - 1, NG * (a + 1)))
                        sp.dma_start(keys[:, a, :], ins["L1_ffn_keys"][:, ds((2 * i + a) * 128, 128)]).then_inc(w_in[a].sem, 16)
                        sp.dma_start(values[:, a, :], ins["L1_ffn_values"][:, ds((2 * i + a) * D, D)]).then_inc(w_in[a].sem, 16)
                passes(sp, run)

            @block.tensor
            def _(pe):
                mm = nc.tensor.matmul

                def up(i, n, first):
                    if n % NG == 0:
                        pe.wait_ge(*w_in[n // NG].at(i, 32))
                    if not (first and n < 4):
                        pe.wait_ge(*relu_ready.at(i, n - 3))
                    mm(H_BANK[n % 4][:], lhsT=keys[:, n // NG, :], rhs=xnT[:, (n % NG) * GT:(n % NG + 1) * GT],
                       start=True, stop=True).then_inc(h_psum.sem, 1)

                def down(i, n, first):
                    pe.wait_ge(*relu_ready.at(i, n + 1))
                    if not (first and n < 4):
                        pe.wait_ge(*added.at(i, n - 3))
                    for b in range(G):
                        last = mm(Y_BANK[n % 4][:, batch(b)], lhsT=relu[:, n % 4, batch(b)], rhs=values[:, n // NG, :],
                                  start=True, stop=True)
                    last.then_inc(y_psum.sem, 1)

                def run(i, first):
                    for n in range(2 * NG):
                        up(i, n, first)
                        if n >= 2:
                            down(i, n - 2, first)
                    down(i, 2 * NG - 2, first)
                    down(i, 2 * NG - 1, first)
                passes(pe, run)

            @block.scalar
            def _(act):
                def run(i, first):
                    for n in range(2 * NG):
                        act.wait_ge(*h_psum.at(i, n + 1))
                        if not (first and n < 4):
                            act.wait_ge(*y_psum.at(i, n - 3))
                        nc.scalar.activation(relu[:, n % 4, :], H_BANK[n % 4][:], ACT.Relu).then_inc(relu_ready.sem, 1)
                passes(act, run)

            @block.vector
            def _(dve):
                v = nc.vector

                def run(i, first):
                    for n in range(2 * NG):
                        a = n // NG
                        if n % NG == 0:
                            if not first:
                                dve.wait_ge(*added.at(i - 1, NG * (a + 1)))
                            v.tensor_copy(gate_now[:, a, :], gates[:, :, ds(2 * i + a, 1)].rearrange("p b a -> p (b a)"))\
                                .then_inc(gate_ready.sem, 1)
                            dve.wait_ge(*gate_ready.at(i, a + 1))
                        dve.wait_ge(*y_psum.at(i, n + 1))
                        if not (first and n < NG):
                            dve.wait_ge(*added.at(i, n - NG + 1))
                        for b in range(G):
                            k = (n % NG) * G + b
                            rows = p.x[:, k * D:(k + 1) * D]
                            last = v.scalar_tensor_tensor(rows, Y_BANK[n % 4][:, batch(b)], gate_now[:, a, k:k + 1],
                                                          rows, ALU.mult, ALU.add)
                        last.then_inc(added.sem, 1)
                passes(dve, run)
        p.passed(E // 2)
        all_statistics(p)


def all_statistics(p):
    with p.nc.Block(no_gpsimd_drain=True) as block:
        @block.vector
        def _(dve):
            for b in range(B):
                p.nc.vector.bn_stats(p.stats[:, b, :], p.x[:, b * D:(b + 1) * D])



def linear_attention(p, name):
    nc, ins, w = p.nc, p.inputs, p.w
    C1 = 6.28125
    C2 = float(np.round((2 * np.pi - C1) * 2 ** 20) / 2 ** 20)
    C3 = 2 * np.pi - C1 - C2
    ROUND = 1.5 * 2 ** 23
    norm_rows(p, name)
    (xn_ready, xnT_psum, xnT_ready, qk_psum, v_psum, u_psum, act_ready, turned, v_ready, u_ready, s_psum, e_ready, o_psum,
     uo_ready, sq_ready, ms_psum, y_psum, ms_in, root_ready, bias_added, tail, x_done) = p.plan(
        xn_ready=G, xnT_psum=1, xnT_ready=1, qk_psum=4, v_psum=1, u_psum=1, silu_ready=4, turned_ready=4, v_ready=G,
        u_ready=1, s_psum=16, masked_ready=16, av_psum=G, gated_ready=1, squares_ready=1, mean_square_psum=1, y_psum=1,
        variance_ready=1, root_ready=1, bias_added=1, tail_steps=1, x_done=1)
    prep, angle, sines = p.plan(stage_prepared=0, angle_steps=0, table_ready=0)
    F_BANK, Y_BANK, O_BANK = p.bank[4:6], p.bank[6], p.bank[7]
    AFTER = 7
    with ExitStack() as ctx:
        t = lambda k, shape, dt=F32: sb(p, ctx, f"{name}_{k}", shape, dt)
        xn, xnT = front(p, name, ctx)
        silu, qk = t("silu", [128, 2, GT]), t("qk", [128, 2, 4, GT])
        uT, uo, sq = t("uT", [128, 2, GT]), t("uo", [128, GT]), t("sq", [128, GT])
        vpad = t("vpad", [128, 2, G, 8 * 32])
        energy = t("energy", [128, 2, 8, S])
        keep = t("keep", [128, 8, S])
        table, pos, th, turns, whole = (t(k, [128, 2, S]) for k in ("table", "pos", "th", "turns", "whole"))
        quarter = t("quarter", [128, 1])
        ones = t("ones", [128, 1])
        veps, root, rs = t("veps", [128, G]), t("root", [128, G]), t("rs", [128, G])

        with nc.Block(no_gpsimd_drain=True) as block:
            @block.gpsimd
            def _(pool):
                then = Chain(pool, prep)
                then(nc.gpsimd.iota(pos[:], pattern=[[0, 2], [1, S]], base=0, channel_multiplier=0,
                                    allow_small_or_imprecise_dtypes=True))
                then(nc.gpsimd.memset(quarter[:], 1.0))
                for j in range(4):
                    rows = quarter[32 * j:32 * j + 32, :]
                    then(nc.gpsimd.affine_select(out=rows, in_=rows, compare_op=ALU.is_ge, fill=0.0, base=15,
                                                 pattern=[[0, 1]], channel_multiplier=-1))
                then(nc.gpsimd.memset(keep[:], 1.0))
                then(nc.gpsimd.affine_select(out=keep[:], in_=keep[:], compare_op=ALU.is_ge, fill=0.0, base=0,
                                             pattern=[[0, 8], [1, S]], channel_multiplier=-1))
                then(nc.gpsimd.memset(vpad[:], 0.0))
                then(nc.gpsimd.memset(ones[:], 1.0))

            @block.vector
            def _(dve):
                v = nc.vector
                then = Chain(dve, angle)
                dve.wait_ge(*prep.at(0, 8))
                for i in range(2):
                    then(v.tensor_scalar(th[:, i, :], pos[:, i, :], w["L1_attn_theta"][:, i:i + 1], None, ALU.mult))
                then(v.tensor_scalar(quarter[:], quarter[:], 0.25, None, ALU.mult))
                then(v.tensor_scalar(turns[:], th[:], 1 / (2 * np.pi), quarter[:], ALU.mult, ALU.add))
                then(v.tensor_scalar(whole[:], turns[:], ROUND, ROUND, ALU.add, ALU.subtract))
                for c in (C1, C2, C3):
                    then(v.scalar_tensor_tensor(th[:], whole[:], -c, th[:], ALU.mult, ALU.add))
                then(v.tensor_scalar(quarter[:], quarter[:], 2 * np.pi, None, ALU.mult))
                then(v.tensor_scalar(th[:], th[:], quarter[:], 3.1415925, ALU.add, ALU.min))
                then(v.tensor_scalar(th[:], th[:], -3.1415925, None, ALU.max))
                for h in range(8):
                    at = keep[:, 2 * (h % 4) + h // 4, :]
                    then(v.tensor_scalar(at, at, w["L1_attn_slope"][:, h:h + 1], None, ALU.mult))

            @block.scalar
            def _(act):
                act.wait_ge(*angle.at(0, 19))
                nc.scalar.activation(table[:], th[:], ACT.Sin)
                nc.scalar.activation(keep[:], keep[:], ACT.Exp)
        prep.base += 10
        angle.base += 19

        with nc.Block(no_gpsimd_drain=True) as block:
            @block.tensor
            def _(pe):
                mm = nc.tensor.matmul

                def scores(g, a, u, first):
                    b, r = u // 4, u % 4
                    if u == 0:
                        pe.wait_ge(*turned.at(g, 4))
                    if not (first and u < 4):
                        pe.wait_ge(*e_ready.at(g, u - 3))
                    rows = slice(32 * r, 32 * r + 32)
                    for i in range(2):
                        last = mm(p.bank[r][:, batch(i)], lhsT=qk[rows, a, 2 + i, batch(b)], rhs=qk[rows, a, i, batch(b)],
                                  start=True, stop=True)
                    last.then_inc(s_psum.sem, 1)

                def values(g, a, b, first):
                    pe.wait_ge(*e_ready.at(g, 4 * b + 4))
                    if b == 0:
                        pe.wait_ge(*v_ready.at(g, G))
                        if not first:
                            pe.wait_ge(*uo_ready.at(g, 0))
                            pe.wait_ge(*sq_ready.at(g, 0))
                    for c in range(2):
                        for j in range(4):
                            h = 2 * j + c
                            last = mm(O_BANK[32 * j:32 * j + 32, batch(b)], lhsT=vpad[:, a, b, 32 * h:32 * h + 32],
                                      rhs=energy[:, b % 2, 2 * (h % 4) + h // 4, :], start=(c == 0), stop=(c == 1),
                                      tile_position=(0, 32 * j), skip_group_check=True)
                    last.then_inc(o_psum.sem, 1)

                def front(g, step, first):
                    if step == 0:
                        if not first:
                            pe.wait_ge(*v_ready.at(g, 0))
                        transpose_xn(p, pe, g, xn, xn_ready, F_BANK[0], xnT_psum)
                    if 1 <= step <= 4:
                        i = step - 1
                        if i == 0:
                            pe.wait_ge(*xnT_ready.at(g, 1))
                        elif i == 1:
                            if not first:
                                pe.wait_ge(*u_ready.at(g, 0))
                        else:
                            pe.wait_ge(*act_ready.at(g, i - 1))
                        mm(F_BANK[i % 2][:], lhsT=w["L1_attn_qk"][:, i, :], rhs=xnT[:], start=True, stop=True).then_inc(qk_psum.sem, 1)
                    if step == 5:
                        pe.wait_ge(*act_ready.at(g, 3))
                        for b in range(G):
                            last = mm(F_BANK[0][:, batch(b)], lhsT=xnT[:, batch(b)], rhs=w["L1_attn_vu"][:, 0, :], start=True, stop=True)
                        last.then_inc(v_psum.sem, 1)
                    if step == 6:
                        pe.wait_ge(*act_ready.at(g, 4))
                        mm(F_BANK[1][:], lhsT=w["L1_attn_vu"][:, 1, :], rhs=xnT[:], start=True, stop=True).then_inc(u_psum.sem, 1)

                def mean_squares(g):
                    pe.wait_ge(*sq_ready.at(g, 1))
                    for b in range(G):
                        last = mm(Y_BANK[:, b:b + 1], lhsT=sq[:, batch(b)], rhs=ones[:], start=True, stop=True)
                    last.then_inc(ms_psum.sem, 1)

                def output(g):
                    pe.wait_ge(*uo_ready.at(g, 1))
                    pe.wait_ge(*ms_in.at(g, 1))
                    for b in range(G):
                        last = mm(Y_BANK[:, batch(b)], lhsT=uo[:, batch(b)], rhs=w["L1_attn_out_w"][:], start=True, stop=True)
                    last.then_inc(y_psum.sem, 1)

                def units(g, a, steps, first, last):
                    if first:
                        for step in range(7):
                            front(g, step, True)
                    for u in range(steps or AFTER):
                        if steps:
                            scores(g, a, u, first)
                        if u % 4 == 1 and not (first and u < 5) and (steps or u < 5):
                            h, ha, hu = before(g, a, u, 5)
                            values(h, ha, hu // 4, first)
                        if u == 4 and not first:
                            mean_squares(g - 1)
                        if u == 6 and not first:
                            output(g - 1)
                        if not last:
                            for step, at in enumerate((2, 4, 5, 7, 9, 11, 12)):
                                if u == at:
                                    front(g + 1, step, False)
                all_groups(pe, units)

            @block.scalar
            def _(act):
                def front(g, a, step):
                    if step == 0:
                        act.wait_ge(*xnT_psum.at(g, 1))
                        nc.scalar.activation(xnT[:], F_BANK[0][:], ACT.Copy).then_inc(xnT_ready.sem, 1)
                    if 1 <= step <= 4:
                        i = step - 1
                        act.wait_ge(*qk_psum.at(g, i + 1))
                        if i >= 2:
                            act.wait_ge(*turned.at(g, i - 1))
                        nc.scalar.activation(silu[:, i % 2, :], F_BANK[i % 2][:], ACT.Silu, bias=w["L1_attn_qk_b"][:, i:i + 1])\
                            .then_inc(act_ready.sem, 1)
                    if step == 6:
                        act.wait_ge(*u_psum.at(g, 1))
                        nc.scalar.activation(uT[:, a, :], F_BANK[1][:], ACT.Identity, bias=w["L1_attn_ub"][:, 0:1]).then_inc(u_ready.sem, 1)

                def units(g, a, steps, first, last):
                    if first:
                        for step in range(7):
                            front(g, a, step)
                    if not first:
                        act.wait_ge(*o_psum.at(g - 1, G))
                        nc.scalar.activation(sq[:], O_BANK[:], ACT.Square).then_inc(sq_ready.sem, 1)
                        if not last:
                            front(g + 1, 1 - a, 0)
                        act.wait_ge(*ms_in.at(g - 1, 1))
                        nc.scalar.activation(root[:], veps[:], ACT.Sqrt).then_inc(root_ready.sem, 1)
                    elif not last:
                        front(g + 1, 1 - a, 0)
                    if not last:
                        for step in range(1, 7):
                            front(g + 1, 1 - a, step)
                all_groups(act, units)

            @block.vector
            def _(dve):
                v = nc.vector

                def front(g, a, step):
                    if step == 0:
                        normalise(p, dve, g, xn, xn_ready)
                    if 1 <= step <= 4:
                        i = step - 1
                        dve.wait_ge(*act_ready.at(g, i + 1))
                        v.tensor_tensor(qk[:, a, i, :].rearrange("p (b n) -> p b n", b=G), silu[:, i % 2, :].rearrange("p (b n) -> p b n", b=G),
                                        table[:, i % 2, :].unsqueeze(1).to_broadcast([128, G, S]), ALU.mult).then_inc(turned.sem, 1)
                    if step == 5:
                        dve.wait_ge(*v_psum.at(g, 1))
                        for b in range(G):
                            q = vpad[:, a, b, 0:256]
                            slots = bass.AP(q.tensor, q.offset, [list(q.ap[0]), [64, 4], [48, 2], [1, 16]])
                            v.tensor_tensor(slots, F_BANK[0][:, batch(b)].rearrange("p (j c d) -> p j c d", j=4, c=2),
                                            w["L1_attn_vb"][:].rearrange("p (j c d) -> p j c d", j=4, c=2), ALU.add).then_inc(v_ready.sem, 1)

                def gated(g, a):
                    dve.wait_ge(*o_psum.at(g, G))
                    dve.wait_ge(*sq_ready.at(g, 1))
                    dve.wait_ge(*u_ready.at(g, 1))
                    v.tensor_tensor(uo[:], O_BANK[:], uT[:, a, :], ALU.mult).then_inc(uo_ready.sem, 1)

                def add_output(g):
                    dve.wait_ge(*root_ready.at(g, 1))
                    v.reciprocal(rs[:], root[:]).then_inc(tail.sem, 1)
                    dve.wait_ge(*tail.at(g, 1))
                    dve.wait_ge(*bias_added.at(g, 1))
                    dve.wait_ge(*y_psum.at(g, 1))
                    for b in range(G):
                        last = v.scalar_tensor_tensor(rows_of_x(p, g, b), Y_BANK[:, batch(b)], rs[:, b:b + 1], rows_of_x(p, g, b),
                                                      ALU.mult, ALU.add)
                    last.then_inc(x_done.sem, 1)

                def units(g, a, steps, first, last):
                    if first:
                        for step in range(7):
                            front(g, a, step)
                    for u in range(steps or AFTER + 2):
                        b, r = u // 4, u % 4
                        if steps:
                            dve.wait_ge(*s_psum.at(g, u + 1))
                            if r == 0 and not (first and b < 2):
                                dve.wait_ge(*o_psum.at(g, b - 1))
                            v.tensor_tensor(energy[:, b % 2, 2 * r:2 * r + 2, :], p.bank[r][:, 0:2 * S].rearrange("p (t n) -> p t n", t=2),
                                            keep[:, 2 * r:2 * r + 2, :], ALU.mult).then_inc(e_ready.sem, 1)
                        if not first:
                            if u == 2:
                                gated(g - 1, 1 - a)
                            if u == 3:
                                for b in range(G):
                                    done = v.tensor_tensor(rows_of_x(p, g - 1, b), rows_of_x(p, g - 1, b), w["L1_attn_out_b"][:], ALU.add)
                                done.then_inc(bias_added.sem, 1)
                            if u == 5:
                                dve.wait_ge(*ms_psum.at(g - 1, 1))
                                v.tensor_scalar(veps[:], Y_BANK[:, 0:G], 1.0 / D, 1e-6, ALU.mult, ALU.add).then_inc(ms_in.sem, 1)
                            if u == 7:
                                add_output(g - 1)
                            if u == 8:
                                row_statistics(p, dve, g - 1, x_done)
                        if not last:
                            for step, at in enumerate((1, 5, 7, 9, 11, 12)):
                                if u == at:
                                    front(g + 1, 1 - a, step)
                all_groups(dve, units)
        p.passed(NG)



def single_head(p, name):
    nc, ins = p.nc, p.inputs
    norm_rows(p, name)
    (ctx_in, rows_in, xn_ready, xnT_psum, xnT_ready, s_psum, max_ready, p_ready, t_psum, pt_ready, y_psum, r_steps, x_done) = p.plan(
        ctx_in=16, ctx_rows_in=16, xn_ready=G, xnT_psum=1, xnT_ready=1, s_psum=1, max_ready=1, p_ready=1, t_psum=1,
        pt_ready=1, y_psum=1, reciprocal_steps=1, x_done=1)
    with ExitStack() as ctx:
        t = lambda k, shape, dt=F32: sb(p, ctx, f"{name}_{k}", shape, dt)
        xn, xnT = front(p, name, ctx)
        ctxT, rows, probs, probsT = (t(k, [128, GT]) for k in ("ctxT", "ctx_rows", "probs", "probsT"))
        nmax, rsum, rrec = t("nmax", [128, G]), t("rsum", [128, G]), t("rrec", [128, G])

        def loop(eng, body):
            with eng.Fori(0, NG - 2) as g:
                body(g, 2)
            body(NG - 2, 1)
            body(NG - 1, 0)

        with nc.Block(no_gpsimd_drain=True) as block:
            @block.sync
            def _(sp):
                def load(g, first):
                    if not first:
                        sp.wait_ge(*s_psum.at(g - 1, 1))
                    sp.dma_start(ctxT[:], ins["ctx_T"][:, ds(g * GT, GT)]).then_inc(ctx_in.sem, 16)
                    if not first:
                        sp.wait_ge(*y_psum.at(g - 1, 1))
                    sp.dma_start(rows[:], ins["ctx_rows"][:, ds(g * GT, GT)]).then_inc(rows_in.sem, 16)
                load(0, True)
                with sp.Fori(1, NG) as g:
                    load(g, False)

            @block.tensor
            def _(pe):
                def front(g):
                    transpose_xn(p, pe, g, xn, xn_ready, p.bank[6], xnT_psum)

                def scores(g):
                    pe.wait_ge(*xnT_ready.at(g, 1))
                    pe.wait_ge(*ctx_in.at(g, 16))
                    for b in range(G):
                        last = nc.tensor.matmul(p.bank[0][:, batch(b)], lhsT=xnT[:, batch(b)], rhs=ctxT[:, batch(b)], start=True, stop=True)
                    last.then_inc(s_psum.sem, 1)

                def body(g, left):
                    if left >= 1:
                        front(g + 1)
                    pe.wait_ge(*p_ready.at(g, 1))
                    for b in range(G):
                        last = nc.tensor.transpose(p.bank[1][:, batch(b)], probs[:, batch(b)], p.ident[:])
                    last.then_inc(t_psum.sem, 1)
                    if left >= 1:
                        scores(g + 1)
                    pe.wait_ge(*pt_ready.at(g, 1))
                    pe.wait_ge(*rows_in.at(g, 16))
                    for b in range(G):
                        last = nc.tensor.matmul(p.bank[2][:, batch(b)], lhsT=probsT[:, batch(b)], rhs=rows[:, batch(b)], start=True, stop=True)
                    last.then_inc(y_psum.sem, 1)

                front(0)
                scores(0)
                loop(pe, body)

            @block.scalar
            def _(act):
                def front(g, first):
                    act.wait_ge(*xnT_psum.at(g, 1))
                    nc.scalar.activation(xnT[:], p.bank[6][:], ACT.Copy, scale=HD ** -0.5).then_inc(xnT_ready.sem, 1)
                    act.wait_ge(*max_ready.at(g, 1))
                    if not first:
                        act.wait_ge(*t_psum.at(g, 0))
                    for b in range(G):
                        last = nc.scalar.activation(probs[:, batch(b)], p.bank[0][:, batch(b)], ACT.Exp, bias=nmax[:, b:b + 1],
                                                    accum_out=rsum[:, b:b + 1])
                    last.then_inc(p_ready.sem, 1)

                nc.scalar.preload_act_table(ACT.Exp)
                front(0, True)
                loop(act, lambda g, left: front(g + 1, False) if left else None)

            @block.vector
            def _(dve):
                v = nc.vector

                def maxima(g):
                    dve.wait_ge(*s_psum.at(g, 1))
                    v.tensor_reduce(nmax[:], p.bank[0][:].rearrange("p (b k) -> p b k", b=G), axis=AX, op=ALU.max, negate=True)\
                        .then_inc(max_ready.sem, 1)

                def body(g, left):
                    dve.wait_ge(*p_ready.at(g, 1))
                    v.reciprocal(rrec[:], rsum[:]).then_inc(r_steps.sem, 1)
                    dve.wait_ge(*t_psum.at(g, 1))
                    v.tensor_copy(probsT[:], p.bank[1][:]).then_inc(pt_ready.sem, 1)
                    if left >= 1:
                        maxima(g + 1)
                    if left >= 2:
                        normalise(p, dve, g + 2, xn, xn_ready)
                    dve.wait_ge(*r_steps.at(g, 1))
                    dve.wait_ge(*y_psum.at(g, 1))
                    for b in range(G):
                        last = v.scalar_tensor_tensor(rows_of_x(p, g, b), p.bank[2][:, batch(b)], rrec[:, b:b + 1], rows_of_x(p, g, b),
                                                      ALU.mult, ALU.add)
                    last.then_inc(x_done.sem, 1)
                    row_statistics(p, dve, g, x_done)

                normalise(p, dve, 0, xn, xn_ready)
                maxima(0)
                normalise(p, dve, 1, xn, xn_ready)
                loop(dve, body)
        p.passed(NG)



def channel_attention(p, name):
    nc, ins, w = p.nc, p.inputs, p.w
    norm_rows(p, name)
    (xn_ready, xnT_psum, xnT_ready, q_psum, k_psum, v_psum, q_ready, k_ready, v_ready, vmask_ready, s_psum, max_ready,
     p_ready, r_steps, qpad_ready, av_psum, x_done) = p.plan(
        xn_ready=G, xnT_psum=1, xnT_ready=1, q_psum=1, k_psum=1, v_psum=1, q_ready=1, k_ready=1, v_ready=1,
        kmask_ready=UNITS, s_psum=UNITS, max_ready=UNITS, p_ready=UNITS, reciprocal_steps=G, qpad_ready=G, av_psum=G, x_done=1)
    prep, = p.plan(stage_prepared=0)
    S_BANK, M_BANK, O_BANK = p.bank[0:4], p.bank[6], p.bank[7]
    with ExitStack() as ctx:
        t = lambda k, shape, dt=F32: sb(p, ctx, f"{name}_{k}", shape, dt)
        xn, xnT = front(p, name, ctx)
        qT, k, vv = t("qT", [128, 2, GT]), t("k", [128, 2, GT]), t("v", [128, 2, GT])
        vmask, qpad = t("vmask", [128, 2, QUADS, PER * S]), t("qpad", [128, 2, H * 32])
        probs = t("probs", [128, 2, QUADS, PER * S])
        nmax, rsum, rrec = t("nmax", [128, G, H]), t("rsum", [128, G, H]), t("rrec", [128, G, H])
        temperature = t("temperature", [128, H])
        with nc.Block(no_gpsimd_drain=True) as block:
            @block.gpsimd
            def _(pool):
                then = Chain(pool, prep)
                then(nc.gpsimd.memset(qpad[:], 0.0))
                then(nc.gpsimd.memset(temperature[:], 1.0))
                then(nc.gpsimd.affine_select(out=temperature[:], in_=temperature[:], compare_op=ALU.is_ge, fill=0.0, base=0,
                                             pattern=[[-HD, H]], channel_multiplier=1))
                then(nc.gpsimd.affine_select(out=temperature[:], in_=temperature[:], compare_op=ALU.is_ge, fill=0.0,
                                             base=HD - 1, pattern=[[HD, H]], channel_multiplier=-1))
                then(nc.gpsimd.tensor_tensor(temperature[:], temperature[:], w["L2_attn_temp"][:].to_broadcast([128, H]), ALU.mult))
        prep.base += 5
        AFTER = 4

        with nc.Block(no_gpsimd_drain=True) as block:
            @block.gpsimd
            def _(pool):
                def units(g, a, steps, first, last):
                    for u in range(steps):
                        b, j = u // 4, u % 4
                        if u == 0:
                            pool.wait_ge(*v_ready.at(g, 1))
                        if not (first and u < 8):
                            pool.wait_ge(*s_psum.at(g, u - 7))
                        nc.gpsimd.tensor_tensor(vmask[:, b % 2, j].rearrange("p (c k) -> p c k", c=PER),
                                                vv[:, a, batch(b)].unsqueeze(1).to_broadcast([128, PER, S]),
                                                temperature[:, PER * j:PER * j + PER].unsqueeze(2).to_broadcast([128, PER, S]),
                                                ALU.mult).then_inc(vmask_ready.sem, 1)
                all_groups(pool, units)

            @block.tensor
            def _(pe):
                mm = nc.tensor.matmul

                def scores(g, a, u, first):
                    b, j = u // 4, u % 4
                    pe.wait_ge(*vmask_ready.at(g, u + 1))
                    if u == 0:
                        pe.wait_ge(*k_ready.at(g, 1))
                    if not (first and u < 4):
                        pe.wait_ge(*p_ready.at(g, u - 3))
                    mm(S_BANK[j][:], lhsT=k[:, a, batch(b)], rhs=vmask[:, b % 2, j], start=True, stop=True).then_inc(s_psum.sem, 1)

                def values(g, b, first):
                    pe.wait_ge(*qpad_ready.at(g, b + 1))
                    if b == 0 and not first:
                        pe.wait_ge(*x_done.at(g, 0))
                    for c in range(PER):
                        for j in range(QUADS):
                            h = j * PER + c
                            last = mm(O_BANK[32 * j:32 * j + 32, batch(b)], lhsT=qpad[:, b % 2, 32 * h:32 * h + 32],
                                      rhs=probs[:, b % 2, j, batch(c)], start=(c == 0), stop=(c == PER - 1),
                                      tile_position=(0, 32 * j), skip_group_check=True)
                    last.then_inc(av_psum.sem, 1)

                def front(g, a, step):
                    if step == 0:
                        transpose_xn(p, pe, g, xn, xn_ready, M_BANK, xnT_psum)
                    if step == 1:
                        pe.wait_ge(*xnT_ready.at(g, 1))
                        for b in range(G):
                            last = mm(M_BANK[:, batch(b)], lhsT=xnT[:, batch(b)], rhs=w["L2_attn_Wv"][:], start=True, stop=True)
                        last.then_inc(v_psum.sem, 1)
                    if step == 2:
                        pe.wait_ge(*v_ready.at(g, 1))
                        for b in range(G):
                            last = mm(M_BANK[:, batch(b)], lhsT=xnT[:, batch(b)], rhs=w["L2_attn_Wk"][:], start=True, stop=True)
                        last.then_inc(k_psum.sem, 1)
                    if step == 3:
                        pe.wait_ge(*k_ready.at(g, 1))
                        mm(M_BANK[:], lhsT=w["L2_attn_Wq"][:], rhs=xnT[:], start=True, stop=True).then_inc(q_psum.sem, 1)

                def units(g, a, steps, first, last):
                    if first:
                        for step in range(4):
                            front(g, a, step)
                    for u in range(steps or AFTER):
                        if steps:
                            scores(g, a, u, first)
                        if u % 4 == 2 and not (first and u < 6):
                            h, ha, hu = before(g, a, u, 6)
                            values(h, hu // 4, first)
                        if not last:
                            if u == 4:
                                pe.wait_ge(*q_ready.at(g, 1))
                            for step, at in enumerate((4, 6, 8, 10)):
                                if u == at:
                                    front(g + 1, 1 - a, step)
                all_groups(pe, units)

            @block.scalar
            def _(act):
                nc.scalar.preload_act_table(ACT.Exp)

                def start(g):
                    act.wait_ge(*xnT_psum.at(g, 1))
                    nc.scalar.activation(xnT[:], M_BANK[:], ACT.Copy).then_inc(xnT_ready.sem, 1)

                def units(g, a, steps, first, last):
                    if first:
                        start(g)
                    for u in range(steps):
                        b, j = u // 4, u % 4
                        act.wait_ge(*max_ready.at(g, u + 1))
                        if j == 0 and not (first and b < 2):
                            act.wait_ge(*av_psum.at(g, b - 1))
                        for c in range(PER):
                            h = 4 * j + c
                            done = nc.scalar.activation(probs[:, b % 2, j, batch(c)], S_BANK[j][:, batch(c)], ACT.Exp,
                                                        bias=nmax[:, b, h:h + 1], accum_out=rsum[:, b, h:h + 1])
                        done.then_inc(p_ready.sem, 1)
                        if u == 4 and not last:
                            start(g + 1)
                all_groups(act, units)

            @block.vector
            def _(dve):
                v = nc.vector

                def scaled_q(g, a, b, first):
                    dve.wait_ge(*p_ready.at(g, 4 * b + 4))
                    v.reciprocal(rrec[:, b, :], rsum[:, b, :]).then_inc(r_steps.sem, 1)
                    dve.wait_ge(*r_steps.at(g, b + 1))
                    if not (first and b < 2):
                        dve.wait_ge(*av_psum.at(g, b - 1))
                    q = qpad[:, b % 2, :]
                    slots = bass.AP(q.tensor, q.offset, [list(q.ap[0]), [128, QUADS], [40, PER], [1, HD]])
                    v.tensor_tensor(slots, qT[:, a, batch(b)].rearrange("p (j c d) -> p j c d", j=QUADS, c=PER),
                                    rrec[:, b, :].rearrange("p (j c) -> p j c", j=QUADS).unsqueeze(3).to_broadcast([128, QUADS, PER, HD]),
                                    ALU.mult).then_inc(qpad_ready.sem, 1)

                def front(g, a, step):
                    if step == 0:
                        normalise(p, dve, g, xn, xn_ready)
                    for i, out, bias, psum, ready in ((1, vv, "L2_attn_bv", v_psum, v_ready), (2, k, "L2_attn_bk", k_psum, k_ready)):
                        if step == i:
                            dve.wait_ge(*psum.at(g, 1))
                            v.tensor_tensor(out[:, a, :].rearrange("p (b c) -> p b c", b=G), M_BANK[:].rearrange("p (b c) -> p b c", b=G),
                                            w[bias][:].unsqueeze(1).to_broadcast([128, G, D]), ALU.add).then_inc(ready.sem, 1)
                    if step == 3:
                        dve.wait_ge(*q_psum.at(g, 1))
                        v.tensor_scalar(qT[:, a, :], M_BANK[:], w["L2_attn_bq"][:, 0:1], None, ALU.add).then_inc(q_ready.sem, 1)

                def units(g, a, steps, first, last):
                    if first:
                        for step in range(4):
                            front(g, a, step)
                    for u in range(steps or AFTER):
                        if steps:
                            dve.wait_ge(*s_psum.at(g, u + 1))
                            v.tensor_reduce(nmax[:, u // 4, 4 * (u % 4):4 * (u % 4) + 4], S_BANK[u % 4][:].rearrange("p (c k) -> p c k", c=PER),
                                            axis=AX, op=ALU.max, negate=True).then_inc(max_ready.sem, 1)
                        if u % 4 == 1 and not (first and u < 5):
                            h, ha, hu = before(g, a, u, 5)
                            scaled_q(h, ha, hu // 4, first)
                        if u == 3 and not first:
                            dve.wait_ge(*av_psum.at(g - 1, G))
                            v.tensor_tensor(rows_of_x(p, g - 1, 0, G), rows_of_x(p, g - 1, 0, G), O_BANK[:], ALU.add).then_inc(x_done.sem, 1)
                            row_statistics(p, dve, g - 1, x_done)
                        if not last:
                            for step, at in enumerate((2, 7, 9, 11)):
                                if u == at:
                                    front(g + 1, 1 - a, step)
                all_groups(dve, units)
        p.passed(NG)


def latent_weights(p):
    nc, w = p.nc, p.w
    sum_ready, down_psum, down_ready, up_psum = p.plan(latent_sum_ready=0, latent_psum=0, latent_ready=0, latent_up_psum=0)
    with ExitStack() as ctx:
        both, down = sb(p, ctx, "latent_both", [128, 128]), sb(p, ctx, "latent_down", [32, 128])
        with nc.Block(no_gpsimd_drain=True) as block:
            @block.vector
            def _(dve):
                nc.vector.tensor_tensor(both[:], w["L3_attn_W_k_T"][:], w["L3_attn_W_v_T"][:], ALU.add).then_inc(sum_ready.sem, 1)

            @block.tensor
            def _(pe):
                pe.wait_ge(*sum_ready.at(0, 1))
                nc.tensor.matmul(p.bank[0][0:32, 0:128], lhsT=w["L3_attn_W_down_kv"][:], rhs=both[:], start=True, stop=True)\
                    .then_inc(down_psum.sem, 1)
                pe.wait_ge(*down_ready.at(0, 1))
                for i, n in enumerate(("L3_attn_W_up_k", "L3_attn_W_up_v")):
                    last = nc.tensor.matmul(p.bank[1][:, batch(i)], lhsT=down[:], rhs=w[n][:], start=True, stop=True)
                last.then_inc(up_psum.sem, 1)

            @block.scalar
            def _(act):
                act.wait_ge(*down_psum.at(0, 1))
                nc.scalar.activation(down[:], p.bank[0][0:32, 0:128], ACT.Copy).then_inc(down_ready.sem, 1)
                act.wait_ge(*up_psum.at(0, 1))
                nc.scalar.activation(w["L3_K"][:], p.bank[1][:, batch(0)], ACT.Copy)
                nc.scalar.activation(w["L3_V"][:], p.bank[1][:, batch(1)], ACT.Copy)
    for s in (sum_ready, down_psum, down_ready, up_psum):
        s.base += 1



SUPPORT = 5


def support_attention(p, name):
    nc, ins, w = p.nc, p.inputs, p.w
    HEADS, HD3, CH = 8, 64, 4
    U, PROJECTIONS = 2 * G, 2 * CH + G
    norm_rows(p, name, again=1e-5)
    (ctx_in, mask_in, xn_ready, xnT_psum, xnT_ready, projected, even_ready, odd_ready, named, order_psum,
     bias_ready, floor_steps, s_psum, raw_max, max_ready, shift_ready, e_ready, p_ready, t_psum, pt_ready, av_psum,
     r_steps, sum_ready, o_ready, oT_psum, oT_ready, y_psum, x_part) = p.plan(
        ctx_in=16, mask_in=16, xn_ready=G, xnT_psum=1, xnT_ready=1, projection_psum=PROJECTIONS,
        even_projections_ready=PROJECTIONS // 2, odd_projections_ready=PROJECTIONS // 2, mask_named=1, mask_order_psum=1,
        mask_ready=1, floor_steps=4, s_psum=U, raw_max=U, max_ready=U, masked_shift_ready=G, masked_exp_ready=G, p_ready=U,
        t_psum=U, pt_ready=U, av_psum=G, reciprocal_steps=G, masked_sum_steps=G, o_ready=G, oT_psum=G, oT_ready=G,
        y_psum=G, expert_added=G)
    prep, = p.plan(stage_prepared=0)
    S_BANK, T_BANK, F_BANK, O_BANK, M_BANK = p.bank[0:2], p.bank[2:4], p.bank[4:6], p.bank[6], p.bank[7]
    with ExitStack() as ctx:
        t = lambda k, shape, dt=F32: sb(p, ctx, f"{name}_{k}", shape, dt)
        xn, xnT = front(p, name, ctx)
        ctxT, mask = t("ctxT", [128, GT]), t("mask", [128, GT], I32)
        named_bf, ones, order = t("named", [128, GT], BF16), t("ones", [128, S], BF16), t("order", [128, S], BF16)
        score_bias = t("score_bias", [128, 2, G, S], BF16)
        kT, qT, vv = t("kT", [128, 2, CH, GT]), t("qT", [128, 2, CH, GT]), t("v", [128, 2, G, HEADS * HD3])
        probs, probsT = t("probs", [128, 4, CH * S]), t("probsT", [128, 4, CH * S])
        nmax, rsum, rrec, rowmax, eshift, e = (t(k, [128, G, HEADS]) for k in ("nmax", "rsum", "rrec", "rowmax", "eshift", "e"))
        pads, nfloor = t("pads", [128, 2, G]), t("nfloor", [128, 2, G])
        o, oT = t("o", [128, 2, HEADS * HD3]), t("oT", [128, CH * S])

        with nc.Block(no_gpsimd_drain=True) as block:
            @block.gpsimd
            def _(pool):
                then = Chain(pool, prep)
                then(nc.gpsimd.memset(order[:], 1.0))
                then(nc.gpsimd.affine_select(out=order[:], in_=order[:], compare_op=ALU.is_ge, fill=0.0, base=0,
                                             pattern=[[1, S]], channel_multiplier=-1))
                then(nc.gpsimd.affine_select(out=order[:], in_=order[:], compare_op=ALU.not_equal, fill=-1024.0, base=0,
                                             pattern=[[1, S]], channel_multiplier=-1))
        prep.base += 3
        AFTER = 6

        def place(a, n):
            return (kT, qT, vv)[n // CH][:, a, n % CH, :]

        with nc.Block(no_gpsimd_drain=True) as block:
            @block.sync
            def _(sp):
                def load(g):
                    sp.dma_start(ctxT[:], ins["ctx_T"][:, ds(g * GT, GT)]).then_inc(ctx_in.sem, 16)
                    sp.dma_start(mask[:], ins["visible"][:, ds(g * GT, GT)]).then_inc(mask_in.sem, 16)
                load(0)
                with sp.Fori(1, NG) as g:
                    sp.wait_ge(*projected.at(g - 1, PROJECTIONS))
                    sp.wait_ge(*named.at(g - 1, 1))
                    load(g)

            @block.tensor
            def _(pe):
                mm = nc.tensor.matmul

                def front(g, a, u, first):
                    if u == 1:
                        if not first:
                            pe.wait_ge(*even_ready.at(g, 0))
                            pe.wait_ge(*odd_ready.at(g, 0))
                        transpose_xn(p, pe, g, xn, xn_ready, F_BANK[0], xnT_psum)
                        pe.wait_ge(*named.at(g, 1))
                        for b in range(G):
                            last = mm(F_BANK[1][:, batch(b)], lhsT=named_bf[:, batch(b)], rhs=order[:], start=True, stop=True)
                        last.then_inc(order_psum.sem, 1)
                    for n in range(2 * (u - 2), 2 * (u - 2) + 2) if u >= 2 else ():
                        if n == 0:
                            pe.wait_ge(*xnT_ready.at(g, 1))
                            pe.wait_ge(*ctx_in.at(g, 16))
                        elif n == 1:
                            pe.wait_ge(*bias_ready.at(g, 1))
                        else:
                            pe.wait_ge(*(odd_ready if n % 2 else even_ready).at(g, n // 2))
                        if n < CH:
                            last = mm(F_BANK[n % 2][:], lhsT=w["L3_xattn_Wkv"][:, batch(n)], rhs=ctxT[:], start=True, stop=True)
                        elif n < 2 * CH:
                            last = mm(F_BANK[n % 2][:], lhsT=w["L3_xattn_Wq"][:, batch(n - CH)], rhs=xnT[:], start=True, stop=True)
                        else:
                            last = mm(F_BANK[n % 2][:], lhsT=ctxT[:, batch(n - 2 * CH)], rhs=w["L3_xattn_Wkv"][:, 512:1024],
                                      start=True, stop=True)
                        last.then_inc(projected.sem, 1)

                def scores(g, a, u, first):
                    b, r = u // 2, u % 2
                    if u == 0:
                        pe.wait_ge(*bias_ready.at(g, 1))
                        pe.wait_ge(*even_ready.at(g, CH))
                        pe.wait_ge(*odd_ready.at(g, CH))
                    if not (first and u < 2):
                        pe.wait_ge(*p_ready.at(g, u - 1))
                    mm(S_BANK[r][:], lhsT=p.ident_bf[:], rhs=score_bias[:, a, b, :].unsqueeze(1).to_broadcast([128, CH, S]),
                       start=True, stop=False, skip_group_check=True)
                    rows = slice(64 * r, 64 * r + 64)
                    for ch in range(CH):
                        last = mm(S_BANK[r][:, batch(ch)], lhsT=qT[rows, a, ch, batch(b)], rhs=kT[rows, a, ch, batch(b)],
                                  start=False, stop=(ch == CH - 1), skip_group_check=True)
                    last.then_inc(s_psum.sem, 1)

                def transposes(g, u, first):
                    pe.wait_ge(*p_ready.at(g, u + 1))
                    if not (first and u < 2):
                        pe.wait_ge(*pt_ready.at(g, u - 1))
                    for ch in range(CH):
                        last = nc.tensor.transpose(T_BANK[u % 2][:, batch(ch)], probs[:, u % 4, batch(ch)], p.ident[:])
                    last.then_inc(t_psum.sem, 1)

                def values(g, a, u, first):
                    b, r = u // 2, u % 2
                    pe.wait_ge(*pt_ready.at(g, u + 1))
                    if u == 0:
                        pe.wait_ge(*even_ready.at(g, PROJECTIONS // 2))
                        pe.wait_ge(*odd_ready.at(g, PROJECTIONS // 2))
                    if r == 0 and not (first and b == 0):
                        pe.wait_ge(*o_ready.at(g, b))
                    for ch in range(CH):
                        h = 2 * ch + r
                        last = mm(O_BANK[:, h * HD3:(h + 1) * HD3], lhsT=probsT[:, u % 4, batch(ch)],
                                  rhs=vv[:, a, b, h * HD3:(h + 1) * HD3], start=True, stop=True)
                    if r == 1:
                        last.then_inc(av_psum.sem, 1)

                def output_transposes(g, b, first):
                    pe.wait_ge(*o_ready.at(g, b + 1))
                    if not (first and b == 0):
                        pe.wait_ge(*x_part.at(g, b))
                    for ch in range(CH):
                        last = nc.tensor.transpose(M_BANK[:, batch(ch)], o[:, b % 2, batch(ch)], p.ident[:])
                    last.then_inc(oT_psum.sem, 1)

                def output(g, b):
                    pe.wait_ge(*oT_ready.at(g, b + 1))
                    for ch in range(CH):
                        last = mm(M_BANK[:, 0:D], lhsT=oT[:, batch(ch)], rhs=w["L3_xattn_Wout"][:, ch, :],
                                  start=(ch == 0), stop=(ch == CH - 1))
                    last.then_inc(y_psum.sem, 1)

                def units(g, a, steps, first, last):
                    if first:
                        for u in range(1, U):
                            front(g, a, u, True)
                    for u in range(steps or AFTER):
                        if steps:
                            scores(g, a, u, first)
                        if not last:
                            front(g + 1, 1 - a, u, False)
                        if (steps or u < 1) and not (first and u < 1):
                            h, _, hu = before(g, a, u, 1, U)
                            transposes(h, hu, first)
                        if (steps or u < 2) and not (first and u < 2):
                            h, ha, hu = before(g, a, u, 2, U)
                            values(h, ha, hu, first)
                        if u % 2 == 1 and not (first and u < 5) and (steps or u < 5):
                            h, _, hu = before(g, a, u, 5, U)
                            output_transposes(h, hu // 2, first)
                        if u % 2 == 0 and not (first and u < 6):
                            h, _, hu = before(g, a, u, 6, U)
                            output(h, hu // 2)
                all_groups(pe, units, U)

            @block.scalar
            def _(act):
                nc.scalar.preload_act_table(ACT.Exp)

                def front(g, a, u):
                    if u == 1:
                        act.wait_ge(*xnT_psum.at(g, 1))
                        nc.scalar.activation(xnT[:], F_BANK[0][:], ACT.Identity, scale=w["L3_xattn_ln_w"][:, 0:1],
                                             bias=w["L3_xattn_ln_b"][:, 0:1]).then_inc(xnT_ready.sem, 1)
                    if u >= 2:
                        n = 2 * (u - 2)
                        act.wait_ge(*projected.at(g, n + 1))
                        nc.scalar.activation(place(a, n), F_BANK[0][:], ACT.Copy, scale=HD3 ** -0.5 if n // CH == 1 else 1.0)\
                            .then_inc(even_ready.sem, 1)

                def units(g, a, steps, first, last):
                    if first:
                        for u in range(1, U):
                            front(g, a, u)
                    for u in range(steps or AFTER):
                        if u % 2 == 0 and not (first and u < 6):
                            h, _, hu = before(g, a, u, 6, U)
                            act.wait_ge(*oT_psum.at(h, hu // 2 + 1))
                            nc.scalar.activation(oT[:], M_BANK[:], ACT.Copy).then_inc(oT_ready.sem, 1)
                        if steps:
                            b, r = u // 2, u % 2
                            act.wait_ge(*max_ready.at(g, u + 1))
                            if not (first and u < 4):
                                act.wait_ge(*t_psum.at(g, u - 3))
                            for ch in range(CH):
                                i = CH * r + ch
                                done = nc.scalar.activation(probs[:, u % 4, batch(ch)], S_BANK[r][:, batch(ch)], ACT.Exp,
                                                            bias=nmax[:, b, i:i + 1], accum_out=rsum[:, b, i:i + 1])
                            done.then_inc(p_ready.sem, 1)
                            if r == 1:
                                act.wait_ge(*shift_ready.at(g, b + 1))
                                nc.scalar.activation(e[:, b, :], eshift[:, b, :], ACT.Exp).then_inc(e_ready.sem, 1)
                        if not last:
                            front(g + 1, 1 - a, u)
                all_groups(act, units, U)

            @block.vector
            def _(dve):
                v = nc.vector

                def front(g, a, u):
                    if u == 0:
                        dve.wait_ge(*mask_in.at(g, 16))
                        v.tensor_scalar(named_bf[:], mask[:], 0.0, None, ALU.not_equal).then_inc(named.sem, 1)
                        normalise(p, dve, g, xn, xn_ready)
                    if u == 1:
                        dve.wait_ge(*order_psum.at(g, 1))
                        v.tensor_scalar(score_bias[:, a].rearrange("p b k -> p (b k)"), F_BANK[1][:], -1024.0 + SUPPORT - 0.5,
                                        MASKED, ALU.is_gt, ALU.mult).then_inc(bias_ready.sem, 1)
                    if u == 2:
                        dve.wait_ge(*bias_ready.at(g, 1))
                        v.tensor_reduce(pads[:, a], score_bias[:, a], axis=AX, op=ALU.add).then_inc(floor_steps.sem, 1)
                        dve.wait_ge(*floor_steps.at(g, 1))
                        v.tensor_scalar(pads[:, a], pads[:, a], 1.0 / MASKED, SUPPORT - S, ALU.mult, ALU.add).then_inc(floor_steps.sem, 1)
                        dve.wait_ge(*floor_steps.at(g, 2))
                        v.tensor_scalar(nfloor[:, a], pads[:, a], 0.5, -3e38, ALU.is_gt, ALU.mult).then_inc(floor_steps.sem, 1)
                        dve.wait_ge(*floor_steps.at(g, 3))
                        v.tensor_scalar(nfloor[:, a], nfloor[:, a], 3e38, 1e4, ALU.add, ALU.max).then_inc(floor_steps.sem, 1)
                        dve.wait_ge(*floor_steps.at(g, 4))
                    if u >= 2:
                        n = 2 * (u - 2) + 1
                        dve.wait_ge(*projected.at(g, n + 1))
                        if n // CH == 1:
                            v.tensor_scalar(place(a, n), F_BANK[1][:], HD3 ** -0.5, None, ALU.mult).then_inc(odd_ready.sem, 1)
                        else:
                            v.tensor_copy(place(a, n), F_BANK[1][:]).then_inc(odd_ready.sem, 1)

                def maxima(g, a, u):
                    b, r = u // 2, u % 2
                    heads = slice(CH * r, CH * r + CH)
                    dve.wait_ge(*s_psum.at(g, u + 1))
                    v.tensor_reduce(rowmax[:, b, heads], S_BANK[r][:].rearrange("p (c k) -> p c k", c=CH),
                                    axis=AX, op=ALU.max, negate=True).then_inc(raw_max.sem, 1)
                    dve.wait_ge(*raw_max.at(g, u + 1))
                    v.tensor_scalar(nmax[:, b, heads], rowmax[:, b, heads], nfloor[:, a, b:b + 1], None, ALU.min).then_inc(max_ready.sem, 1)
                    if r == 1:
                        dve.wait_ge(*max_ready.at(g, u + 1))
                        v.tensor_scalar(eshift[:, b, :], nmax[:, b, :], 1e4, -1e4, ALU.min, ALU.add).then_inc(shift_ready.sem, 1)

                def copy_out(g, u, first):
                    dve.wait_ge(*t_psum.at(g, u + 1))
                    if not (first and u < 4) and u % 2 == 0:
                        dve.wait_ge(*av_psum.at(g, u // 2 - 1))
                    v.tensor_copy(probsT[:, u % 4, :], T_BANK[u % 2][:]).then_inc(pt_ready.sem, 1)

                def reciprocals(g, a, b):
                    dve.wait_ge(*e_ready.at(g, b + 1))
                    v.scalar_tensor_tensor(rsum[:, b, :], e[:, b, :], pads[:, a, b:b + 1], rsum[:, b, :], ALU.mult, ALU.add)\
                        .then_inc(sum_ready.sem, 1)
                    dve.wait_ge(*sum_ready.at(g, b + 1))
                    v.reciprocal(rrec[:, b, :], rsum[:, b, :]).then_inc(r_steps.sem, 1)

                def divided(g, b):
                    dve.wait_ge(*r_steps.at(g, b + 1))
                    dve.wait_ge(*av_psum.at(g, b + 1))
                    v.tensor_tensor(o[:, b % 2, :].rearrange("p (c r d) -> p c r d", c=CH, r=2), O_BANK[:].rearrange("p (c r d) -> p c r d", c=CH, r=2),
                                    rrec[:, b, :].rearrange("p (r c) -> p c r", r=2).unsqueeze(3).to_broadcast([128, CH, 2, HD3]),
                                    ALU.mult).then_inc(o_ready.sem, 1)

                def add_output(g, b):
                    dve.wait_ge(*y_psum.at(g, b + 1))
                    v.tensor_tensor(rows_of_x(p, g, b), rows_of_x(p, g, b), M_BANK[:, 0:D], ALU.add).then_inc(x_part.sem, 1)
                    if b == G - 1:
                        row_statistics(p, dve, g, x_part, G)

                def units(g, a, steps, first, last):
                    if first:
                        for u in range(U):
                            front(g, a, u)
                    for u in range(steps or AFTER):
                        if u % 2 == 0 and not (first and u < 4) and (steps or u < 4):
                            h, _, hu = before(g, a, u, 4, U)
                            divided(h, hu // 2)
                        if u % 2 == 1 and not (first and u < 7):
                            h, _, hu = before(g, a, u, 7, U)
                            add_output(h, hu // 2)
                        if steps:
                            maxima(g, a, u)
                        if not last and u:
                            front(g + 1, 1 - a, u)
                        if (steps or u < 1) and not (first and u < 1):
                            h, _, hu = before(g, a, u, 1, U)
                            copy_out(h, hu, first)
                        if u % 2 == 1 and not (first and u < 3) and (steps or u < 3):
                            h, ha, hu = before(g, a, u, 3, U)
                            reciprocals(h, ha, hu // 2)
                        if not last and u == 0:
                            front(g + 1, 1 - a, u)
                all_groups(dve, units, U)
        p.passed(NG)



def quantised_ffn(p, name):
    nc, ins, w = p.nc, p.inputs, p.w
    F, CH = 512, 4
    ROUND = 1.5 * 2 ** 23
    norm_rows(p, name, again=1e-6)
    (xn_ready, q_steps, qT_psum, qT_ready, h_psum, h_in, h_ready, sums_ready, am_ready, ms_in, root_ready, tail, q2_steps,
     t_psum, t_ready, y_psum, x_done, added_steps) = p.plan(
        xn_ready=G, quantise_steps=5 + G + 1, xnT_psum=1, xnT_ready=1, h_psum=G, relu_ready=G, h_ready=G, squares_ready=G,
        max_ready=G, variance_ready=1, root_ready=1, tail_steps=5, quantise_2_steps=2 * G, t_psum=G, pt_ready=G, y_psum=1,
        x_done=1, added_steps=G)
    w_in, prep, prep_sum, prep_psum, prep_steps = p.plan(expert_weights_in=0, stage_prepared=0, weight_sums_ready=0, product_psum=0, angle_steps=0)
    M_BANK, T_BANK, Y_BANK = p.bank[6], p.bank[4:6], p.bank[7]
    with ExitStack() as ctx:
        t = lambda k, shape, dt=F32: sb(p, ctx, f"{name}_{k}", shape, dt)
        xn, y = t("xn", [128, GT]), t("y", [128, GT])
        w1, w2, q1, q2 = t("w1", [128, F]), t("w2", [128, CH * D]), t("q1", [128, F], BF16), t("q2", [128, CH * D], BF16)
        ones, sums, mean, wscale = t("ones", [128, 128]), t("sums", [128, 2]), t("mean", [128, 2]), t("wscale", [128, 2])
        most, scale, back = t("most", [128, G]), t("scale", [128, G]), t("back", [128, G])
        xqT = t("xqT", [128, GT], BF16)
        pre, h, junk = t("pre", [128, 2, F]), t("h", [128, 2, G, F]), t("junk", [128, F])
        ss, most2, veps, root, rs, scale2, back2 = (t(k, [128, G]) for k in ("ss", "most2", "veps", "root", "rs", "scale2", "back2"))
        hqT = t("hqT", [128, 2, CH * S], BF16)

        with nc.Block(no_gpsimd_drain=True) as block:
            @block.sync
            def _(sp):
                sp.dma_start(w1[:], ins["L3_ffn_w1T"]).then_inc(w_in.sem, 16)
                sp.dma_start(w2[:], ins["L3_ffn_w2T"]).then_inc(w_in.sem, 16)

            @block.gpsimd
            def _(pool):
                Chain(pool, prep)(nc.gpsimd.memset(ones[:], 1.0))

            @block.tensor
            def _(pe):
                pe.wait_ge(*prep.at(0, 1))
                pe.wait_ge(*prep_sum.at(0, 2))
                nc.tensor.matmul(M_BANK[:, 0:2], lhsT=ones[:], rhs=sums[:], start=True, stop=True).then_inc(prep_psum.sem, 1)

            @block.vector
            def _(dve):
                v = nc.vector
                then = Chain(dve, prep_steps)
                dve.wait_ge(*w_in.at(0, 32))
                for i, m in enumerate((w1, w2)):
                    v.tensor_reduce(sums[:, i:i + 1], m[:], axis=AX, op=ALU.add, apply_absolute_value=True).then_inc(prep_sum.sem, 1)
                dve.wait_ge(*prep_psum.at(0, 1))
                then(v.tensor_scalar(mean[:], M_BANK[:, 0:2], 1.0 / (F * D), 1e-5, ALU.mult, ALU.max))
                then(v.reciprocal(wscale[:], mean[:]))
                for i, (m, q) in enumerate(((w1, q1), (w2, q2))):
                    then(v.tensor_scalar(m[:], m[:], wscale[:, i:i + 1], ROUND, ALU.mult, ALU.add))
                    then(v.tensor_scalar(m[:], m[:], ROUND, -1.0, ALU.subtract, ALU.max))
                    then(v.tensor_scalar(q[:], m[:], 1.0, None, ALU.min))
                then(v.tensor_scalar(mean[:], mean[:], 1.0 / 127.0, None, ALU.mult))
        for s, n in ((w_in, 32), (prep, 1), (prep_sum, 2), (prep_psum, 1), (prep_steps, 9)):
            s.base += n

        with nc.Block(no_gpsimd_drain=True) as block:
            @block.tensor
            def _(pe):
                mm = nc.tensor.matmul

                def first_half(g, first):
                    pe.wait_ge(*q_steps.at(g, q_steps.per))
                    for b in range(G):
                        last = nc.tensor.transpose(M_BANK[:, batch(b)], xn[:, batch(b)], p.ident[:])
                    last.then_inc(qT_psum.sem, 1)
                    pe.wait_ge(*qT_ready.at(g, 1))
                    for b in range(G):
                        if not first:
                            pe.wait_ge(*h_in.at(g - 1, b + 1))
                        mm(p.bank[b][:], lhsT=xqT[:, batch(b)], rhs=q1[:], start=True, stop=True).then_inc(h_psum.sem, 1)

                def second_half(g, a, first):
                    def down(b):
                        pe.wait_ge(*t_ready.at(g, b + 1))
                        if b == 0 and not first:
                            pe.wait_ge(*added_steps.at(g - 1, G))
                        for ch in range(CH):
                            last = mm(Y_BANK[:, batch(b)], lhsT=hqT[:, b % 2, batch(ch)], rhs=q2[:, batch(ch)],
                                      start=(ch == 0), stop=(ch == CH - 1))
                        return last

                    for b in range(G):
                        pe.wait_ge(*q2_steps.at(g, 2 * b + 2))
                        if not (first and b < 2):
                            pe.wait_ge(*t_ready.at(g, b - 1))
                        for ch in range(CH):
                            last = nc.tensor.transpose(T_BANK[b % 2][:, batch(ch)], h[:, a, b, batch(ch)], p.ident[:])
                        last.then_inc(t_psum.sem, 1)
                        if b:
                            down(b - 1)
                    down(G - 1).then_inc(y_psum.sem, 1)

                def units(g, a, steps, first, last):
                    if first:
                        first_half(g, True)
                    if steps:
                        if not last:
                            first_half(g + 1, False)
                        second_half(g, a, first)
                all_groups(pe, units, 1)

            @block.scalar
            def _(act):
                def copy_in(g):
                    act.wait_ge(*qT_psum.at(g, 1))
                    nc.scalar.activation(xqT[:], M_BANK[:], ACT.Copy).then_inc(qT_ready.sem, 1)

                def gelu(g, a, b):
                    act.wait_ge(*h_in.at(g, b + 1))
                    nc.scalar.activation(h[:, a, b, :], pre[:, b % 2, :], ACT.Gelu).then_inc(h_ready.sem, 1)
                    act.wait_ge(*h_ready.at(g, b + 1))
                    nc.scalar.activation(junk[:], h[:, a, b, :], ACT.Square, accum_out=ss[:, b:b + 1]).then_inc(sums_ready.sem, 1)

                def copy_h(g, b):
                    act.wait_ge(*t_psum.at(g, b + 1))
                    nc.scalar.activation(hqT[:, b % 2, :], T_BANK[b % 2][:], ACT.Copy).then_inc(t_ready.sem, 1)

                def units(g, a, steps, first, last):
                    if first:
                        copy_in(g)
                        for b in range(G):
                            gelu(g, a, b)
                    if steps:
                        if not last:
                            copy_in(g + 1)
                        act.wait_ge(*ms_in.at(g, 1))
                        nc.scalar.activation(root[:], veps[:], ACT.Sqrt).then_inc(root_ready.sem, 1)
                        if last:
                            for b in range(G):
                                copy_h(g, b)
                        else:
                            gelu(g + 1, 1 - a, 0)
                            gelu(g + 1, 1 - a, 1)
                            copy_h(g, 0)
                            copy_h(g, 1)
                            gelu(g + 1, 1 - a, 2)
                            copy_h(g, 2)
                            gelu(g + 1, 1 - a, 3)
                            copy_h(g, 3)
                all_groups(act, units, 1)

            @block.vector
            def _(dve):
                v = nc.vector

                def quantise_x(g):
                    normalise(p, dve, g, xn, xn_ready)
                    dve.wait_ge(*xn_ready.at(g, G))
                    then = Chain(dve, q_steps, g)
                    then(v.tensor_reduce(most[:], xn[:].rearrange("p (b d) -> p b d", b=G), axis=AX, op=ALU.max, apply_absolute_value=True))
                    then(v.tensor_scalar(most[:], most[:], 1e-5, None, ALU.max))
                    then(v.reciprocal(scale[:], most[:]))
                    then(v.tensor_scalar(scale[:], scale[:], 127.0, None, ALU.mult))
                    then(v.tensor_scalar(back[:], most[:], mean[:, 0:1], None, ALU.mult))
                    for b in range(G):
                        v.tensor_scalar(xn[:, batch(b)], xn[:, batch(b)], scale[:, b:b + 1], ROUND, ALU.mult, ALU.add).then_inc(q_steps.sem, 1)
                    then.n += G
                    dve.wait_ge(*q_steps.at(g, then.n))
                    then(v.tensor_scalar(xn[:], xn[:], ROUND, None, ALU.subtract))
                    then.ends()

                def scale_back(g, b):
                    dve.wait_ge(*h_psum.at(g, b + 1))
                    if b >= 2:
                        dve.wait_ge(*h_ready.at(g, b - 1))
                    v.scalar_tensor_tensor(pre[:, b % 2, :], p.bank[b][:], back[:, b:b + 1], w["L3_ffn_b1"][:], ALU.mult, ALU.add)\
                        .then_inc(h_in.sem, 1)

                def most_of_h(g, a, b):
                    dve.wait_ge(*h_ready.at(g, b + 1))
                    v.tensor_reduce(most2[:, b:b + 1], h[:, a, b, :], axis=AX, op=ALU.max, apply_absolute_value=True).then_inc(am_ready.sem, 1)

                def mean_squares(g):
                    dve.wait_ge(*sums_ready.at(g, G))
                    v.tensor_scalar(veps[:], ss[:], 1.0 / F, 1e-6, ALU.mult, ALU.add).then_inc(ms_in.sem, 1)

                def quantise_h(g, a):
                    dve.wait_ge(*root_ready.at(g, 1))
                    then = Chain(dve, tail, g)
                    dve.wait_ge(*am_ready.at(g, G))
                    then(v.reciprocal(rs[:], root[:]))
                    then(v.tensor_tensor(most2[:], most2[:], rs[:], ALU.mult))
                    then(v.tensor_scalar(most2[:], most2[:], 1e-5, None, ALU.max))
                    then(v.reciprocal(scale2[:], most2[:]))
                    v.tensor_scalar(back2[:], most2[:], mean[:, 1:2], None, ALU.mult)
                    then(v.scalar_tensor_tensor(scale2[:], scale2[:], 127.0, rs[:], ALU.mult, ALU.mult))
                    then.ends()
                    for b in range(G):
                        v.tensor_scalar(h[:, a, b, :], h[:, a, b, :], scale2[:, b:b + 1], ROUND, ALU.mult, ALU.add).then_inc(q2_steps.sem, 1)
                        dve.wait_ge(*q2_steps.at(g, 2 * b + 1))
                        v.tensor_scalar(h[:, a, b, :], h[:, a, b, :], ROUND, None, ALU.subtract).then_inc(q2_steps.sem, 1)

                def add_output(g):
                    dve.wait_ge(*y_psum.at(g, 1))
                    for b in range(G):
                        v.scalar_tensor_tensor(y[:, batch(b)], Y_BANK[:, batch(b)], back2[:, b:b + 1], w["L3_ffn_b2"][:], ALU.mult, ALU.add)\
                            .then_inc(added_steps.sem, 1)
                    dve.wait_ge(*added_steps.at(g, G))
                    v.tensor_tensor(rows_of_x(p, g, 0, G), rows_of_x(p, g, 0, G), y[:], ALU.add).then_inc(x_done.sem, 1)
                    dve.wait_ge(*x_done.at(g, 1))

                def units(g, a, steps, first, last):
                    if first:
                        quantise_x(g)
                        for b in range(G):
                            scale_back(g, b)
                        for b in range(G):
                            most_of_h(g, a, b)
                    if steps:
                        if not last:
                            quantise_x(g + 1)
                        mean_squares(g)
                        if not last:
                            scale_back(g + 1, 0)
                            scale_back(g + 1, 1)
                        quantise_h(g, a)
                        if not last:
                            for b in (2, 3):
                                scale_back(g + 1, b)
                            for b in range(G):
                                most_of_h(g + 1, 1 - a, b)
                        add_output(g)
                all_groups(dve, units, 1)
        p.passed(NG)


def store_out(p, out):
    nc, stored = p.nc, p.count_of("out_stored")
    with nc.Block(no_gpsimd_drain=True) as block:
        @block.sync
        def _(sp):
            for i in range(4):
                sp.dma_start(out[:, i * 1024:(i + 1) * 1024], p.x[:, i * 1024:(i + 1) * 1024]).then_inc(stored.sem, 16)
            sp.wait_ge(stored.sem, 64)


def build(nc, inputs, out, stages=12):
    with ExitStack() as ctx:
        p = Program(nc, ctx, inputs)
        load_all(p)
        for stage in STAGES[:stages]:
            stage(p)
        store_out(p, out)


STAGES = [
    lambda p: attention16(p, "L0a", "L0_attn_WQ", "L0_attn_WK", "L0_attn_WV", "L0_attn_WO", scale=HD ** -0.5, causal=True),
    lambda p: attention16(p, "L0x", "L0_xattn_w_q", "L0_xattn_w_k", "L0_xattn_w_v", "L0_xattn_w_o", cross=True,
                          b_q="L0_xattn_b_q", b_k="L0_xattn_b_k", b_v="L0_xattn_b_v", b_o="L0_xattn_b_o",
                          scale=HD ** -0.5, where_mask=True),
    lambda p: ffn_squared_relu(p, "L0f"),
    lambda p: linear_attention(p, "L1a"),
    lambda p: single_head(p, "L1x"),
    lambda p: ffn_sigmoid_experts(p, "L1f"),
    lambda p: channel_attention(p, "L2a"),
    lambda p: attention16(p, "L2x", "L2_xattn_Wq", "L2_xattn_Wk", "L2_xattn_Wv", cross=True, b_q="L2_xattn_bq",
                          b_k="L2_xattn_bk", b_v="L2_xattn_bv", key_mask=True),
    lambda p: ffn_linear_experts(p, "L2f"),
    lambda p: (latent_weights(p), attention16(p, "L3a", "L3_attn_W_q", "L3_K", "L3_V", "L3_attn_W_o", scale=D ** -0.5, decay=True)),
    lambda p: support_attention(p, "L3x"),
    lambda p: quantised_ffn(p, "L3f"),
]



def layouts(i):
    a = {k: np.asarray(v) for k, v in i.items()}
    T = lambda m: np.ascontiguousarray(m.T)
    rows = lambda m: np.ascontiguousarray(m.transpose(1, 0, 2)).reshape(128, -1)
    cols = lambda m: np.ascontiguousarray(m.transpose(2, 0, 1)).reshape(128, -1)
    o = {"x": rows(a["x"]), "ctx_T": cols(a["ctx_1024"]), "ctx_rows": rows(a["ctx_1024"])}
    m = a["mask_Bx1xSxS2_if1"][:, 0]
    o["mask_qk"], o["mask_kq"] = rows(m), cols(m)
    o["key_mask"] = a["mask_BxS2_ik0"]
    o["visible"] = rows(a["mask_BxS2xS_ik0"])
    for n in ["L0_attn_WQ", "L0_attn_WK", "L0_attn_WV", "L0_attn_WO", "L2_xattn_Wq", "L2_xattn_Wk", "L2_xattn_Wv",
              "L1_attn_out_w"]:
        o[n] = T(a[n])
    for n in ["L0_xattn_w_q", "L0_xattn_w_k", "L0_xattn_w_v", "L0_xattn_w_o", "L2_attn_Wq", "L2_attn_Wk",
              "L2_attn_Wv", "L3_attn_W_q", "L3_attn_W_o", "L0_xattn_b_q", "L0_xattn_b_k", "L2_attn_bq",
              "L2_xattn_bq", "L2_xattn_bk", "L3_xattn_ln_w", "L3_xattn_ln_b", "L0_xattn_b_v", "L0_xattn_b_o",
              "L1_attn_out_b", "L2_attn_bk", "L2_attn_bv", "L2_xattn_bv", "L3_ffn_b1", "L3_ffn_b2", "L0_ffn_Wg",
              "L2_ffn_Wr", "L3_xattn_Wq", "L3_xattn_Wkv", "L3_attn_W_down_kv", "L3_attn_W_up_k", "L3_attn_W_up_v"]:
        o[n] = a[n]
    o["L0_ffn_W1"] = np.ascontiguousarray(a["L0_ffn_W1"].transpose(1, 0, 2))
    o["L0_ffn_W2"] = np.ascontiguousarray(a["L0_ffn_W2"].reshape(8, 2, 128, 128).transpose(2, 0, 1, 3))
    o["L2_ffn_WiT"] = np.ascontiguousarray(a["L2_ffn_Wi"].transpose(2, 0, 1))
    o["L2_ffn_Wo"] = np.ascontiguousarray(a["L2_ffn_Wo"].transpose(1, 0, 2))
    o["L1_ffn_keys"] = cols(a["L1_ffn_keys"].transpose(0, 2, 1))
    o["L1_ffn_values"] = rows(a["L1_ffn_values"])
    o["L3_ffn_w1T"] = T(a["L3_ffn_w1"])
    o["L3_ffn_w2T"] = rows(np.ascontiguousarray(a["L3_ffn_w2"].T).reshape(4, 128, 128))
    o["L1_ffn_sel"] = T(a["L1_ffn_expert_sel"])
    o["L3_attn_W_k_T"], o["L3_attn_W_v_T"] = T(a["L3_attn_W_k"]), T(a["L3_attn_W_v"])
    o["L3_xattn_Wout"] = np.ascontiguousarray(a["L3_xattn_Wout"].reshape(4, 128, 128).transpose(1, 0, 2))
    w, bias = a["L1_attn_qkvu_w"], a["L1_attn_qkvu_b"]
    twice = np.concatenate([np.r_[16 * h:16 * h + 16, 16 * h:16 * h + 16] for h in range(8)])
    order = np.concatenate([twice, 128 + twice])
    o["L1_attn_qk"] = np.ascontiguousarray(w[order].reshape(4, 128, 128).transpose(2, 0, 1))
    o["L1_attn_qk_b"] = np.ascontiguousarray(bias[order].reshape(4, 128).T)
    o["L1_attn_vu"] = np.ascontiguousarray(w[256:].reshape(2, 128, 128).transpose(2, 0, 1))
    o["L1_attn_vb"] = bias[256:384].copy()
    o["L1_attn_ub"] = bias[384:].reshape(128, 1).copy()
    th = a["L1_attn_theta"].reshape(128)[twice]
    o["L1_attn_theta"] = np.ascontiguousarray(th.reshape(2, 128).T)
    o["L1_attn_slope"] = a["L1_attn_slope_rate"].reshape(8)
    o["L2_attn_temp"] = np.repeat(a["L2_attn_temperature"].reshape(16), 8).reshape(128, 1)
    return o


def kernel(**inputs):
    import concourse.bacc as bacc
    from concourse.bass_utils import run_bass_kernel_spmd

    nc = bacc.Bacc("TRN2", target_bir_lowering=False, num_devices=1)
    arrays = layouts(inputs)
    aps = {n: nc.dram_tensor(n, a.shape, mybir.dt.from_np(a.dtype), kind="ExternalInput").ap() for n, a in arrays.items()}
    out = nc.dram_tensor("out", (128, B * D), F32, kind="ExternalOutput").ap()
    build(nc, aps, out)
    got = run_bass_kernel_spmd(nc, [arrays], core_ids=[0]).results[0]["out"]
    return np.ascontiguousarray(got.reshape(128, B, D).transpose(1, 0, 2))
```

```python
import numpy as np
from contextlib import ExitStack

import concourse.bass as bass
import concourse.mybir as mybir

F32 = mybir.dt.float32
BF16 = mybir.dt.bfloat16
I32 = mybir.dt.int32
U32 = mybir.dt.uint32
ALU = mybir.AluOpType
ACT = mybir.ActivationFunctionType
AX = mybir.AxisListType.X

B, S, D = 32, 128, 128
G = 4
NG = B // G
GT = G * S
H, HD = 16, 8
QUADS, PER = 4, 4
LN_EPS = 1e-5
MASKED = -2.0 ** 100
ds = bass.ds


class Count:

    def __init__(self, sem):
        self.sem, self.base, self.per = sem, 0, 0

    def at(self, g, n):
        return self.sem, g * self.per + (self.base + n)


class Program:

    def __init__(self, nc, ctx, inputs):
        self.nc, self.ctx, self.inputs = nc, ctx, inputs
        self.counts = {}

    def count_of(self, name):
        if name not in self.counts:
            self.counts[name] = Count(self.ctx.enter_context(self.nc.semaphore(name)))
        return self.counts[name]

    def plan(self, **per):
        for name, n in per.items():
            self.count_of(name).per = n
        return [self.count_of(name) for name in per]

    def passed(self, passes):
        for s in self.counts.values():
            s.base += s.per * passes
            s.per = 0


def sb(p, ctx, name, shape, dt=F32):
    return ctx.enter_context(p.nc.sbuf_tensor(name, shape, dt))


class Chain:

    def __init__(self, eng, steps, g=0):
        self.eng, self.steps, self.g, self.n = eng, steps, g, 0

    def __call__(self, instruction):
        self.n += 1
        instruction.then_inc(self.steps.sem, 1)
        self.eng.wait_ge(*self.steps.at(self.g, self.n))

    def ends(self):
        assert self.n == self.steps.per, (self.steps.sem, self.n, self.steps.per)



class rotation_tables:
    C1 = 6.28125
    C2 = float(np.round((2 * np.pi - C1) * 2 ** 20) / 2 ** 20)
    C3 = 2 * np.pi - C1 - C2
    ROUND = 1.5 * 2 ** 23

    def __init__(self, p, here):
        self.p = p
        p.table, p.keep = sb(p, p.ctx, "table", [128, 2, S]), sb(p, p.ctx, "keep", [128, 8, S])
        self.pos, self.th, self.turns, self.whole = (sb(p, here, "table_" + k, [128, 2, S]) for k in ("pos", "th", "turns", "whole"))
        self.quarter = sb(p, here, "table_quarter", [128, 1])
        self.made, self.angle = p.count_of("table_steps"), p.count_of("angle_steps")

    def gpsimd(self, pool):
        nc, keep, quarter = self.p.nc, self.p.keep, self.quarter
        then = Chain(pool, self.made)
        then(nc.gpsimd.iota(self.pos[:], pattern=[[0, 2], [1, S]], base=0, channel_multiplier=0,
                            allow_small_or_imprecise_dtypes=True))
        then(nc.gpsimd.memset(quarter[:], 1.0))
        for j in range(4):
            rows = quarter[32 * j:32 * j + 32, :]
            then(nc.gpsimd.affine_select(out=rows, in_=rows, compare_op=ALU.is_ge, fill=0.0, base=15,
                                         pattern=[[0, 1]], channel_multiplier=-1))
        then(nc.gpsimd.memset(keep[:], 1.0))
        then(nc.gpsimd.affine_select(out=keep[:], in_=keep[:], compare_op=ALU.is_ge, fill=0.0, base=0,
                                     pattern=[[0, 8], [1, S]], channel_multiplier=-1))

    def vector(self, dve):
        v, w, th, quarter, turns, whole = self.p.nc.vector, self.p.w, self.th, self.quarter, self.turns, self.whole
        then = Chain(dve, self.angle)
        dve.wait_ge(*self.made.at(0, 8))
        for i in range(2):
            then(v.tensor_scalar(th[:, i, :], self.pos[:, i, :], w["L1_attn_theta"][:, i:i + 1], None, ALU.mult))
        then(v.tensor_scalar(quarter[:], quarter[:], 0.25, None, ALU.mult))
        then(v.tensor_scalar(turns[:], th[:], 1 / (2 * np.pi), quarter[:], ALU.mult, ALU.add))
        then(v.tensor_scalar(whole[:], turns[:], self.ROUND, self.ROUND, ALU.add, ALU.subtract))
        for c in (self.C1, self.C2, self.C3):
            then(v.scalar_tensor_tensor(th[:], whole[:], -c, th[:], ALU.mult, ALU.add))
        then(v.tensor_scalar(quarter[:], quarter[:], 2 * np.pi, None, ALU.mult))
        then(v.tensor_scalar(th[:], th[:], quarter[:], 3.1415925, ALU.add, ALU.min))
        then(v.tensor_scalar(th[:], th[:], -3.1415925, None, ALU.max))
        for h in range(8):
            at = self.p.keep[:, 2 * (h % 4) + h // 4, :]
            then(v.tensor_scalar(at, at, w["L1_attn_slope"][:, h:h + 1], None, ALU.mult))

    def scalar(self, act):
        act.wait_ge(*self.angle.at(0, 19))
        self.p.nc.scalar.activation(self.p.table[:], self.th[:], ACT.Sin)
        self.p.nc.scalar.activation(self.p.keep[:], self.p.keep[:], ACT.Exp)


def load_all(p):
    nc, ctx, ins = p.nc, p.ctx, p.inputs
    p.x = sb(p, ctx, "x_res", [128, B * D])
    p.stats = sb(p, ctx, "row_stats", [128, B, 6])
    p.rstd = sb(p, ctx, "ln_scale", [128, B])
    p.shift = sb(p, ctx, "ln_shift", [128, B])
    p.ident = sb(p, ctx, "ident", [128, 128])
    p.ident_bf = sb(p, ctx, "ident_bf", [128, 128], BF16)
    p.bank = [ctx.enter_context(nc.psum_tensor(f"bank{i}", [128, GT], F32)) for i in range(8)]
    p.w = {}

    def weight(name, shape, src=None):
        p.w[name] = sb(p, ctx, "w_" + name, shape)
        return p.w[name], ins[src or name]

    square = ["L0_attn_WQ", "L0_attn_WK", "L0_attn_WV", "L0_attn_WO", "L0_xattn_w_q", "L0_xattn_w_k",
              "L0_xattn_w_v", "L0_xattn_w_o", "L2_attn_Wq", "L2_attn_Wk", "L2_attn_Wv",
              "L2_xattn_Wq", "L2_xattn_Wk", "L2_xattn_Wv", "L3_attn_W_q", "L3_attn_W_o", "L1_attn_out_w"]
    loads = [weight(n, [128, 128]) for n in square]
    for n in ["L0_xattn_b_q", "L0_xattn_b_k", "L2_attn_bq", "L2_xattn_bq", "L2_xattn_bk",
              "L3_xattn_ln_w", "L3_xattn_ln_b"]:
        t, src = weight(n, [128, 1])
        loads.append((t, src.rearrange("(p a) -> p a", a=1)))
    rows = {"L0_xattn_b_v": 128, "L0_xattn_b_o": 128, "L1_attn_out_b": 128, "L2_attn_bk": 128,
            "L2_attn_bv": 128, "L2_xattn_bv": 128, "L3_ffn_b1": 512, "L3_ffn_b2": 128}
    for n, width in rows.items():
        t, src = weight(n, [128, width])
        loads.append((t, src.rearrange("(a n) -> a n", a=1).to_broadcast([128, width])))
    loads.append(weight("L0_ffn_Wg", [128, 8]))
    loads.append(weight("L2_ffn_Wr", [128, 8]))
    loads.append(weight("L1_ffn_sel", [128, 64]))
    loads.append(weight("L3_xattn_Wq", [128, 512]))
    loads.append(weight("L3_xattn_Wkv", [128, 1024]))
    loads.append(weight("L3_xattn_Wout", [128, 4, 128]))
    loads.append(weight("L1_attn_qk", [128, 4, 128]))
    loads.append(weight("L1_attn_vu", [128, 2, 128]))
    loads.append(weight("L1_attn_qk_b", [128, 4]))
    loads.append(weight("L1_attn_theta", [128, 2]))
    t, src = weight("L1_attn_vb", [128, 128])
    loads.append((t, src.rearrange("(a n) -> a n", a=1).to_broadcast([128, 128])))
    loads.append(weight("L1_attn_ub", [128, 1]))
    t, src = weight("L1_attn_slope", [128, 8])
    loads.append((t, src.rearrange("(a n) -> a n", a=1).to_broadcast([128, 8])))
    loads.append(weight("L2_attn_temp", [128, 1]))
    loads.append(weight("L3_attn_W_k_T", [128, 128]))
    loads.append(weight("L3_attn_W_v_T", [128, 128]))
    loads.append(weight("L3_attn_W_down_kv", [128, 32]))
    loads.append(weight("L3_attn_W_up_k", [32, 128]))
    loads.append(weight("L3_attn_W_up_v", [32, 128]))
    p.w["L3_K"] = sb(p, ctx, "w_L3_K", [128, 128])
    p.w["L3_V"] = sb(p, ctx, "w_L3_V", [128, 128])

    for n, shape in (("L0_ffn_W1", [128, 8, 256]), ("L0_ffn_W2", [128, 8, 2, D]), ("L2_ffn_WiT", [128, 8, 128]),
                     ("L2_ffn_Wo", [128, 8, D]), ("L3_ffn_w1T", [128, 512]), ("L3_ffn_w2T", [128, 512])):
        loads.append(weight(n, shape))

    early = [p.w[n] for n in ("L1_attn_theta", "L1_attn_slope", "L0_attn_WQ", "L0_attn_WK", "L0_attn_WV", "L0_attn_WO")]
    first = sorted((l for l in loads if l[0] in early), key=lambda l: early.index(l[0]))
    p.later = [l for l in loads if l[0] not in early]
    CHUNKS = 4
    x_in = [p.count_of(f"x_in_{i}") for i in range(CHUNKS)]
    w_in, ones_m = p.count_of("first_weights_in"), p.count_of("constant_steps")
    with ExitStack() as here:
        tables = rotation_tables(p, here)
        with nc.Block(no_gpsimd_drain=True) as block:
            @block.sync
            def _(sp):
                for t, src in first[:2]:
                    sp.dma_start(t[:], src).then_inc(w_in.sem, 16)
                for i in range(CHUNKS):
                    part = slice(i * B * D // CHUNKS, (i + 1) * B * D // CHUNKS)
                    sp.dma_start(p.x[:, part], ins["x"][:, part]).then_inc(x_in[i].sem, 16)
                for t, src in first[2:]:
                    sp.dma_start(t[:], src).then_inc(w_in.sem, 16)
                sp.wait_ge(w_in.sem, 16 * len(first))

            @block.gpsimd
            def _(pool):
                then = Chain(pool, ones_m)
                then(nc.gpsimd.memset(p.ident[:], 0.0))
                then(nc.gpsimd.affine_select(out=p.ident[:], in_=p.ident[:], compare_op=ALU.not_equal, fill=1.0, base=0,
                                             pattern=[[-1, 128]], channel_multiplier=1))
                tables.gpsimd(pool)

            @block.scalar
            def _(act):
                tables.scalar(act)

            @block.vector
            def _(dve):
                dve.wait_ge(ones_m.sem, 2)
                nc.vector.tensor_copy(p.ident_bf[:], p.ident[:])
                for b in range(B):
                    if b % (B // CHUNKS) == 0:
                        dve.wait_ge(x_in[b * CHUNKS // B].sem, 16)
                    nc.vector.bn_stats(p.stats[:, b, :], p.x[:, b * D:(b + 1) * D])
                dve.wait_ge(w_in.sem, 16 * len(first))
                tables.vector(dve)


def load_later(p, sp):
    w_in = p.count_of("weights_in")
    for t, src in p.later:
        sp.dma_start(t[:], src).then_inc(w_in.sem, 16)
    sp.wait_ge(w_in.sem, 16 * len(p.later))


class Norm:

    def __init__(self, p, ctx, name, again=None, table=ACT.Exp):
        self.p, self.again, self.table, self.rounds = p, again, table, 2 if again else 1
        self.a, self.b, self.var, self.y, self.h, self.mean, self.root, self.veps = (
            sb(p, ctx, f"{name}_norm_{k}", [128, B]) for k in ("a", "b", "var", "y", "h", "mean", "root", "veps"))
        self.steps, self.var_ready, self.root_ready = (p.count_of(n) for n in ("norm_steps", "norm_variance_ready", "norm_root_ready"))

    def scalar(self, act):
        nc = self.p.nc
        nc.scalar.preload_act_table(ACT.Sqrt)
        for r in range(self.rounds):
            act.wait_ge(*self.var_ready.at(0, r + 1))
            nc.scalar.activation(self.root[:], self.veps[:], ACT.Sqrt).then_inc(self.root_ready.sem, 1)
        nc.scalar.preload_act_table(self.table)

    def vector(self, dve):
        p, v, then = self.p, self.p.nc.vector, Chain(dve, self.steps)
        a, b, var, y, h, mean, root, veps = self.a, self.b, self.var, self.y, self.h, self.mean, self.root, self.veps

        def inverse_root(out, r):
            dve.wait_ge(*self.root_ready.at(0, r + 1))
            then(v.reciprocal(y[:], root[:]))
            then(v.tensor_tensor(h[:], y[:], veps[:], ALU.mult))
            then(v.scalar_tensor_tensor(h[:], h[:], -0.5, y[:], ALU.mult, ALU.mult))
            then(v.scalar_tensor_tensor(out[:], h[:], 1.5, y[:], ALU.add, ALU.mult))

        me, mo, qe, qo = (p.stats[:, :, i] for i in (1, 4, 2, 5))
        v.tensor_tensor(mean[:], me, mo, ALU.add).then_inc(self.steps.sem, 1)
        v.tensor_tensor(a[:], me, mo, ALU.subtract).then_inc(self.steps.sem, 1)
        v.tensor_tensor(b[:], qe, qo, ALU.add).then_inc(self.steps.sem, 1)
        then.n += 3
        dve.wait_ge(*self.steps.at(0, then.n))
        v.tensor_tensor(a[:], a[:], a[:], ALU.mult).then_inc(self.steps.sem, 1)
        v.tensor_scalar(b[:], b[:], 1.0 / D, None, ALU.mult).then_inc(self.steps.sem, 1)
        then.n += 2
        dve.wait_ge(*self.steps.at(0, then.n))
        then(v.scalar_tensor_tensor(var[:], a[:], 0.25, b[:], ALU.mult, ALU.add))
        v.tensor_scalar(veps[:], var[:], LN_EPS, None, ALU.add).then_inc(self.var_ready.sem, 1)
        inverse_root(p.rstd, 0)
        then(v.scalar_tensor_tensor(p.shift[:], mean[:], -0.5, p.rstd[:], ALU.mult, ALU.mult))
        if self.again:
            then(v.tensor_tensor(a[:], p.rstd[:], p.rstd[:], ALU.mult))
            then(v.tensor_tensor(a[:], a[:], var[:], ALU.mult))
            v.tensor_scalar(veps[:], a[:], self.again, None, ALU.add).then_inc(self.var_ready.sem, 1)
            inverse_root(a, 1)
            then(v.tensor_tensor(p.rstd[:], p.rstd[:], a[:], ALU.mult))
            then(v.tensor_tensor(p.shift[:], p.shift[:], a[:], ALU.mult))
        self.done = then.n

    def passed(self):
        self.steps.base += self.done
        self.var_ready.base += self.rounds
        self.root_ready.base += self.rounds


def norm_rows(p, name, again=None, table=ACT.Exp, gpsimd=None, tensor=None, scalar=None, vector=None):
    with ExitStack() as ctx:
        norm = Norm(p, ctx, name, again, table)
        with p.nc.Block(no_gpsimd_drain=True) as block:
            @block.scalar
            def _(act):
                norm.scalar(act)
                if scalar:
                    scalar(act)

            if gpsimd:
                block.gpsimd(gpsimd)
            if tensor:
                block.tensor(tensor)

            @block.vector
            def _(dve):
                norm.vector(dve)
                if vector:
                    vector(dve)
        norm.passed()



def rows_of_x(p, g, b, n=1):
    return p.x[:, ds(g * (G * D) + b * D, n * D)]


def normalise(p, dve, g, xn, xn_ready):
    for b in range(G):
        one = ds(g * G + b, 1)
        p.nc.vector.tensor_scalar(xn[:, b * D:(b + 1) * D], rows_of_x(p, g, b), p.rstd[:, one], p.shift[:, one],
                                  ALU.mult, ALU.add).then_inc(xn_ready.sem, 1)


def transpose_xn(p, pe, g, xn, xn_ready, bank, xnT_psum):
    for b in range(G):
        pe.wait_ge(*xn_ready.at(g, b + 1))
        last = p.nc.tensor.transpose(bank[:, b * S:(b + 1) * S], xn[:, b * D:(b + 1) * D], p.ident[:])
    last.then_inc(xnT_psum.sem, 1)


def row_statistics(p, dve, g, x_done, n=1):
    dve.wait_ge(*x_done.at(g, n))
    for b in range(G):
        p.nc.vector.bn_stats(p.stats[:, ds(g * G + b, 1), :].rearrange("p a s -> p (a s)"), rows_of_x(p, g, b))


def batch(b):
    return slice(b * S, (b + 1) * S)


UNITS = 4 * G


def all_groups(eng, units, n=UNITS):
    units(0, 0, n, True, False)
    with eng.Fori(0, NG // 2 - 1) as i:
        units(i * 2 + 1, 1, n, False, False)
        units(i * 2 + 2, 0, n, False, False)
    units(NG - 1, 1, n, False, True)
    units(NG, 0, 0, False, True)


def run_ahead(eng, body):
    body(0, 0, 3)
    with eng.Fori(0, NG // 2 - 2) as i:
        body(i * 2 + 1, 1, 3)
        body(i * 2 + 2, 0, 3)
    for g in range(NG - 3, NG):
        body(g, g % 2, NG - 1 - g)


def before(g, a, u, lag, n=UNITS):
    return (g, a, u - lag) if u >= lag else (g - 1, 1 - a, u - lag + n)



def attention16(p, name, w_q, w_k, w_v, w_o=None, cross=False, b_q=None, b_k=None, b_v=None, b_o=None,
                scale=1.0, causal=False, where_mask=False, key_mask=False, decay=False):
    nc, ins = p.nc, p.inputs
    U = UNITS
    (xn_ready, xnT_psum, xnT_ready, q_psum, k_psum, v_psum, q_ready, k_ready, kmask_ready, v_ready, s_psum, max_ready,
     p_ready, t_psum, pt_ready, av_psum, r_ready, rT_psum, rT_ready, oT_ready, y_psum, x_done) = p.plan(
        xn_ready=G, xnT_psum=1, xnT_ready=1, q_psum=1, k_psum=1, v_psum=1, q_ready=1, k_ready=1, kmask_ready=U,
        v_ready=1, s_psum=U, max_ready=U, p_ready=U, t_psum=U, pt_ready=U, av_psum=G, r_ready=G,
        rT_psum=1, rT_ready=1, oT_ready=1, y_psum=1, x_done=1)
    ctx_in, mask_in, mask_ready, prep_ready = p.plan(ctx_in=16 * cross, mask_in=16 * (key_mask + 2 * where_mask),
                                                     mask_ready=(key_mask or 2 * where_mask), stage_prepared=0)
    raw_max, decayed, floor_steps, e_in, e_ready, z_psum, z_ready, ze_ready, sum_ready = p.plan(
        raw_max=U * where_mask, decayed=U * decay, floor_steps=4 * where_mask, masked_shift_ready=G * where_mask,
        masked_exp_ready=G * where_mask, masked_v_psum=where_mask, masked_v_ready=where_mask,
        masked_v_scaled=G * where_mask, masked_sum_steps=G * where_mask)
    r_steps, bias_added = p.plan(reciprocal_steps=G, bias_added=bool(b_o))
    w = p.w
    S_BANK, T_BANK, M_BANK, O_BANK = p.bank[0:4], p.bank[4:6], p.bank[6], p.bank[7]
    masked = causal or where_mask or key_mask

    with ExitStack() as ctx:
        t = lambda k, shape, dt=F32: sb(p, ctx, f"{name}_{k}", shape, dt)
        xn, xnT, qT, kT = t("xn", [128, GT]), t("xnT", [128, GT]), t("qT", [128, 2, GT]), t("kT", [128, 2, GT])
        ctxT = t("ctxT", [128, GT]) if cross else xnT
        kmask = t("kmask", [128, 2, QUADS, PER * S])
        vpad = t("vpad", [128, 2, G * H * 32])
        nmax, rsum, rrec = t("nmax", [128, G, H]), t("rsum", [128, G, H]), t("rrec", [128, G, H])
        probs = t("probs", [128, 4, PER * S])
        probsT = t("probsT", [128, 2, QUADS, PER * S])
        rrep, rT, oT = t("rrep", [128, GT]), t("rT", [128, GT]), t("oT", [128, GT])
        scaled_mask = t("scaled_mask", [128, H])
        spare = t("spare", [128, 1])
        if masked:
            score_bias = t("score_bias", [128, 1 if causal else 2, 1 if causal else G, S], BF16)
        if key_mask or where_mask:
            mask_q = t("mask_q", [128, G, S], I32)
        if where_mask:
            mask_k, masked_k = t("mask_k", [128, G * S], I32), t("masked_k", [128, G * S])
            least, nfloor, count = (t(k, [128, 2, G]) for k in ("least", "nfloor", "count"))
            rowmax, eshift, e = (t(k, [128, G, H]) for k in ("rowmax", "eshift", "e"))
            z, ze = t("masked_v", [128, 2, GT]), t("masked_v_scaled", [128, G, D])
        if decay:
            decay_m, distance = t("decay", [128, S]), t("distance", [128, S])
            scored = t("scored", [128, 4, PER * S])

        def head_slots(a, b=None):
            q = vpad[:, a, :] if b is None else vpad[:, a, b * H * 32:(b + 1) * H * 32]
            return bass.AP(q.tensor, q.offset, [list(q.ap[0]), [128, QUADS * (G if b is None else 1)], [40, PER], [1, HD]])

        def prepare(pool):
            then = Chain(pool, prep_ready)
            then(nc.gpsimd.memset(vpad[:], 0.0))
            then(nc.gpsimd.memset(spare[:], 0.0))
            then(nc.gpsimd.memset(scaled_mask[:], scale))
            then(nc.gpsimd.affine_select(out=scaled_mask[:], in_=scaled_mask[:], compare_op=ALU.is_ge, fill=0.0, base=0,
                                         pattern=[[-HD, H]], channel_multiplier=1))
            then(nc.gpsimd.affine_select(out=scaled_mask[:], in_=scaled_mask[:], compare_op=ALU.is_ge, fill=0.0,
                                         base=HD - 1, pattern=[[HD, H]], channel_multiplier=-1))
            if causal:
                then(nc.gpsimd.memset(score_bias[:], 0.0))
                then(nc.gpsimd.affine_select(out=score_bias[:, 0, 0, :], in_=score_bias[:, 0, 0, :], compare_op=ALU.is_ge,
                                             fill=MASKED, base=0, pattern=[[-1, S]], channel_multiplier=1))
            if decay:
                then(nc.gpsimd.iota(distance[:], pattern=[[1, S]], base=0, channel_multiplier=-1,
                                    allow_small_or_imprecise_dtypes=True))

        def prepare_decay(act):
            act.wait_ge(*prep_ready.at(0, 6))
            nc.scalar.activation(decay_m[:], distance[:], ACT.Abs).then_inc(prep_ready.sem, 1)
            act.wait_ge(*prep_ready.at(0, 7))
            nc.scalar.activation(decay_m[:], decay_m[:], ACT.Exp, scale=-0.01).then_inc(prep_ready.sem, 1)

        norm = Norm(p, ctx, name)
        prepared = 5 + 2 * causal + 3 * decay

        FIRST_STEPS = (2, 3, 0, 1, 4) if cross else (0, 1, 2, 3, 4)
        front_banks = lambda first: (M_BANK, S_BANK[0], S_BANK[1]) if first else (M_BANK, M_BANK, M_BANK)
        LAG = 3
        AFTER = LAG + 4

        with nc.Block(no_gpsimd_drain=True) as block:
            if p.later:
                @block.sync
                def _(sp):
                    load_later(p, sp)
                    p.later = []
            if cross:
                @block.sync
                def _(sp):
                    def load(g):
                        sp.dma_start(ctxT[:], ins["ctx_T"][:, ds(g * GT, GT)]).then_inc(ctx_in.sem, 16)
                        if key_mask:
                            sp.dma_start(mask_q[:], ins["key_mask"].rearrange("(a b) k -> a b k", a=1)[:, ds(g * G, G), :]
                                         .to_broadcast([128, G, S])).then_inc(mask_in.sem, 16)
                        if where_mask:
                            sp.dma_start(mask_q[:].rearrange("p b k -> p (b k)"), ins["mask_qk"][:, ds(g * GT, GT)]).then_inc(mask_in.sem, 16)
                            sp.dma_start(mask_k[:], ins["mask_kq"][:, ds(g * GT, GT)]).then_inc(mask_in.sem, 16)
                    load(0)
                    with sp.Fori(1, NG) as g:
                        sp.wait_ge(*s_psum.at(g - 1, 1))
                        load(g)

            @block.gpsimd
            def _(pool):
                def masks(g, a):
                    if key_mask or where_mask:
                        pool.wait_ge(*mask_in.at(g, mask_in.per))
                        nc.gpsimd.tensor_tensor(spare[:], spare[:], spare[:], ALU.mult)
                        nc.gpsimd.tensor_scalar(score_bias[:, a].rearrange("p b k -> p (b k)"), mask_q[:].rearrange("p b k -> p (b k)"),
                                                0.0, -1e10 if key_mask else MASKED,
                                                ALU.is_equal, ALU.mult).then_inc(mask_ready.sem, 1)
                    if where_mask:
                        nc.gpsimd.tensor_scalar(masked_k[:], mask_k[:], 0.0, None, ALU.is_equal).then_inc(mask_ready.sem, 1)

                def units(g, a, steps, first, last):
                    if first:
                        masks(g, a)
                    for u in range(steps):
                        b, j = u // 4, u % 4
                        if u == 0:
                            pool.wait_ge(*k_ready.at(g, 1))
                        if not (first and u < 8):
                            pool.wait_ge(*s_psum.at(g, u - 7))
                        if u == 11 and not last:
                            masks(g + 1, 1 - a)
                        nc.gpsimd.tensor_tensor(kmask[:, b % 2, j].rearrange("p (c k) -> p c k", c=PER),
                                                kT[:, a, batch(b)].unsqueeze(1).to_broadcast([128, PER, S]),
                                                scaled_mask[:, PER * j:PER * j + PER].unsqueeze(2).to_broadcast([128, PER, S]),
                                                ALU.mult).then_inc(kmask_ready.sem, 1)
                prepare(pool)
                all_groups(pool, units)

            @block.tensor
            def _(pe):
                mm = nc.tensor.matmul

                def scores(g, a, u, first):
                    b, j = u // 4, u % 4
                    pe.wait_ge(*kmask_ready.at(g, u + 1))
                    if first and u == 1:
                        pe.wait_ge(*v_ready.at(g, 1))
                    if u == 0:
                        pe.wait_ge(*q_ready.at(g, 1))
                        if where_mask or key_mask:
                            pe.wait_ge(*mask_ready.at(g, 1))
                    if not (first and u < 4):
                        pe.wait_ge(*(decayed if decay else p_ready).at(g, u - 3))
                    if masked:
                        bias = score_bias[:, 0, 0, :] if causal else score_bias[:, a, b, :]
                        mm(S_BANK[j][:], lhsT=p.ident_bf[:], rhs=bias.unsqueeze(1).to_broadcast([128, PER, S]),
                           start=True, stop=False)
                    mm(S_BANK[j][:], lhsT=qT[:, a, batch(b)], rhs=kmask[:, b % 2, j],
                       start=not masked, stop=True).then_inc(s_psum.sem, 1)

                def transposes(g, a, u, first):
                    pe.wait_ge(*p_ready.at(g, u + 1))
                    if not (first and u < 2):
                        pe.wait_ge(*pt_ready.at(g, u - 1))
                    for c in range(PER):
                        last = nc.tensor.transpose(T_BANK[u % 2][:, batch(c)], probs[:, u % 4, batch(c)], p.ident[:])
                    last.then_inc(t_psum.sem, 1)

                def values(g, a, b, first):
                    pe.wait_ge(*pt_ready.at(g, 4 * b + 4))
                    if b == 0:
                        pe.wait_ge(*v_ready.at(g, 1))
                        if not first:
                            pe.wait_ge(*oT_ready.at(g, 0))
                    if where_mask:
                        pe.wait_ge(*ze_ready.at(g, b + 1))
                        mm(O_BANK[:, batch(b)], lhsT=ze[:, b, :], rhs=p.ident[:], start=True, stop=False,
                           skip_group_check=True)
                    for c in range(PER):
                        for j in range(QUADS):
                            s = (b * H + j * PER + c) * 32
                            last = mm(O_BANK[32 * j:32 * j + 32, batch(b)], lhsT=vpad[:, a, s:s + 32],
                                      rhs=probsT[:, b % 2, j, batch(c)], start=(c == 0 and not where_mask),
                                      stop=(c == PER - 1), tile_position=(0, 32 * j), skip_group_check=True)
                    last.then_inc(av_psum.sem, 1)

                def front(g, a, step, first=False):
                    q_bank, k_bank, v_bank = front_banks(first)
                    if step == 0:
                        transpose_xn(p, pe, g, xn, xn_ready, M_BANK, xnT_psum)
                    if step == 1:
                        pe.wait_ge(*xnT_ready.at(g, 1))
                        mm(q_bank[:], lhsT=w[w_q][:], rhs=xnT[:], start=True, stop=True).then_inc(q_psum.sem, 1)
                    if step == 2:
                        if cross:
                            pe.wait_ge(*ctx_in.at(g, 16))
                        if not first:
                            pe.wait_ge(*q_ready.at(g, 1))
                        mm(k_bank[:], lhsT=w[w_k][:], rhs=ctxT[:], start=True, stop=True).then_inc(k_psum.sem, 1)
                    if step == 3:
                        if not first:
                            pe.wait_ge(*k_ready.at(g, 1))
                        for b in range(G):
                            last = mm(v_bank[:, batch(b)], lhsT=ctxT[:, batch(b)], rhs=w[w_v][:], start=True, stop=True)
                        last.then_inc(v_psum.sem, 1)
                    if step == 4 and where_mask:
                        pe.wait_ge(*mask_ready.at(g, 2))
                        pe.wait_ge(*v_ready.at(g, 1))
                        pe.wait_ge(*q_ready.at(g, 1))
                        for b in range(G):
                            last = mm(M_BANK[:, batch(b)], lhsT=masked_k[:, batch(b)], rhs=head_slots(a, b),
                                      start=True, stop=True)
                        last.then_inc(z_psum.sem, 1)

                def divisors(g):
                    pe.wait_ge(*r_ready.at(g, G))
                    for b in range(G):
                        last = nc.tensor.transpose(M_BANK[:, batch(b)], rrep[:, batch(b)], p.ident[:])
                    last.then_inc(rT_psum.sem, 1)

                def outputs(g):
                    pe.wait_ge(*oT_ready.at(g, 1))
                    for b in range(G):
                        if w_o:
                            last = mm(M_BANK[:, batch(b)], lhsT=oT[:, batch(b)], rhs=w[w_o][:], start=True, stop=True)
                        else:
                            last = nc.tensor.transpose(M_BANK[:, batch(b)], oT[:, batch(b)], p.ident[:])
                    last.then_inc(y_psum.sem, 1)

                def units(g, a, steps, first, last):
                    if first:
                        for step in FIRST_STEPS:
                            front(g, a, step, True)
                    for u in range(steps or AFTER):
                        if steps:
                            scores(g, a, u, first)
                        if (steps or u < LAG) and not (first and u < LAG):
                            h, ha, hu = before(g, a, u, LAG)
                            transposes(h, ha, hu, first)
                        if u % 4 == LAG and not (first and u < LAG + 4) and (steps or u == LAG):
                            h, ha, hu = before(g, a, u, LAG + 4)
                            values(h, ha, hu // 4, first)
                        if u == LAG and not first:
                            if steps:
                                pe.wait_ge(*(z_ready if where_mask else v_ready).at(g, 1))
                            divisors(g - 1)
                        if u == LAG + 2 and not first:
                            outputs(g - 1)
                        if not last:
                            if u == LAG + 4 and not first:
                                pe.wait_ge(*x_done.at(g - 1, 1))
                            if u == LAG + 4 and first:
                                pe.wait_ge(*(z_ready if where_mask else v_ready).at(g, 1))
                            for step, at in enumerate((4, 6, 8, 10, 12)):
                                if u == LAG + at:
                                    front(g + 1, 1 - a, step)
                all_groups(pe, units)

            @block.scalar
            def _(act):
                def units(g, a, steps, first, last):
                    def start(g, a):
                        act.wait_ge(*xnT_psum.at(g, 1))
                        nc.scalar.activation(xnT[:], M_BANK[:], ACT.Copy).then_inc(xnT_ready.sem, 1)

                    def masked_values(g, a):
                        act.wait_ge(*z_psum.at(g, 1))
                        nc.scalar.activation(z[:, a, :], M_BANK[:], ACT.Copy).then_inc(z_ready.sem, 1)

                    if first:
                        start(g, a)
                        if where_mask:
                            masked_values(g, a)
                    for u in range(steps or AFTER):
                        if steps:
                            b, j = u // 4, u % 4
                            act.wait_ge(*max_ready.at(g, u + 1))
                            if not (first and u < 4):
                                act.wait_ge(*t_psum.at(g, u - 3))
                            src = scored[:, u % 4, :] if decay else S_BANK[j][:]
                            for c in range(PER):
                                h = 4 * j + c
                                done = nc.scalar.activation(probs[:, u % 4, batch(c)], src[:, batch(c)], ACT.Exp,
                                                            bias=nmax[:, b, h:h + 1], accum_out=rsum[:, b, h:h + 1])
                            done.then_inc(p_ready.sem, 1)
                            if where_mask and j == 3:
                                act.wait_ge(*e_in.at(g, b + 1))
                                nc.scalar.activation(e[:, b, :], eshift[:, b, :], ACT.Exp).then_inc(e_ready.sem, 1)
                        if u == LAG and not first:
                            act.wait_ge(*rT_psum.at(g - 1, 1))
                            nc.scalar.activation(rT[:], M_BANK[:], ACT.Copy).then_inc(rT_ready.sem, 1)
                        if u == LAG + 4 and not last:
                            start(g + 1, 1 - a)
                        if u == LAG + 12 and not last and where_mask:
                            masked_values(g + 1, 1 - a)
                norm.scalar(act)
                if decay:
                    prepare_decay(act)
                all_groups(act, units)

            @block.vector
            def _(dve):
                v = nc.vector

                def row_max(g, a, u, first):
                    b, j = u // 4, u % 4
                    dve.wait_ge(*s_psum.at(g, u + 1))
                    heads = slice(4 * j, 4 * j + 4)
                    src = S_BANK[j][:].rearrange("p (c k) -> p c k", c=PER)
                    if decay:
                        if not (first and u < 4):
                            dve.wait_ge(*p_ready.at(g, u - 3))
                        out = scored[:, u % 4, :].rearrange("p (c k) -> p c k", c=PER)
                        v.tensor_tensor(out, src, decay_m[:].unsqueeze(1).to_broadcast([128, PER, S]),
                                        ALU.mult).then_inc(decayed.sem, 1)
                        dve.wait_ge(*decayed.at(g, u + 1))
                        src = out
                    if where_mask:
                        v.tensor_reduce(rowmax[:, b, heads], src, axis=AX, op=ALU.max, negate=True).then_inc(raw_max.sem, 1)
                        dve.wait_ge(*raw_max.at(g, u + 1))
                        v.tensor_scalar(nmax[:, b, heads], rowmax[:, b, heads], nfloor[:, a, b:b + 1], None,
                                        ALU.min).then_inc(max_ready.sem, 1)
                        if j == 3:
                            dve.wait_ge(*max_ready.at(g, u + 1))
                            v.tensor_scalar(eshift[:, b, :], nmax[:, b, :], 1e4, -1e4, ALU.min, ALU.add).then_inc(e_in.sem, 1)
                    else:
                        v.tensor_reduce(nmax[:, b, heads], src, axis=AX, op=ALU.max, negate=True).then_inc(max_ready.sem, 1)

                def copy_out(g, a, u, first):
                    b, j = u // 4, u % 4
                    dve.wait_ge(*t_psum.at(g, u + 1))
                    if j == 0 and not (first and b < 2):
                        dve.wait_ge(*av_psum.at(g, b - 1))
                    v.tensor_copy(probsT[:, b % 2, j, :], T_BANK[u % 2][:]).then_inc(pt_ready.sem, 1)

                def reciprocals(g, b):
                    dve.wait_ge(*p_ready.at(g, 4 * b + 4))
                    if where_mask:
                        dve.wait_ge(*sum_ready.at(g, b + 1))
                    v.reciprocal(rrec[:, b, :], rsum[:, b, :]).then_inc(r_steps.sem, 1)
                    dve.wait_ge(*r_steps.at(g, b + 1))
                    v.tensor_copy(rrep[:, batch(b)].rearrange("p (h d) -> p h d", h=H),
                                  rrec[:, b, :].unsqueeze(2).to_broadcast([128, H, HD])).then_inc(r_ready.sem, 1)

                def masked_terms(g, a, b):
                    dve.wait_ge(*e_ready.at(g, b + 1))
                    if b == 0:
                        dve.wait_ge(*z_ready.at(g, 1))
                    v.tensor_tensor(ze[:, b, :].rearrange("p (h d) -> p h d", h=H),
                                    z[:, a, batch(b)].rearrange("p (h d) -> p h d", h=H),
                                    e[:, b, :].unsqueeze(2).to_broadcast([128, H, HD]), ALU.mult).then_inc(ze_ready.sem, 1)
                    v.scalar_tensor_tensor(rsum[:, b, :], e[:, b, :], count[:, a, b:b + 1], rsum[:, b, :],
                                           ALU.mult, ALU.add).then_inc(sum_ready.sem, 1)

                def floors(g, a):
                    dve.wait_ge(*mask_ready.at(g, 1))
                    v.tensor_reduce(least[:, a], score_bias[:, a], axis=AX, op=ALU.add).then_inc(floor_steps.sem, 1)
                    dve.wait_ge(*floor_steps.at(g, 1))
                    v.tensor_scalar(count[:, a], least[:, a], 1.0 / MASKED, None, ALU.mult).then_inc(floor_steps.sem, 1)
                    v.tensor_scalar(nfloor[:, a], least[:, a], 0.0, -3e38, ALU.is_lt, ALU.mult).then_inc(floor_steps.sem, 1)
                    dve.wait_ge(*floor_steps.at(g, 3))
                    v.tensor_scalar(nfloor[:, a], nfloor[:, a], 3e38, 1e4, ALU.add, ALU.max).then_inc(floor_steps.sem, 1)
                    dve.wait_ge(*floor_steps.at(g, 4))

                def projected(out, bank, bias, psum, ready, g):
                    dve.wait_ge(*psum.at(g, 1))
                    if bias:
                        v.tensor_scalar(out, bank[:], w[bias][:, 0:1], None, ALU.add).then_inc(ready.sem, 1)
                    else:
                        v.tensor_copy(out, bank[:]).then_inc(ready.sem, 1)

                def front(g, a, step, first=False):
                    q_bank, k_bank, v_bank = front_banks(first)
                    if step == 0:
                        normalise(p, dve, g, xn, xn_ready)
                    if step == 1 and where_mask:
                        floors(g, a)
                    if step == 2:
                        projected(qT[:, a, :], q_bank, b_q, q_psum, q_ready, g)
                    if step == 3:
                        projected(kT[:, a, :], k_bank, b_k, k_psum, k_ready, g)
                    if step == 4:
                        dve.wait_ge(*v_psum.at(g, 1))
                        if b_v:
                            for b in range(G):
                                last = v.tensor_tensor(head_slots(a, b), v_bank[:, batch(b)].rearrange("p (j c d) -> p j c d", j=QUADS, c=PER),
                                                       w[b_v][:].rearrange("p (j c d) -> p j c d", j=QUADS, c=PER), ALU.add)
                        else:
                            last = v.tensor_copy(head_slots(a), v_bank[:].rearrange("p (j c d) -> p j c d", j=QUADS * G, c=PER))
                        last.then_inc(v_ready.sem, 1)

                def divided(g):
                    dve.wait_ge(*rT_ready.at(g, 1))
                    dve.wait_ge(*av_psum.at(g, G))
                    v.tensor_tensor(oT[:], O_BANK[:], rT[:], ALU.mult).then_inc(oT_ready.sem, 1)

                def output_bias(g):
                    for b in range(G):
                        last = v.tensor_tensor(rows_of_x(p, g, b), rows_of_x(p, g, b), w[b_o][:], ALU.add)
                    last.then_inc(bias_added.sem, 1)

                def add_output(g):
                    if b_o:
                        dve.wait_ge(*bias_added.at(g, 1))
                    dve.wait_ge(*y_psum.at(g, 1))
                    v.tensor_tensor(rows_of_x(p, g, 0, G), rows_of_x(p, g, 0, G), M_BANK[:], ALU.add).then_inc(x_done.sem, 1)

                def units(g, a, steps, first, last):
                    if first:
                        dve.wait_ge(*prep_ready.at(0, prepared))
                        for step in (0, 3, 4, 2, 1) if cross else (0, 1, 2, 3, 4):
                            front(g, a, step, True)
                    for u in range(steps or AFTER + 1):
                        if steps:
                            row_max(g, a, u, first)
                        if u % 4 == LAG - 1 and not (first and u < LAG + 3) and (steps or u == LAG - 1):
                            h, ha, hu = before(g, a, u, LAG + 3)
                            if where_mask:
                                masked_terms(h, ha, hu // 4)
                        if not (first and u < LAG) and (steps or u < LAG):
                            copy_out(*before(g, a, u, LAG), first)
                        if u % 4 == LAG - 1 and not (first and u < LAG + 3) and (steps or u == LAG - 1):
                            reciprocals(h, hu // 4)
                        if not first:
                            if u == LAG and b_o:
                                output_bias(g - 1)
                            if u == LAG + 1:
                                divided(g - 1)
                            if u == LAG + 3:
                                add_output(g - 1)
                            if u == LAG + 4:
                                row_statistics(p, dve, g - 1, x_done)
                        if not last:
                            for step, at in enumerate((2, 6, 7, 9, 11)):
                                if u == LAG + at:
                                    front(g + 1, 1 - a, step)
                norm.vector(dve)
                all_groups(dve, units)
        p.passed(NG)
        norm.passed()
        prep_ready.base += prepared


def front(p, name, ctx):
    return sb(p, ctx, f"{name}_xn", [128, GT]), sb(p, ctx, f"{name}_xnT", [128, GT])


class Router:

    def __init__(self, p, ctx, name, experts, kept, sigmoid=False, renormalise=False):
        t = lambda k, shape, dt=F32: sb(p, ctx, f"{name}_{k}", shape, dt)
        self.p, self.experts, self.kept, self.sigmoid, self.renormalise = p, experts, kept, sigmoid, renormalise
        self.logits, self.scores = t("logits", [128, G, experts]), t("scores", [128, G, experts])
        self.spare = t("spare", [128, 1])
        self.most, self.total = t("most", [128, G]), t("total", [128, G])
        self.top, self.where, self.where_f = t("top", [128, G, 8]), t("where", [128, G, 8], U32), t("where_f", [128, G, 8])
        self.number, self.part = t("number", [128, experts]), t("part", [128, G, experts])
        self.steps, self.logits_psum, self.logits_ready, self.scores_ready = p.plan(
            route_steps=(0 if sigmoid else 4) + G + G + 1 + (4 if renormalise else 0) + 2 * kept + kept - 2,
            logits_psum=1, logits_ready=1, scores_ready=1)

    def prepare(self, pool, prep_ready):
        return self.p.nc.gpsimd.iota(self.number[:], pattern=[[1, self.experts]], base=0, channel_multiplier=0,
                                     allow_small_or_imprecise_dtypes=True)

    def tensor(self, pe, g, xnT, w, bank):
        for b in range(G):
            last = self.p.nc.tensor.matmul(bank[:, b * self.experts:(b + 1) * self.experts], lhsT=xnT[:, batch(b)],
                                           rhs=w[:], start=True, stop=True)
        last.then_inc(self.logits_psum.sem, 1)

    def wide(self, x, m):
        return x.unsqueeze(2).to_broadcast([128, G, m])

    def scalar(self, act, g):
        act.wait_ge(*self.logits_ready.at(g, 1))
        self.p.nc.scalar.activation(self.scores[:], self.logits[:], ACT.Sigmoid if self.sigmoid else ACT.Exp)\
            .then_inc(self.scores_ready.sem, 1)

    def vector(self, dve, g, bank, gates, gates_ready):
        self.finish(dve, g, self.begin(dve, g, bank), gates, gates_ready)

    def begin(self, dve, g, bank):
        v, n = self.p.nc.vector, self.experts
        then = Chain(dve, self.steps, g)
        dve.wait_ge(*self.logits_psum.at(g, 1))
        src = bank[:, 0:G * n].rearrange("p (b e) -> p b e", b=G)
        if self.sigmoid:
            v.tensor_copy(self.logits[:], src).then_inc(self.logits_ready.sem, 1)
        else:
            then(v.tensor_reduce(self.most[:], src, axis=AX, op=ALU.max))
            v.tensor_tensor(self.logits[:], src, self.wide(self.most[:], n), ALU.subtract).then_inc(self.logits_ready.sem, 1)
        return then

    def chain(self, dve, g):
        then = Chain(dve, self.steps, g)
        then.n = 0 if self.sigmoid else 1
        return then

    def finish(self, dve, g, then, gates, gates_ready):
        v, n, k, wide = self.p.nc.vector, self.experts, self.kept, self.wide
        dve.wait_ge(*self.scores_ready.at(g, 1))
        if not self.sigmoid:
            then(v.tensor_reduce(self.total[:], self.scores[:], axis=AX, op=ALU.add))
            then(v.reciprocal(self.most[:], self.total[:]))
            then(v.tensor_tensor(self.scores[:], self.scores[:], wide(self.most[:], n), ALU.mult))
        v.memset(self.spare[:], 0.0)
        for b in range(G):
            v.max(self.top[:, b, :], self.scores[:, b, :]).then_inc(self.steps.sem, 1)
        then.n += G
        dve.wait_ge(*self.steps.at(g, then.n))
        v.memset(self.spare[:], 0.0)
        for b in range(G):
            v.max_index(self.where[:, b, :], self.top[:, b, :], self.scores[:, b, :]).then_inc(self.steps.sem, 1)
        then.n += G
        dve.wait_ge(*self.steps.at(g, then.n))
        then(v.tensor_copy(self.where_f[:], self.where[:]))
        if self.renormalise:
            then(v.tensor_reduce(self.total[:], self.top[:, :, 0:k], axis=AX, op=ALU.add))
            then(v.tensor_scalar(self.total[:], self.total[:], 1e-8, None, ALU.add))
            then(v.reciprocal(self.most[:], self.total[:]))
            then(v.tensor_tensor(self.top[:, :, 0:k], self.top[:, :, 0:k], wide(self.most[:], k), ALU.mult))
        number = self.number[:].unsqueeze(1).to_broadcast([128, G, n])
        for i in range(k):
            out = gates if i == 0 else self.part[:]
            then(v.tensor_tensor(out, number, wide(self.where_f[:, :, i], n), ALU.is_equal))
            if i == 0:
                then(v.tensor_tensor(gates, gates, wide(self.top[:, :, 0], n), ALU.mult))
            else:
                then(v.tensor_tensor(self.part[:], self.part[:], wide(self.top[:, :, i], n), ALU.mult))
                last = v.tensor_tensor(gates, gates, self.part[:], ALU.add)
                if i < k - 1:
                    then(last)
        last.then_inc(gates_ready.sem, 1)
        then.ends()


def ffn_squared_relu(p, name):
    nc, ins, w = p.nc, p.inputs, p.w
    E, HALVES = 8, 2
    (xn_ready, xnT_psum, xnT_ready, h_psum, relu_ready, h_ready, y_psum, added, gates_ready) = p.plan(
        xn_ready=G, xnT_psum=1, xnT_ready=1, h_psum=E * HALVES, relu_ready=E * HALVES, h_ready=E * HALVES,
        y_psum=E, expert_added=E, gates_ready=1)
    prep, = p.plan(stage_prepared=0)
    H_BANK, Y_BANK, L_BANK, M_BANK = p.bank[0:4], p.bank[4:6], p.bank[7], p.bank[6]
    with ExitStack() as ctx:
        t = lambda k, shape, dt=F32: sb(p, ctx, f"{name}_{k}", shape, dt)
        xn, xnT = t("xn", [128, GT]), t("xnT", [128, 2, GT])
        w1, w2 = w["L0_ffn_W1"], w["L0_ffn_W2"]
        relu, h = t("relu", [128, 4, GT]), t("h", [128, 8, GT])
        gates = t("gates", [128, 2, G, E])
        router = Router(p, ctx, name, E, 2, renormalise=True)
        norm_rows(p, name, gpsimd=lambda pool: Chain(pool, prep)(router.prepare(pool, prep)))
        prep.base += 1

        with nc.Block(no_gpsimd_drain=True) as block:
            @block.tensor
            def _(pe):
                mm = nc.tensor.matmul

                def up(g, a, e, half, first):
                    n = 2 * e + half
                    if n == 0:
                        pe.wait_ge(*xnT_ready.at(g, 1))
                    if not (first and n < 4):
                        pe.wait_ge(*relu_ready.at(g, n - 3))
                    mm(H_BANK[n % 4][:], lhsT=w1[:, e, 128 * half:128 * half + 128], rhs=xnT[:, a, :], start=True, stop=True)\
                        .then_inc(h_psum.sem, 1)

                def down(g, e, first):
                    pe.wait_ge(*h_ready.at(g, 2 * e + 2))
                    if not (first and e < 2):
                        pe.wait_ge(*added.at(g, e - 1))
                    for b in range(G):
                        for half in range(HALVES):
                            last = mm(Y_BANK[e % 2][:, batch(b)], lhsT=h[:, (2 * e + half) % 8, batch(b)], rhs=w2[:, e, half, :],
                                      start=(half == 0), stop=(half == 1))
                    last.then_inc(y_psum.sem, 1)

                def units(g, a, steps, first, last):
                    if first:
                        transpose_xn(p, pe, g, xn, xn_ready, M_BANK, xnT_psum)
                        pe.wait_ge(*xnT_ready.at(g, 1))
                        router.tensor(pe, g, xnT[:, a, :], w["L0_ffn_Wg"], L_BANK)
                    for e in range(steps or 2):
                        if steps:
                            up(g, a, e, 0, first)
                            up(g, a, e, 1, first)
                        if not (first and e < 2):
                            h_, _, he = before(g, a, e, 2, E)
                            down(h_, he, first)
                        if e == 1 and not last:
                            transpose_xn(p, pe, g + 1, xn, xn_ready, M_BANK, xnT_psum)
                        if e == 2 and not last:
                            pe.wait_ge(*xnT_ready.at(g + 1, 1))
                            router.tensor(pe, g + 1, xnT[:, 1 - a, :], w["L0_ffn_Wg"], L_BANK)
                all_groups(pe, units, E)

            @block.scalar
            def _(act):
                def copy(g, a):
                    act.wait_ge(*xnT_psum.at(g, 1))
                    nc.scalar.activation(xnT[:, a, :], M_BANK[:], ACT.Copy).then_inc(xnT_ready.sem, 1)

                def units(g, a, steps, first, last):
                    if first:
                        copy(g, a)
                        router.scalar(act, g)
                    for n in range(2 * steps):
                        act.wait_ge(*h_psum.at(g, n + 1))
                        if not (first and n < 4):
                            act.wait_ge(*h_ready.at(g, n - 3))
                        nc.scalar.activation(relu[:, n % 4, :], H_BANK[n % 4][:], ACT.Relu).then_inc(relu_ready.sem, 1)
                        if n == 3 and not last:
                            copy(g + 1, 1 - a)
                        if n == 7 and not last:
                            router.scalar(act, g + 1)
                all_groups(act, units, E)

            @block.vector
            def _(dve):
                v = nc.vector

                def add_expert(g, a, e):
                    dve.wait_ge(*y_psum.at(g, e + 1))
                    if e:
                        dve.wait_ge(*added.at(g, e))
                    else:
                        dve.wait_ge(*gates_ready.at(g, 1))
                    for b in range(G):
                        last = v.scalar_tensor_tensor(rows_of_x(p, g, b), Y_BANK[e % 2][:, batch(b)], gates[:, a, b, e:e + 1],
                                                      rows_of_x(p, g, b), ALU.mult, ALU.add)
                    last.then_inc(added.sem, 1)
                    if e == E - 1:
                        row_statistics(p, dve, g, added, E)

                def units(g, a, steps, first, last):
                    if first:
                        normalise(p, dve, g, xn, xn_ready)
                        router.vector(dve, g, L_BANK, gates[:, a], gates_ready)
                    for e in range(steps or 2):
                        if e == 0 and not last:
                            normalise(p, dve, g + 1, xn, xn_ready)
                        for n in (2 * e, 2 * e + 1) if steps else ():
                            dve.wait_ge(*relu_ready.at(g, n + 1))
                            if not (first and n < 8) and n % 2 == 0:
                                dve.wait_ge(*y_psum.at(g, e - 3))
                            v.tensor_tensor(h[:, n % 8, :], relu[:, n % 4, :], relu[:, n % 4, :], ALU.mult).then_inc(h_ready.sem, 1)
                        if not (first and e < 2):
                            add_expert(*before(g, a, e, 2, E))
                        if e == 3 and not last:
                            chain = router.begin(dve, g + 1, L_BANK)
                        if e == 4 and not last:
                            router.finish(dve, g + 1, chain, gates[:, 1 - a], gates_ready)
                all_groups(dve, units, E)
        p.passed(NG)


def ffn_linear_experts(p, name):
    nc, ins, w = p.nc, p.inputs, p.w
    E = 8
    xn_ready, xnT_psum, xnT_ready, y_psum, added, gates_ready = p.plan(
        xn_ready=G, xnT_psum=1, xnT_ready=1, y_psum=2 * G, expert_added=2 * G * 4, gates_ready=1)
    prep, product = p.plan(stage_prepared=0, product_psum=0)
    Y_BANK, L_BANK, M_BANK = p.bank[0:4], p.bank[7], p.bank[6]
    ORDER = [(0, 0), (1, 0), (0, 1), (1, 1), (2, 0), (3, 0), (2, 1), (3, 1)]
    with ExitStack() as ctx:
        t = lambda k, shape, dt=F32: sb(p, ctx, f"{name}_{k}", shape, dt)
        xn, xnT = t("xn", [128, GT]), t("xnT", [128, 2, GT])
        wi, wo, wio = w["L2_ffn_WiT"], w["L2_ffn_Wo"], t("wio", [128, E, D])
        gates = t("gates", [128, G, E])
        router = Router(p, ctx, name, E, 2)
        def products(pe):
            for e in range(E):
                last = nc.tensor.matmul(p.bank[e // 4][:, batch(e % 4)], lhsT=wi[:, e, :], rhs=wo[:, e, :], start=True, stop=True)
            last.then_inc(product.sem, 1)

        def copy_products(act):
            act.wait_ge(*product.at(0, 1))
            for i in range(2):
                nc.scalar.activation(wio[:, 4 * i:4 * i + 4, :].rearrange("p e d -> p (e d)"), p.bank[i][:], ACT.Copy)

        norm_rows(p, name, gpsimd=lambda pool: Chain(pool, prep)(router.prepare(pool, prep)), tensor=products,
                  scalar=copy_products)
        prep.base += 1
        product.base += 1

        with nc.Block(no_gpsimd_drain=True) as block:
            @block.tensor
            def _(pe):
                def front(g, a, first):
                    transpose_xn(p, pe, g, xn, xn_ready, M_BANK, xnT_psum)
                    pe.wait_ge(*xnT_ready.at(g, 1))
                    router.tensor(pe, g, xnT[:, a, :], w["L2_ffn_Wr"], L_BANK)

                def units(g, a, steps, first, last):
                    if first:
                        front(g, a, True)
                    for n in range(2 * G if steps else 0):
                        b, i = ORDER[n]
                        if not (first and n < 4):
                            pe.wait_ge(*added.at(g, 8 * ((n - 4) // 2) + 8))
                        nc.tensor.matmul(Y_BANK[(2 * b + i) % 4][:], lhsT=xnT[:, a, batch(b)],
                                         rhs=wio[:, 4 * i:4 * i + 4, :].rearrange("p e d -> p (e d)"),
                                         start=True, stop=True).then_inc(y_psum.sem, 1)
                    if steps and not last:
                        front(g + 1, 1 - a, False)
                all_groups(pe, units, 1)

            @block.scalar
            def _(act):
                def units(g, a, steps, first, last):
                    def front(g, a):
                        act.wait_ge(*xnT_psum.at(g, 1))
                        nc.scalar.activation(xnT[:, a, :], M_BANK[:], ACT.Copy).then_inc(xnT_ready.sem, 1)
                        router.scalar(act, g)
                    if first:
                        front(g, a)
                    if not last:
                        front(g + 1, 1 - a)
                all_groups(act, units, 1)

            @block.vector
            def _(dve):
                v = nc.vector

                def add_experts(g, n0):
                    n = 8 * n0 // 2
                    for i in range(2):
                        for e in range(4):
                            for b in (n0 // 2, n0 // 2 + 1):
                                y = 2 * b + i
                                if e == 0:
                                    dve.wait_ge(*y_psum.at(g, ORDER.index((b, i)) + 1))
                                if n % 16 >= 2:
                                    dve.wait_ge(*added.at(g, n - 1))
                                v.scalar_tensor_tensor(rows_of_x(p, g, b), Y_BANK[y % 4][:, batch(e)],
                                                       gates[:, b, 4 * i + e:4 * i + e + 1], rows_of_x(p, g, b),
                                                       ALU.mult, ALU.add).then_inc(added.sem, 1)
                                n += 1

                def units(g, a, steps, first, last):
                    if first:
                        normalise(p, dve, g, xn, xn_ready)
                        router.vector(dve, g, L_BANK, gates[:], gates_ready)
                        dve.wait_ge(*gates_ready.at(g, 1))
                    if steps:
                        if not last:
                            normalise(p, dve, g + 1, xn, xn_ready)
                        add_experts(g, 0)
                        add_experts(g, 4)
                        if not last:
                            chain = router.begin(dve, g + 1, L_BANK)
                        row_statistics(p, dve, g, added, 8 * G)
                        if not last:
                            router.finish(dve, g + 1, chain, gates[:], gates_ready)
                            dve.wait_ge(*gates_ready.at(g + 1, 1))
                all_groups(dve, units, 1)
        p.passed(NG)


def ffn_sigmoid_experts(p, name):
    nc, ins, w = p.nc, p.inputs, p.w
    E = 64
    xn_ready, xnT_psum, xnT_ready, gates_ready = p.plan(xn_ready=G, xnT_psum=1, xnT_ready=1, gates_ready=1)
    prep, = p.plan(stage_prepared=0)
    H_BANK, Y_BANK, L_BANK, M_BANK = p.bank[0:4], p.bank[4:8], p.bank[7], p.bank[6]
    with ExitStack() as ctx:
        t = lambda k, shape, dt=F32: sb(p, ctx, f"{name}_{k}", shape, dt)
        xn, xnT_now = front(p, name, ctx)
        gates_now = t("gates_now", [128, G, E])
        xnT, gates = t("xnT_all", [128, B * S]), t("gates", [128, B, E])
        keys, values = t("keys", [128, 2, 128]), t("values", [128, 2, D])
        relu = t("relu", [128, 4, GT])
        gate_now = t("gate_pair", [128, 2, B])
        router = Router(p, ctx, name, E, 4, sigmoid=True)
        norm_rows(p, name, table=ACT.Sigmoid, gpsimd=lambda pool: Chain(pool, prep)(router.prepare(pool, prep)))
        prep.base += 1

        w_in = p.plan(even_expert_weights_in=0, odd_expert_weights_in=0)

        def load(sp, i, a):
            sp.dma_start(keys[:, a, :], ins["L1_ffn_keys"][:, ds((2 * i + a) * 128, 128)]).then_inc(w_in[a].sem, 16)
            sp.dma_start(values[:, a, :], ins["L1_ffn_values"][:, ds((2 * i + a) * D, D)]).then_inc(w_in[a].sem, 16)

        with nc.Block(no_gpsimd_drain=True) as block:
            @block.sync
            def _(sp):
                load(sp, 0, 0)
                load(sp, 0, 1)

            @block.tensor
            def _(pe):
                with pe.Fori(0, NG) as g:
                    transpose_xn(p, pe, g, xn, xn_ready, M_BANK, xnT_psum)
                    pe.wait_ge(*xnT_ready.at(g, 1))
                    router.tensor(pe, g, xnT_now, w["L1_ffn_sel"], L_BANK)

            @block.scalar
            def _(act):
                with act.Fori(0, NG) as g:
                    act.wait_ge(*xnT_psum.at(g, 1))
                    nc.scalar.activation(xnT_now[:], M_BANK[:], ACT.Copy)
                    nc.scalar.activation(xnT[:, ds(g * GT, GT)], M_BANK[:], ACT.Copy).then_inc(xnT_ready.sem, 1)
                    router.scalar(act, g)

            @block.vector
            def _(dve):
                def finish(g, chain):
                    router.finish(dve, g, chain, gates_now[:], gates_ready)
                    dve.wait_ge(*gates_ready.at(g, 1))
                    nc.vector.tensor_copy(gates[:, ds(g * G, G), :], gates_now[:])

                normalise(p, dve, 0, xn, xn_ready)
                router.begin(dve, 0, L_BANK)
                with dve.Fori(1, NG) as g:
                    normalise(p, dve, g, xn, xn_ready)
                    finish(g - 1, router.chain(dve, g - 1))
                    router.begin(dve, g, L_BANK)
                finish(NG - 1, router.chain(dve, NG - 1))
        p.passed(NG)

        for s in w_in:
            s.per = 32
        h_psum, relu_ready, y_psum, added, gate_ready = p.plan(
            h_psum=2 * NG, relu_ready=2 * NG, y_psum=2 * NG, expert_added=2 * NG, gates_ready=2)

        def passes(eng, run):
            run(0, True)
            with eng.Fori(1, E // 2 - 1) as i:
                run(i, False)
            run(E // 2 - 1, False)

        with nc.Block(no_gpsimd_drain=True) as block:
            @block.sync
            def _(sp):
                with sp.Fori(1, E // 2) as i:
                    for a in range(2):
                        sp.wait_ge(*y_psum.at(i - 1, NG * (a + 1)))
                        load(sp, i, a)

            @block.tensor
            def _(pe):
                mm = nc.tensor.matmul

                def up(i, n, first):
                    if n % NG == 0:
                        pe.wait_ge(*w_in[n // NG].at(i, 32))
                    if not (first and n < 4):
                        pe.wait_ge(*relu_ready.at(i, n - 3))
                    mm(H_BANK[n % 4][:], lhsT=keys[:, n // NG, :], rhs=xnT[:, (n % NG) * GT:(n % NG + 1) * GT],
                       start=True, stop=True).then_inc(h_psum.sem, 1)

                def down(i, n, first):
                    pe.wait_ge(*relu_ready.at(i, n + 1))
                    if not (first and n < 4):
                        pe.wait_ge(*added.at(i, n - 3))
                    for b in range(G):
                        last = mm(Y_BANK[n % 4][:, batch(b)], lhsT=relu[:, n % 4, batch(b)], rhs=values[:, n // NG, :],
                                  start=True, stop=True)
                    last.then_inc(y_psum.sem, 1)

                def run(i, first):
                    for n in range(2 * NG):
                        up(i, n, first)
                        if n >= 2:
                            down(i, n - 2, first)
                        elif not first:
                            down(i - 1, 2 * NG - 2 + n, False)
                passes(pe, run)
                down(E // 2 - 1, 2 * NG - 2, False)
                down(E // 2 - 1, 2 * NG - 1, False)

            @block.scalar
            def _(act):
                def run(i, first):
                    for n in range(2 * NG):
                        act.wait_ge(*h_psum.at(i, n + 1))
                        if not (first and n < 4):
                            act.wait_ge(*y_psum.at(i, n - 3))
                        nc.scalar.activation(relu[:, n % 4, :], H_BANK[n % 4][:], ACT.Relu).then_inc(relu_ready.sem, 1)
                passes(act, run)

            @block.vector
            def _(dve):
                v = nc.vector

                def run(i, first):
                    for n in range(2 * NG):
                        a = n // NG
                        if n % NG == 0:
                            if not first:
                                dve.wait_ge(*added.at(i - 1, NG * (a + 1)))
                            v.tensor_copy(gate_now[:, a, :], gates[:, :, ds(2 * i + a, 1)].rearrange("p b a -> p (b a)"))\
                                .then_inc(gate_ready.sem, 1)
                            dve.wait_ge(*gate_ready.at(i, a + 1))
                        dve.wait_ge(*y_psum.at(i, n + 1))
                        if not (first and n < NG):
                            dve.wait_ge(*added.at(i, n - NG + 1))
                        for b in range(G):
                            k = (n % NG) * G + b
                            rows = p.x[:, k * D:(k + 1) * D]
                            last = v.scalar_tensor_tensor(rows, Y_BANK[n % 4][:, batch(b)], gate_now[:, a, k:k + 1],
                                                          rows, ALU.mult, ALU.add)
                        last.then_inc(added.sem, 1)
                        if isinstance(i, int) and i == E // 2 - 1 and a:
                            dve.wait_ge(*added.at(i, n + 1))
                            for k in range((n % NG) * G, (n % NG) * G + G):
                                v.bn_stats(p.stats[:, k, :], p.x[:, k * D:(k + 1) * D])
                passes(dve, run)
        p.passed(E // 2)



def linear_attention(p, name):
    nc, ins, w = p.nc, p.inputs, p.w
    (xn_ready, xnT_psum, xnT_ready, qk_psum, v_psum, u_psum, act_ready, turned, v_ready, u_ready, s_psum, e_ready, o_psum,
     uo_ready, sq_ready, ms_psum, y_psum, ms_in, root_ready, bias_added, tail, x_done) = p.plan(
        xn_ready=G, xnT_psum=1, xnT_ready=1, qk_psum=4, v_psum=1, u_psum=1, silu_ready=4, turned_ready=4, v_ready=G,
        u_ready=1, s_psum=16, masked_ready=16, av_psum=G, gated_ready=1, squares_ready=1, mean_square_psum=1, y_psum=1,
        variance_ready=1, root_ready=1, bias_added=1, tail_steps=1, x_done=1)
    prep, = p.plan(stage_prepared=0)
    F_BANK, Y_BANK, O_BANK = p.bank[4:6], p.bank[6], p.bank[7]
    AFTER = 7
    with ExitStack() as ctx:
        t = lambda k, shape, dt=F32: sb(p, ctx, f"{name}_{k}", shape, dt)
        xn, xnT = front(p, name, ctx)
        silu, qk = t("silu", [128, 2, GT]), t("qk", [128, 2, 4, GT])
        uT, uo, sq = t("uT", [128, 2, GT]), t("uo", [128, GT]), t("sq", [128, GT])
        vpad = t("vpad", [128, 2, G, 8 * 32])
        energy = t("energy", [128, 2, 8, S])
        keep, table = p.keep, p.table
        ones = t("ones", [128, 1])
        veps, root, rs = t("veps", [128, G]), t("root", [128, G]), t("rs", [128, G])

        def prepare(pool):
            then = Chain(pool, prep)
            then(nc.gpsimd.memset(vpad[:], 0.0))
            then(nc.gpsimd.memset(ones[:], 1.0))

        norm_rows(p, name, table=ACT.Silu, gpsimd=prepare)
        prep.base += 2

        with nc.Block(no_gpsimd_drain=True) as block:
            @block.tensor
            def _(pe):
                mm = nc.tensor.matmul

                def scores(g, a, u, first):
                    b, r = u // 4, u % 4
                    if u == 0:
                        pe.wait_ge(*turned.at(g, 4))
                    if not (first and u < 4):
                        pe.wait_ge(*e_ready.at(g, u - 3))
                    rows = slice(32 * r, 32 * r + 32)
                    for i in range(2):
                        last = mm(p.bank[r][:, batch(i)], lhsT=qk[rows, a, 2 + i, batch(b)], rhs=qk[rows, a, i, batch(b)],
                                  start=True, stop=True)
                    last.then_inc(s_psum.sem, 1)

                def values(g, a, b, first):
                    pe.wait_ge(*e_ready.at(g, 4 * b + 4))
                    if b == 0:
                        pe.wait_ge(*v_ready.at(g, G))
                        if not first:
                            pe.wait_ge(*uo_ready.at(g, 0))
                            pe.wait_ge(*sq_ready.at(g, 0))
                    for c in range(2):
                        for j in range(4):
                            h = 2 * j + c
                            last = mm(O_BANK[32 * j:32 * j + 32, batch(b)], lhsT=vpad[:, a, b, 32 * h:32 * h + 32],
                                      rhs=energy[:, b % 2, 2 * (h % 4) + h // 4, :], start=(c == 0), stop=(c == 1),
                                      tile_position=(0, 32 * j), skip_group_check=True)
                    last.then_inc(o_psum.sem, 1)

                def front(g, step, first):
                    if step == 0:
                        if not first:
                            pe.wait_ge(*v_ready.at(g, 0))
                        transpose_xn(p, pe, g, xn, xn_ready, F_BANK[0], xnT_psum)
                    if 1 <= step <= 4:
                        i = step - 1
                        if i == 0:
                            pe.wait_ge(*xnT_ready.at(g, 1))
                        elif i == 1:
                            if not first:
                                pe.wait_ge(*u_ready.at(g, 0))
                        else:
                            pe.wait_ge(*act_ready.at(g, i - 1))
                        mm(F_BANK[i % 2][:], lhsT=w["L1_attn_qk"][:, i, :], rhs=xnT[:], start=True, stop=True).then_inc(qk_psum.sem, 1)
                    if step == 5:
                        pe.wait_ge(*act_ready.at(g, 3))
                        for b in range(G):
                            last = mm(F_BANK[0][:, batch(b)], lhsT=xnT[:, batch(b)], rhs=w["L1_attn_vu"][:, 0, :], start=True, stop=True)
                        last.then_inc(v_psum.sem, 1)
                    if step == 6:
                        pe.wait_ge(*act_ready.at(g, 4))
                        mm(F_BANK[1][:], lhsT=w["L1_attn_vu"][:, 1, :], rhs=xnT[:], start=True, stop=True).then_inc(u_psum.sem, 1)

                def mean_squares(g):
                    pe.wait_ge(*sq_ready.at(g, 1))
                    for b in range(G):
                        last = mm(Y_BANK[:, b:b + 1], lhsT=sq[:, batch(b)], rhs=ones[:], start=True, stop=True)
                    last.then_inc(ms_psum.sem, 1)

                def output(g):
                    pe.wait_ge(*uo_ready.at(g, 1))
                    pe.wait_ge(*ms_in.at(g, 1))
                    for b in range(G):
                        last = mm(Y_BANK[:, batch(b)], lhsT=uo[:, batch(b)], rhs=w["L1_attn_out_w"][:], start=True, stop=True)
                    last.then_inc(y_psum.sem, 1)

                def units(g, a, steps, first, last):
                    if first:
                        for step in range(7):
                            front(g, step, True)
                    for u in range(steps or AFTER):
                        if steps:
                            scores(g, a, u, first)
                        if u % 4 == 1 and not (first and u < 5) and (steps or u < 5):
                            h, ha, hu = before(g, a, u, 5)
                            values(h, ha, hu // 4, first)
                        if u == 4 and not first:
                            mean_squares(g - 1)
                        if u == 6 and not first:
                            output(g - 1)
                        if not last:
                            for step, at in enumerate((2, 4, 5, 7, 9, 11, 12)):
                                if u == at:
                                    front(g + 1, step, False)
                all_groups(pe, units)

            @block.scalar
            def _(act):
                def front(g, a, step):
                    if step == 0:
                        act.wait_ge(*xnT_psum.at(g, 1))
                        nc.scalar.activation(xnT[:], F_BANK[0][:], ACT.Copy).then_inc(xnT_ready.sem, 1)
                    if 1 <= step <= 4:
                        i = step - 1
                        act.wait_ge(*qk_psum.at(g, i + 1))
                        if i >= 2:
                            act.wait_ge(*turned.at(g, i - 1))
                        nc.scalar.activation(silu[:, i % 2, :], F_BANK[i % 2][:], ACT.Silu, bias=w["L1_attn_qk_b"][:, i:i + 1])\
                            .then_inc(act_ready.sem, 1)
                    if step == 6:
                        act.wait_ge(*u_psum.at(g, 1))
                        nc.scalar.activation(uT[:, a, :], F_BANK[1][:], ACT.Identity, bias=w["L1_attn_ub"][:, 0:1]).then_inc(u_ready.sem, 1)

                def units(g, a, steps, first, last):
                    if first:
                        for step in range(7):
                            front(g, a, step)
                    if not first:
                        act.wait_ge(*o_psum.at(g - 1, G))
                        nc.scalar.activation(sq[:], O_BANK[:], ACT.Square).then_inc(sq_ready.sem, 1)
                        if not last:
                            front(g + 1, 1 - a, 0)
                        act.wait_ge(*ms_in.at(g - 1, 1))
                        nc.scalar.activation(root[:], veps[:], ACT.Sqrt).then_inc(root_ready.sem, 1)
                    elif not last:
                        front(g + 1, 1 - a, 0)
                    if not last:
                        for step in range(1, 7):
                            front(g + 1, 1 - a, step)
                all_groups(act, units)

            @block.vector
            def _(dve):
                v = nc.vector

                def front(g, a, step):
                    if step == 0:
                        normalise(p, dve, g, xn, xn_ready)
                    if 1 <= step <= 4:
                        i = step - 1
                        dve.wait_ge(*act_ready.at(g, i + 1))
                        v.tensor_tensor(qk[:, a, i, :].rearrange("p (b n) -> p b n", b=G), silu[:, i % 2, :].rearrange("p (b n) -> p b n", b=G),
                                        table[:, i % 2, :].unsqueeze(1).to_broadcast([128, G, S]), ALU.mult).then_inc(turned.sem, 1)
                    if step == 5:
                        dve.wait_ge(*v_psum.at(g, 1))
                        for b in range(G):
                            q = vpad[:, a, b, 0:256]
                            slots = bass.AP(q.tensor, q.offset, [list(q.ap[0]), [64, 4], [48, 2], [1, 16]])
                            v.tensor_tensor(slots, F_BANK[0][:, batch(b)].rearrange("p (j c d) -> p j c d", j=4, c=2),
                                            w["L1_attn_vb"][:].rearrange("p (j c d) -> p j c d", j=4, c=2), ALU.add).then_inc(v_ready.sem, 1)

                def gated(g, a):
                    dve.wait_ge(*o_psum.at(g, G))
                    dve.wait_ge(*sq_ready.at(g, 1))
                    dve.wait_ge(*u_ready.at(g, 1))
                    v.tensor_tensor(uo[:], O_BANK[:], uT[:, a, :], ALU.mult).then_inc(uo_ready.sem, 1)

                def add_output(g):
                    dve.wait_ge(*root_ready.at(g, 1))
                    v.reciprocal(rs[:], root[:]).then_inc(tail.sem, 1)
                    dve.wait_ge(*tail.at(g, 1))
                    dve.wait_ge(*bias_added.at(g, 1))
                    dve.wait_ge(*y_psum.at(g, 1))
                    for b in range(G):
                        last = v.scalar_tensor_tensor(rows_of_x(p, g, b), Y_BANK[:, batch(b)], rs[:, b:b + 1], rows_of_x(p, g, b),
                                                      ALU.mult, ALU.add)
                    last.then_inc(x_done.sem, 1)

                def units(g, a, steps, first, last):
                    if first:
                        for step in range(7):
                            front(g, a, step)
                    for u in range(steps or AFTER + 2):
                        b, r = u // 4, u % 4
                        if steps:
                            dve.wait_ge(*s_psum.at(g, u + 1))
                            if r == 0 and not (first and b < 2):
                                dve.wait_ge(*o_psum.at(g, b - 1))
                            v.tensor_tensor(energy[:, b % 2, 2 * r:2 * r + 2, :], p.bank[r][:, 0:2 * S].rearrange("p (t n) -> p t n", t=2),
                                            keep[:, 2 * r:2 * r + 2, :], ALU.mult).then_inc(e_ready.sem, 1)
                        if not first:
                            if u == 2:
                                gated(g - 1, 1 - a)
                            if u == 3:
                                for b in range(G):
                                    done = v.tensor_tensor(rows_of_x(p, g - 1, b), rows_of_x(p, g - 1, b), w["L1_attn_out_b"][:], ALU.add)
                                done.then_inc(bias_added.sem, 1)
                            if u == 5:
                                dve.wait_ge(*ms_psum.at(g - 1, 1))
                                v.tensor_scalar(veps[:], Y_BANK[:, 0:G], 1.0 / D, 1e-6, ALU.mult, ALU.add).then_inc(ms_in.sem, 1)
                            if u == 7:
                                add_output(g - 1)
                            if u == 8:
                                row_statistics(p, dve, g - 1, x_done)
                        if not last:
                            for step, at in enumerate((1, 5, 7, 9, 11, 12)):
                                if u == at:
                                    front(g + 1, 1 - a, step)
                all_groups(dve, units)
        p.passed(NG)



def single_head(p, name):
    nc, ins = p.nc, p.inputs
    norm_rows(p, name)
    (xn_ready, xnT_psum, xnT_ready, s_psum, max_ready, p_ready, t_psum, pt_ready, y_psum, r_steps, x_done) = p.plan(
        xn_ready=G, xnT_psum=1, xnT_ready=1, s_psum=1, max_ready=1, p_ready=1, t_psum=1,
        pt_ready=1, y_psum=1, reciprocal_steps=1, x_done=1)
    ctx_in = p.plan(even_ctx_in=8, odd_ctx_in=8)
    rows_in = p.plan(even_ctx_rows_in=8, odd_ctx_rows_in=8)
    loaded = lambda halves, g, a: halves[a].at(g, 16 - 8 * a)
    S_BANK, T_BANK, Y_BANK, M_BANK = p.bank[0:2], p.bank[2], p.bank[3], p.bank[6]
    with ExitStack() as ctx:
        t = lambda k, shape, dt=F32: sb(p, ctx, f"{name}_{k}", shape, dt)
        xn, xnT = front(p, name, ctx)
        ctxT, rows, probsT = t("ctxT", [128, 2, GT]), t("ctx_rows", [128, 2, GT]), t("probsT", [128, GT])
        probs = t("probs", [128, 2, GT])
        nmax, rsum, rrec = (t(k, [128, 2, G]) for k in ("nmax", "rsum", "rrec"))

        with nc.Block(no_gpsimd_drain=True) as block:
            @block.sync
            def _(sp):
                def load_context(g, a, first=False):
                    if not first:
                        sp.wait_ge(*s_psum.at(g - 2, 1))
                    sp.dma_start(ctxT[:, a, :], ins["ctx_T"][:, ds(g * GT, GT)]).then_inc(ctx_in[a].sem, 16)

                def load_rows(g, a, first=False):
                    if not first:
                        sp.wait_ge(*y_psum.at(g - 2, 1))
                    sp.dma_start(rows[:, a, :], ins["ctx_rows"][:, ds(g * GT, GT)]).then_inc(rows_in[a].sem, 16)

                for a in range(2):
                    load_context(a, a, True)
                    load_rows(a, a, True)
                load_context(2, 0)
                load_context(3, 1)
                with sp.Fori(1, NG // 2 - 1) as i:
                    for a in range(2):
                        load_rows(i * 2 + a, a)
                        load_context(i * 2 + (a + 2), a)
                load_rows(NG - 2, 0)
                load_rows(NG - 1, 1)

            @block.tensor
            def _(pe):
                def scores(g, a):
                    pe.wait_ge(*xnT_ready.at(g, 1))
                    pe.wait_ge(*loaded(ctx_in, g, a))
                    for b in range(G):
                        last = nc.tensor.matmul(S_BANK[a][:, batch(b)], lhsT=xnT[:, batch(b)], rhs=ctxT[:, a, batch(b)], start=True, stop=True)
                    last.then_inc(s_psum.sem, 1)

                def body(g, a, left):
                    if left >= 2:
                        transpose_xn(p, pe, g + 2, xn, xn_ready, M_BANK, xnT_psum)
                    pe.wait_ge(*p_ready.at(g, 1))
                    for b in range(G):
                        last = nc.tensor.transpose(T_BANK[:, batch(b)], probs[:, a, batch(b)], p.ident[:])
                    last.then_inc(t_psum.sem, 1)
                    if left >= 2:
                        scores(g + 2, a)
                    pe.wait_ge(*pt_ready.at(g, 1))
                    pe.wait_ge(*loaded(rows_in, g, a))
                    for b in range(G):
                        last = nc.tensor.matmul(Y_BANK[:, batch(b)], lhsT=probsT[:, batch(b)], rhs=rows[:, a, batch(b)], start=True, stop=True)
                    last.then_inc(y_psum.sem, 1)

                for g in range(2):
                    transpose_xn(p, pe, g, xn, xn_ready, M_BANK, xnT_psum)
                    scores(g, g)
                run_ahead(pe, body)

            @block.scalar
            def _(act):
                def copy(g):
                    act.wait_ge(*xnT_psum.at(g, 1))
                    nc.scalar.activation(xnT[:], M_BANK[:], ACT.Copy, scale=HD ** -0.5).then_inc(xnT_ready.sem, 1)

                def exponentials(g, a):
                    act.wait_ge(*max_ready.at(g, 1))
                    for b in range(G):
                        last = nc.scalar.activation(probs[:, a, batch(b)], S_BANK[a][:, batch(b)], ACT.Exp, bias=nmax[:, a, b:b + 1],
                                                    accum_out=rsum[:, a, b:b + 1])
                    last.then_inc(p_ready.sem, 1)

                def body(g, a, left):
                    if left >= 2:
                        copy(g + 2)
                    if left:
                        if not (isinstance(g, int) and g == 0):
                            act.wait_ge(*t_psum.at(g - 1, 1))
                        exponentials(g + 1, 1 - a)

                copy(0)
                copy(1)
                exponentials(0, 0)
                run_ahead(act, body)

            @block.vector
            def _(dve):
                v = nc.vector

                def maxima(g, a):
                    dve.wait_ge(*s_psum.at(g, 1))
                    v.tensor_reduce(nmax[:, a, :], S_BANK[a][:].rearrange("p (b k) -> p b k", b=G), axis=AX, op=ALU.max, negate=True)\
                        .then_inc(max_ready.sem, 1)

                def body(g, a, left):
                    dve.wait_ge(*p_ready.at(g, 1))
                    v.reciprocal(rrec[:, a, :], rsum[:, a, :]).then_inc(r_steps.sem, 1)
                    dve.wait_ge(*t_psum.at(g, 1))
                    v.tensor_copy(probsT[:], T_BANK[:]).then_inc(pt_ready.sem, 1)
                    if left >= 2:
                        maxima(g + 2, a)
                    if left >= 3:
                        normalise(p, dve, g + 3, xn, xn_ready)
                    dve.wait_ge(*r_steps.at(g, 1))
                    dve.wait_ge(*y_psum.at(g, 1))
                    for b in range(G):
                        last = v.scalar_tensor_tensor(rows_of_x(p, g, b), Y_BANK[:, batch(b)], rrec[:, a, b:b + 1], rows_of_x(p, g, b),
                                                      ALU.mult, ALU.add)
                    last.then_inc(x_done.sem, 1)
                    row_statistics(p, dve, g, x_done)

                for g in range(3):
                    normalise(p, dve, g, xn, xn_ready)
                    if g < 2:
                        maxima(g, g)
                run_ahead(dve, body)
        p.passed(NG)



def channel_attention(p, name):
    nc, ins, w = p.nc, p.inputs, p.w
    (xn_ready, xnT_psum, xnT_ready, q_psum, k_psum, v_psum, q_ready, k_ready, v_ready, vmask_ready, s_psum, max_ready,
     p_ready, r_steps, qpad_ready, av_psum, x_done) = p.plan(
        xn_ready=G, xnT_psum=1, xnT_ready=1, q_psum=1, k_psum=1, v_psum=1, q_ready=1, k_ready=1, v_ready=1,
        kmask_ready=UNITS, s_psum=UNITS, max_ready=UNITS, p_ready=UNITS, reciprocal_steps=G, qpad_ready=G, av_psum=G, x_done=1)
    prep, = p.plan(stage_prepared=0)
    S_BANK, M_BANK, O_BANK = p.bank[0:4], p.bank[6], p.bank[7]
    with ExitStack() as ctx:
        t = lambda k, shape, dt=F32: sb(p, ctx, f"{name}_{k}", shape, dt)
        xn, xnT = front(p, name, ctx)
        qT, k, vv = t("qT", [128, 2, GT]), t("k", [128, 2, GT]), t("v", [128, 2, GT])
        vmask, qpad = t("vmask", [128, 2, QUADS, PER * S]), t("qpad", [128, 2, H * 32])
        probs = t("probs", [128, 2, QUADS, PER * S])
        nmax, rsum, rrec = t("nmax", [128, G, H]), t("rsum", [128, G, H]), t("rrec", [128, G, H])
        temperature = t("temperature", [128, H])
        def prepare(pool):
            then = Chain(pool, prep)
            then(nc.gpsimd.memset(qpad[:], 0.0))
            then(nc.gpsimd.memset(temperature[:], 1.0))
            then(nc.gpsimd.affine_select(out=temperature[:], in_=temperature[:], compare_op=ALU.is_ge, fill=0.0, base=0,
                                         pattern=[[-HD, H]], channel_multiplier=1))
            then(nc.gpsimd.affine_select(out=temperature[:], in_=temperature[:], compare_op=ALU.is_ge, fill=0.0,
                                         base=HD - 1, pattern=[[HD, H]], channel_multiplier=-1))
            then(nc.gpsimd.tensor_tensor(temperature[:], temperature[:], w["L2_attn_temp"][:].to_broadcast([128, H]), ALU.mult))

        norm_rows(p, name, gpsimd=prepare)
        prep.base += 5
        AFTER = 4

        with nc.Block(no_gpsimd_drain=True) as block:
            @block.gpsimd
            def _(pool):
                def units(g, a, steps, first, last):
                    for u in range(steps):
                        b, j = u // 4, u % 4
                        if u == 0:
                            pool.wait_ge(*v_ready.at(g, 1))
                        if not (first and u < 8):
                            pool.wait_ge(*s_psum.at(g, u - 7))
                        nc.gpsimd.tensor_tensor(vmask[:, b % 2, j].rearrange("p (c k) -> p c k", c=PER),
                                                vv[:, a, batch(b)].unsqueeze(1).to_broadcast([128, PER, S]),
                                                temperature[:, PER * j:PER * j + PER].unsqueeze(2).to_broadcast([128, PER, S]),
                                                ALU.mult).then_inc(vmask_ready.sem, 1)
                all_groups(pool, units)

            @block.tensor
            def _(pe):
                mm = nc.tensor.matmul

                def scores(g, a, u, first):
                    b, j = u // 4, u % 4
                    pe.wait_ge(*vmask_ready.at(g, u + 1))
                    if u == 0:
                        pe.wait_ge(*k_ready.at(g, 1))
                    if not (first and u < 4):
                        pe.wait_ge(*p_ready.at(g, u - 3))
                    mm(S_BANK[j][:], lhsT=k[:, a, batch(b)], rhs=vmask[:, b % 2, j], start=True, stop=True).then_inc(s_psum.sem, 1)

                def values(g, b, first):
                    pe.wait_ge(*qpad_ready.at(g, b + 1))
                    if b == 0 and not first:
                        pe.wait_ge(*x_done.at(g, 0))
                    for c in range(PER):
                        for j in range(QUADS):
                            h = j * PER + c
                            last = mm(O_BANK[32 * j:32 * j + 32, batch(b)], lhsT=qpad[:, b % 2, 32 * h:32 * h + 32],
                                      rhs=probs[:, b % 2, j, batch(c)], start=(c == 0), stop=(c == PER - 1),
                                      tile_position=(0, 32 * j), skip_group_check=True)
                    last.then_inc(av_psum.sem, 1)

                def front(g, a, step):
                    if step == 0:
                        transpose_xn(p, pe, g, xn, xn_ready, M_BANK, xnT_psum)
                    if step == 1:
                        pe.wait_ge(*xnT_ready.at(g, 1))
                        for b in range(G):
                            last = mm(M_BANK[:, batch(b)], lhsT=xnT[:, batch(b)], rhs=w["L2_attn_Wv"][:], start=True, stop=True)
                        last.then_inc(v_psum.sem, 1)
                    if step == 2:
                        pe.wait_ge(*v_ready.at(g, 1))
                        for b in range(G):
                            last = mm(M_BANK[:, batch(b)], lhsT=xnT[:, batch(b)], rhs=w["L2_attn_Wk"][:], start=True, stop=True)
                        last.then_inc(k_psum.sem, 1)
                    if step == 3:
                        pe.wait_ge(*k_ready.at(g, 1))
                        mm(M_BANK[:], lhsT=w["L2_attn_Wq"][:], rhs=xnT[:], start=True, stop=True).then_inc(q_psum.sem, 1)

                def units(g, a, steps, first, last):
                    if first:
                        for step in range(4):
                            front(g, a, step)
                    for u in range(steps or AFTER):
                        if steps:
                            scores(g, a, u, first)
                        if u % 4 == 2 and not (first and u < 6):
                            h, ha, hu = before(g, a, u, 6)
                            values(h, hu // 4, first)
                        if not last:
                            if u == 5:
                                pe.wait_ge(*q_ready.at(g, 1))
                            for step, at in enumerate((5, 7, 9, 11)):
                                if u == at:
                                    front(g + 1, 1 - a, step)
                all_groups(pe, units)

            @block.scalar
            def _(act):

                def start(g):
                    act.wait_ge(*xnT_psum.at(g, 1))
                    nc.scalar.activation(xnT[:], M_BANK[:], ACT.Copy).then_inc(xnT_ready.sem, 1)

                def units(g, a, steps, first, last):
                    if first:
                        start(g)
                    for u in range(steps):
                        b, j = u // 4, u % 4
                        act.wait_ge(*max_ready.at(g, u + 1))
                        if j == 0 and not (first and b < 2):
                            act.wait_ge(*av_psum.at(g, b - 1))
                        for c in range(PER):
                            h = 4 * j + c
                            done = nc.scalar.activation(probs[:, b % 2, j, batch(c)], S_BANK[j][:, batch(c)], ACT.Exp,
                                                        bias=nmax[:, b, h:h + 1], accum_out=rsum[:, b, h:h + 1])
                        done.then_inc(p_ready.sem, 1)
                        if u == 4 and not last:
                            start(g + 1)
                all_groups(act, units)

            @block.vector
            def _(dve):
                v = nc.vector

                def scaled_q(g, a, b, first):
                    dve.wait_ge(*p_ready.at(g, 4 * b + 4))
                    v.reciprocal(rrec[:, b, :], rsum[:, b, :]).then_inc(r_steps.sem, 1)
                    dve.wait_ge(*r_steps.at(g, b + 1))
                    if not (first and b < 2):
                        dve.wait_ge(*av_psum.at(g, b - 1))
                    q = qpad[:, b % 2, :]
                    slots = bass.AP(q.tensor, q.offset, [list(q.ap[0]), [128, QUADS], [40, PER], [1, HD]])
                    v.tensor_tensor(slots, qT[:, a, batch(b)].rearrange("p (j c d) -> p j c d", j=QUADS, c=PER),
                                    rrec[:, b, :].rearrange("p (j c) -> p j c", j=QUADS).unsqueeze(3).to_broadcast([128, QUADS, PER, HD]),
                                    ALU.mult).then_inc(qpad_ready.sem, 1)

                def front(g, a, step):
                    if step == 0:
                        normalise(p, dve, g, xn, xn_ready)
                    for i, out, bias, psum, ready in ((1, vv, "L2_attn_bv", v_psum, v_ready), (2, k, "L2_attn_bk", k_psum, k_ready)):
                        if step == i:
                            dve.wait_ge(*psum.at(g, 1))
                            v.tensor_tensor(out[:, a, :].rearrange("p (b c) -> p b c", b=G), M_BANK[:].rearrange("p (b c) -> p b c", b=G),
                                            w[bias][:].unsqueeze(1).to_broadcast([128, G, D]), ALU.add).then_inc(ready.sem, 1)
                    if step == 3:
                        dve.wait_ge(*q_psum.at(g, 1))
                        v.tensor_scalar(qT[:, a, :], M_BANK[:], w["L2_attn_bq"][:, 0:1], None, ALU.add).then_inc(q_ready.sem, 1)

                def units(g, a, steps, first, last):
                    if first:
                        for step in range(4):
                            front(g, a, step)
                    for u in range(steps or AFTER):
                        if steps:
                            dve.wait_ge(*s_psum.at(g, u + 1))
                            v.tensor_reduce(nmax[:, u // 4, 4 * (u % 4):4 * (u % 4) + 4], S_BANK[u % 4][:].rearrange("p (c k) -> p c k", c=PER),
                                            axis=AX, op=ALU.max, negate=True).then_inc(max_ready.sem, 1)
                        if u % 4 == 1 and not (first and u < 5):
                            h, ha, hu = before(g, a, u, 5)
                            scaled_q(h, ha, hu // 4, first)
                        if u == 3 and not first:
                            dve.wait_ge(*av_psum.at(g - 1, G))
                            v.tensor_tensor(rows_of_x(p, g - 1, 0, G), rows_of_x(p, g - 1, 0, G), O_BANK[:], ALU.add).then_inc(x_done.sem, 1)
                            row_statistics(p, dve, g - 1, x_done)
                        if not last:
                            for step, at in enumerate((2, 7, 9, 11)):
                                if u == at:
                                    front(g + 1, 1 - a, step)
                all_groups(dve, units)
        p.passed(NG)


def latent_weights(p):
    nc, w = p.nc, p.w
    sum_ready, down_psum, down_ready, up_psum = p.plan(latent_sum_ready=0, latent_psum=0, latent_ready=0, latent_up_psum=0)
    with ExitStack() as ctx:
        both, down = sb(p, ctx, "latent_both", [128, 128]), sb(p, ctx, "latent_down", [32, 128])
        with nc.Block(no_gpsimd_drain=True) as block:
            @block.vector
            def _(dve):
                nc.vector.tensor_tensor(both[:], w["L3_attn_W_k_T"][:], w["L3_attn_W_v_T"][:], ALU.add).then_inc(sum_ready.sem, 1)

            @block.tensor
            def _(pe):
                pe.wait_ge(*sum_ready.at(0, 1))
                nc.tensor.matmul(p.bank[0][0:32, 0:128], lhsT=w["L3_attn_W_down_kv"][:], rhs=both[:], start=True, stop=True)\
                    .then_inc(down_psum.sem, 1)
                pe.wait_ge(*down_ready.at(0, 1))
                for i, n in enumerate(("L3_attn_W_up_k", "L3_attn_W_up_v")):
                    last = nc.tensor.matmul(p.bank[1][:, batch(i)], lhsT=down[:], rhs=w[n][:], start=True, stop=True)
                last.then_inc(up_psum.sem, 1)

            @block.scalar
            def _(act):
                act.wait_ge(*down_psum.at(0, 1))
                nc.scalar.activation(down[:], p.bank[0][0:32, 0:128], ACT.Copy).then_inc(down_ready.sem, 1)
                act.wait_ge(*up_psum.at(0, 1))
                nc.scalar.activation(w["L3_K"][:], p.bank[1][:, batch(0)], ACT.Copy)
                nc.scalar.activation(w["L3_V"][:], p.bank[1][:, batch(1)], ACT.Copy)
    for s in (sum_ready, down_psum, down_ready, up_psum):
        s.base += 1



SUPPORT = 5


def support_attention(p, name):
    nc, ins, w = p.nc, p.inputs, p.w
    HEADS, HD3, CH = 8, 64, 4
    U, PROJECTIONS = 2 * G, 2 * CH + G
    (ctx_in, mask_in, xn_ready, xnT_psum, xnT_ready, projected, even_ready, odd_ready, named, order_psum,
     bias_ready, floor_steps, s_psum, raw_max, max_ready, shift_ready, e_ready, p_ready, t_psum, pt_ready, av_psum,
     r_steps, sum_ready, o_ready, oT_psum, oT_ready, y_psum, x_part) = p.plan(
        ctx_in=16, mask_in=16, xn_ready=G, xnT_psum=1, xnT_ready=1, projection_psum=PROJECTIONS,
        even_projections_ready=PROJECTIONS // 2, odd_projections_ready=PROJECTIONS // 2, mask_named=1, mask_order_psum=1,
        mask_ready=1, floor_steps=4, s_psum=U, raw_max=U, max_ready=U, masked_shift_ready=G, masked_exp_ready=G, p_ready=U,
        t_psum=U, pt_ready=U, av_psum=G, reciprocal_steps=G, masked_sum_steps=G, o_ready=G, oT_psum=G, oT_ready=G,
        y_psum=G, expert_added=G)
    prep, = p.plan(stage_prepared=0)
    S_BANK, T_BANK, F_BANK, O_BANK, M_BANK = p.bank[0:2], p.bank[2:4], p.bank[4:6], p.bank[6], p.bank[7]
    with ExitStack() as ctx:
        t = lambda k, shape, dt=F32: sb(p, ctx, f"{name}_{k}", shape, dt)
        xn, xnT = front(p, name, ctx)
        ctxT, mask = t("ctxT", [128, GT]), t("mask", [128, GT], I32)
        named_bf, ones, order = t("named", [128, GT], BF16), t("ones", [128, S], BF16), t("order", [128, S], BF16)
        score_bias = t("score_bias", [128, 2, G, S], BF16)
        kT, qT, vv = t("kT", [128, 2, CH, GT]), t("qT", [128, 2, CH, GT]), t("v", [128, 2, G, HEADS * HD3])
        probs, probsT = t("probs", [128, 4, CH * S]), t("probsT", [128, 4, CH * S])
        nmax, rsum, rrec, rowmax, eshift, e = (t(k, [128, G, HEADS]) for k in ("nmax", "rsum", "rrec", "rowmax", "eshift", "e"))
        pads, nfloor = t("pads", [128, 2, G]), t("nfloor", [128, 2, G])
        o, oT = t("o", [128, 2, HEADS * HD3]), t("oT", [128, CH * S])

        def prepare(pool):
            then = Chain(pool, prep)
            then(nc.gpsimd.memset(order[:], 1.0))
            then(nc.gpsimd.affine_select(out=order[:], in_=order[:], compare_op=ALU.is_ge, fill=0.0, base=0,
                                         pattern=[[1, S]], channel_multiplier=-1))
            then(nc.gpsimd.affine_select(out=order[:], in_=order[:], compare_op=ALU.not_equal, fill=-1024.0, base=0,
                                         pattern=[[1, S]], channel_multiplier=-1))

        norm_rows(p, name, again=1e-5, gpsimd=prepare)
        prep.base += 3
        AFTER = 6

        def place(a, n):
            return (kT, qT, vv)[n // CH][:, a, n % CH, :]

        with nc.Block(no_gpsimd_drain=True) as block:
            @block.sync
            def _(sp):
                def load(g):
                    sp.dma_start(ctxT[:], ins["ctx_T"][:, ds(g * GT, GT)]).then_inc(ctx_in.sem, 16)
                    sp.dma_start(mask[:], ins["visible"][:, ds(g * GT, GT)]).then_inc(mask_in.sem, 16)
                load(0)
                with sp.Fori(1, NG) as g:
                    sp.wait_ge(*projected.at(g - 1, PROJECTIONS))
                    sp.wait_ge(*named.at(g - 1, 1))
                    load(g)

            @block.tensor
            def _(pe):
                mm = nc.tensor.matmul

                def front(g, a, u, first):
                    if u == 1:
                        if not first:
                            pe.wait_ge(*even_ready.at(g, 0))
                            pe.wait_ge(*odd_ready.at(g, 0))
                        transpose_xn(p, pe, g, xn, xn_ready, F_BANK[0], xnT_psum)
                        pe.wait_ge(*named.at(g, 1))
                        for b in range(G):
                            last = mm(F_BANK[1][:, batch(b)], lhsT=named_bf[:, batch(b)], rhs=order[:], start=True, stop=True)
                        last.then_inc(order_psum.sem, 1)
                    for n in range(2 * (u - 2), 2 * (u - 2) + 2) if u >= 2 else ():
                        if n == 0:
                            pe.wait_ge(*xnT_ready.at(g, 1))
                            pe.wait_ge(*ctx_in.at(g, 16))
                        elif n == 1:
                            pe.wait_ge(*bias_ready.at(g, 1))
                        else:
                            pe.wait_ge(*(odd_ready if n % 2 else even_ready).at(g, n // 2))
                        if n < CH:
                            last = mm(F_BANK[n % 2][:], lhsT=w["L3_xattn_Wkv"][:, batch(n)], rhs=ctxT[:], start=True, stop=True)
                        elif n < 2 * CH:
                            last = mm(F_BANK[n % 2][:], lhsT=w["L3_xattn_Wq"][:, batch(n - CH)], rhs=xnT[:], start=True, stop=True)
                        else:
                            last = mm(F_BANK[n % 2][:], lhsT=ctxT[:, batch(n - 2 * CH)], rhs=w["L3_xattn_Wkv"][:, 512:1024],
                                      start=True, stop=True)
                        last.then_inc(projected.sem, 1)

                def scores(g, a, u, first):
                    b, r = u // 2, u % 2
                    if u == 0:
                        pe.wait_ge(*bias_ready.at(g, 1))
                        pe.wait_ge(*even_ready.at(g, CH))
                        pe.wait_ge(*odd_ready.at(g, CH))
                    if not (first and u < 2):
                        pe.wait_ge(*p_ready.at(g, u - 1))
                    mm(S_BANK[r][:], lhsT=p.ident_bf[:], rhs=score_bias[:, a, b, :].unsqueeze(1).to_broadcast([128, CH, S]),
                       start=True, stop=False, skip_group_check=True)
                    rows = slice(64 * r, 64 * r + 64)
                    for ch in range(CH):
                        last = mm(S_BANK[r][:, batch(ch)], lhsT=qT[rows, a, ch, batch(b)], rhs=kT[rows, a, ch, batch(b)],
                                  start=False, stop=(ch == CH - 1), skip_group_check=True)
                    last.then_inc(s_psum.sem, 1)

                def transposes(g, u, first):
                    pe.wait_ge(*p_ready.at(g, u + 1))
                    if not (first and u < 2):
                        pe.wait_ge(*pt_ready.at(g, u - 1))
                    for ch in range(CH):
                        last = nc.tensor.transpose(T_BANK[u % 2][:, batch(ch)], probs[:, u % 4, batch(ch)], p.ident[:])
                    last.then_inc(t_psum.sem, 1)

                def values(g, a, u, first):
                    b, r = u // 2, u % 2
                    pe.wait_ge(*pt_ready.at(g, u + 1))
                    if u == 0:
                        pe.wait_ge(*even_ready.at(g, PROJECTIONS // 2))
                        pe.wait_ge(*odd_ready.at(g, PROJECTIONS // 2))
                    if r == 0 and not (first and b == 0):
                        pe.wait_ge(*o_ready.at(g, b))
                    for ch in range(CH):
                        h = 2 * ch + r
                        last = mm(O_BANK[:, h * HD3:(h + 1) * HD3], lhsT=probsT[:, u % 4, batch(ch)],
                                  rhs=vv[:, a, b, h * HD3:(h + 1) * HD3], start=True, stop=True)
                    if r == 1:
                        last.then_inc(av_psum.sem, 1)

                def output_transposes(g, b, first):
                    pe.wait_ge(*o_ready.at(g, b + 1))
                    if not (first and b == 0):
                        pe.wait_ge(*x_part.at(g, b))
                    for ch in range(CH):
                        last = nc.tensor.transpose(M_BANK[:, batch(ch)], o[:, b % 2, batch(ch)], p.ident[:])
                    last.then_inc(oT_psum.sem, 1)

                def output(g, b):
                    pe.wait_ge(*oT_ready.at(g, b + 1))
                    for ch in range(CH):
                        last = mm(M_BANK[:, 0:D], lhsT=oT[:, batch(ch)], rhs=w["L3_xattn_Wout"][:, ch, :],
                                  start=(ch == 0), stop=(ch == CH - 1))
                    last.then_inc(y_psum.sem, 1)

                def units(g, a, steps, first, last):
                    if first:
                        for u in range(1, U):
                            front(g, a, u, True)
                    for u in range(steps or AFTER):
                        if steps:
                            scores(g, a, u, first)
                        if not last:
                            front(g + 1, 1 - a, u, False)
                        if (steps or u < 1) and not (first and u < 1):
                            h, _, hu = before(g, a, u, 1, U)
                            transposes(h, hu, first)
                        if (steps or u < 2) and not (first and u < 2):
                            h, ha, hu = before(g, a, u, 2, U)
                            values(h, ha, hu, first)
                        if u % 2 == 1 and not (first and u < 5) and (steps or u < 5):
                            h, _, hu = before(g, a, u, 5, U)
                            output_transposes(h, hu // 2, first)
                        if u % 2 == 0 and not (first and u < 6):
                            h, _, hu = before(g, a, u, 6, U)
                            output(h, hu // 2)
                all_groups(pe, units, U)

            @block.scalar
            def _(act):

                def front(g, a, u):
                    if u == 1:
                        act.wait_ge(*xnT_psum.at(g, 1))
                        nc.scalar.activation(xnT[:], F_BANK[0][:], ACT.Identity, scale=w["L3_xattn_ln_w"][:, 0:1],
                                             bias=w["L3_xattn_ln_b"][:, 0:1]).then_inc(xnT_ready.sem, 1)
                    if u >= 2:
                        n = 2 * (u - 2)
                        act.wait_ge(*projected.at(g, n + 1))
                        nc.scalar.activation(place(a, n), F_BANK[0][:], ACT.Copy, scale=HD3 ** -0.5 if n // CH == 1 else 1.0)\
                            .then_inc(even_ready.sem, 1)

                def units(g, a, steps, first, last):
                    if first:
                        for u in range(1, U):
                            front(g, a, u)
                    for u in range(steps or AFTER):
                        if u % 2 == 0 and not (first and u < 6):
                            h, _, hu = before(g, a, u, 6, U)
                            act.wait_ge(*oT_psum.at(h, hu // 2 + 1))
                            nc.scalar.activation(oT[:], M_BANK[:], ACT.Copy).then_inc(oT_ready.sem, 1)
                        if steps:
                            b, r = u // 2, u % 2
                            act.wait_ge(*max_ready.at(g, u + 1))
                            if not (first and u < 4):
                                act.wait_ge(*t_psum.at(g, u - 3))
                            for ch in range(CH):
                                i = CH * r + ch
                                done = nc.scalar.activation(probs[:, u % 4, batch(ch)], S_BANK[r][:, batch(ch)], ACT.Exp,
                                                            bias=nmax[:, b, i:i + 1], accum_out=rsum[:, b, i:i + 1])
                            done.then_inc(p_ready.sem, 1)
                            if r == 1:
                                act.wait_ge(*shift_ready.at(g, b + 1))
                                nc.scalar.activation(e[:, b, :], eshift[:, b, :], ACT.Exp).then_inc(e_ready.sem, 1)
                        if not last:
                            front(g + 1, 1 - a, u)
                all_groups(act, units, U)

            @block.vector
            def _(dve):
                v = nc.vector

                def front(g, a, u):
                    if u == 0:
                        dve.wait_ge(*mask_in.at(g, 16))
                        v.tensor_scalar(named_bf[:], mask[:], 0.0, None, ALU.not_equal).then_inc(named.sem, 1)
                        normalise(p, dve, g, xn, xn_ready)
                    if u == 1:
                        dve.wait_ge(*order_psum.at(g, 1))
                        v.tensor_scalar(score_bias[:, a].rearrange("p b k -> p (b k)"), F_BANK[1][:], -1024.0 + SUPPORT - 0.5,
                                        MASKED, ALU.is_gt, ALU.mult).then_inc(bias_ready.sem, 1)
                    if u == 2:
                        dve.wait_ge(*bias_ready.at(g, 1))
                        v.tensor_reduce(pads[:, a], score_bias[:, a], axis=AX, op=ALU.add).then_inc(floor_steps.sem, 1)
                        dve.wait_ge(*floor_steps.at(g, 1))
                        v.tensor_scalar(pads[:, a], pads[:, a], 1.0 / MASKED, SUPPORT - S, ALU.mult, ALU.add).then_inc(floor_steps.sem, 1)
                        dve.wait_ge(*floor_steps.at(g, 2))
                        v.tensor_scalar(nfloor[:, a], pads[:, a], 0.5, -3e38, ALU.is_gt, ALU.mult).then_inc(floor_steps.sem, 1)
                        dve.wait_ge(*floor_steps.at(g, 3))
                        v.tensor_scalar(nfloor[:, a], nfloor[:, a], 3e38, 1e4, ALU.add, ALU.max).then_inc(floor_steps.sem, 1)
                        dve.wait_ge(*floor_steps.at(g, 4))
                    if u >= 2:
                        n = 2 * (u - 2) + 1
                        dve.wait_ge(*projected.at(g, n + 1))
                        if n // CH == 1:
                            v.tensor_scalar(place(a, n), F_BANK[1][:], HD3 ** -0.5, None, ALU.mult).then_inc(odd_ready.sem, 1)
                        else:
                            v.tensor_copy(place(a, n), F_BANK[1][:]).then_inc(odd_ready.sem, 1)

                def maxima(g, a, u):
                    b, r = u // 2, u % 2
                    heads = slice(CH * r, CH * r + CH)
                    dve.wait_ge(*s_psum.at(g, u + 1))
                    v.tensor_reduce(rowmax[:, b, heads], S_BANK[r][:].rearrange("p (c k) -> p c k", c=CH),
                                    axis=AX, op=ALU.max, negate=True).then_inc(raw_max.sem, 1)
                    dve.wait_ge(*raw_max.at(g, u + 1))
                    v.tensor_scalar(nmax[:, b, heads], rowmax[:, b, heads], nfloor[:, a, b:b + 1], None, ALU.min).then_inc(max_ready.sem, 1)
                    if r == 1:
                        dve.wait_ge(*max_ready.at(g, u + 1))
                        v.tensor_scalar(eshift[:, b, :], nmax[:, b, :], 1e4, -1e4, ALU.min, ALU.add).then_inc(shift_ready.sem, 1)

                def copy_out(g, u, first):
                    dve.wait_ge(*t_psum.at(g, u + 1))
                    if not (first and u < 4) and u % 2 == 0:
                        dve.wait_ge(*av_psum.at(g, u // 2 - 1))
                    v.tensor_copy(probsT[:, u % 4, :], T_BANK[u % 2][:]).then_inc(pt_ready.sem, 1)

                def reciprocals(g, a, b):
                    dve.wait_ge(*e_ready.at(g, b + 1))
                    v.scalar_tensor_tensor(rsum[:, b, :], e[:, b, :], pads[:, a, b:b + 1], rsum[:, b, :], ALU.mult, ALU.add)\
                        .then_inc(sum_ready.sem, 1)
                    dve.wait_ge(*sum_ready.at(g, b + 1))
                    v.reciprocal(rrec[:, b, :], rsum[:, b, :]).then_inc(r_steps.sem, 1)

                def divided(g, b):
                    dve.wait_ge(*r_steps.at(g, b + 1))
                    dve.wait_ge(*av_psum.at(g, b + 1))
                    v.tensor_tensor(o[:, b % 2, :].rearrange("p (c r d) -> p c r d", c=CH, r=2), O_BANK[:].rearrange("p (c r d) -> p c r d", c=CH, r=2),
                                    rrec[:, b, :].rearrange("p (r c) -> p c r", r=2).unsqueeze(3).to_broadcast([128, CH, 2, HD3]),
                                    ALU.mult).then_inc(o_ready.sem, 1)

                def add_output(g, b):
                    dve.wait_ge(*y_psum.at(g, b + 1))
                    v.tensor_tensor(rows_of_x(p, g, b), rows_of_x(p, g, b), M_BANK[:, 0:D], ALU.add).then_inc(x_part.sem, 1)
                    if b == G - 1:
                        row_statistics(p, dve, g, x_part, G)

                def units(g, a, steps, first, last):
                    if first:
                        for u in range(U):
                            front(g, a, u)
                    for u in range(steps or AFTER):
                        if u % 2 == 0 and not (first and u < 4) and (steps or u < 4):
                            h, _, hu = before(g, a, u, 4, U)
                            divided(h, hu // 2)
                        if u % 2 == 1 and not (first and u < 7):
                            h, _, hu = before(g, a, u, 7, U)
                            add_output(h, hu // 2)
                        if steps:
                            maxima(g, a, u)
                        if not last and u:
                            front(g + 1, 1 - a, u)
                        if (steps or u < 1) and not (first and u < 1):
                            h, _, hu = before(g, a, u, 1, U)
                            copy_out(h, hu, first)
                        if u % 2 == 1 and not (first and u < 3) and (steps or u < 3):
                            h, ha, hu = before(g, a, u, 3, U)
                            reciprocals(h, ha, hu // 2)
                        if not last and u == 0:
                            front(g + 1, 1 - a, u)
                all_groups(dve, units, U)
        p.passed(NG)



def quantised_ffn(p, name, out):
    nc, ins, w = p.nc, p.inputs, p.w
    F, CH = 512, 4
    ROUND = 1.5 * 2 ** 23
    (xn_ready, q_steps, qT_psum, qT_ready, h_psum, h_in, h_ready, sums_ready, am_ready, ms_in, root_ready, tail, q2_steps,
     t_psum, t_ready, y_psum, x_done, added_steps) = p.plan(
        xn_ready=G, quantise_steps=5 + G, xnT_psum=1, xnT_ready=1, h_psum=G, relu_ready=G, h_ready=G, squares_ready=G,
        max_ready=G, variance_ready=1, root_ready=1, tail_steps=5, quantise_2_steps=G, t_psum=G, pt_ready=G, y_psum=1,
        x_done=1, added_steps=G)
    stored = p.count_of("out_stored")
    prep, prep_sum, prep_psum, prep_steps = p.plan(stage_prepared=0, weight_sums_ready=0, product_psum=0, weight_steps=0)
    M_BANK, T_BANK, Y_BANK = p.bank[6], p.bank[4:6], p.bank[7]
    with ExitStack() as ctx:
        t = lambda k, shape, dt=F32: sb(p, ctx, f"{name}_{k}", shape, dt)
        xn, y = t("xn", [128, GT]), t("y", [128, GT])
        w1, w2, q1, q2 = w["L3_ffn_w1T"], w["L3_ffn_w2T"], t("q1", [128, F], BF16), t("q2", [128, CH * D], BF16)
        ones, sums, mean, wscale = t("ones", [128, 128]), t("sums", [128, 2]), t("mean", [128, 2]), t("wscale", [128, 2])
        most, scale, back = t("most", [128, G]), t("scale", [128, G]), t("back", [128, G])
        xqT = t("xqT", [128, GT], BF16)
        pre, h, junk = t("pre", [128, G, F]), t("h", [128, 2, G, F]), t("junk", [128, F])
        ss, most2, veps, root, rs, scale2, back2 = (t(k, [128, G]) for k in ("ss", "most2", "veps", "root", "rs", "scale2", "back2"))
        hqT = t("hqT", [128, 2, CH * S], BF16)

        def weight_sums(pe):
            pe.wait_ge(*prep.at(0, 1))
            pe.wait_ge(*prep_sum.at(0, 2))
            nc.tensor.matmul(M_BANK[:, 0:2], lhsT=ones[:], rhs=sums[:], start=True, stop=True).then_inc(prep_psum.sem, 1)

        def quantise_weights(dve):
            v = nc.vector
            then = Chain(dve, prep_steps)
            for i, m in enumerate((w1, w2)):
                v.tensor_reduce(sums[:, i:i + 1], m[:], axis=AX, op=ALU.add, apply_absolute_value=True).then_inc(prep_sum.sem, 1)
            dve.wait_ge(*prep_psum.at(0, 1))
            then(v.tensor_scalar(mean[:], M_BANK[:, 0:2], 1.0 / (F * D), 1e-5, ALU.mult, ALU.max))
            then(v.reciprocal(wscale[:], mean[:]))
            for i, (m, q) in enumerate(((w1, q1), (w2, q2))):
                then(v.tensor_scalar(m[:], m[:], wscale[:, i:i + 1], ROUND, ALU.mult, ALU.add))
                then(v.tensor_scalar(m[:], m[:], ROUND, -1.0, ALU.subtract, ALU.max))
                then(v.tensor_scalar(q[:], m[:], 1.0, None, ALU.min))
            then(v.tensor_scalar(mean[:], mean[:], 1.0 / 127.0, None, ALU.mult))

        norm_rows(p, name, again=1e-6, table=ACT.Gelu, gpsimd=lambda pool: Chain(pool, prep)(nc.gpsimd.memset(ones[:], 1.0)),
                  tensor=weight_sums, vector=quantise_weights)
        for s, n in ((prep, 1), (prep_sum, 2), (prep_psum, 1), (prep_steps, 9)):
            s.base += n

        with nc.Block(no_gpsimd_drain=True) as block:
            @block.sync
            def _(sp):
                with sp.Fori(0, NG) as g:
                    sp.wait_ge(*x_done.at(g, 1))
                    sp.dma_start(out[:, ds(g * GT, GT)], rows_of_x(p, g, 0, G)).then_inc(stored.sem, 16)
                sp.wait_ge(stored.sem, 16 * NG)

            @block.tensor
            def _(pe):
                mm = nc.tensor.matmul

                def turn_x(g):
                    pe.wait_ge(*q_steps.at(g, q_steps.per))
                    for b in range(G):
                        last = nc.tensor.transpose(M_BANK[:, batch(b)], xn[:, batch(b)], p.ident[:])
                    last.then_inc(qT_psum.sem, 1)

                def up(g, first):
                    pe.wait_ge(*qT_ready.at(g, 1))
                    for b in range(G):
                        if not first:
                            pe.wait_ge(*h_in.at(g - 1, b + 1))
                        mm(p.bank[b][:], lhsT=xqT[:, batch(b)], rhs=q1[:], start=True, stop=True).then_inc(h_psum.sem, 1)

                def second_half(g, a, first, left):
                    def down(b):
                        pe.wait_ge(*t_ready.at(g, b + 1))
                        if b == 0 and not first:
                            pe.wait_ge(*added_steps.at(g - 1, G))
                        for ch in range(CH):
                            last = mm(Y_BANK[:, batch(b)], lhsT=hqT[:, b % 2, batch(ch)], rhs=q2[:, batch(ch)],
                                      start=(ch == 0), stop=(ch == CH - 1))
                        return last

                    for b in range(G):
                        pe.wait_ge(*q2_steps.at(g, b + 1))
                        if not (first and b < 2):
                            pe.wait_ge(*t_ready.at(g, b - 1))
                        for ch in range(CH):
                            last = nc.tensor.transpose(T_BANK[b % 2][:, batch(ch)], h[:, a, b, batch(ch)], p.ident[:])
                        last.then_inc(t_psum.sem, 1)
                        if b:
                            down(b - 1)
                    if left >= 2:
                        turn_x(g + 2)
                    down(G - 1).then_inc(y_psum.sem, 1)

                def body(g, a, left):
                    second_half(g, a, isinstance(g, int) and g == 0, left)
                    if left >= 2:
                        up(g + 2, False)

                for g in range(2):
                    turn_x(g)
                    up(g, g == 0)
                run_ahead(pe, body)

            @block.scalar
            def _(act):
                def copy_in(g):
                    act.wait_ge(*qT_psum.at(g, 1))
                    nc.scalar.activation(xqT[:], M_BANK[:], ACT.Copy, bias=-ROUND).then_inc(qT_ready.sem, 1)

                def gelu(g, a, b):
                    act.wait_ge(*h_in.at(g, b + 1))
                    nc.scalar.activation(h[:, a, b, :], pre[:, b, :], ACT.Gelu).then_inc(h_ready.sem, 1)
                    act.wait_ge(*h_ready.at(g, b + 1))
                    nc.scalar.activation(junk[:], h[:, a, b, :], ACT.Square, accum_out=ss[:, b:b + 1]).then_inc(sums_ready.sem, 1)

                def take_root(g):
                    act.wait_ge(*ms_in.at(g, 1))
                    nc.scalar.activation(root[:], veps[:], ACT.Sqrt).then_inc(root_ready.sem, 1)

                def copy_h(g, b):
                    act.wait_ge(*t_psum.at(g, b + 1))
                    nc.scalar.activation(hqT[:, b % 2, :], T_BANK[b % 2][:], ACT.Copy, bias=-ROUND).then_inc(t_ready.sem, 1)

                def body(g, a, left):
                    if left:
                        gelu(g + 1, 1 - a, 0)
                        gelu(g + 1, 1 - a, 1)
                    copy_h(g, 0)
                    copy_h(g, 1)
                    if left:
                        gelu(g + 1, 1 - a, 2)
                    copy_h(g, 2)
                    if left:
                        gelu(g + 1, 1 - a, 3)
                    copy_h(g, 3)
                    if left >= 2:
                        copy_in(g + 2)
                    if left:
                        take_root(g + 1)

                copy_in(0)
                for b in range(G):
                    gelu(0, 0, b)
                copy_in(1)
                take_root(0)
                run_ahead(act, body)

            @block.vector
            def _(dve):
                v = nc.vector

                def quantise_x(g):
                    normalise(p, dve, g, xn, xn_ready)
                    dve.wait_ge(*xn_ready.at(g, G))
                    then = Chain(dve, q_steps, g)
                    then(v.tensor_reduce(most[:], xn[:].rearrange("p (b d) -> p b d", b=G), axis=AX, op=ALU.max, apply_absolute_value=True))
                    then(v.tensor_scalar(most[:], most[:], 1e-5, None, ALU.max))
                    then(v.reciprocal(scale[:], most[:]))
                    then(v.tensor_scalar(scale[:], scale[:], 127.0, None, ALU.mult))
                    then(v.tensor_scalar(back[:], most[:], mean[:, 0:1], None, ALU.mult))
                    for b in range(G):
                        v.tensor_scalar(xn[:, batch(b)], xn[:, batch(b)], scale[:, b:b + 1], ROUND, ALU.mult, ALU.add).then_inc(q_steps.sem, 1)
                    then.n += G
                    then.ends()

                def scale_back(g, b):
                    dve.wait_ge(*h_psum.at(g, b + 1))
                    v.scalar_tensor_tensor(pre[:, b, :], p.bank[b][:], back[:, b:b + 1], w["L3_ffn_b1"][:], ALU.mult, ALU.add)\
                        .then_inc(h_in.sem, 1)

                def most_of_h(g, a, b):
                    dve.wait_ge(*h_ready.at(g, b + 1))
                    v.tensor_reduce(most2[:, b:b + 1], h[:, a, b, :], axis=AX, op=ALU.max, apply_absolute_value=True).then_inc(am_ready.sem, 1)

                def mean_squares(g):
                    dve.wait_ge(*sums_ready.at(g, G))
                    v.tensor_scalar(veps[:], ss[:], 1.0 / F, 1e-6, ALU.mult, ALU.add).then_inc(ms_in.sem, 1)

                def quantise_h(g, a):
                    dve.wait_ge(*root_ready.at(g, 1))
                    then = Chain(dve, tail, g)
                    dve.wait_ge(*am_ready.at(g, G))
                    then(v.reciprocal(rs[:], root[:]))
                    then(v.tensor_tensor(most2[:], most2[:], rs[:], ALU.mult))
                    then(v.tensor_scalar(most2[:], most2[:], 1e-5, None, ALU.max))
                    then(v.reciprocal(scale2[:], most2[:]))
                    v.tensor_scalar(back2[:], most2[:], mean[:, 1:2], None, ALU.mult)
                    then(v.scalar_tensor_tensor(scale2[:], scale2[:], 127.0, rs[:], ALU.mult, ALU.mult))
                    then.ends()
                    for b in range(G):
                        v.tensor_scalar(h[:, a, b, :], h[:, a, b, :], scale2[:, b:b + 1], ROUND, ALU.mult, ALU.add).then_inc(q2_steps.sem, 1)

                def add_output(g):
                    dve.wait_ge(*y_psum.at(g, 1))
                    for b in range(G):
                        v.scalar_tensor_tensor(y[:, batch(b)], Y_BANK[:, batch(b)], back2[:, b:b + 1], w["L3_ffn_b2"][:], ALU.mult, ALU.add)\
                            .then_inc(added_steps.sem, 1)
                    dve.wait_ge(*added_steps.at(g, G))
                    v.tensor_tensor(rows_of_x(p, g, 0, G), rows_of_x(p, g, 0, G), y[:], ALU.add).then_inc(x_done.sem, 1)
                    dve.wait_ge(*x_done.at(g, 1))

                def body(g, a, left):
                    if left:
                        for b in range(G):
                            scale_back(g + 1, b)
                    quantise_h(g, a)
                    if left >= 2:
                        quantise_x(g + 2)
                    if left:
                        for b in range(G):
                            most_of_h(g + 1, 1 - a, b)
                        mean_squares(g + 1)
                    add_output(g)

                quantise_x(0)
                for b in range(G):
                    scale_back(0, b)
                quantise_x(1)
                for b in range(G):
                    most_of_h(0, 0, b)
                mean_squares(0)
                run_ahead(dve, body)
        p.passed(NG)


def build(nc, inputs, out):
    with ExitStack() as ctx:
        p = Program(nc, ctx, inputs)
        p.out = out
        load_all(p)
        for stage in STAGES:
            stage(p)


STAGES = [
    lambda p: attention16(p, "L0a", "L0_attn_WQ", "L0_attn_WK", "L0_attn_WV", "L0_attn_WO", scale=HD ** -0.5, causal=True),
    lambda p: attention16(p, "L0x", "L0_xattn_w_q", "L0_xattn_w_k", "L0_xattn_w_v", "L0_xattn_w_o", cross=True,
                          b_q="L0_xattn_b_q", b_k="L0_xattn_b_k", b_v="L0_xattn_b_v", b_o="L0_xattn_b_o",
                          scale=HD ** -0.5, where_mask=True),
    lambda p: ffn_squared_relu(p, "L0f"),
    lambda p: linear_attention(p, "L1a"),
    lambda p: single_head(p, "L1x"),
    lambda p: ffn_sigmoid_experts(p, "L1f"),
    lambda p: channel_attention(p, "L2a"),
    lambda p: attention16(p, "L2x", "L2_xattn_Wq", "L2_xattn_Wk", "L2_xattn_Wv", cross=True, b_q="L2_xattn_bq",
                          b_k="L2_xattn_bk", b_v="L2_xattn_bv", key_mask=True),
    lambda p: ffn_linear_experts(p, "L2f"),
    lambda p: (latent_weights(p), attention16(p, "L3a", "L3_attn_W_q", "L3_K", "L3_V", "L3_attn_W_o", scale=D ** -0.5, decay=True)),
    lambda p: support_attention(p, "L3x"),
    lambda p: quantised_ffn(p, "L3f", p.out),
]



def layouts(i):
    a = {k: np.asarray(v) for k, v in i.items()}
    T = lambda m: np.ascontiguousarray(m.T)
    rows = lambda m: np.ascontiguousarray(m.transpose(1, 0, 2)).reshape(128, -1)
    cols = lambda m: np.ascontiguousarray(m.transpose(2, 0, 1)).reshape(128, -1)
    o = {"x": rows(a["x"]), "ctx_T": cols(a["ctx_1024"]), "ctx_rows": rows(a["ctx_1024"])}
    m = a["mask_Bx1xSxS2_if1"][:, 0]
    o["mask_qk"], o["mask_kq"] = rows(m), cols(m)
    o["key_mask"] = a["mask_BxS2_ik0"]
    o["visible"] = rows(a["mask_BxS2xS_ik0"])
    for n in ["L0_attn_WQ", "L0_attn_WK", "L0_attn_WV", "L0_attn_WO", "L2_xattn_Wq", "L2_xattn_Wk", "L2_xattn_Wv",
              "L1_attn_out_w"]:
        o[n] = T(a[n])
    for n in ["L0_xattn_w_q", "L0_xattn_w_k", "L0_xattn_w_v", "L0_xattn_w_o", "L2_attn_Wq", "L2_attn_Wk",
              "L2_attn_Wv", "L3_attn_W_q", "L3_attn_W_o", "L0_xattn_b_q", "L0_xattn_b_k", "L2_attn_bq",
              "L2_xattn_bq", "L2_xattn_bk", "L3_xattn_ln_w", "L3_xattn_ln_b", "L0_xattn_b_v", "L0_xattn_b_o",
              "L1_attn_out_b", "L2_attn_bk", "L2_attn_bv", "L2_xattn_bv", "L3_ffn_b1", "L3_ffn_b2", "L0_ffn_Wg",
              "L2_ffn_Wr", "L3_xattn_Wq", "L3_xattn_Wkv", "L3_attn_W_down_kv", "L3_attn_W_up_k", "L3_attn_W_up_v"]:
        o[n] = a[n]
    o["L0_ffn_W1"] = np.ascontiguousarray(a["L0_ffn_W1"].transpose(1, 0, 2))
    o["L0_ffn_W2"] = np.ascontiguousarray(a["L0_ffn_W2"].reshape(8, 2, 128, 128).transpose(2, 0, 1, 3))
    o["L2_ffn_WiT"] = np.ascontiguousarray(a["L2_ffn_Wi"].transpose(2, 0, 1))
    o["L2_ffn_Wo"] = np.ascontiguousarray(a["L2_ffn_Wo"].transpose(1, 0, 2))
    o["L1_ffn_keys"] = cols(a["L1_ffn_keys"].transpose(0, 2, 1))
    o["L1_ffn_values"] = rows(a["L1_ffn_values"])
    o["L3_ffn_w1T"] = T(a["L3_ffn_w1"])
    o["L3_ffn_w2T"] = rows(np.ascontiguousarray(a["L3_ffn_w2"].T).reshape(4, 128, 128))
    o["L1_ffn_sel"] = T(a["L1_ffn_expert_sel"])
    o["L3_attn_W_k_T"], o["L3_attn_W_v_T"] = T(a["L3_attn_W_k"]), T(a["L3_attn_W_v"])
    o["L3_xattn_Wout"] = np.ascontiguousarray(a["L3_xattn_Wout"].reshape(4, 128, 128).transpose(1, 0, 2))
    w, bias = a["L1_attn_qkvu_w"], a["L1_attn_qkvu_b"]
    twice = np.concatenate([np.r_[16 * h:16 * h + 16, 16 * h:16 * h + 16] for h in range(8)])
    order = np.concatenate([twice, 128 + twice])
    o["L1_attn_qk"] = np.ascontiguousarray(w[order].reshape(4, 128, 128).transpose(2, 0, 1))
    o["L1_attn_qk_b"] = np.ascontiguousarray(bias[order].reshape(4, 128).T)
    o["L1_attn_vu"] = np.ascontiguousarray(w[256:].reshape(2, 128, 128).transpose(2, 0, 1))
    o["L1_attn_vb"] = bias[256:384].copy()
    o["L1_attn_ub"] = bias[384:].reshape(128, 1).copy()
    th = a["L1_attn_theta"].reshape(128)[twice]
    o["L1_attn_theta"] = np.ascontiguousarray(th.reshape(2, 128).T)
    o["L1_attn_slope"] = a["L1_attn_slope_rate"].reshape(8)
    o["L2_attn_temp"] = np.repeat(a["L2_attn_temperature"].reshape(16), 8).reshape(128, 1)
    return o


def kernel(**inputs):
    import concourse.bacc as bacc
    from concourse.bass_utils import run_bass_kernel_spmd

    nc = bacc.Bacc("TRN2", target_bir_lowering=False, num_devices=1)
    arrays = layouts(inputs)
    aps = {n: nc.dram_tensor(n, a.shape, mybir.dt.from_np(a.dtype), kind="ExternalInput").ap() for n, a in arrays.items()}
    out = nc.dram_tensor("out", (128, B * D), F32, kind="ExternalOutput").ap()
    build(nc, aps, out)
    got = run_bass_kernel_spmd(nc, [arrays], core_ids=[0]).results[0]["out"]
    return np.ascontiguousarray(got.reshape(128, B, D).transpose(1, 0, 2))
```
